# Optimizing a Trainium2 kernel written in Bass

```python
import numpy as np
import jax
import jax.numpy as jnp

def _softmax(x, axis=-1):
    return jax.nn.softmax(x, axis=axis)

def _gelu(x):
    return jax.nn.gelu(x, approximate=True)

def _silu(x):
    return jax.nn.silu(x)

def _sigmoid(x):
    return jax.nn.sigmoid(x)

def _layernorm(x, axis=-1, eps=1e-05):
    m = jnp.mean(x, axis=axis, keepdims=True)
    v = jnp.var(x, axis=axis, keepdims=True)
    return (x - m) / jnp.sqrt(v + eps)

def _scatter_add(tgt, idx, src, axis=0):
    return tgt.at[idx].add(src)

def _segment_sum(src, seg, n):
    return jax.ops.segment_sum(src, seg, n)
kernel_name = 'mk_decoder_postln_d4_seqx_r4_60b82e'

def setup_inputs(seed: int=0):
    np.random.seed(seed)
    _w = jnp.asarray

    def _rec_inputs():
        import jax
        import jax.numpy as jnp
        _rk = jax.random.key(seed)
        x = 7.22e-05 + 1 * jax.random.normal(jax.random.fold_in(_rk, 1), (8, 100, 256), jnp.float32)
        _lenS = 100 - jax.random.randint(jax.random.fold_in(_rk, 7), (8,), 0, max(1, 100 // 4) + 1, jnp.int32)
        _lenS2 = 361 - jax.random.randint(jax.random.fold_in(_rk, 8), (8,), 0, max(1, 361 // 4) + 1, jnp.int32)
        _ctx_1024P = jax.random.normal(jax.random.fold_in(_rk, 11), (8, 16, 256), jnp.float32)
        _ctx_1024c = jax.random.dirichlet(jax.random.fold_in(_rk, 511), 0.3 * jnp.ones((16,), jnp.float32), (8, 361))
        _ctx_1024t = jnp.einsum('bsk,bkd->bsd', _ctx_1024c, _ctx_1024P)
        _ctx_1024t = _ctx_1024t * jax.lax.rsqrt(jnp.mean(jnp.square(_ctx_1024t)) + 1e-12) * 0.953939
        ctx_1024 = 4.13588e-05 + 0.999923 * (_ctx_1024t + 0.3 * jax.random.normal(jax.random.fold_in(_rk, 611), (8, 361, 256), jnp.float32))
        _validS = jnp.arange(100)[None, :] < _lenS[:, None]
        _validS2 = jnp.arange(361)[None, :] < _lenS2[:, None]
        _causal = jnp.tril(jnp.ones((100, 100), dtype=bool))
        mask_SxS_bc0 = jnp.logical_not(jnp.broadcast_to(_causal[:, :], (100, 100)))
        mask_Bx1xSxS2_ik0 = jnp.where(jnp.broadcast_to(_validS2[:, None, None, :], (8, 1, 100, 361)), 0, 1).astype(jnp.int32)
        return (x, ctx_1024, mask_SxS_bc0, mask_Bx1xSxS2_ik0)
    x, ctx_1024, mask_SxS_bc0, mask_Bx1xSxS2_ik0 = _rec_inputs()

    def _L0_attn_setup():
        import jax, jax.numpy as jnp
        import numpy as np
        from math import sqrt
        EMBED_DIM = 256
        NUM_HEADS = 16
        HEAD_DIM = EMBED_DIM // NUM_HEADS
        CAUSAL = True
        key = jax.random.key(seed)
        ks = jax.random.split(key, 5)
        B, S, E = (2, 512, EMBED_DIM)
        x = jax.random.normal(ks[0], (B, S, E), dtype=jnp.float32)
        scale = 1.0 / sqrt(E)
        Wq = jax.random.normal(ks[1], (E, E), dtype=jnp.float32) * scale
        Wk = jax.random.normal(ks[2], (E, E), dtype=jnp.float32) * scale
        Wv = jax.random.normal(ks[3], (E, E), dtype=jnp.float32) * scale
        Wo = jax.random.normal(ks[4], (E, E), dtype=jnp.float32) * scale
        return {'x': x, 'Wq': Wq, 'Wk': Wk, 'Wv': Wv, 'Wo': Wo}
    _L0_attn_all = _L0_attn_setup()
    _L0_attn_in = {k: v for k, v in _L0_attn_all.items() if k in ('Wq', 'Wk', 'Wv', 'Wo')}
    del _L0_attn_all

    def _L0_xattn_setup():
        import jax, jax.numpy as jnp
        import numpy as np
        NUM_HEADS = 16

        def softmax_one(x, axis=-1):
            m = jnp.max(x, axis=axis, keepdims=True)
            e = jnp.exp(x - m)
            return e / (jnp.exp(-m) * 0 + 1.0 + jnp.sum(e, axis=axis, keepdims=True))
        key = jax.random.key(seed)
        ks = jax.random.split(key, 10)
        B, Nq, Nk, D = (4, 512, 512, 256)
        s = 1.0 / np.sqrt(D)
        return {'q': jax.random.normal(ks[0], (B, Nq, D), jnp.float32), 'kv': jax.random.normal(ks[1], (B, Nk, D), jnp.float32), 'Wq': jax.random.normal(ks[2], (D, D), jnp.float32) * s, 'bq': jax.random.normal(ks[3], (D,), jnp.float32) * 0.01, 'Wk': jax.random.normal(ks[4], (D, D), jnp.float32) * s, 'bk': jax.random.normal(ks[5], (D,), jnp.float32) * 0.01, 'Wv': jax.random.normal(ks[6], (D, D), jnp.float32) * s, 'bv': jax.random.normal(ks[7], (D,), jnp.float32) * 0.01, 'Wp': jax.random.normal(ks[8], (D, D), jnp.float32) * s, 'bp': jax.random.normal(ks[9], (D,), jnp.float32) * 0.01}
    _L0_xattn_all = _L0_xattn_setup()
    _L0_xattn_in = {k: v for k, v in _L0_xattn_all.items() if k in ('Wq', 'bq', 'Wk', 'bk', 'Wv', 'bv', 'Wp', 'bp')}
    del _L0_xattn_all

    def _L0_ffn_setup():
        import jax, jax.numpy as jnp
        import numpy as np
        LN_EPS = 0.001
        EPS = 1e-05
        QB = 128.0

        def ste_round(x):
            return x + jax.lax.stop_gradient(jnp.round(x) - x)
        key = jax.random.key(seed)
        k1, k2 = jax.random.split(key)
        x = jax.random.normal(k1, (4, 2048, 256), dtype=jnp.float32)
        weight = jax.random.normal(k2, (256, 256), dtype=jnp.float32) * 0.02
        ln_gamma = jnp.ones((256,), dtype=jnp.float32)
        ln_beta = jnp.zeros((256,), dtype=jnp.float32)
        return {'x': x, 'weight': weight, 'ln_gamma': ln_gamma, 'ln_beta': ln_beta}
    _L0_ffn_all = _L0_ffn_setup()
    _L0_ffn_in = {k: v for k, v in _L0_ffn_all.items() if k in ('weight', 'ln_gamma', 'ln_beta')}
    del _L0_ffn_all

    def _L1_attn_setup():
        import jax, jax.numpy as jnp
        import numpy as np
        from functools import partial
        B_, L_, H_, DIN_, K_, N_, R_ = (2, 512, 256, 512, 4, 16, 64)

        def _selective_scan(x, delta, A, Bm, Cm, D):
            dA = jnp.exp(jnp.einsum('bld,dn->bldn', delta, A))
            dBx = jnp.einsum('bld,bln->bldn', delta * x, Bm)
            b, l, d, n = dA.shape

            def step(z, inp):
                dA_t, dBx_t, c_t = inp
                z = dA_t * z + dBx_t
                y = jnp.einsum('bdn,bn->bd', z, c_t)
                return (z, y)
            z0 = jnp.zeros((b, d, n), x.dtype)
            _, ys = jax.lax.scan(step, z0, (jnp.moveaxis(dA, 1, 0), jnp.moveaxis(dBx, 1, 0), jnp.moveaxis(Cm, 1, 0)))
            y = jnp.moveaxis(ys, 0, 1)
            return y + x * D
        key = jax.random.key(seed)
        ks = jax.random.split(key, 9)
        s = lambda f: 1.0 / f ** 0.5
        A = jnp.tile(jnp.arange(1, N_ + 1, dtype=jnp.float32)[None, :], (DIN_, 1))
        return {'hidden_states': jax.random.normal(ks[0], (B_, L_, H_), jnp.float32), 'w_in': jax.random.normal(ks[1], (2 * DIN_, H_), jnp.float32) * s(H_), 'w_conv': jax.random.normal(ks[2], (DIN_, 1, K_), jnp.float32) * s(DIN_), 'w_xproj': jax.random.normal(ks[3], (R_ + 2 * N_, DIN_), jnp.float32) * s(DIN_), 'w_dt': jax.random.normal(ks[4], (DIN_, R_), jnp.float32) * s(R_), 'b_dt': jnp.zeros((DIN_,), jnp.float32), 'A_log': jnp.log(A), 'D': jnp.ones((DIN_,), jnp.float32), 'w_out': jax.random.normal(ks[5], (H_, DIN_), jnp.float32) * s(DIN_)}
    _L1_attn_all = _L1_attn_setup()
    _L1_attn_in = {k: v for k, v in _L1_attn_all.items() if k in ('w_in', 'w_conv', 'w_xproj', 'w_dt', 'b_dt', 'A_log', 'D', 'w_out')}
    del _L1_attn_all

    def _L1_xattn_setup():
        import jax, jax.numpy as jnp
        import numpy as np
        NUM_HEADS = 16
        KEY_SIZE = 64
        VALUE_SIZE = 64
        MODEL_SIZE = 256
        B, S, D = (2, 512, 256)

        def _vs_init(key, shape):
            fan_in = shape[0]
            stddev = np.sqrt(1.0 / fan_in) / 0.8796256610342398
            return stddev * jax.random.truncated_normal(key, -2.0, 2.0, shape, dtype=jnp.float32)
        key = jax.random.key(seed)
        ks = jax.random.split(key, 7)
        query = jax.random.normal(ks[0], (B, S, D), dtype=jnp.float32)
        k_in = jax.random.normal(ks[1], (B, S, D), dtype=jnp.float32)
        v_in = jax.random.normal(ks[2], (B, S, D), dtype=jnp.float32)
        Wq = _vs_init(ks[3], (D, NUM_HEADS * KEY_SIZE))
        Wk = _vs_init(ks[4], (D, NUM_HEADS * KEY_SIZE))
        Wv = _vs_init(ks[5], (D, NUM_HEADS * VALUE_SIZE))
        Wo = _vs_init(ks[6], (NUM_HEADS * VALUE_SIZE, MODEL_SIZE))
        bq = jnp.zeros((NUM_HEADS * KEY_SIZE,), jnp.float32)
        bk = jnp.zeros((NUM_HEADS * KEY_SIZE,), jnp.float32)
        bv = jnp.zeros((NUM_HEADS * VALUE_SIZE,), jnp.float32)
        bo = jnp.zeros((MODEL_SIZE,), jnp.float32)
        return {'query': query, 'key': k_in, 'value': v_in, 'Wq': Wq, 'bq': bq, 'Wk': Wk, 'bk': bk, 'Wv': Wv, 'bv': bv, 'Wo': Wo, 'bo': bo}
    _L1_xattn_all = _L1_xattn_setup()
    _L1_xattn_in = {k: v for k, v in _L1_xattn_all.items() if k in ('Wq', 'bq', 'Wk', 'bk', 'Wv', 'bv', 'Wo', 'bo')}
    del _L1_xattn_all

    def _L1_ffn_setup():
        import jax, jax.numpy as jnp
        import numpy as np
        D = 256
        H = 16
        HD = D // H
        E = 32
        ES = 128
        K = 4
        B, S = (2, 256)
        ROPE_BASE = 10000.0

        def _layernorm(x, g, b):
            m = x.mean(-1, keepdims=True)
            v = ((x - m) ** 2).mean(-1, keepdims=True)
            return (x - m) * jax.lax.rsqrt(v + 1e-05) * g + b

        def _forward(src, wq, wk, wv, wp, wo, ln1_g, ln1_b, ln2_g, ln2_b, sel_w, keys, values):
            Bs, Ss, Ds = src.shape
            scale = 1.0 / jnp.sqrt(jnp.array(HD, dtype=src.dtype))
            x = _layernorm(src, ln1_g, ln1_b)
            q = (x @ wq).reshape(Bs, Ss, H, HD)
            k = (x @ wk).reshape(Bs, Ss, H, HD)
            v = (x @ wv).reshape(Bs, Ss, H, HD)
            pos = jnp.arange(Ss - 1, -Ss, -1, dtype=src.dtype)
            inv_freq = 1.0 / ROPE_BASE ** (jnp.arange(0, Ds, 2, dtype=src.dtype) / Ds)
            ang = pos[:, None] * inv_freq[None, :]
            pe = jnp.concatenate([jnp.sin(ang), jnp.cos(ang)], axis=-1)
            p = (pe @ wp).reshape(2 * Ss - 1, H, HD)
            ac = jnp.einsum('bihd,bjhd->bhij', q, k)
            bd_full = jnp.einsum('bihd,phd->bhip', q, p)
            rel = jnp.arange(Ss)[:, None] - jnp.arange(Ss)[None, :] + (Ss - 1)
            bd = bd_full[:, :, jnp.arange(Ss)[:, None], rel]
            att = jax.nn.softmax((ac + bd) * scale, axis=-1)
            attn_out = jnp.einsum('bhij,bjhd->bihd', att, v).reshape(Bs, Ss, Ds) @ wo
            src = src + attn_out
            x2 = _layernorm(src, ln2_g, ln2_b)
            sel = jax.nn.sigmoid(x2 @ sel_w)
            scores, idx = jax.lax.top_k(sel, K)
            gate = (jax.nn.one_hot(idx, E, dtype=sel.dtype) * scores[..., None]).sum(-2)
            h = jax.nn.relu(jnp.einsum('bsd,edh->bseh', x2, keys))
            moe_out = jnp.einsum('bseh,ehd,bse->bsd', h, values, gate)
            return src + moe_out
        key = jax.random.key(seed)
        ks = jax.random.split(key, 10)
        std_scale = np.sqrt(2.0 / 18)
        w_std = std_scale / np.sqrt(D)
        return {'src': jax.random.normal(ks[0], (B, S, D), jnp.float32), 'wq': jax.random.normal(ks[1], (D, H * HD), jnp.float32) * w_std, 'wk': jax.random.normal(ks[2], (D, H * HD), jnp.float32) * w_std, 'wv': jax.random.normal(ks[3], (D, H * HD), jnp.float32) * w_std, 'wp': jax.random.normal(ks[4], (D, H * HD), jnp.float32) * w_std, 'wo': jax.random.normal(ks[5], (H * HD, D), jnp.float32) * w_std, 'ln1_g': jnp.ones((D,), jnp.float32), 'ln1_b': jnp.zeros((D,), jnp.float32), 'ln2_g': jnp.ones((D,), jnp.float32), 'ln2_b': jnp.zeros((D,), jnp.float32), 'sel_w': jax.random.normal(ks[6], (D, E), jnp.float32) / np.sqrt(D), 'keys': jax.random.normal(ks[7], (E, D, ES), jnp.float32) * w_std, 'values': jax.random.normal(ks[8], (E, ES, D), jnp.float32) * (std_scale / np.sqrt(ES))}
    _L1_ffn_all = _L1_ffn_setup()
    _L1_ffn_in = {k: v for k, v in _L1_ffn_all.items() if k in ('wq', 'wk', 'wv', 'wp', 'wo', 'ln1_g', 'ln1_b', 'ln2_g', 'ln2_b', 'sel_w', 'keys', 'values')}
    del _L1_ffn_all

    def _L2_attn_setup():
        import jax, jax.numpy as jnp
        import numpy as np
        import math
        B, L, HID, NH = (4, 1024, 256, 8)
        DH = HID // NH
        THETA = 10000.0

        def _rope_tables(seq_len, dh):
            half = dh // 2
            inv_freq = 1.0 / THETA ** (jnp.arange(half, dtype=jnp.float32) / half)
            freqs = jnp.arange(seq_len, dtype=jnp.float32)[:, None] * inv_freq[None, :]
            return (jnp.cos(freqs), jnp.sin(freqs))

        def _apply_rope(x, cos, sin):
            half = x.shape[-1] // 2
            x1, x2 = (x[..., :half], x[..., half:2 * half])
            c = cos[None, None]
            s = sin[None, None]
            return jnp.concatenate([x1 * c - x2 * s, x1 * s + x2 * c], axis=-1)
        key = jax.random.key(seed)
        ks = jax.random.split(key, 9)

        def xav(k, sh):
            lim = math.sqrt(6.0 / (sh[0] + sh[1]))
            return jax.random.uniform(k, sh, jnp.float32, -lim, lim)
        return {'x': jax.random.normal(ks[0], (B, L, HID), jnp.float32), 'norm_w': jnp.ones((HID,), jnp.float32), 'Wq': xav(ks[1], (HID, HID)), 'Wk': xav(ks[2], (HID, HID)), 'Wv': xav(ks[3], (HID, HID)), 'Wbeta': xav(ks[4], (NH, HID)), 'bbeta': jnp.full((NH,), 2.0, jnp.float32), 'Wig': xav(ks[5], (NH, HID)), 'big': jnp.zeros((NH,), jnp.float32), 'Wog': xav(ks[6], (NH, HID)), 'bog': jnp.zeros((NH,), jnp.float32), 'Wout': xav(ks[7], (HID, HID)), 'bout': jnp.zeros((HID,), jnp.float32)}
    _L2_attn_all = _L2_attn_setup()
    _L2_attn_in = {k: v for k, v in _L2_attn_all.items() if k in ('norm_w', 'Wq', 'Wk', 'Wv', 'Wbeta', 'bbeta', 'Wig', 'big', 'Wog', 'bog', 'Wout', 'bout')}
    del _L2_attn_all

    def _L2_xattn_setup():
        import jax, jax.numpy as jnp
        import numpy as np
        from jax import lax
        H = 16
        K1, K2 = (3, 3)
        LN_EPS = 1e-05

        def _ln(x, g, b):
            m = jnp.mean(x, axis=-1, keepdims=True)
            v = jnp.mean(jnp.square(x - m), axis=-1, keepdims=True)
            return (x - m) * lax.rsqrt(v + LN_EPS) * g + b

        def _gelu(x):
            return jax.nn.gelu(x, approximate=False)
        key = jax.random.key(seed)
        B, T, D, Th = (4, 256, 256, 64)
        C = 2 * D
        ks = jax.random.split(key, 16)

        def w(k, shape):
            fan_in = shape[0]
            return (jax.random.normal(k, shape, jnp.float32) / np.sqrt(fan_in)).astype(jnp.float32)
        inp = {'x': jax.random.normal(ks[0], (B, T, D), jnp.float32), 'historical_data': jax.random.normal(ks[1], (B, Th, D), jnp.float32), 'Wq': w(ks[2], (D, D)), 'Wk': w(ks[3], (D, D)), 'Wv': w(ks[4], (D, D)), 'hist_W': w(ks[5], (D, C)), 'hist_b': jnp.zeros((C,), jnp.float32), 'hist_ln_g': jnp.ones((C,), jnp.float32), 'hist_ln_b': jnp.zeros((C,), jnp.float32), 'ctx_W1': w(ks[6], (C, C // 4)), 'ctx_b1': jnp.zeros((C // 4,), jnp.float32), 'ctx_W2': w(ks[7], (C // 4, 1)), 'ctx_b2': jnp.zeros((1,), jnp.float32), 'kg_W1': w(ks[8], (C, D)), 'kg_b1': jnp.zeros((D,), jnp.float32), 'kg_ln_g': jnp.ones((D,), jnp.float32), 'kg_ln_b': jnp.zeros((D,), jnp.float32), 'kg_W2': w(ks[9], (D, H * K1 * K2)), 'kg_b2': jnp.zeros((H * K1 * K2,), jnp.float32), 'proj_W': w(ks[10], (D, D)), 'proj_b': jnp.zeros((D,), jnp.float32), 'causal_mask': jnp.triu(jnp.ones((T, T), bool), k=1)}
        return inp
    _L2_xattn_all = _L2_xattn_setup()
    _L2_xattn_in = {k: v for k, v in _L2_xattn_all.items() if k in ('Wq', 'Wk', 'Wv', 'hist_W', 'hist_b', 'hist_ln_g', 'hist_ln_b', 'ctx_W1', 'ctx_b1', 'ctx_W2', 'ctx_b2', 'kg_W1', 'kg_b1', 'kg_ln_g', 'kg_ln_b', 'kg_W2', 'kg_b2', 'proj_W', 'proj_b')}
    del _L2_xattn_all

    def _L2_ffn_setup():
        import jax, jax.numpy as jnp
        import numpy as np
        S, B, D = (256, 2, 256)
        E, TOPK = (15, 3)
        F = 256
        FS = 512

        def _uinit(k, shape, out_dim):
            std = out_dim ** (-0.5)
            return jax.random.uniform(k, shape, jnp.float32, -std, std)
        key = jax.random.key(seed)
        ks = jax.random.split(key, 10)
        return {'x': jax.random.normal(ks[0], (S, B, D), jnp.float32), 'gate_w': jax.random.normal(ks[1], (E, D), jnp.float32) * D ** (-0.5), 'fc1_w': _uinit(ks[2], (E, 2 * F, D), 2 * F), 'fc1_b': _uinit(ks[3], (E, 2 * F), 2 * F), 'geglu_mult': jnp.ones((E, F), jnp.float32), 'fc2_w': _uinit(ks[4], (E, D, F), D), 'fc2_b': _uinit(ks[5], (E, D), D), 's_fc1_w': _uinit(ks[6], (2 * FS, D), 2 * FS), 's_fc1_b': _uinit(ks[7], (2 * FS,), 2 * FS), 's_geglu_mult': jnp.ones((FS,), jnp.float32), 's_fc2_w': _uinit(ks[8], (D, FS), D), 's_fc2_b': _uinit(ks[9], (D,), D)}
    _L2_ffn_all = _L2_ffn_setup()
    _L2_ffn_in = {k: v for k, v in _L2_ffn_all.items() if k in ('gate_w', 'fc1_w', 'fc1_b', 'geglu_mult', 'fc2_w', 'fc2_b', 's_fc1_w', 's_fc1_b', 's_geglu_mult', 's_fc2_w', 's_fc2_b')}
    del _L2_ffn_all

    def _L3_attn_setup():
        import jax, jax.numpy as jnp
        import numpy as np
        D_MODEL = 256
        key = jax.random.key(seed)
        k1, k2, k3 = jax.random.split(key, 3)
        x = jax.random.normal(k1, (4, 512, D_MODEL), dtype=jnp.float32)
        wqk = jax.random.normal(k2, (D_MODEL, D_MODEL), dtype=jnp.float32) * 0.02
        wov = jax.random.normal(k3, (D_MODEL, D_MODEL), dtype=jnp.float32) * 0.02
        return {'x': x, 'wqk': wqk, 'wov': wov}
    _L3_attn_all = _L3_attn_setup()
    _L3_attn_in = {k: v for k, v in _L3_attn_all.items() if k in ('wqk', 'wov')}
    del _L3_attn_all

    def _L3_xattn_setup():
        import jax, jax.numpy as jnp
        import numpy as np
        D_MODEL = 256
        N_HEADS = 16
        D_K = D_MODEL // N_HEADS
        B, S = (2, 512)

        def _rope_emb(seq_len, d_k):
            inv_freq = 1.0 / 10000.0 ** (jnp.arange(0, d_k, 2, dtype=jnp.float32) / d_k)
            t = jnp.arange(seq_len, dtype=jnp.float32)
            freqs = jnp.outer(t, inv_freq)
            return jnp.concatenate([freqs, freqs], axis=-1)

        def _rotate_half(x):
            x1, x2 = jnp.split(x, 2, axis=-1)
            return jnp.concatenate([-x2, x1], axis=-1)

        def _apply_rope(x, emb):
            return x * jnp.cos(emb)[None, None] + _rotate_half(x) * jnp.sin(emb)[None, None]
        key = jax.random.key(seed)
        ks = jax.random.split(key, 7)
        scale = 1.0 / np.sqrt(D_MODEL)
        q = jax.random.normal(ks[0], (B, S, D_MODEL), dtype=jnp.float32)
        k = jax.random.normal(ks[1], (B, S, D_MODEL), dtype=jnp.float32)
        v = jax.random.normal(ks[2], (B, S, D_MODEL), dtype=jnp.float32)
        W_q = jax.random.normal(ks[3], (D_MODEL, D_MODEL), dtype=jnp.float32) * scale
        W_k = jax.random.normal(ks[4], (D_MODEL, D_MODEL), dtype=jnp.float32) * scale
        W_v = jax.random.normal(ks[5], (D_MODEL, D_MODEL), dtype=jnp.float32) * scale
        W_o = jax.random.normal(ks[6], (D_MODEL, D_MODEL), dtype=jnp.float32) * scale
        mask = jnp.tril(jnp.ones((S, S), dtype=jnp.int32))[None, None]
        mask = jnp.broadcast_to(mask, (B, 1, S, S))
        return {'query': q, 'key': k, 'value': v, 'mask': mask, 'W_q': W_q, 'W_k': W_k, 'W_v': W_v, 'W_o': W_o}
    _L3_xattn_all = _L3_xattn_setup()
    _L3_xattn_in = {k: v for k, v in _L3_xattn_all.items() if k in ('W_q', 'W_k', 'W_v', 'W_o')}
    del _L3_xattn_all

    def _L3_ffn_setup():
        import jax, jax.numpy as jnp
        import numpy as np
        B, T, C = (2, 256, 256)
        H = 1024
        E_R, E_S, K = (8, 2, 2)

        def _rmsnorm(x, g):
            eps = jnp.finfo(x.dtype).eps
            return x * jax.lax.rsqrt(jnp.mean(x * x, axis=-1, keepdims=True) + eps) * g

        def _experts_mlp(x, g, W1, b1, W2, b2):
            xn = _rmsnorm(x, g)
            h = jnp.einsum('btc,ech->bteh', xn, W1) + b1
            h = jax.nn.gelu(h, approximate=False)
            return jnp.einsum('bteh,ehc->btec', h, W2) + b2
        key = jax.random.key(seed)
        ks = jax.random.split(key, 12)
        s = 0.02
        return {'u': jax.random.normal(ks[0], (B, T, C), dtype=jnp.float32), 'g_shared': jnp.ones((C,), jnp.float32), 'W1_s': jax.random.normal(ks[1], (E_S, C, H), jnp.float32) * s, 'b1_s': jax.random.normal(ks[2], (E_S, H), jnp.float32) * s, 'W2_s': jax.random.normal(ks[3], (E_S, H, C), jnp.float32) * s, 'b2_s': jax.random.normal(ks[4], (E_S, C), jnp.float32) * s, 'g_routed': jnp.ones((C,), jnp.float32), 'W1_r': jax.random.normal(ks[5], (E_R, C, H), jnp.float32) * s, 'b1_r': jax.random.normal(ks[6], (E_R, H), jnp.float32) * s, 'W2_r': jax.random.normal(ks[7], (E_R, H, C), jnp.float32) * s, 'b2_r': jax.random.normal(ks[8], (E_R, C), jnp.float32) * s, 'centroids': jax.random.normal(ks[9], (C, E_R), jnp.float32) * s}
    _L3_ffn_all = _L3_ffn_setup()
    _L3_ffn_in = {k: v for k, v in _L3_ffn_all.items() if k in ('g_shared', 'W1_s', 'b1_s', 'W2_s', 'b2_s', 'g_routed', 'W1_r', 'b1_r', 'W2_r', 'b2_r', 'centroids')}
    del _L3_ffn_all
    return {'x': x, 'ctx_1024': ctx_1024, 'mask_SxS_bc0': mask_SxS_bc0, 'mask_Bx1xSxS2_ik0': mask_Bx1xSxS2_ik0, 'L0_attn_Wq': _L0_attn_in['Wq'], 'L0_attn_Wk': _L0_attn_in['Wk'], 'L0_attn_Wv': _L0_attn_in['Wv'], 'L0_attn_Wo': _L0_attn_in['Wo'], 'L0_xattn_Wq': _L0_xattn_in['Wq'], 'L0_xattn_bq': _L0_xattn_in['bq'], 'L0_xattn_Wk': _L0_xattn_in['Wk'], 'L0_xattn_bk': _L0_xattn_in['bk'], 'L0_xattn_Wv': _L0_xattn_in['Wv'], 'L0_xattn_bv': _L0_xattn_in['bv'], 'L0_xattn_Wp': _L0_xattn_in['Wp'], 'L0_xattn_bp': _L0_xattn_in['bp'], 'L0_ffn_weight': _L0_ffn_in['weight'], 'L0_ffn_ln_gamma': _L0_ffn_in['ln_gamma'], 'L0_ffn_ln_beta': _L0_ffn_in['ln_beta'], 'L1_attn_w_in': _L1_attn_in['w_in'], 'L1_attn_w_conv': _L1_attn_in['w_conv'], 'L1_attn_w_xproj': _L1_attn_in['w_xproj'], 'L1_attn_w_dt': _L1_attn_in['w_dt'], 'L1_attn_b_dt': _L1_attn_in['b_dt'], 'L1_attn_A_log': _L1_attn_in['A_log'], 'L1_attn_D': _L1_attn_in['D'], 'L1_attn_w_out': _L1_attn_in['w_out'], 'L1_xattn_Wq': _L1_xattn_in['Wq'], 'L1_xattn_bq': _L1_xattn_in['bq'], 'L1_xattn_Wk': _L1_xattn_in['Wk'], 'L1_xattn_bk': _L1_xattn_in['bk'], 'L1_xattn_Wv': _L1_xattn_in['Wv'], 'L1_xattn_bv': _L1_xattn_in['bv'], 'L1_xattn_Wo': _L1_xattn_in['Wo'], 'L1_xattn_bo': _L1_xattn_in['bo'], 'L1_ffn_wq': _L1_ffn_in['wq'], 'L1_ffn_wk': _L1_ffn_in['wk'], 'L1_ffn_wv': _L1_ffn_in['wv'], 'L1_ffn_wp': _L1_ffn_in['wp'], 'L1_ffn_wo': _L1_ffn_in['wo'], 'L1_ffn_ln1_g': _L1_ffn_in['ln1_g'], 'L1_ffn_ln1_b': _L1_ffn_in['ln1_b'], 'L1_ffn_ln2_g': _L1_ffn_in['ln2_g'], 'L1_ffn_ln2_b': _L1_ffn_in['ln2_b'], 'L1_ffn_sel_w': _L1_ffn_in['sel_w'], 'L1_ffn_keys': _L1_ffn_in['keys'], 'L1_ffn_values': _L1_ffn_in['values'], 'L2_attn_norm_w': _L2_attn_in['norm_w'], 'L2_attn_Wq': _L2_attn_in['Wq'], 'L2_attn_Wk': _L2_attn_in['Wk'], 'L2_attn_Wv': _L2_attn_in['Wv'], 'L2_attn_Wbeta': _L2_attn_in['Wbeta'], 'L2_attn_bbeta': _L2_attn_in['bbeta'], 'L2_attn_Wig': _L2_attn_in['Wig'], 'L2_attn_big': _L2_attn_in['big'], 'L2_attn_Wog': _L2_attn_in['Wog'], 'L2_attn_bog': _L2_attn_in['bog'], 'L2_attn_Wout': _L2_attn_in['Wout'], 'L2_attn_bout': _L2_attn_in['bout'], 'L2_xattn_Wq': _L2_xattn_in['Wq'], 'L2_xattn_Wk': _L2_xattn_in['Wk'], 'L2_xattn_Wv': _L2_xattn_in['Wv'], 'L2_xattn_hist_W': _L2_xattn_in['hist_W'], 'L2_xattn_hist_b': _L2_xattn_in['hist_b'], 'L2_xattn_hist_ln_g': _L2_xattn_in['hist_ln_g'], 'L2_xattn_hist_ln_b': _L2_xattn_in['hist_ln_b'], 'L2_xattn_ctx_W1': _L2_xattn_in['ctx_W1'], 'L2_xattn_ctx_b1': _L2_xattn_in['ctx_b1'], 'L2_xattn_ctx_W2': _L2_xattn_in['ctx_W2'], 'L2_xattn_ctx_b2': _L2_xattn_in['ctx_b2'], 'L2_xattn_kg_W1': _L2_xattn_in['kg_W1'], 'L2_xattn_kg_b1': _L2_xattn_in['kg_b1'], 'L2_xattn_kg_ln_g': _L2_xattn_in['kg_ln_g'], 'L2_xattn_kg_ln_b': _L2_xattn_in['kg_ln_b'], 'L2_xattn_kg_W2': _L2_xattn_in['kg_W2'], 'L2_xattn_kg_b2': _L2_xattn_in['kg_b2'], 'L2_xattn_proj_W': _L2_xattn_in['proj_W'], 'L2_xattn_proj_b': _L2_xattn_in['proj_b'], 'L2_ffn_gate_w': _L2_ffn_in['gate_w'], 'L2_ffn_fc1_w': _L2_ffn_in['fc1_w'], 'L2_ffn_fc1_b': _L2_ffn_in['fc1_b'], 'L2_ffn_geglu_mult': _L2_ffn_in['geglu_mult'], 'L2_ffn_fc2_w': _L2_ffn_in['fc2_w'], 'L2_ffn_fc2_b': _L2_ffn_in['fc2_b'], 'L2_ffn_s_fc1_w': _L2_ffn_in['s_fc1_w'], 'L2_ffn_s_fc1_b': _L2_ffn_in['s_fc1_b'], 'L2_ffn_s_geglu_mult': _L2_ffn_in['s_geglu_mult'], 'L2_ffn_s_fc2_w': _L2_ffn_in['s_fc2_w'], 'L2_ffn_s_fc2_b': _L2_ffn_in['s_fc2_b'], 'L3_attn_wqk': _L3_attn_in['wqk'], 'L3_attn_wov': _L3_attn_in['wov'], 'L3_xattn_W_q': _L3_xattn_in['W_q'], 'L3_xattn_W_k': _L3_xattn_in['W_k'], 'L3_xattn_W_v': _L3_xattn_in['W_v'], 'L3_xattn_W_o': _L3_xattn_in['W_o'], 'L3_ffn_g_shared': _L3_ffn_in['g_shared'], 'L3_ffn_W1_s': _L3_ffn_in['W1_s'], 'L3_ffn_b1_s': _L3_ffn_in['b1_s'], 'L3_ffn_W2_s': _L3_ffn_in['W2_s'], 'L3_ffn_b2_s': _L3_ffn_in['b2_s'], 'L3_ffn_g_routed': _L3_ffn_in['g_routed'], 'L3_ffn_W1_r': _L3_ffn_in['W1_r'], 'L3_ffn_b1_r': _L3_ffn_in['b1_r'], 'L3_ffn_W2_r': _L3_ffn_in['W2_r'], 'L3_ffn_b2_r': _L3_ffn_in['b2_r'], 'L3_ffn_centroids': _L3_ffn_in['centroids']}

def reference(x, ctx_1024, mask_SxS_bc0, mask_Bx1xSxS2_ik0, L0_attn_Wq, L0_attn_Wk, L0_attn_Wv, L0_attn_Wo, L0_xattn_Wq, L0_xattn_bq, L0_xattn_Wk, L0_xattn_bk, L0_xattn_Wv, L0_xattn_bv, L0_xattn_Wp, L0_xattn_bp, L0_ffn_weight, L0_ffn_ln_gamma, L0_ffn_ln_beta, L1_attn_w_in, L1_attn_w_conv, L1_attn_w_xproj, L1_attn_w_dt, L1_attn_b_dt, L1_attn_A_log, L1_attn_D, L1_attn_w_out, L1_xattn_Wq, L1_xattn_bq, L1_xattn_Wk, L1_xattn_bk, L1_xattn_Wv, L1_xattn_bv, L1_xattn_Wo, L1_xattn_bo, L1_ffn_wq, L1_ffn_wk, L1_ffn_wv, L1_ffn_wp, L1_ffn_wo, L1_ffn_ln1_g, L1_ffn_ln1_b, L1_ffn_ln2_g, L1_ffn_ln2_b, L1_ffn_sel_w, L1_ffn_keys, L1_ffn_values, L2_attn_norm_w, L2_attn_Wq, L2_attn_Wk, L2_attn_Wv, L2_attn_Wbeta, L2_attn_bbeta, L2_attn_Wig, L2_attn_big, L2_attn_Wog, L2_attn_bog, L2_attn_Wout, L2_attn_bout, L2_xattn_Wq, L2_xattn_Wk, L2_xattn_Wv, L2_xattn_hist_W, L2_xattn_hist_b, L2_xattn_hist_ln_g, L2_xattn_hist_ln_b, L2_xattn_ctx_W1, L2_xattn_ctx_b1, L2_xattn_ctx_W2, L2_xattn_ctx_b2, L2_xattn_kg_W1, L2_xattn_kg_b1, L2_xattn_kg_ln_g, L2_xattn_kg_ln_b, L2_xattn_kg_W2, L2_xattn_kg_b2, L2_xattn_proj_W, L2_xattn_proj_b, L2_ffn_gate_w, L2_ffn_fc1_w, L2_ffn_fc1_b, L2_ffn_geglu_mult, L2_ffn_fc2_w, L2_ffn_fc2_b, L2_ffn_s_fc1_w, L2_ffn_s_fc1_b, L2_ffn_s_geglu_mult, L2_ffn_s_fc2_w, L2_ffn_s_fc2_b, L3_attn_wqk, L3_attn_wov, L3_xattn_W_q, L3_xattn_W_k, L3_xattn_W_v, L3_xattn_W_o, L3_ffn_g_shared, L3_ffn_W1_s, L3_ffn_b1_s, L3_ffn_W2_s, L3_ffn_b2_s, L3_ffn_g_routed, L3_ffn_W1_r, L3_ffn_b1_r, L3_ffn_W2_r, L3_ffn_b2_r, L3_ffn_centroids):
    import jax
    import jax.numpy as jnp

    def _L0_attn_ref(x, Wq, Wk, Wv, Wo):
        import jax, jax.numpy as jnp
        import numpy as np
        from math import sqrt
        EMBED_DIM = 256
        NUM_HEADS = 16
        HEAD_DIM = EMBED_DIM // NUM_HEADS
        CAUSAL = True
        B, S, E = x.shape
        H, D = (NUM_HEADS, HEAD_DIM)

        def proj(W):
            y = jnp.einsum('bse,fe->bsf', x, W)
            return y.reshape(B, S, H, D).transpose(0, 2, 1, 3)
        q, k, v = (proj(Wq), proj(Wk), proj(Wv))
        scores = jnp.einsum('bhsd,bhtd->bhst', q, k)
        if CAUSAL:
            mask = jnp.triu(jnp.ones((S, S), dtype=bool), k=1)
            scores = jnp.where(mask, -jnp.inf, scores)
        attn = jax.nn.softmax(scores / sqrt(D), axis=-1)
        out = jnp.einsum('bhst,bhtd->bhsd', attn, v)
        out = out.transpose(0, 2, 1, 3).reshape(B, S, E)
        return jnp.einsum('bse,fe->bsf', out, Wo)

    def _L0_xattn_ref(q, kv, Wq, bq, Wk, bk, Wv, bv, Wp, bp):
        import jax, jax.numpy as jnp
        import numpy as np
        NUM_HEADS = 16

        def softmax_one(x, axis=-1):
            m = jnp.max(x, axis=axis, keepdims=True)
            e = jnp.exp(x - m)
            return e / (jnp.exp(-m) * 0 + 1.0 + jnp.sum(e, axis=axis, keepdims=True))
        B, Nq, D = q.shape
        Nk = kv.shape[1]
        H = NUM_HEADS
        hd = D // H
        scale = hd ** (-0.5)
        qh = (q @ Wq.T + bq).reshape(B, Nq, H, hd).transpose(0, 2, 1, 3)
        kh = (kv @ Wk.T + bk).reshape(B, Nk, H, hd).transpose(0, 2, 1, 3)
        vh = (kv @ Wv.T + bv).reshape(B, Nk, H, hd).transpose(0, 2, 1, 3)
        attn = jnp.einsum('bhqd,bhkd->bhqk', qh * scale, kh)
        attn = softmax_one(attn, axis=-1)
        x = jnp.einsum('bhqk,bhkd->bhqd', attn, vh)
        x = x.transpose(0, 2, 1, 3).reshape(B, Nq, D)
        return x @ Wp.T + bp

    def _L0_ffn_ref(x, weight, ln_gamma, ln_beta):
        import jax, jax.numpy as jnp
        import numpy as np
        LN_EPS = 0.001
        EPS = 1e-05
        QB = 128.0

        def ste_round(x):
            return x + jax.lax.stop_gradient(jnp.round(x) - x)
        mu = jnp.mean(x, axis=-1, keepdims=True)
        var = jnp.var(x, axis=-1, keepdims=True)
        xn = (x - mu) * jax.lax.rsqrt(var + LN_EPS) * ln_gamma + ln_beta
        beta = jnp.mean(jnp.abs(weight))
        w_q = jnp.clip(ste_round(weight / (beta + EPS)), -1.0, 1.0)
        gamma = jnp.max(jnp.abs(xn))
        xq = jnp.clip(xn * QB / gamma, -QB + EPS, QB - EPS)
        y = jnp.einsum('bsd,du->bsu', xq, w_q)
        return y * (gamma * beta / QB)

    def _L1_attn_ref(hidden_states, w_in, w_conv, w_xproj, w_dt, b_dt, A_log, D, w_out):
        import jax, jax.numpy as jnp
        import numpy as np
        from functools import partial
        B_, L_, H_, DIN_, K_, N_, R_ = (2, 512, 256, 512, 4, 16, 64)

        def _selective_scan(x, delta, A, Bm, Cm, D):
            dA = jnp.exp(jnp.einsum('bld,dn->bldn', delta, A))
            dBx = jnp.einsum('bld,bln->bldn', delta * x, Bm)
            b, l, d, n = dA.shape

            def step(z, inp):
                dA_t, dBx_t, c_t = inp
                z = dA_t * z + dBx_t
                y = jnp.einsum('bdn,bn->bd', z, c_t)
                return (z, y)
            z0 = jnp.zeros((b, d, n), x.dtype)
            _, ys = jax.lax.scan(step, z0, (jnp.moveaxis(dA, 1, 0), jnp.moveaxis(dBx, 1, 0), jnp.moveaxis(Cm, 1, 0)))
            y = jnp.moveaxis(ys, 0, 1)
            return y + x * D
        b, l, h = hidden_states.shape
        d_in, n = A_log.shape
        hs_res = hidden_states @ w_in.T
        hs, res = (hs_res[..., :d_in], hs_res[..., d_in:])
        xc = jnp.moveaxis(hs, 1, 2)
        xc = jax.lax.conv_general_dilated(xc, w_conv, window_strides=(1,), padding=[(K_ - 1, 0)], dimension_numbers=('NCH', 'OIH', 'NCH'), feature_group_count=d_in)
        hs = jax.nn.silu(jnp.moveaxis(xc, 1, 2))
        A = -jnp.exp(A_log)
        x_dbl = hs @ w_xproj.T
        dt, Bm, Cm = (x_dbl[..., :R_], x_dbl[..., R_:R_ + n], x_dbl[..., R_ + n:])
        delta = jax.nn.softplus(dt @ w_dt.T + b_dt)
        y = _selective_scan(hs, delta, A, Bm, Cm, D)
        y = y * jax.nn.silu(res)
        return y @ w_out.T

    def _L1_xattn_ref(query, key, value, Wq, bq, Wk, bk, Wv, bv, Wo, bo):
        import jax, jax.numpy as jnp
        import numpy as np
        NUM_HEADS = 16
        KEY_SIZE = 64
        VALUE_SIZE = 64
        MODEL_SIZE = 256
        B, S, D = (2, 512, 256)

        def _vs_init(key, shape):
            fan_in = shape[0]
            stddev = np.sqrt(1.0 / fan_in) / 0.8796256610342398
            return stddev * jax.random.truncated_normal(key, -2.0, 2.0, shape, dtype=jnp.float32)
        b, s, _ = query.shape
        q = (query @ Wq + bq).reshape(b, s, NUM_HEADS, KEY_SIZE)
        k = (key @ Wk + bk).reshape(b, key.shape[1], NUM_HEADS, KEY_SIZE)
        v = (value @ Wv + bv).reshape(b, value.shape[1], NUM_HEADS, VALUE_SIZE)
        logits = jnp.einsum('bshd,bShd->bhsS', q, k) / np.sqrt(KEY_SIZE).astype(np.float32)
        weights = jax.nn.softmax(logits, axis=-1)
        attn = jnp.einsum('bhsS,bShd->bshd', weights, v).reshape(b, s, NUM_HEADS * VALUE_SIZE)
        return attn @ Wo + bo

    def _L1_ffn_ref(src, wq, wk, wv, wp, wo, ln1_g, ln1_b, ln2_g, ln2_b, sel_w, keys, values):
        import jax, jax.numpy as jnp
        import numpy as np
        D = 256
        H = 16
        HD = D // H
        E = 32
        ES = 128
        K = 4
        B, S = (2, 256)
        ROPE_BASE = 10000.0

        def _layernorm(x, g, b):
            m = x.mean(-1, keepdims=True)
            v = ((x - m) ** 2).mean(-1, keepdims=True)
            return (x - m) * jax.lax.rsqrt(v + 1e-05) * g + b

        def _forward(src, wq, wk, wv, wp, wo, ln1_g, ln1_b, ln2_g, ln2_b, sel_w, keys, values):
            Bs, Ss, Ds = src.shape
            scale = 1.0 / jnp.sqrt(jnp.array(HD, dtype=src.dtype))
            x = _layernorm(src, ln1_g, ln1_b)
            q = (x @ wq).reshape(Bs, Ss, H, HD)
            k = (x @ wk).reshape(Bs, Ss, H, HD)
            v = (x @ wv).reshape(Bs, Ss, H, HD)
            pos = jnp.arange(Ss - 1, -Ss, -1, dtype=src.dtype)
            inv_freq = 1.0 / ROPE_BASE ** (jnp.arange(0, Ds, 2, dtype=src.dtype) / Ds)
            ang = pos[:, None] * inv_freq[None, :]
            pe = jnp.concatenate([jnp.sin(ang), jnp.cos(ang)], axis=-1)
            p = (pe @ wp).reshape(2 * Ss - 1, H, HD)
            ac = jnp.einsum('bihd,bjhd->bhij', q, k)
            bd_full = jnp.einsum('bihd,phd->bhip', q, p)
            rel = jnp.arange(Ss)[:, None] - jnp.arange(Ss)[None, :] + (Ss - 1)
            bd = bd_full[:, :, jnp.arange(Ss)[:, None], rel]
            att = jax.nn.softmax((ac + bd) * scale, axis=-1)
            attn_out = jnp.einsum('bhij,bjhd->bihd', att, v).reshape(Bs, Ss, Ds) @ wo
            src = src + attn_out
            x2 = _layernorm(src, ln2_g, ln2_b)
            sel = jax.nn.sigmoid(x2 @ sel_w)
            scores, idx = jax.lax.top_k(sel, K)
            gate = (jax.nn.one_hot(idx, E, dtype=sel.dtype) * scores[..., None]).sum(-2)
            h = jax.nn.relu(jnp.einsum('bsd,edh->bseh', x2, keys))
            moe_out = jnp.einsum('bseh,ehd,bse->bsd', h, values, gate)
            return src + moe_out
        return _forward(src, wq, wk, wv, wp, wo, ln1_g, ln1_b, ln2_g, ln2_b, sel_w, keys, values)

    def _L2_attn_ref(x, norm_w, Wq, Wk, Wv, Wbeta, bbeta, Wig, big, Wog, bog, Wout, bout):
        import jax, jax.numpy as jnp
        import numpy as np
        import math
        B, L, HID, NH = (4, 1024, 256, 8)
        DH = HID // NH
        THETA = 10000.0

        def _rope_tables(seq_len, dh):
            half = dh // 2
            inv_freq = 1.0 / THETA ** (jnp.arange(half, dtype=jnp.float32) / half)
            freqs = jnp.arange(seq_len, dtype=jnp.float32)[:, None] * inv_freq[None, :]
            return (jnp.cos(freqs), jnp.sin(freqs))

        def _apply_rope(x, cos, sin):
            half = x.shape[-1] // 2
            x1, x2 = (x[..., :half], x[..., half:2 * half])
            c = cos[None, None]
            s = sin[None, None]
            return jnp.concatenate([x1 * c - x2 * s, x1 * s + x2 * c], axis=-1)
        Bq, Lq, _ = x.shape
        h = x * jax.lax.rsqrt(jnp.mean(x * x, axis=-1, keepdims=True) + 1e-06) * norm_w

        def heads(W):
            return jnp.einsum('bld,ed->ble', h, W).reshape(Bq, Lq, NH, DH).transpose(0, 2, 1, 3)
        q, k, v = (heads(Wq), heads(Wk), heads(Wv))
        cos, sin = _rope_tables(Lq, DH)
        q = _apply_rope(q, cos, sin)
        k = _apply_rope(k, cos, sin)

        def gate(W, b):
            return jax.nn.sigmoid(jnp.einsum('bld,hd->blh', h, W) + b).transpose(0, 2, 1)
        beta, ig, og = (gate(Wbeta, bbeta), gate(Wig, big), gate(Wog, bog))
        scale = 1.0 / math.sqrt(DH)
        qT = q.transpose(2, 0, 1, 3)
        kT = k.transpose(2, 0, 1, 3)
        vT = v.transpose(2, 0, 1, 3)
        fT = beta.transpose(2, 0, 1)
        gT = ig.transpose(2, 0, 1)
        oT = og.transpose(2, 0, 1)
        M0 = jnp.zeros((Bq, NH, DH, DH), x.dtype)

        def step(M, inp):
            q_t, k_t, v_t, f_t, g_t, o_t = inp
            M = M * f_t[..., None, None] + g_t[..., None, None] * scale * (k_t[..., :, None] * v_t[..., None, :])
            y_t = jnp.einsum('bhd,bhde->bhe', q_t, M) * o_t[..., None]
            return (M, y_t)
        _, yT = jax.lax.scan(step, M0, (qT, kT, vT, fT, gT, oT))
        y = yT.transpose(1, 0, 2, 3).reshape(Bq, Lq, HID)
        return jnp.einsum('bld,ed->ble', y, Wout) + bout

    def _L2_xattn_ref(x, historical_data, Wq, Wk, Wv, hist_W, hist_b, hist_ln_g, hist_ln_b, ctx_W1, ctx_b1, ctx_W2, ctx_b2, kg_W1, kg_b1, kg_ln_g, kg_ln_b, kg_W2, kg_b2, proj_W, proj_b, causal_mask):
        import jax, jax.numpy as jnp
        import numpy as np
        from jax import lax
        H = 16
        K1, K2 = (3, 3)
        LN_EPS = 1e-05

        def _ln(x, g, b):
            m = jnp.mean(x, axis=-1, keepdims=True)
            v = jnp.mean(jnp.square(x - m), axis=-1, keepdims=True)
            return (x - m) * lax.rsqrt(v + LN_EPS) * g + b

        def _gelu(x):
            return jax.nn.gelu(x, approximate=False)
        B, T, D = x.shape
        hd = D // H
        scale = hd ** (-0.5)
        q = (x @ Wq).reshape(B, T, H, hd).transpose(0, 2, 1, 3)
        k = (x @ Wk).reshape(B, T, H, hd).transpose(0, 2, 1, 3)
        v = (x @ Wv).reshape(B, T, H, hd).transpose(0, 2, 1, 3)
        attn = jnp.einsum('bhqd,bhkd->bhqk', q, k) * scale
        eh = _gelu(_ln(historical_data @ hist_W + hist_b, hist_ln_g, hist_ln_b))
        aw = _gelu(eh @ ctx_W1 + ctx_b1) @ ctx_W2 + ctx_b2
        aw = jax.nn.softmax(aw, axis=1)
        cc = jnp.sum(eh * aw, axis=1)
        kp = _gelu(_ln(cc @ kg_W1 + kg_b1, kg_ln_g, kg_ln_b)) @ kg_W2 + kg_b2
        kernels = jax.nn.softmax(kp.reshape(B, H, K1 * K2), axis=-1)
        kernels = kernels.reshape(B * H, 1, K1, K2)
        mask = causal_mask[None, None]
        attn0 = jnp.where(mask, 0.0, attn).reshape(1, B * H, T, T)
        attn = lax.conv_general_dilated(attn0, kernels, window_strides=(1, 1), padding=((K1 // 2, K1 // 2), (K2 // 2, K2 // 2)), feature_group_count=B * H, dimension_numbers=('NCHW', 'OIHW', 'NCHW')).reshape(B, H, T, T)
        attn = jnp.where(mask, -jnp.inf, attn)
        p = jax.nn.softmax(attn, axis=-1)
        out = jnp.einsum('bhqk,bhkd->bhqd', p, v)
        out = out.transpose(0, 2, 1, 3).reshape(B, T, D)
        return out @ proj_W + proj_b

    def _L2_ffn_ref(x, gate_w, fc1_w, fc1_b, geglu_mult, fc2_w, fc2_b, s_fc1_w, s_fc1_b, s_geglu_mult, s_fc2_w, s_fc2_b):
        import jax, jax.numpy as jnp
        import numpy as np
        S, B, D = (256, 2, 256)
        E, TOPK = (15, 3)
        F = 256
        FS = 512

        def _uinit(k, shape, out_dim):
            std = out_dim ** (-0.5)
            return jax.random.uniform(k, shape, jnp.float32, -std, std)
        s, b, d = x.shape
        xt = x.reshape(-1, d)
        T = xt.shape[0]
        logits = xt @ gate_w.T
        scores = jax.nn.softmax(logits, axis=-1)
        topk_w, topk_idx = jax.lax.top_k(scores, TOPK)
        topk_w = topk_w / (jnp.sum(topk_w, axis=-1, keepdims=True) + 1e-20)
        comb = jnp.zeros((T, E), xt.dtype).at[jnp.arange(T)[:, None], topk_idx].add(topk_w)
        h = jnp.einsum('td,efd->etf', xt, fc1_w) + fc1_b[:, None, :]
        xh, g = (h[..., :F], h[..., F:])
        a = jax.nn.gelu(g, approximate=False) * xh * geglu_mult[:, None, :]
        yexp = jnp.einsum('etf,edf->etd', a, fc2_w) + fc2_b[:, None, :]
        y = jnp.einsum('etd,te->td', yexp, comb)
        hs = xt @ s_fc1_w.T + s_fc1_b
        xs, gs = (hs[..., :FS], hs[..., FS:])
        as_ = jax.nn.gelu(gs, approximate=False) * xs * s_geglu_mult
        ys = as_ @ s_fc2_w.T + s_fc2_b
        return (y + ys).reshape(s, b, d)

    def _L3_attn_ref(x, wqk, wov):
        import jax, jax.numpy as jnp
        import numpy as np
        D_MODEL = 256
        b, n, d = x.shape
        mask = jnp.triu(jnp.full((n, n), -jnp.inf, dtype=x.dtype), k=1)
        q = jnp.einsum('bnd,de->bne', x, wqk)
        scores = jnp.einsum('bne,bme->bnm', q, x) + mask
        attn = jax.nn.softmax(scores, axis=-1)
        ctx = jnp.einsum('bnm,bmd->bnd', attn, x)
        return jnp.einsum('bnd,de->bne', ctx, wov)

    def _L3_xattn_ref(query, key, value, mask, W_q, W_k, W_v, W_o):
        import jax, jax.numpy as jnp
        import numpy as np
        D_MODEL = 256
        N_HEADS = 16
        D_K = D_MODEL // N_HEADS
        B, S = (2, 512)

        def _rope_emb(seq_len, d_k):
            inv_freq = 1.0 / 10000.0 ** (jnp.arange(0, d_k, 2, dtype=jnp.float32) / d_k)
            t = jnp.arange(seq_len, dtype=jnp.float32)
            freqs = jnp.outer(t, inv_freq)
            return jnp.concatenate([freqs, freqs], axis=-1)

        def _rotate_half(x):
            x1, x2 = jnp.split(x, 2, axis=-1)
            return jnp.concatenate([-x2, x1], axis=-1)

        def _apply_rope(x, emb):
            return x * jnp.cos(emb)[None, None] + _rotate_half(x) * jnp.sin(emb)[None, None]
        b = query.shape[0]

        def proj(x, W):
            y = jnp.einsum('bsd,ed->bse', x, W)
            return y.reshape(b, -1, N_HEADS, D_K).transpose(0, 2, 1, 3)
        Q = proj(query, W_q)
        K = proj(key, W_k)
        V = proj(value, W_v)
        emb_q = _rope_emb(Q.shape[2], D_K)
        emb_k = _rope_emb(K.shape[2], D_K)
        Q = _apply_rope(Q, emb_q)
        K = _apply_rope(K, emb_k)
        scores = jnp.einsum('bhqd,bhkd->bhqk', Q, K) / jnp.sqrt(jnp.float32(D_K))
        scores = jnp.where(mask == 0, jnp.float32(-jnp.inf), scores)
        attn = jax.nn.softmax(scores, axis=-1)
        ctx = jnp.einsum('bhqk,bhkd->bhqd', attn, V)
        ctx = ctx.transpose(0, 2, 1, 3).reshape(b, -1, D_MODEL)
        return jnp.einsum('bsd,ed->bse', ctx, W_o)

    def _L3_ffn_ref(u, g_shared, W1_s, b1_s, W2_s, b2_s, g_routed, W1_r, b1_r, W2_r, b2_r, centroids):
        import jax, jax.numpy as jnp
        import numpy as np
        B, T, C = (2, 256, 256)
        H = 1024
        E_R, E_S, K = (8, 2, 2)

        def _rmsnorm(x, g):
            eps = jnp.finfo(x.dtype).eps
            return x * jax.lax.rsqrt(jnp.mean(x * x, axis=-1, keepdims=True) + eps) * g

        def _experts_mlp(x, g, W1, b1, W2, b2):
            xn = _rmsnorm(x, g)
            h = jnp.einsum('btc,ech->bteh', xn, W1) + b1
            h = jax.nn.gelu(h, approximate=False)
            return jnp.einsum('bteh,ehc->btec', h, W2) + b2
        h_s = _experts_mlp(u, g_shared, W1_s, b1_s, W2_s, b2_s).sum(axis=-2)
        scores = jax.nn.sigmoid(u @ centroids)
        gpk, i_topk = jax.lax.top_k(scores, K)
        gk = gpk / scores.sum(axis=-1, keepdims=True)
        routed_all = _experts_mlp(u, g_routed, W1_r, b1_r, W2_r, b2_r)
        routed_topk = jnp.take_along_axis(routed_all, i_topk[..., None], axis=2)
        h_r = (gk[..., None] * routed_topk).sum(axis=-2)
        return u + h_s + h_r
    x = _layernorm(x + _L0_attn_ref(x, L0_attn_Wq, L0_attn_Wk, L0_attn_Wv, L0_attn_Wo), axis=-1)
    x = _layernorm(x + _L0_xattn_ref(x, ctx_1024, L0_xattn_Wq, L0_xattn_bq, L0_xattn_Wk, L0_xattn_bk, L0_xattn_Wv, L0_xattn_bv, L0_xattn_Wp, L0_xattn_bp), axis=-1)
    x = _layernorm(x + _L0_ffn_ref(x, L0_ffn_weight, L0_ffn_ln_gamma, L0_ffn_ln_beta), axis=-1)
    x = _layernorm(x + _L1_attn_ref(x, L1_attn_w_in, L1_attn_w_conv, L1_attn_w_xproj, L1_attn_w_dt, L1_attn_b_dt, L1_attn_A_log, L1_attn_D, L1_attn_w_out), axis=-1)
    x = _layernorm(x + _L1_xattn_ref(x, ctx_1024, ctx_1024, L1_xattn_Wq, L1_xattn_bq, L1_xattn_Wk, L1_xattn_bk, L1_xattn_Wv, L1_xattn_bv, L1_xattn_Wo, L1_xattn_bo), axis=-1)
    x = _layernorm(x + _L1_ffn_ref(x, L1_ffn_wq, L1_ffn_wk, L1_ffn_wv, L1_ffn_wp, L1_ffn_wo, L1_ffn_ln1_g, L1_ffn_ln1_b, L1_ffn_ln2_g, L1_ffn_ln2_b, L1_ffn_sel_w, L1_ffn_keys, L1_ffn_values), axis=-1)
    x = _layernorm(x + _L2_attn_ref(x, L2_attn_norm_w, L2_attn_Wq, L2_attn_Wk, L2_attn_Wv, L2_attn_Wbeta, L2_attn_bbeta, L2_attn_Wig, L2_attn_big, L2_attn_Wog, L2_attn_bog, L2_attn_Wout, L2_attn_bout), axis=-1)
    x = _layernorm(x + _L2_xattn_ref(x, ctx_1024, L2_xattn_Wq, L2_xattn_Wk, L2_xattn_Wv, L2_xattn_hist_W, L2_xattn_hist_b, L2_xattn_hist_ln_g, L2_xattn_hist_ln_b, L2_xattn_ctx_W1, L2_xattn_ctx_b1, L2_xattn_ctx_W2, L2_xattn_ctx_b2, L2_xattn_kg_W1, L2_xattn_kg_b1, L2_xattn_kg_ln_g, L2_xattn_kg_ln_b, L2_xattn_kg_W2, L2_xattn_kg_b2, L2_xattn_proj_W, L2_xattn_proj_b, mask_SxS_bc0), axis=-1)
    x = _layernorm(x + _L2_ffn_ref(x, L2_ffn_gate_w, L2_ffn_fc1_w, L2_ffn_fc1_b, L2_ffn_geglu_mult, L2_ffn_fc2_w, L2_ffn_fc2_b, L2_ffn_s_fc1_w, L2_ffn_s_fc1_b, L2_ffn_s_geglu_mult, L2_ffn_s_fc2_w, L2_ffn_s_fc2_b), axis=-1)
    x = _layernorm(x + _L3_attn_ref(x, L3_attn_wqk, L3_attn_wov), axis=-1)
    x = _layernorm(x + _L3_xattn_ref(x, ctx_1024, ctx_1024, mask_Bx1xSxS2_ik0, L3_xattn_W_q, L3_xattn_W_k, L3_xattn_W_v, L3_xattn_W_o), axis=-1)
    x = _layernorm(x + _L3_ffn_ref(x, L3_ffn_g_shared, L3_ffn_W1_s, L3_ffn_b1_s, L3_ffn_W2_s, L3_ffn_b2_s, L3_ffn_g_routed, L3_ffn_W1_r, L3_ffn_b1_r, L3_ffn_W2_r, L3_ffn_b2_r, L3_ffn_centroids), axis=-1)
    return x

_drawn_inputs = setup_inputs


def setup_inputs(seed=0):
    import zlib

    import numpy as np

    out = dict(_drawn_inputs(seed))
    spreads = {'L0_ffn_ln_gamma': (1.0, 0.2),
     'L0_ffn_ln_beta': (0.0, 0.1),
     'L1_attn_b_dt': (0.0, 0.8),
     'L1_attn_D': (1.0, 0.6),
     'L1_xattn_bq': (0.0, 0.1),
     'L1_xattn_bk': (0.0, 2.0),
     'L1_xattn_bv': (0.0, 0.1),
     'L1_xattn_bo': (0.0, 0.1),
     'L1_ffn_ln1_g': (1.0, 0.6),
     'L1_ffn_ln1_b': (0.0, 0.562),
     'L1_ffn_ln2_g': (1.0, 0.2),
     'L1_ffn_ln2_b': (0.0, 0.1),
     'L2_attn_norm_w': (1.0, 0.2),
     'L2_attn_bbeta': (2.0, 0.2),
     'L2_attn_big': (0.0, 0.413),
     'L2_attn_bog': (0.0, 0.428),
     'L2_attn_bout': (0.0, 0.1),
     'L2_xattn_hist_b': (0.0, 0.8),
     'L2_xattn_hist_ln_g': (1.0, 0.6),
     'L2_xattn_hist_ln_b': (0.0, 0.8),
     'L2_xattn_ctx_b1': (0.0, 0.8),
     'L2_xattn_kg_b1': (0.0, 0.8),
     'L2_xattn_kg_ln_g': (1.0, 0.6),
     'L2_xattn_kg_ln_b': (0.0, 0.8),
     'L2_xattn_kg_b2': (0.0, 0.8),
     'L2_xattn_proj_b': (0.0, 0.1),
     'L2_ffn_geglu_mult': (1.0, 0.6),
     'L2_ffn_s_geglu_mult': (1.0, 0.6),
     'L3_ffn_g_shared': (1.0, 0.6),
     'L3_ffn_g_routed': (1.0, 0.6)}
    factors = {'L0_xattn_bq': 8.0,
     'L0_xattn_bk': 64.0,
     'L0_xattn_bv': 3.609,
     'L0_xattn_bp': 3.403,
     'L1_attn_w_xproj': 8.0,
     'L1_attn_w_dt': 8.0,
     'L1_attn_A_log': 8.0,
     'L1_ffn_wq': 8.0,
     'L1_ffn_wk': 8.0,
     'L1_ffn_wp': 8.0,
     'L2_xattn_hist_W': 2.939,
     'L2_xattn_ctx_W1': 8.0,
     'L2_xattn_ctx_W2': 8.0,
     'L2_ffn_fc1_b': 8.0,
     'L2_ffn_s_fc1_b': 8.0,
     'L3_ffn_b1_s': 8.0,
     'L3_ffn_b2_s': 4.457,
     'L3_ffn_W1_r': 4.846,
     'L3_ffn_b1_r': 8.0,
     'L3_ffn_W2_r': 4.722,
     'L3_ffn_b2_r': 22.858,
     'L3_ffn_centroids': 5.569}
    for name, (base, spread) in spreads.items():
        noise = np.random.default_rng([zlib.crc32(name.encode()), seed]).standard_normal(out[name].shape)
        drawn = base * np.exp(spread * noise) if base else spread * noise
        out[name] = jnp.asarray(drawn.astype(out[name].dtype))
    for name, factor in factors.items():
        out[name] = (out[name] * factor).astype(out[name].dtype)
    return out
```

```python
from collections import namedtuple
from contextlib import ExitStack, contextmanager

import numpy as np

import concourse.bass as bass
import concourse.mybir as mybir

F32 = mybir.dt.float32
I32 = mybir.dt.int32
U8 = mybir.dt.uint8
ALU = mybir.AluOpType
ACT = mybir.ActivationFunctionType
AX = mybir.AxisListType

B, S, D = 8, 100, 256
KEYS = 361
P = 128
KT = D // P
TOK = B * S
KROWS = 121
BANK = 512
MASKED = -1.0e30


class State:
    pass


Attention = namedtuple("Attention", "q k v o")
Rotation = namedtuple("Rotation", "cos sin swap")
Convolution = namedtuple("Convolution", "kern keep mask")


@contextmanager
def stage_sems(nc, names):
    with ExitStack() as ctx:
        handles = {n: ctx.enter_context(nc.semaphore(n)) for n in names}
        yield namedtuple("Semaphores", handles)(**handles)
        for h in handles.values():
            nc.gpsimd.sem_clear(h)
        nc.all_engine_barrier()


NORM_SEMS = ["y_ready", "resid_ready", "stats_ready", "meanvar_ready", "vareps_ready", "rstd_ready",
             "xnew_ready", "xnew_turned", "x_stored", "affine_step"]


def norm_vector(dve, st, s, y, x_b, bias, eps_unused=None):
    dve.wait_ge(s.y_ready, 1)
    steps = 1
    if bias is None:
        dve.tensor_tensor(st.resid[:], y, x_b, ALU.add).then_inc(s.resid_ready, 1)
    else:
        dve.tensor_tensor(st.resid[:], y, x_b, ALU.add).then_inc(s.resid_ready, 1)
        dve.wait_ge(s.resid_ready, 1)
        dve.tensor_tensor(st.resid[:], st.resid[:], bias, ALU.add).then_inc(s.resid_ready, 1)
        steps = 2
    dve.wait_ge(s.resid_ready, steps)
    norm_stats_vector(dve, st, s)


def norm_stats_vector(dve, st, s, gain=None, shift=None):
    dve.bn_stats(st.stats[:], st.resid[:]).then_inc(s.stats_ready, 1)
    dve.wait_ge(s.stats_ready, 1)
    dve.bn_aggr(st.meanvar[:], st.stats[:]).then_inc(s.meanvar_ready, 1)
    dve.wait_ge(s.rstd_ready, 1)
    if gain is None:
        dve.tensor_scalar(st.xnew[:], st.resid[:], st.meanvar[:, 0:1], st.rstd[:, 0:1],
                          ALU.subtract, ALU.mult).then_inc(s.xnew_ready, 1)
        return
    dve.tensor_scalar(st.xnew[:], st.resid[:], st.meanvar[:, 0:1], st.rstd[:, 0:1],
                      ALU.subtract, ALU.mult).then_inc(s.affine_step, 1)
    dve.wait_ge(s.affine_step, 1)
    dve.tensor_tensor(st.xnew[:], st.xnew[:], gain, ALU.mult).then_inc(s.affine_step, 1)
    dve.wait_ge(s.affine_step, 2)
    dve.tensor_tensor(st.xnew[:], st.xnew[:], shift, ALU.add).then_inc(s.xnew_ready, 1)


def rstd_pool(pool, st, s, eps=1e-5):
    pool.wait_ge(s.meanvar_ready, 1)
    pool.tensor_scalar(st.vareps[:], st.meanvar[:, 1:2], eps, None, ALU.add).then_inc(s.vareps_ready, 1)
    pool.wait_ge(s.vareps_ready, 1)
    pool.tensor_tensor(st.rstd[:], st.vareps[:], st.minus_half[0:S, 0:1], ALU.pow).then_inc(s.rstd_ready, 1)


def norm_pool(pool, st, s, x_b, eps=1e-5):
    rstd_pool(pool, st, s, eps)
    pool.wait_ge(s.xnew_ready, 1)
    pool.tensor_copy(x_b, st.xnew[:]).then_inc(s.x_stored, 1)


def norm_tensor(pe, st, s, bank):
    pe.wait_ge(s.xnew_ready, 1)
    for k in range(KT):
        last = pe.transpose(st.ps[:, bank, k * S:(k + 1) * S], st.xnew[:, k * P:(k + 1) * P], st.ident[0:S, 0:S])
    last.then_inc(s.xnew_turned, 1)


def norm_scalar(act, st, s, bank, xt_b):
    act.wait_ge(s.xnew_turned, 1)
    act.activation(xt_b, st.ps[:, bank, 0:KT * S].rearrange("p (k t) -> p k t", k=KT), ACT.Copy)


def attention(nc, st, name, heads, hd, cross, w, bias=None, plus_one=False, mask=None, mask_dram=None,
              rope=None, xT=None, tail=None, bd=None, conv=None):
    nk = KEYS if cross else S
    krows, ktiles = (KROWS, 3) if cross else (S, 1)
    nkp = krows * ktiles
    width = heads * hd
    nq = w.q.shape[2] // P
    nf = width // P
    own = w.k is None
    scale = float(hd) ** -0.5 if hd < 256 else 1.0
    per_group = 1 if heads == 1 else (2 if cross else 4)
    groups = heads // per_group
    order = list(range(heads))
    if hd == 16:
        order = [x for g in range(4) for x in (2 * g, 2 * g + 1, 8 + 2 * g, 9 + 2 * g)]
        if cross:
            order = [x for h in (0, 1, 4, 5, 8, 9, 12, 13) for x in (h, h + 2)]
    bias = bias or {}
    s_banks = per_group if cross else 1
    masked = mask is not None or mask_dram is not None or bd is not None or conv is not None
    xT = st.XT if xT is None else xT
    lead = 1 if conv else 0
    n_s = 2
    with ExitStack() as ctx:
        def sb(n, shape, dt=F32):
            return ctx.enter_context(nc.sbuf_tensor(f"{name}_{n}", shape, dt))

        q_pad = sb("qT", [P, nq, S + 2 * lead])
        qT = q_pad[:, :, lead:lead + S]
        kT = sb("kT", [P, nf, nk]) if not own else None
        vals = sb("vals", [krows, ktiles, width])
        probs = sb("probs", [S, 2, per_group, nkp])
        probsT = sb("probsT", [krows, 2, per_group * ktiles * S] if not cross else [krows, 2, ktiles * S])
        nmax = sb("nmax", [S, heads])
        rsum = sb("rsum", [S, heads])
        rinv = sb("rinv", [S, heads])
        o_sb = sb("o_sb", [S, width])
        oT = sb("oT", [P, nf, S])
        xcur = sb("xcur", [P, KT, S])
        ctx_cur = sb("ctx_cur", [P, KT, KEYS]) if cross else None
        s_sb = sb("s_sb", [S, 2, per_group, nk]) if masked else None
        bd_cur = sb("bd_cur", [S, heads, S]) if bd is not None else None
        sm = sb("sm", [S, 3, per_group, S + 2]) if conv else None
        kern_cur = sb("kern_cur", [S, heads * 9]) if conv else None
        mask_i = sb("mask_i", [S, KEYS], I32) if mask_dram is not None else None
        mask_b = sb("mask_b", [S, KEYS]) if mask_dram is not None else None
        swapped = sb("swapped", [P, nq, S]) if rope else None
        kswapped = sb("kswapped", [P, nf, nk]) if rope else None

        with stage_sems(nc, ["buffers_cleared"]) as s, nc.Block() as block:

            @block.gpsimd
            def _(pool):
                pool.memset(probs[:], 0.0).then_inc(s.buffers_cleared, 1)
                pool.memset(vals[:], 0.0).then_inc(s.buffers_cleared, 1)
                if conv:
                    pool.memset(q_pad[:], 0.0).then_inc(s.buffers_cleared, 1)
                    pool.memset(sm[:], 0.0).then_inc(s.buffers_cleared, 1)

        sems = ["xcur_ready", "ctx_ready", "proj_ready", "proj_act", "proj_dve", "scores_ready", "masked_ready",
                "max_ready", "exp_done", "probs_turned", "probsT_ready", "values_done", "rsum_ready",
                "rinv_ready", "o_ready", "o_turned", "oT_ready", "mask_loaded", "mask_ready", "rope_ready",
                "swap_ready", "qk_done", "bd_loaded", "kern_ready", "sm_ready", "tap_done", "conv_done"]
        with nc.Fori(0, B) as b, stage_sems(nc, sems + NORM_SEMS + (tail.sems if tail else [])) as s, nc.Block() as block:
            src = st.ctxT[:, b, :, :] if cross else xcur
            turn_src = ctx_cur if cross else xcur
            keysT = xcur if own else kT

            chunks = []
            qper = min(nq, 4)
            for m0 in range(0, nq, qper):
                def q_out(dve, bank, m0=m0):
                    ps = st.ps[:, bank, 0:qper * S].rearrange("p (m t) -> p m t", m=qper)
                    if "q" in bias:
                        return dve.scalar_tensor_tensor(
                            qT[:, m0:m0 + qper, :], ps, scale,
                            bias["q"][:, m0:m0 + qper].unsqueeze(2).to_broadcast([P, qper, S]), ALU.mult, ALU.add)
                    return dve.tensor_scalar(qT[:, m0:m0 + qper, :], ps, scale, None, ALU.mult)
                chunks.append(("dve", [(lambda bank, m=m, i=i: st.ps[:, bank, i * S:(i + 1) * S],
                                        lambda k, m=m: w.q[:, k, m * P:(m + 1) * P],
                                        lambda k: xcur[:, k, :]) for i, m in enumerate(range(m0, m0 + qper))], q_out))
            for m in range(0 if own else nf):
                def k_out(act, bank, m=m):
                    if "k" in bias:
                        return act.activation(kT[:, m, :], st.ps[:, bank, 0:nk], ACT.Identity, bias=bias["k"][:, m:m + 1])
                    return act.activation(kT[:, m, :], st.ps[:, bank, 0:nk], ACT.Copy)
                chunks.append(("act", [(lambda bank: st.ps[:, bank, 0:nk],
                                        lambda k, m=m: w.k[:, k, m * P:(m + 1) * P],
                                        lambda k: src[:, k, :])], k_out))
            vw = min(width, BANK)
            for t in range(0 if own else ktiles):
                rows = min(krows, nk - t * krows)
                for c0 in range(0, width, vw):
                    def v_out(dve, bank, t=t, rows=rows, c0=c0):
                        ps = st.ps[0:rows, bank, 0:vw]
                        if "v" in bias:
                            return dve.tensor_tensor(vals[0:rows, t, c0:c0 + vw], ps, bias["v"][0:rows, c0:c0 + vw], ALU.add)
                        return dve.tensor_copy(vals[0:rows, t, c0:c0 + vw], ps)
                    chunks.append(("dve", [(lambda bank, rows=rows: st.ps[0:rows, bank, 0:vw],
                                            lambda k, t=t, rows=rows: turn_src[:, k, t * krows:t * krows + rows],
                                            lambda k, c0=c0: w.v[:, k, c0:c0 + vw])], v_out))
            n_act = sum(c[0] == "act" for c in chunks)
            n_dve = len(chunks) - n_act
            PROJ_BANKS = 6

            def emptied(i):
                return chunks[i][0], sum(c[0] == chunks[i][0] for c in chunks[:i + 1])

            def score_tile(g):
                b0 = (g % 2) * s_banks
                if cross:
                    return st.ps[0:S, b0:b0 + per_group, 0:nk]
                return st.ps[0:S, b0, 0:per_group * S].rearrange("q (h k) -> q h k", h=per_group)

            def head_rows(h):
                if hd == 16:
                    half, r = divmod(h, 8)
                    return [(2 * (r % 2) + half, half)], 32 * (r // 2), 32
                if hd == 64:
                    return [(h // 2, h // 2)], 64 * (h % 2), 64
                return [(m, m) for m in range(nf)], 0, P

            @block.sync
            def _(sp):
                if mask_dram is not None:
                    sp.dma_start(mask_i[:], mask_dram[b]).then_inc(s.mask_loaded, 16)
                if bd is not None:
                    sp.dma_start(bd_cur[:], bd(b)).then_inc(s.bd_loaded, 16)
                    sp.wait_ge(s.bd_loaded, 16)

            @block.gpsimd
            def _(pool):
                pool.tensor_copy(xcur[:], xT[:, :, b, :]).then_inc(s.xcur_ready, 1)
                if cross:
                    pool.tensor_copy(ctx_cur[:], st.ctxT[:, b, :, :]).then_inc(s.ctx_ready, 1)
                if own:
                    pool.tensor_copy(vals[:, 0, :], st.X[:, b, :]).then_inc(s.ctx_ready, 1)
                if conv:
                    pool.tensor_copy(kern_cur[:], conv.kern[0:S, b, :]).then_inc(s.kern_ready, 1)
                if tail:
                    tail.pool(pool, s, b)
                else:
                    norm_pool(pool, st, s, st.X[:, b, :])

            @block.tensor
            def _(pe):
                pe.wait_ge(s.xcur_ready, 1)
                for i, (eng, prods, _) in enumerate(chunks):
                    if i >= PROJ_BANKS:
                        e, n = emptied(i - PROJ_BANKS)
                        pe.wait_ge(s.proj_act if e == "act" else s.proj_dve, n)
                    if cross and i == len(chunks) - ktiles * (width // vw):
                        pe.wait_ge(s.ctx_ready, 1)
                    for out, lhs, rhs in prods:
                        for k in range(KT):
                            last = pe.matmul(out(i % PROJ_BANKS), lhs(k), rhs(k), start=(k == 0), stop=(k == KT - 1))
                    last.then_inc(s.proj_ready, 1)
                if own:
                    pe.wait_ge(s.ctx_ready, 1)
                else:
                    pe.wait_ge(s.proj_act, n_act)
                pe.wait_ge(s.proj_dve, n_dve)
                if rope:
                    for m in range(nq):
                        last = pe.matmul(st.ps[:, 0, m * S:(m + 1) * S], rope.swap, qT[:, m, :], start=True, stop=True)
                    for m in range(nf):
                        last = pe.matmul(st.ps[:, 1 + m, 0:nk], rope.swap, kT[:, m, :], start=True, stop=True)
                    last.then_inc(s.swap_ready, 1)
                    pe.wait_ge(s.rope_ready, 1)

                def scores(g):
                    if conv:
                        if g >= 1:
                            pe.wait_ge(s.sm_ready, 3 * g)
                        for i in range(per_group):
                            ((mq, mk),), p0, n = head_rows(order[g * per_group + i])
                            for r in range(3):
                                last = pe.matmul(st.ps[0:S, r, i * S:(i + 1) * S], q_pad[p0:p0 + n, mq, r:r + S],
                                                 keysT[p0:p0 + n, mk, :], start=True, stop=True)
                        last.then_inc(s.scores_ready, 1)
                        return
                    if g >= 2:
                        if masked:
                            pe.wait_ge(s.masked_ready, g - 1)
                        else:
                            pe.wait_ge(s.exp_done, (g - 1) * per_group)
                    out = score_tile(g)
                    for i in range(per_group):
                        tiles, p0, n = head_rows(order[g * per_group + i])
                        for j, (mq, mk) in enumerate(tiles):
                            last = pe.matmul(out[:, i, :], qT[p0:p0 + n, mq, :], keysT[p0:p0 + n, mk, :],
                                             start=(j == 0), stop=(j == len(tiles) - 1))
                    last.then_inc(s.scores_ready, 1)

                def turn_probs(g):
                    pe.wait_ge(s.exp_done, (g + 1) * per_group)
                    for i in range(per_group):
                        h = g * per_group + i
                        if cross:
                            if h >= 2:
                                pe.wait_ge(s.probsT_ready, h - 1)
                            for t in range(ktiles):
                                last = pe.transpose(st.ps[0:krows, 4 + h % 2, t * S:(t + 1) * S],
                                                    probs[:, g % 2, i, t * krows:(t + 1) * krows], st.ident[0:S, 0:S])
                            last.then_inc(s.probs_turned, 1)
                        else:
                            if i == 0 and g >= 2:
                                pe.wait_ge(s.probsT_ready, g - 1)
                            last = pe.transpose(st.ps[0:krows, 4 + g % 2, i * S:(i + 1) * S],
                                                probs[:, g % 2, i, :], st.ident[0:S, 0:S])
                    if not cross:
                        last.then_inc(s.probs_turned, 1)

                def values(g):
                    for i in range(per_group):
                        h = g * per_group + i
                        pe.wait_ge(s.probsT_ready, h + 1 if cross else g + 1)
                        c = order[h] * hd
                        out = st.ps[0:S, 6 + c // BANK, c % BANK:c % BANK + hd]
                        for t in range(ktiles):
                            lhs = probsT[:, h % 2, t * S:(t + 1) * S] if cross else probsT[:, g % 2, i * S:(i + 1) * S]
                            last = pe.matmul(out, lhs, vals[:, t, c:c + hd], start=(t == 0), stop=(t == ktiles - 1))
                        last.then_inc(s.values_done, 1)

                for i in range(groups + 2):
                    if i < groups:
                        scores(i)
                    if 1 <= i <= groups:
                        turn_probs(i - 1)
                    if i >= 2:
                        values(i - 2)
                pe.wait_ge(s.o_ready, 1)
                for m in range(nf):
                    last = pe.transpose(st.ps[:, 4 + m // 4, (m % 4) * S:(m % 4 + 1) * S], o_sb[:, m * P:(m + 1) * P],
                                        st.ident[0:S, 0:S])
                last.then_inc(s.o_turned, 1)
                pe.wait_ge(s.oT_ready, (nf + 3) // 4)
                for m in range(nf):
                    last = pe.matmul(st.ps[0:S, 0, 0:D], oT[:, m, :], w.o[:, m, :], start=(m == 0), stop=(m == nf - 1))
                last.then_inc(s.y_ready, 1)
                if tail:
                    tail.tensor(pe, s)
                else:
                    norm_tensor(pe, st, s, 1)

            @block.scalar
            def _(act):
                for i, (eng, _, out) in enumerate(chunks):
                    if eng == "act":
                        act.wait_ge(s.proj_ready, i + 1)
                        out(act, i % PROJ_BANKS).then_inc(s.proj_act, 1)
                for g in range(groups):
                    act.wait_ge(s.max_ready, g + 1)
                    if g >= 2:
                        act.wait_ge(s.probs_turned, (g - 1) * (per_group if cross else 1))
                    for i in range(per_group):
                        h = g * per_group + i
                        srct = s_sb[:, g % 2, i, :] if masked else score_tile(g)[:, i, :]
                        act.activation(probs[:, g % 2, i, 0:nk], srct, ACT.Exp, bias=nmax[:, h:h + 1],
                                       accum_out=rsum[:, order[h]:order[h] + 1]).then_inc(s.exp_done, 1)
                act.wait_ge(s.o_turned, 1)
                for m0 in range(0, nf, 4):
                    n = min(4, nf - m0)
                    act.activation(oT[:, m0:m0 + n, :], st.ps[:, 4 + m0 // 4, 0:n * S].rearrange("p (m t) -> p m t", m=n),
                                   ACT.Copy).then_inc(s.oT_ready, 1)
                if tail:
                    tail.scalar(act, s, b)
                else:
                    norm_scalar(act, st, s, 1, st.XT[:, :, b, :])

            @block.vector
            def _(dve):
                if mask_dram is not None:
                    dve.wait_ge(s.mask_loaded, 16)
                    dve.tensor_scalar(mask_b[:], mask_i[:], 0, MASKED, ALU.is_equal, ALU.mult).then_inc(s.mask_ready, 1)
                    dve.wait_ge(s.mask_ready, 1)
                for i, (eng, _, out) in enumerate(chunks):
                    if eng == "dve":
                        dve.wait_ge(s.proj_ready, i + 1)
                        out(dve, i % PROJ_BANKS).then_inc(s.proj_dve, 1)
                if rope:
                    dve.wait_ge(s.proj_dve, n_dve)
                    dve.wait_ge(s.swap_ready, 1)
                    dve.tensor_tensor(swapped[:], st.ps[:, 0, 0:nq * S].rearrange("p (m t) -> p m t", m=nq),
                                      rope.sin[:, 0:S].unsqueeze(1).to_broadcast([P, nq, S]), ALU.mult).then_inc(s.qk_done, 1)
                    dve.tensor_tensor(kswapped[:], st.ps[:, 1:1 + nf, 0:nk],
                                      rope.sin[:, 0:nk].unsqueeze(1).to_broadcast([P, nf, nk]), ALU.mult).then_inc(s.qk_done, 1)
                    dve.tensor_tensor(qT, qT, rope.cos[:, 0:S].unsqueeze(1).to_broadcast([P, nq, S]), ALU.mult).then_inc(s.qk_done, 1)
                    dve.wait_ge(s.proj_act, n_act)
                    dve.tensor_tensor(kT[:], kT[:], rope.cos[:, 0:nk].unsqueeze(1).to_broadcast([P, nf, nk]), ALU.mult).then_inc(s.qk_done, 1)
                    dve.wait_ge(s.qk_done, 4)
                    dve.tensor_tensor(qT, qT, swapped[:], ALU.add).then_inc(s.qk_done, 1)
                    dve.wait_ge(s.qk_done, 5)
                    dve.tensor_tensor(kT[:], kT[:], kswapped[:], ALU.add).then_inc(s.rope_ready, 1)

                def convolve(g):
                    for r in range(3):
                        dve.tensor_tensor(sm[:, r, :, 1:S + 1], score_rows(r), conv.keep[:, r, :].unsqueeze(1).to_broadcast([S, per_group, S]),
                                          ALU.mult).then_inc(s.sm_ready, 1)
                    dve.wait_ge(s.sm_ready, 3 * (g + 1))
                    if g == 0:
                        dve.wait_ge(s.kern_ready, 1)
                    if g >= 2:
                        dve.wait_ge(s.exp_done, (g - 1) * per_group)
                    for tap in range(9):
                        for i in range(per_group):
                            n = (g * 9 + tap) * per_group + i
                            wt = kern_cur[:, order[g * per_group + i] * 9 + tap:order[g * per_group + i] * 9 + tap + 1]
                            src_rows = sm[:, tap // 3, i, tap % 3:tap % 3 + S]
                            acc = s_sb[:, g % 2, i, :]
                            if tap == 0:
                                dve.tensor_scalar(acc, src_rows, wt, None, ALU.mult).then_inc(s.tap_done, 1)
                            else:
                                dve.wait_ge(s.tap_done, n - per_group + 1)
                                dve.scalar_tensor_tensor(acc, src_rows, wt, acc, ALU.mult, ALU.add).then_inc(s.tap_done, 1)
                    dve.wait_ge(s.tap_done, (g + 1) * 9 * per_group)
                    dve.tensor_tensor(s_sb[:, g % 2], s_sb[:, g % 2], conv.mask.unsqueeze(1).to_broadcast([S, per_group, S]),
                                      ALU.add).then_inc(s.conv_done, 1)
                    dve.wait_ge(s.conv_done, g + 1)

                def score_rows(r):
                    return st.ps[0:S, r, 0:per_group * S].rearrange("q (h k) -> q h k", h=per_group)

                def maxima(g):
                    dve.wait_ge(s.scores_ready, g + 1)
                    if conv:
                        convolve(g)
                        rows = s_sb[:, g % 2]
                    else:
                        rows = score_tile(g)
                    if masked and not conv:
                        if g >= 2:
                            dve.wait_ge(s.exp_done, (g - 1) * per_group)
                        if bd is not None:
                            if g == 0:
                                dve.wait_ge(s.bd_loaded, 16)
                            m = bd_cur[:, g * per_group:(g + 1) * per_group, :]
                        else:
                            m = (mask if mask is not None else mask_b[:]).unsqueeze(1).to_broadcast([S, per_group, nk])
                        dve.tensor_tensor(s_sb[:, g % 2], rows, m, ALU.add).then_inc(s.masked_ready, 1)
                        dve.wait_ge(s.masked_ready, g + 1)
                        rows = s_sb[:, g % 2]
                    dve.tensor_reduce(nmax[:, g * per_group:(g + 1) * per_group], rows, AX.X, ALU.max,
                                      negate=True).then_inc(s.max_ready, 1)

                def copy_probs(g):
                    for i in range(per_group if cross else 1):
                        n = g * per_group + i if cross else g
                        dve.wait_ge(s.probs_turned, n + 1)
                        if n >= 2:
                            dve.wait_ge(s.values_done, (n - 1) if cross else (n - 1) * per_group)
                        cols = probsT.shape[2]
                        dve.tensor_copy(probsT[:, n % 2, :], st.ps[0:krows, 4 + n % 2, 0:cols]).then_inc(s.probsT_ready, 1)

                for g in range(groups + 1):
                    if g < groups:
                        maxima(g)
                    if g >= 1:
                        copy_probs(g - 1)
                dve.wait_ge(s.exp_done, heads)
                sums = rsum
                if plus_one:
                    dve.tensor_scalar(rsum[:], rsum[:], 1.0, None, ALU.add).then_inc(s.rsum_ready, 1)
                    dve.wait_ge(s.rsum_ready, 1)
                dve.reciprocal(rinv[:], sums[:]).then_inc(s.rinv_ready, 1)
                dve.wait_ge(s.rinv_ready, 1)
                dve.wait_ge(s.values_done, heads)
                o_ps = st.ps[0:S, 6:6 + max(1, width // BANK), 0:min(width, BANK)]
                hb = heads // max(1, width // BANK)
                for j in range(max(1, width // BANK)):
                    last = dve.tensor_tensor(o_sb[:, j * hb * hd:(j + 1) * hb * hd].rearrange("q (h d) -> q h d", d=hd),
                                             o_ps[:, j, :].rearrange("q (h d) -> q h d", d=hd),
                                             rinv[:, j * hb:(j + 1) * hb].unsqueeze(2).to_broadcast([S, hb, hd]), ALU.mult)
                last.then_inc(s.o_ready, 1)
                if tail:
                    tail.vector(dve, s, b, st.ps[0:S, 0, 0:D])
                else:
                    norm_vector(dve, st, s, st.ps[0:S, 0, 0:D], st.X[:, b, :], bias["o"][0:S, :] if "o" in bias else None)


def l0_ffn(nc, st, dram):
    QB, EPS, LN_EPS = 128.0, 1e-5, 1e-3
    ROUND = 12582912.0
    wt = st.w["f2w"]
    with ExitStack() as ctx:
        def sb(n, shape, dt=F32):
            return ctx.enter_context(nc.sbuf_tensor(f"l0f_{n}", shape, dt))

        xq = sb("xq", [S, B, D])
        stats, mv = sb("stats", [S, B, 6]), sb("mv", [S, B, 2])
        vareps, rstd = sb("vareps", [S, B]), sb("rstd", [S, B])
        wabs, beta = sb("wabs", [P, 1]), sb("beta", [P, 4])
        ones = sb("ones", [P, P])
        absmax, gmax = sb("absmax", [S, 1]), sb("gmax", [S, 4])
        xq_cur, xqT = sb("xq_cur", [S, D]), sb("xqT", [P, KT, S])

        with stage_sems(nc, ["ones_set", "wabs_ready", "wsum_ready", "beta_step", "stats_done", "mv_done",
                             "vareps_done", "rstd_done", "norm_done", "affine_done", "absmax_ready", "gmax_ready",
                             "g_step", "xq_done", "wq_step"]) as s, nc.Block() as block:
            @block.gpsimd
            def _(pool):
                pool.memset(ones[:], 1.0).then_inc(s.ones_set, 1)
                pool.wait_ge(s.mv_done, B)
                pool.tensor_scalar(vareps[:], mv[:, :, 1], LN_EPS, None, ALU.add).then_inc(s.vareps_done, 1)
                pool.wait_ge(s.vareps_done, 1)
                pool.tensor_tensor(rstd[:], vareps[:], st.minus_half[0:S, :].to_broadcast([S, B]), ALU.pow).then_inc(s.rstd_done, 1)
                pool.wait_ge(s.absmax_ready, 1)
                pool.partition_all_reduce(gmax[:, 0:1], absmax[:], S, bass.bass_isa.ReduceOp.max).then_inc(s.gmax_ready, 1)

            @block.tensor
            def _(pe):
                pe.wait_ge(s.ones_set, 1)
                pe.wait_ge(s.wabs_ready, 1)
                pe.matmul(st.ps[:, 0, 0:1], ones[:], wabs[:], start=True, stop=True).then_inc(s.wsum_ready, 1)

            @block.vector
            def _(dve):
                dve.tensor_reduce(wabs[:], wt, AX.X, ALU.add, apply_absolute_value=True).then_inc(s.wabs_ready, 1)
                for b in range(B):
                    dve.bn_stats(stats[:, b, :], st.X[:, b, :]).then_inc(s.stats_done, 1)
                for b in range(B):
                    dve.wait_ge(s.stats_done, b + 1)
                    dve.bn_aggr(mv[:, b, :], stats[:, b, :]).then_inc(s.mv_done, 1)
                dve.wait_ge(s.wsum_ready, 1)
                dve.tensor_scalar(beta[:, 0:1], st.ps[:, 0, 0:1], 1.0 / (D * D), None, ALU.mult).then_inc(s.beta_step, 1)
                dve.wait_ge(s.beta_step, 1)
                dve.tensor_scalar(beta[:, 1:2], beta[:, 0:1], EPS, None, ALU.add).then_inc(s.beta_step, 1)
                dve.wait_ge(s.beta_step, 2)
                dve.reciprocal(beta[:, 2:3], beta[:, 1:2]).then_inc(s.beta_step, 1)
                dve.wait_ge(s.beta_step, 3)
                dve.tensor_scalar(wt, wt, beta[:, 2:3], 1.0, ALU.mult, ALU.min).then_inc(s.wq_step, 1)
                dve.wait_ge(s.wq_step, 1)
                dve.tensor_scalar(wt, wt, -1.0, ROUND, ALU.max, ALU.add).then_inc(s.wq_step, 1)
                dve.wait_ge(s.wq_step, 2)
                dve.tensor_scalar(wt, wt, ROUND, None, ALU.subtract).then_inc(s.wq_step, 1)
                dve.wait_ge(s.rstd_done, 1)
                for b in range(B):
                    dve.tensor_scalar(xq[:, b, :], st.X[:, b, :], mv[:, b, 0:1], rstd[:, b:b + 1],
                                      ALU.subtract, ALU.mult).then_inc(s.norm_done, 1)
                dve.wait_ge(s.norm_done, B)
                dve.tensor_tensor(xq[:], xq[:], st.w["f2g"][0:S, :].unsqueeze(1).to_broadcast([S, B, D]), ALU.mult).then_inc(s.affine_done, 1)
                dve.wait_ge(s.affine_done, 1)
                dve.tensor_tensor(xq[:], xq[:], st.w["f2b"][0:S, :].unsqueeze(1).to_broadcast([S, B, D]), ALU.add).then_inc(s.affine_done, 1)
                dve.wait_ge(s.affine_done, 2)
                dve.tensor_reduce(absmax[:], xq[:], AX.XY, ALU.max, apply_absolute_value=True).then_inc(s.absmax_ready, 1)
                dve.wait_ge(s.gmax_ready, 1)
                dve.reciprocal(gmax[:, 1:2], gmax[:, 0:1]).then_inc(s.g_step, 1)
                dve.tensor_scalar(gmax[:, 3:4], gmax[:, 0:1], beta[0:S, 0:1], 1.0 / QB, ALU.mult, ALU.mult).then_inc(s.g_step, 1)
                dve.wait_ge(s.g_step, 2)
                dve.tensor_scalar(gmax[:, 2:3], gmax[:, 1:2], QB, None, ALU.mult).then_inc(s.g_step, 1)
                dve.wait_ge(s.g_step, 3)
                dve.tensor_scalar(xq[:], xq[:], gmax[:, 2:3], QB - EPS, ALU.mult, ALU.min).then_inc(s.xq_done, 1)
                dve.wait_ge(s.xq_done, 1)
                dve.tensor_scalar(xq[:], xq[:], -QB + EPS, None, ALU.max).then_inc(s.xq_done, 1)

        with nc.Fori(0, B) as b, stage_sems(nc, ["cur_ready", "cur_turned", "curT_ready"] + NORM_SEMS) as s, nc.Block() as block:
            @block.gpsimd
            def _(pool):
                pool.tensor_copy(xq_cur[:], xq[:, b, :]).then_inc(s.cur_ready, 1)
                norm_pool(pool, st, s, st.X[:, b, :])

            @block.tensor
            def _(pe):
                pe.wait_ge(s.cur_ready, 1)
                for k in range(KT):
                    last = pe.transpose(st.ps[:, 2, k * S:(k + 1) * S], xq_cur[:, k * P:(k + 1) * P], st.ident[0:S, 0:S])
                last.then_inc(s.cur_turned, 1)
                pe.wait_ge(s.curT_ready, 1)
                for k in range(KT):
                    last = pe.matmul(st.ps[0:S, 0, 0:D], xqT[:, k, :], wt[:, k * D:(k + 1) * D], start=(k == 0), stop=(k == KT - 1))
                last.then_inc(s.y_ready, 1)
                norm_tensor(pe, st, s, 1)

            @block.scalar
            def _(act):
                act.wait_ge(s.cur_turned, 1)
                act.activation(xqT[:], st.ps[:, 2, 0:KT * S].rearrange("p (k t) -> p k t", k=KT), ACT.Copy).then_inc(s.curT_ready, 1)
                norm_scalar(act, st, s, 1, st.XT[:, :, b, :])

            @block.vector
            def _(dve):
                dve.wait_ge(s.y_ready, 1)
                dve.scalar_tensor_tensor(st.resid[:], st.ps[0:S, 0, 0:D], gmax[:, 3:4], st.X[:, b, :],
                                         ALU.mult, ALU.add).then_inc(s.resid_ready, 1)
                dve.wait_ge(s.resid_ready, 1)
                norm_stats_vector(dve, st, s)


def l1_attn(nc, st, dram):
    DIN, NS, R, TAPS = 512, 16, 64, 4
    M = DIN // P
    HALF = TOK // 2
    pad = TAPS - 1
    w_in = st.w["m_in"].rearrange("p (k n) -> p k n", k=KT)
    w_xp = st.w["m_xproj"].rearrange("p (k n) -> p k n", k=M)
    w_out = st.w["m_out"].rearrange("p (k n) -> p k n", k=M)
    w_conv = st.w["m_conv"].rearrange("p (m j) -> p m j", m=M)
    a_log = st.w["m_alog"].rearrange("p (m n) -> p m n", m=M)
    XTf = st.XT[:].rearrange("p k b t -> p k (b t)")
    with ExitStack() as ctx:
        def sb(n, shape, dt=F32):
            return ctx.enter_context(nc.sbuf_tensor(f"l1a_{n}", shape, dt))

        hs = sb("hs", [P, M, TOK])
        gate = sb("gate", [P, M, TOK])
        xdbl = sb("xdbl", [R + 2 * NS, TOK])
        delta = sb("delta", [P, M, TOK])

        with ExitStack() as ctx2:
            def sb2(n, shape, dt=F32):
                return ctx2.enter_context(nc.sbuf_tensor(f"l1a_{n}", shape, dt))

            hpad = sb2("hpad", [P, M, B, pad + S])
            conv = sb2("conv", [P, 2, TOK])
            vraw = sb2("vraw", [P, TOK])
            ev, lg = sb2("ev", [P, TOK]), sb2("lg", [P, TOK])
            er = sb2("er", [P, TOK])
            with stage_sems(nc, ["hpad_zero", "proj_ready", "hs_raw", "gate_done", "conv_step", "hs_done", "xdbl_ready",
                                 "xdbl_done", "dt_ready", "v_done", "abs_done", "exp_done", "log_done", "sp_step",
                                 "delta_done", "a_done", "a_negative"]) as s, nc.Block() as block:
                @block.gpsimd
                def _(pool):
                    pool.memset(hpad[:], 0.0).then_inc(s.hpad_zero, 1)
                    pool.wait_ge(s.a_done, 1)
                    pool.tensor_scalar(st.w["m_alog"], st.w["m_alog"], -1.0, None, ALU.mult).then_inc(s.a_negative, 1)

                @block.tensor
                def _(pe):
                    for m in range(2 * M):
                        if m >= 4:
                            pe.wait_ge(s.hs_raw, m - 3)
                        for j in range(2):
                            for k in range(KT):
                                last = pe.matmul(st.ps[:, 2 * (m % 4) + j, 0:HALF], w_in[:, k, m * P:(m + 1) * P],
                                                 XTf[:, k, j * HALF:(j + 1) * HALF], start=(k == 0), stop=(k == KT - 1))
                        last.then_inc(s.proj_ready, 1)
                    pe.wait_ge(s.hs_raw, M)
                    pe.wait_ge(s.gate_done, 1)
                    pe.wait_ge(s.hs_done, M)
                    for j in range(2):
                        for k in range(M):
                            last = pe.matmul(st.ps[0:R + 2 * NS, j, 0:HALF], w_xp[:, k, :], hs[:, k, j * HALF:(j + 1) * HALF],
                                             start=(k == 0), stop=(k == M - 1))
                    last.then_inc(s.xdbl_ready, 1)
                    pe.wait_ge(s.xdbl_done, 1)
                    for m in range(M):
                        if m >= 2:
                            pe.wait_ge(s.v_done, m - 1)
                        else:
                            pe.wait_ge(s.gate_done, M)
                        for j in range(2):
                            last = pe.matmul(st.ps[:, 4 + 2 * (m % 2) + j, 0:HALF], st.w["m_dt"][0:R, m * P:(m + 1) * P],
                                             xdbl[0:R, j * HALF:(j + 1) * HALF], start=True, stop=True)
                        last.then_inc(s.dt_ready, 1)

                @block.scalar
                def _(act):
                    act.wait_ge(s.hpad_zero, 1)
                    for m in range(2 * M):
                        act.wait_ge(s.proj_ready, m + 1)
                        for j in range(2):
                            ps = st.ps[:, 2 * (m % 4) + j, 0:HALF]
                            if m < M:
                                last = act.activation(hpad[:, m, j * B // 2:(j + 1) * B // 2, pad:],
                                                      ps.rearrange("p (b t) -> p b t", t=S), ACT.Copy)
                            else:
                                last = act.activation(gate[:, m - M, j * HALF:(j + 1) * HALF], ps, ACT.Silu)
                        last.then_inc(s.hs_raw if m < M else s.gate_done, 1)
                    for m in range(M):
                        act.wait_ge(s.conv_step, TAPS * (m + 1))
                        act.activation(hs[:, m, :], conv[:, m % 2, :], ACT.Silu).then_inc(s.hs_done, 1)
                    act.wait_ge(s.xdbl_ready, 1)
                    act.activation(xdbl[:].rearrange("p (j t) -> p j t", j=2), st.ps[0:R + 2 * NS, 0:2, 0:HALF], ACT.Copy).then_inc(s.xdbl_done, 1)
                    act.activation(st.w["m_alog"], st.w["m_alog"], ACT.Exp).then_inc(s.a_done, 1)
                    for m in range(M):
                        act.wait_ge(s.dt_ready, m + 1)
                        if m >= 1:
                            act.wait_ge(s.delta_done, m)
                        act.activation(vraw[:].rearrange("p (j t) -> p j t", j=2), st.ps[:, 4 + 2 * (m % 2):6 + 2 * (m % 2), 0:HALF],
                                       ACT.Identity, bias=st.w["m_bdt"][:, m:m + 1]).then_inc(s.v_done, 1)
                        act.wait_ge(s.v_done, m + 1)
                        act.activation(ev[:], vraw[:], ACT.Abs).then_inc(s.abs_done, 1)
                        act.wait_ge(s.abs_done, m + 1)
                        act.activation(ev[:], ev[:], ACT.Exp, scale=-1.0).then_inc(s.exp_done, 1)
                        act.wait_ge(s.exp_done, m + 1)
                        act.activation(lg[:], ev[:], ACT.Ln, bias=1.0).then_inc(s.log_done, 1)

                @block.vector
                def _(dve):
                    for m in range(M):
                        dve.wait_ge(s.hs_raw, m + 1)
                        if m >= 2:
                            dve.wait_ge(s.hs_done, m - 1)
                        acc = conv[:, m % 2, :].rearrange("p (b t) -> p b t", t=S)
                        dve.tensor_scalar(acc, hpad[:, m, :, 0:S], w_conv[:, m, 0:1], None, ALU.mult).then_inc(s.conv_step, 1)
                        for j in range(1, TAPS):
                            dve.wait_ge(s.conv_step, TAPS * m + j)
                            dve.scalar_tensor_tensor(acc, hpad[:, m, :, j:j + S], w_conv[:, m, j:j + 1], acc,
                                                     ALU.mult, ALU.add).then_inc(s.conv_step, 1)
                    for m in range(M):
                        dve.wait_ge(s.exp_done, m + 1)
                        dve.tensor_scalar(er[:], ev[:], 1.0, 1.0, ALU.add, ALU.subtract).then_inc(s.sp_step, 1)
                        dve.wait_ge(s.sp_step, 3 * m + 1)
                        dve.tensor_tensor(er[:], ev[:], er[:], ALU.subtract).then_inc(s.sp_step, 1)
                        dve.wait_ge(s.sp_step, 3 * m + 2)
                        dve.scalar_tensor_tensor(er[:], vraw[:], 0.0, er[:], ALU.max, ALU.add).then_inc(s.sp_step, 1)
                        dve.wait_ge(s.sp_step, 3 * m + 3)
                        dve.wait_ge(s.log_done, m + 1)
                        dve.tensor_tensor(delta[:, m, :], lg[:], er[:], ALU.add).then_inc(s.delta_done, 1)

        halves = lambda t: t[:].rearrange("p m (j t) -> p m j t", j=2)
        hs_h, gate_h, delta_h = halves(hs), halves(gate), halves(delta)
        xdbl_h = xdbl[:].rearrange("p (j t) -> p j t", j=2)
        scan_ctx = ExitStack()
        sc = lambda n, shape: scan_ctx.enter_context(nc.sbuf_tensor(f"l1a_{n}", shape, F32))
        bcs = sc("bcs", [P, 2 * NS, HALF])
        da, dbx = sc("da", [P, 2, HALF]), sc("dbx", [P, 2, HALF])
        z, zc = sc("z", [P, 2, HALF]), sc("zc", [P, 2, HALF])
        a_cur, d_cur = sc("a_cur", [P, NS]), sc("d_cur", [P, 1])
        dx_cur = sc("dx_cur", [P, HALF])
        ysum = z[:, 0, :]
        with scan_ctx, nc.Fori(0, 2) as j:
            with stage_sems(nc, ["bc_ready", "bc_act", "bc_dve"]) as s, nc.Block() as block:
                @block.tensor
                def _(pe):
                    for n in range(2 * NS):
                        if n >= 8:
                            pe.wait_ge(s.bc_act if n % 2 else s.bc_dve, (n - 8) // 2 + 1)
                        pe.matmul(st.ps[:, n % 8, 0:HALF], st.ident[0:R + 2 * NS, R + n:R + n + 1].to_broadcast([R + 2 * NS, P]),
                                  xdbl_h[:, j, :], start=True, stop=True).then_inc(s.bc_ready, 1)

                @block.scalar
                def _(act):
                    for n in range(1, 2 * NS, 2):
                        act.wait_ge(s.bc_ready, n + 1)
                        act.activation(bcs[:, n, :], st.ps[:, n % 8, 0:HALF], ACT.Copy).then_inc(s.bc_act, 1)

                @block.vector
                def _(dve):
                    for n in range(0, 2 * NS, 2):
                        dve.wait_ge(s.bc_ready, n + 1)
                        dve.tensor_copy(bcs[:, n, :], st.ps[:, n % 8, 0:HALF]).then_inc(s.bc_dve, 1)

            with nc.Fori(0, M) as m, stage_sems(nc, ["a_ready", "da_ready", "da_reset", "dbx_ready", "scan_done", "zc_ready", "sum_done",
                                                     "skip_done", "tile_done", "d_ready", "dx_ready"]) as s, nc.Block() as block:
                @block.gpsimd
                def _(pool):
                    pool.tensor_copy(a_cur[:], a_log[:, m, :]).then_inc(s.a_ready, 1)
                    pool.tensor_tensor(dx_cur[:], delta_h[:, m, j, :], hs_h[:, m, j, :], ALU.mult).then_inc(s.dx_ready, 1)
                    pool.tensor_copy(d_cur[:], st.w["m_d"].unsqueeze(2)[:, m, :]).then_inc(s.d_ready, 1)
                    pool.wait_ge(s.dx_ready, 1)
                    for n in range(NS):
                        if n >= 2:
                            pool.wait_ge(s.scan_done, n - 1)
                        pool.tensor_tensor(dbx[:, n % 2, :], dx_cur[:], bcs[:, n, :], ALU.mult).then_inc(s.dbx_ready, 1)

                @block.scalar
                def _(act):
                    act.wait_ge(s.a_ready, 1)
                    for n in range(NS):
                        if n >= 2:
                            act.wait_ge(s.scan_done, n - 1)
                        act.activation(da[:, n % 2, :], delta_h[:, m, j, :], ACT.Exp, scale=a_cur[:, n:n + 1]).then_inc(s.da_ready, 1)
                        act.wait_ge(s.da_ready, n + 1)
                        act.mul(da[:, n % 2, 0:HALF:S], da[:, n % 2, 0:HALF:S], 0.0).then_inc(s.da_reset, 1)

                @block.vector
                def _(dve):
                    def times_c(n):
                        dve.wait_ge(s.scan_done, n + 1)
                        if n >= 2:
                            dve.wait_ge(s.sum_done, n - 1)
                        dve.tensor_tensor(zc[:, n % 2, :], z[:, n % 2, :], bcs[:, NS + n, :], ALU.mult).then_inc(s.zc_ready, 1)

                    for n in range(NS):
                        dve.wait_ge(s.da_reset, n + 1)
                        dve.wait_ge(s.dbx_ready, n + 1)
                        if n >= 2:
                            dve.wait_ge(s.zc_ready, n - 1)
                        dve.tensor_tensor_scan(z[:, n % 2, :], da[:, n % 2, :], dbx[:, n % 2, :], 0.0, ALU.mult, ALU.add).then_inc(s.scan_done, 1)
                        if n >= 1:
                            times_c(n - 1)
                    times_c(NS - 1)
                    dve.wait_ge(s.sum_done, NS)
                    dve.wait_ge(s.d_ready, 1)
                    dve.scalar_tensor_tensor(ysum, hs_h[:, m, j, :], d_cur[:, 0:1], st.ps[:, 0, 0:HALF],
                                             ALU.mult, ALU.add).then_inc(s.skip_done, 1)
                    dve.wait_ge(s.skip_done, 1)
                    dve.tensor_tensor(gate_h[:, m, j, :], ysum, gate_h[:, m, j, :], ALU.mult).then_inc(s.tile_done, 1)

                @block.tensor
                def _(pe):
                    for n in range(NS):
                        pe.wait_ge(s.zc_ready, n + 1)
                        pe.matmul(st.ps[:, 0, 0:HALF], st.ident, zc[:, n % 2, :],
                                  start=(n == 0), stop=(n == NS - 1)).then_inc(s.sum_done, 1)

        y_cur = sb("y_cur", [P, M, S])
        with nc.Fori(0, B) as b, stage_sems(nc, ["cur_ready"] + NORM_SEMS) as s, nc.Block() as block:
            @block.gpsimd
            def _(pool):
                pool.tensor_copy(y_cur[:], gate[:].rearrange("p m (b t) -> p m b t", b=B)[:, :, b, :]).then_inc(s.cur_ready, 1)
                norm_pool(pool, st, s, st.X[:, b, :])

            @block.tensor
            def _(pe):
                pe.wait_ge(s.cur_ready, 1)
                for k in range(M):
                    last = pe.matmul(st.ps[0:S, 0, 0:D], y_cur[:, k, :], w_out[:, k, :], start=(k == 0), stop=(k == M - 1))
                last.then_inc(s.y_ready, 1)
                norm_tensor(pe, st, s, 1)

            @block.scalar
            def _(act):
                norm_scalar(act, st, s, 1, st.XT[:, :, b, :])

            @block.vector
            def _(dve):
                norm_vector(dve, st, s, st.ps[0:S, 0, 0:D], st.X[:, b, :], None)


GATE_SEMS = ["cur_ready", "logits_ready", "score_ready", "score_step", "top_ready", "picked_ready", "left_ready", "gate_step",
             "gate_ready", "gate_turned", "gateT_stored"]


class Gate:

    def __init__(self, nc, ctx, name, experts, top, ones_in_front, ones_behind, turns_per_gate=1):
        def sb(n, shape):
            return ctx.enter_context(nc.sbuf_tensor(f"{name}_{n}", shape, F32))

        self.experts, self.top, self.front = experts, top, ones_in_front
        self.marks = 8 - top
        self.width = ones_in_front + experts + ones_behind
        self.scores = sb("scores", [S, experts + self.marks])
        self.left = sb("left", [S, experts + self.marks])
        self.top8, self.picked = sb("top8", [S, 8]), sb("picked", [S, 8])
        self.gate = sb("gate", [S, self.width])
        self.total, self.rtotal = sb("total", [S, 2]), sb("rtotal", [S, 1])
        self.gateT = sb("gateT", [self.width, B, S])
        self.cur = sb("gate_cur", [P, KT, S])
        self.dram = nc.dram_tensor(f"{name}_gates", (self.width, turns_per_gate, TOK), F32).ap()
        self.repeats = turns_per_gate
        with stage_sems(nc, ["marks_set"]) as s, nc.Block() as block:
            @block.gpsimd
            def _(pool):
                pool.memset(self.scores[:], -1.0).then_inc(s.marks_set, 1)
                pool.memset(self.picked[:], -1.0).then_inc(s.marks_set, 1)
                pool.memset(self.gate[:], 1.0).then_inc(s.marks_set, 1)

    def tensor_logits(self, pe, st, s, wg, bank):
        pe.wait_ge(s.cur_ready, 1)
        for k in range(KT):
            last = pe.matmul(st.ps[0:S, bank, 0:self.experts], self.cur[:, k, :], wg[:, k, :], start=(k == 0), stop=(k == KT - 1))
        last.then_inc(s.logits_ready, 1)

    def vector_pick(self, dve, s):
        e = self.experts
        dve.wait_ge(s.score_ready, 1)
        dve.max(self.top8[:], self.scores[:, 0:e]).then_inc(s.top_ready, 1)
        dve.wait_ge(s.top_ready, 1)
        dve.tensor_copy(self.picked[:, 0:self.top], self.top8[:, 0:self.top]).then_inc(s.picked_ready, 1)
        dve.wait_ge(s.picked_ready, 1)
        dve.match_replace(self.left[:], self.picked[:], self.scores[:], 0.0).then_inc(s.left_ready, 1)
        dve.wait_ge(s.left_ready, 1)
        return self.gate[:, self.front:self.front + e], self.scores[:, 0:e], self.left[:, 0:e]

    def tensor_turn(self, pe, st, s, bank):
        pe.wait_ge(s.gate_ready, 1)
        pe.transpose(st.ps[0:self.width, bank, 0:S], self.gate[:], st.ident[0:S, 0:S]).then_inc(s.gate_turned, 1)

    def scalar_store(self, act, st, s, bank, b):
        act.wait_ge(s.gate_turned, 1)
        act.activation(self.gateT[:, b, :], st.ps[0:self.width, bank, 0:S], ACT.Copy).then_inc(s.gateT_stored, 1)


def experts(nc, st, name, kind, units, unit_cols, dram_w, gate, gate_row, inputs, b2):
    HALF = TOK // 2
    geglu = kind == "geglu"
    up = 4 if geglu else 2
    n_gates = 2 if kind == "relu" else 1
    off2 = KT * up * P
    offb = off2 + 2 * D
    yT = st.yT
    with ExitStack() as ctx:
        def sb(n, shape, dt=F32):
            return ctx.enter_context(nc.sbuf_tensor(f"{name}_{n}", shape, dt))

        slot = [sb(f"slot{i}", [P, unit_cols]) for i in range(2)]
        gates = [sb(f"gates{i}", [P, n_gates, TOK]) for i in range(2)]
        act_out = sb("act_out", [P, 2, TOK]) if kind != "relu" else None
        prod = sb("prod", [P, 2, TOK]) if geglu else None
        hg = sb("hg", [P, 2, TOK])
        sems = ["gates_stored", "weights_loaded0", "weights_loaded1", "h_ready", "gelu_done", "prod_done", "hg_ready",
                "y_done", "y_copied"]
        with stage_sems(nc, sems) as s, nc.Block() as block:
            loaded = [s.weights_loaded0, s.weights_loaded1]
            gate_rows = gate.dram.rearrange("e r t -> (e r) t").rearrange("(u g) t -> u g t", g=n_gates)

            def w1(sl, k, m):
                return slot[sl][:, k * up * P + m * P:k * up * P + (m + 1) * P]

            def w2(sl, t, m):
                return slot[sl][:, off2 + t * D + m * P:off2 + t * D + (m + 1) * P]

            def col(sl, i):
                return slot[sl][:, offb + i:offb + i + 1]

            def halves(t, i):
                return t[:, i, :].rearrange("p (j c) -> p j c", j=2)

            turns = (units + 1) // 2
            cuts = sorted({1, turns - 1} | {u // 2 for u, _ in inputs if u // 2 > 0})

            def run(eng, body):
                body(0, inputs[0][1])
                for lo, hi in zip(cuts[:-1], cuts[1:]):
                    x = [x for u, x in inputs if u // 2 <= lo][-1]
                    with eng.Fori(lo, hi) as i:
                        body(i, x)
                body(turns - 1, inputs[-1][1])

            def tiles_of(i):
                n = 2 if type(i) is int and 2 * i + 1 >= units else 4
                return [(c, c // 2, c % 2) for c in range(n)]

            def after(eng, sem, value, least=1):
                if type(value) is not int or value >= least:
                    eng.wait_ge(sem, value)

            @block.sync
            def _(sp):
                for r in range(gate.repeats):
                    sp.dma_start(gate.dram[:, r, :], gate.gateT[:].rearrange("e b t -> e (b t)")).then_inc(s.gates_stored, 16)
                sp.wait_ge(s.gates_stored, 16 * gate.repeats)

                def body(i, _):
                    for sl in sorted({sl for _, sl, _ in tiles_of(i)}):
                        u = i * 2 + sl
                        after(sp, s.y_done, 4 * i + 2 * sl - 2)
                        sp.dma_start(slot[sl][:], dram_w[u]).then_inc(loaded[sl], 16)
                        sp.dma_start(gates[sl][:], gate_rows[gate_row(i, sl)].partition_broadcast(P)).then_inc(loaded[sl], 16)
                run(sp, body)

            @block.tensor
            def _(pe):
                if b2 is not None:
                    for m in range(2):
                        for j in range(2):
                            pe.matmul(st.ps[:, 2 * m + j, 0:HALF], b2[0:gate.width, m * P:(m + 1) * P],
                                      gate.gateT[:].rearrange("e b t -> e (b t)")[:, j * HALF:(j + 1) * HALF], start=True, stop=False)

                def down(n, sl, t, first, last_tile):
                    pe.wait_ge(s.hg_ready, n + 1)
                    for m in range(2):
                        for j in range(2):
                            last = pe.matmul(st.ps[:, 2 * m + j, 0:HALF], w2(sl, t, m), hg[:, t, j * HALF:(j + 1) * HALF],
                                             start=first, stop=last_tile)
                    last.then_inc(s.y_done, 1)

                def body(i, x):
                    tiles = tiles_of(i)
                    for c, sl, t in tiles:
                        n = i * 4 + c
                        if t == 0:
                            pe.wait_ge(loaded[sl], i * 32 + 32)
                        if geglu:
                            after(pe, s.gelu_done, n)
                            after(pe, s.prod_done, n)
                        elif kind == "gelu":
                            after(pe, s.gelu_done, n - 1)
                        else:
                            after(pe, s.hg_ready, n - 1)
                        for half in range(2 if geglu else 1):
                            for j in range(2):
                                bank = 4 + 2 * half + j if geglu else 4 + 2 * t + j
                                for k in range(KT):
                                    last = pe.matmul(st.ps[:, bank, 0:HALF], w1(sl, k, t + 2 * half), x[:, k, j * HALF:(j + 1) * HALF],
                                                     start=(k == 0), stop=(k == KT - 1))
                        last.then_inc(s.h_ready, 1)
                        if not (type(i) is int and i == 0 and c == 0):
                            down(n - 1, 1 - sl if t == 0 else sl, 1 - t, b2 is None and type(i) is int and n == 1, False)
                run(pe, body)
                c, sl, t = tiles_of(turns - 1)[-1]
                down(2 * units - 1, sl, t, False, True)

            if kind != "relu":
                @block.scalar
                def _(act):
                    def body(i, _):
                        for c, sl, t in tiles_of(i):
                            n = i * 4 + c
                            act.wait_ge(s.h_ready, n + 1)
                            after(act, s.hg_ready, n - 1)
                            bank = 6 if geglu else 4 + 2 * t
                            act.activation(halves(act_out, t), st.ps[:, bank:bank + 2, 0:HALF], ACT.Gelu,
                                           bias=col(sl, 2 + t if geglu else t)).then_inc(s.gelu_done, 1)
                    run(act, body)

            @block.vector
            def _(dve):
                def body(i, _):
                    for c, sl, t in tiles_of(i):
                        n = i * 4 + c
                        if kind == "relu":
                            dve.wait_ge(s.h_ready, n + 1)
                            if t == 0:
                                dve.wait_ge(loaded[sl], i * 32 + 32)
                            after(dve, s.y_done, n - 1)
                            dve.scalar_tensor_tensor(halves(hg, t), st.ps[:, 4 + 2 * t:6 + 2 * t, 0:HALF], 0.0, halves(gates[sl], t),
                                                     ALU.max, ALU.mult).then_inc(s.hg_ready, 1)
                            continue
                        if t == 0:
                            dve.wait_ge(loaded[sl], i * 32 + 32)
                        if geglu:
                            dve.wait_ge(s.gelu_done, n + 1)
                            dve.scalar_tensor_tensor(halves(prod, t), st.ps[:, 4:6, 0:HALF], col(sl, t), halves(act_out, t),
                                                     ALU.add, ALU.mult).then_inc(s.prod_done, 1)
                            after(dve, s.y_done, n - 1)
                            dve.wait_ge(s.prod_done, n + 1)
                            dve.scalar_tensor_tensor(hg[:, t, :], prod[:, t, :], col(sl, 4 + t), gates[sl][:, 0, :],
                                                     ALU.mult, ALU.mult).then_inc(s.hg_ready, 1)
                        else:
                            dve.wait_ge(s.gelu_done, n + 1)
                            after(dve, s.y_done, n - 1)
                            dve.tensor_tensor(hg[:, t, :], act_out[:, t, :], gates[sl][:, 0, :], ALU.mult).then_inc(s.hg_ready, 1)
                run(dve, body)
                dve.wait_ge(s.y_done, 2 * units)
                for m in range(2):
                    dve.tensor_copy(halves(yT, m), st.ps[:, 2 * m:2 * m + 2, 0:HALF]).then_inc(s.y_copied, 1)


def experts_tail(nc, st):
    with nc.Fori(0, B) as b, stage_sems(nc, ["cur_ready"] + NORM_SEMS) as s, nc.Block() as block:
        @block.gpsimd
        def _(pool):
            pool.tensor_copy(st.ycur[:], st.yT[:].rearrange("p m (b t) -> p m b t", b=B)[:, :, b, :]).then_inc(s.cur_ready, 1)
            norm_pool(pool, st, s, st.X[:, b, :])

        @block.tensor
        def _(pe):
            pe.wait_ge(s.cur_ready, 1)
            for m in range(KT):
                last = pe.transpose(st.ps[0:S, 0, m * P:(m + 1) * P], st.ycur[:, m, :], st.ident)
            last.then_inc(s.y_ready, 1)
            norm_tensor(pe, st, s, 1)

        @block.scalar
        def _(act):
            norm_scalar(act, st, s, 1, st.XT[:, :, b, :])

        @block.vector
        def _(dve):
            norm_vector(dve, st, s, st.ps[0:S, 0, 0:D], st.X[:, b, :], None)


def l2_ffn(nc, st, dram):
    E, TOP, EPS = 15, 3, 1e-20
    with ExitStack() as ctx:
        sb = lambda n, shape: ctx.enter_context(nc.sbuf_tensor(f"l2f_{n}", shape, F32))
        st.yT, st.ycur = sb("yT", [P, KT, TOK]), sb("ycur", [P, KT, S])
        nmax, raw, expsum = sb("nmax", [S, 1]), sb("raw", [S, E]), sb("expsum", [S, 1])
        gate = Gate(nc, ctx, "l2f", E, TOP, 0, 2)
        wg = st.w["f8gate"].rearrange("p (k e) -> p k e", k=KT)
        with nc.Fori(0, B) as b, stage_sems(nc, GATE_SEMS) as s, nc.Block() as block:
            @block.gpsimd
            def _(pool):
                pool.tensor_copy(gate.cur[:], st.XT[:, :, b, :]).then_inc(s.cur_ready, 1)

            @block.tensor
            def _(pe):
                gate.tensor_logits(pe, st, s, wg, 0)
                gate.tensor_turn(pe, st, s, 1)

            @block.scalar
            def _(act):
                act.wait_ge(s.score_step, 1)
                act.activation(raw[:], st.ps[0:S, 0, 0:E], ACT.Exp, bias=nmax[:, 0:1], accum_out=expsum[:, 0:1]).then_inc(s.score_step, 1)
                gate.scalar_store(act, st, s, 1, b)

            @block.vector
            def _(dve):
                dve.wait_ge(s.logits_ready, 1)
                dve.tensor_reduce(nmax[:], st.ps[0:S, 0, 0:E], AX.X, ALU.max, negate=True).then_inc(s.score_step, 1)
                dve.wait_ge(s.score_step, 2)
                dve.reciprocal(gate.rtotal[:], expsum[:]).then_inc(s.score_step, 1)
                dve.wait_ge(s.score_step, 3)
                dve.tensor_scalar(gate.scores[:, 0:E], raw[:], gate.rtotal[:, 0:1], None, ALU.mult).then_inc(s.score_ready, 1)
                out, scores, left = gate.vector_pick(dve, s)
                dve.tensor_tensor(raw[:], scores, left, ALU.subtract).then_inc(s.gate_step, 1)
                dve.tensor_reduce(gate.total[:, 0:1], gate.top8[:, 0:TOP], AX.X, ALU.add).then_inc(s.gate_step, 1)
                dve.wait_ge(s.gate_step, 2)
                dve.tensor_scalar(gate.total[:, 1:2], gate.total[:, 0:1], EPS, None, ALU.add).then_inc(s.gate_step, 1)
                dve.wait_ge(s.gate_step, 3)
                dve.reciprocal(gate.total[:, 0:1], gate.total[:, 1:2]).then_inc(s.gate_step, 1)
                dve.wait_ge(s.gate_step, 4)
                dve.tensor_scalar(out, raw[:], gate.total[:, 0:1], None, ALU.mult).then_inc(s.gate_ready, 1)

        xf = st.XT[:].rearrange("p k b t -> p k (b t)")
        experts(nc, st, "l2f", "geglu", E + 2, KT * 4 * P + 2 * D + 6, dram["l2_ffn_units"], gate,
                lambda i, sl: i * 2 + sl, [(0, xf)], st.w["f8b2"])
        experts_tail(nc, st)


def l3_ffn(nc, st, dram):
    E, TOP, EPS = 8, 2, float(np.finfo(np.float32).eps)
    with ExitStack() as ctx:
        sb = lambda n, shape: ctx.enter_context(nc.sbuf_tensor(f"l3f_{n}", shape, F32))
        st.yT, st.ycur = sb("yT", [P, KT, TOK]), sb("ycur", [P, KT, S])
        xs, xr = sb("xs", [P, KT, B, S]), sb("xr", [P, KT, B, S])
        sq, ss, ms = sb("sq", [S, D]), sb("ss", [S, 1]), sb("ms", [S, 1])
        x_cur = sb("x_cur", [S, D])
        gate = Gate(nc, ctx, "l3f", E, TOP, 2, 0, turns_per_gate=2)
        wg = st.w["f11gate"].rearrange("p (k e) -> p k e", k=KT)
        with nc.Fori(0, B) as b, stage_sems(nc, GATE_SEMS + ["sq_ready", "ms_ready", "rms_ready", "xn_ready", "xn_turned", "xs_done",
                                                              "twice_done", "xcur_ready", "sum_ready"]) as s, nc.Block() as block:
            @block.gpsimd
            def _(pool):
                pool.tensor_copy(gate.cur[:], st.XT[:, :, b, :]).then_inc(s.cur_ready, 1)
                pool.tensor_copy(x_cur[:], st.X[:, b, :]).then_inc(s.xcur_ready, 1)
                pool.wait_ge(s.xcur_ready, 1)
                pool.tensor_tensor(st.X[:, b, :], x_cur[:], x_cur[:], ALU.add).then_inc(s.twice_done, 1)
                pool.wait_ge(s.sq_ready, 1)
                pool.tensor_scalar(ms[:], ss[:], 1.0 / D, EPS, ALU.mult, ALU.add).then_inc(s.ms_ready, 1)
                pool.wait_ge(s.ms_ready, 1)
                pool.tensor_tensor(st.rstd[:], ms[:], st.minus_half[0:S, :], ALU.pow).then_inc(s.rms_ready, 1)

            @block.tensor
            def _(pe):
                gate.tensor_logits(pe, st, s, wg, 0)
                pe.wait_ge(s.xn_ready, 1)
                for k in range(KT):
                    last = pe.transpose(st.ps[:, 2, k * S:(k + 1) * S], st.xnew[:, k * P:(k + 1) * P], st.ident[0:S, 0:S])
                last.then_inc(s.xn_turned, 1)
                gate.tensor_turn(pe, st, s, 1)

            @block.scalar
            def _(act):
                act.wait_ge(s.logits_ready, 1)
                act.activation(gate.scores[:, 0:E], st.ps[0:S, 0, 0:E], ACT.Sigmoid, accum_out=gate.total[:, 0:1]).then_inc(s.score_ready, 1)
                act.wait_ge(s.xn_turned, 1)
                for k in range(KT):
                    ps = st.ps[:, 2, k * S:(k + 1) * S]
                    act.activation(xs[:, k, b, :], ps, ACT.Copy, scale=st.w["f11gs"][:, k:k + 1]).then_inc(s.xs_done, 1)
                    act.activation(xr[:, k, b, :], ps, ACT.Copy, scale=st.w["f11gr"][:, k:k + 1]).then_inc(s.xs_done, 1)
                gate.scalar_store(act, st, s, 1, b)

            @block.vector
            def _(dve):
                dve.wait_ge(s.xcur_ready, 1)
                dve.scalar_tensor_tensor(sq[:], x_cur[:], 1.0, x_cur[:], ALU.mult, ALU.mult, accum_out=ss[:, 0:1]).then_inc(s.sq_ready, 1)
                out, scores, left = gate.vector_pick(dve, s)
                dve.reciprocal(gate.rtotal[:], gate.total[:, 0:1]).then_inc(s.gate_step, 1)
                dve.tensor_tensor(out, scores, left, ALU.subtract).then_inc(s.gate_step, 1)
                dve.wait_ge(s.gate_step, 2)
                dve.tensor_scalar(out, out, gate.rtotal[:, 0:1], None, ALU.mult).then_inc(s.gate_ready, 1)
                dve.wait_ge(s.rms_ready, 1)
                dve.tensor_scalar(st.xnew[:], x_cur[:], st.rstd[:, 0:1], None, ALU.mult).then_inc(s.xn_ready, 1)

        flat = lambda t: t[:].rearrange("p k b t -> p k (b t)")
        experts(nc, st, "l3f", "gelu", 40, KT * 2 * P + 2 * D + 2, dram["l3_ffn_units"], gate,
                lambda i, sl: i, [(0, flat(xs)), (8, flat(xr))], st.w["f11b2"])
        experts_tail(nc, st)


class AttnInFfn:

    sems = ["src_ready", "x_summed"]

    def __init__(self, st, x2T):
        self.st, self.x2T = st, x2T

    def vector(self, dve, s, b, y):
        st = self.st
        dve.wait_ge(s.y_ready, 1)
        dve.tensor_tensor(st.resid[:], y, st.X[:, b, :], ALU.add).then_inc(s.resid_ready, 1)
        dve.wait_ge(s.resid_ready, 1)
        norm_stats_vector(dve, st, s, st.w["f5g2"][0:S, :], st.w["f5s2"][0:S, :])

    def pool(self, pool, s, b):
        st = self.st
        rstd_pool(pool, st, s)
        pool.tensor_tensor(st.X[:, b, :], st.resid[:], st.X[:, b, :], ALU.add).then_inc(s.x_summed, 1)

    def tensor(self, pe, s):
        norm_tensor(pe, self.st, s, 1)

    def scalar(self, act, s, b):
        norm_scalar(act, self.st, s, 1, self.x2T[:, :, b, :])


def l1_ffn(nc, st, dram):
    E, TOP, H = 32, 4, 16
    REL = 2 * S - 1
    ROW, PITCH = 200, 3300
    scratch = nc.dram_tensor("l1f_positions", (B, S * PITCH), F32).ap()
    order = [x for g in range(4) for x in (2 * g, 2 * g + 1, 8 + 2 * g, 9 + 2 * g)]
    wq = st.w["f5q"].rearrange("p (k n) -> p k n", k=KT)
    wp = st.w["f5p"].rearrange("p (k n) -> p k n", k=KT)
    pe_table = st.w["f5pe"].rearrange("p (k n) -> p k n", k=KT)
    with ExitStack() as ctx:
        sb = lambda n, shape: ctx.enter_context(nc.sbuf_tensor(f"l1f_{n}", shape, F32))
        st.yT, st.ycur = sb("yT", [P, KT, TOK]), sb("ycur", [P, KT, S])
        x2T = sb("x2T", [P, KT, B, S])
        with ExitStack() as ctx2:
            sb2 = lambda n, shape: ctx2.enter_context(nc.sbuf_tensor(f"l1f_{n}", shape, F32))
            x1T = sb2("x1T", [P, KT, B, S])
            with ExitStack() as ctx3:
                sb3 = lambda n, shape: ctx3.enter_context(nc.sbuf_tensor(f"l1f_{n}", shape, F32))
                pT = sb3("pT", [P, KT, REL])
                q1, x1_cur = sb3("q1", [P, 4, S]), sb3("x1_cur", [P, KT, S])
                bd = sb3("bd", [S, H, REL])
                with stage_sems(nc, ["p_ready", "p_done"]) as s, nc.Block() as block:
                    @block.tensor
                    def _(pe):
                        for m in range(KT):
                            for k in range(KT):
                                last = pe.matmul(st.ps[:, m, 0:REL], wp[:, k, m * P:(m + 1) * P], pe_table[:, k, :], start=(k == 0), stop=(k == KT - 1))
                        last.then_inc(s.p_ready, 1)

                    @block.scalar
                    def _(act):
                        act.wait_ge(s.p_ready, 1)
                        act.activation(pT[:], st.ps[:, 0:KT, 0:REL], ACT.Copy).then_inc(s.p_done, 1)

                with nc.Fori(0, B) as b, stage_sems(nc, NORM_SEMS + ["xcur_done", "x1T_done", "q_ready", "q_done", "bd_ready", "bd_dve", "bd_act",
                                                                     "xin_ready", "bd_stored"]) as s, nc.Block() as block:
                    @block.gpsimd
                    def _(pool):
                        pool.tensor_copy(st.resid[:], st.X[:, b, :]).then_inc(s.resid_ready, 1)
                        rstd_pool(pool, st, s)

                    @block.vector
                    def _(dve):
                        dve.wait_ge(s.resid_ready, 1)
                        norm_stats_vector(dve, st, s, st.w["f5g1"][0:S, :], st.w["f5s1"][0:S, :])
                        dve.wait_ge(s.q_ready, 1)
                        dve.tensor_scalar(q1[:], st.ps[:, 2, 0:4 * S].rearrange("p (m t) -> p m t", m=4), 0.25, None, ALU.mult).then_inc(s.q_done, 1)
                        for n in range(0, 8, 2):
                            dve.wait_ge(s.bd_ready, n + 1)
                            dve.tensor_copy(bd[:, 2 * n:2 * n + 2, :], st.ps[0:S, n, 0:2 * REL].rearrange("p (h r) -> p h r", h=2)).then_inc(s.bd_dve, 1)

                    @block.tensor
                    def _(pe):
                        norm_tensor(pe, st, s, 1)
                        pe.wait_ge(s.xcur_done, 1)
                        for m in range(4):
                            for k in range(KT):
                                last = pe.matmul(st.ps[:, 2, m * S:(m + 1) * S], wq[:, k, m * P:(m + 1) * P], x1_cur[:, k, :], start=(k == 0), stop=(k == KT - 1))
                        last.then_inc(s.q_ready, 1)
                        pe.wait_ge(s.q_done, 1)
                        pe.wait_ge(s.x1T_done, 1)
                        for n in range(8):
                            for i in range(2):
                                h = order[2 * n + i]
                                half, r = divmod(h, 8)
                                p0 = 32 * (r // 2)
                                last = pe.matmul(st.ps[0:S, n, i * REL:(i + 1) * REL], q1[p0:p0 + 32, 2 * (r % 2) + half, :],
                                                 pT[p0:p0 + 32, half, :], start=True, stop=True)
                            last.then_inc(s.bd_ready, 1)

                    @block.scalar
                    def _(act):
                        act.wait_ge(s.xnew_turned, 1)
                        ps = st.ps[:, 1, 0:KT * S].rearrange("p (k t) -> p k t", k=KT)
                        act.activation(x1_cur[:], ps, ACT.Copy).then_inc(s.xcur_done, 1)
                        act.activation(x1T[:, :, b, :], ps, ACT.Copy).then_inc(s.x1T_done, 1)
                        for n in range(1, 8, 2):
                            act.wait_ge(s.bd_ready, n + 1)
                            act.activation(bd[:, 2 * n:2 * n + 2, :], st.ps[0:S, n, 0:2 * REL].rearrange("p (h r) -> p h r", h=2), ACT.Copy).then_inc(s.bd_act, 1)

                    @block.sync
                    def _(sp):
                        sp.wait_ge(s.bd_dve, 4)
                        sp.wait_ge(s.bd_act, 4)
                        rows = scratch[b, :].rearrange("(i c) -> i c", c=PITCH)[:, 0:H * ROW].rearrange("i (h r) -> i h r", r=ROW)
                        sp.dma_start(rows[:, :, 0:REL], bd[:]).then_inc(s.bd_stored, 16)
                        sp.wait_ge(s.bd_stored, 16)

            def skewed(b):
                rows = scratch[b, S - 1:S - 1 + S * (PITCH - 1)].rearrange("(i c) -> i c", c=PITCH - 1)
                return rows[:, 0:H * ROW].rearrange("i (h r) -> i h r", r=ROW)[:, :, 0:S]

            w = weights(st, "f5")
            attention(nc, st, "l1f", H, 16, False, w, xT=x1T, tail=AttnInFfn(st, x2T), bd=skewed)

        gate = Gate(nc, ctx, "l1f", E, TOP, 0, 0)
        wg = st.w["f5sel"].rearrange("p (k e) -> p k e", k=KT)
        with nc.Fori(0, B) as b, stage_sems(nc, GATE_SEMS) as s, nc.Block() as block:
            @block.gpsimd
            def _(pool):
                pool.tensor_copy(gate.cur[:], x2T[:, :, b, :]).then_inc(s.cur_ready, 1)

            @block.tensor
            def _(pe):
                gate.tensor_logits(pe, st, s, wg, 0)
                gate.tensor_turn(pe, st, s, 1)

            @block.scalar
            def _(act):
                act.wait_ge(s.logits_ready, 1)
                act.activation(gate.scores[:, 0:E], st.ps[0:S, 0, 0:E], ACT.Sigmoid).then_inc(s.score_ready, 1)
                gate.scalar_store(act, st, s, 1, b)

            @block.vector
            def _(dve):
                out, scores, left = gate.vector_pick(dve, s)
                dve.tensor_tensor(out, scores, left, ALU.subtract).then_inc(s.gate_ready, 1)

        experts(nc, st, "l1f", "relu", E // 2, KT * 2 * P + 2 * D, dram["l1_ffn_units"], gate,
                lambda i, sl: i * 2 + sl, [(0, x2T[:].rearrange("p k b t -> p k (b t)"))], None)
        experts_tail(nc, st)


def l2_attn(nc, st, dram):
    H, HD, EPS = 8, 32, 1e-6
    view = lambda n: st.w[n].rearrange("p (k n) -> p k n", k=KT)
    wq, wk, wv, wbeta, wgates, wout = (view(n) for n in ("a6q", "a6k", "a6v", "a6beta", "a6gates", "a6o"))
    norm_w, gate_bias, beta_bias = st.w["a6norm"][0:S, :], st.w["a6bgates"][0:S, :], st.w["a6bbeta"][0:H, 0:1]
    cos, sin, swap = st.w["a6cos"], st.w["a6sin"], st.w["a6swap"]
    with ExitStack() as ctx:
        sb = lambda n, shape: ctx.enter_context(nc.sbuf_tensor(f"l2a_{n}", shape, F32))
        sq, ss, ms = sb("sq", [S, D]), sb("ss", [S, 1]), sb("ms", [S, 1])
        hT, qT, kT = sb("hT", [P, KT, S]), sb("qT", [P, KT, S]), sb("kT", [P, KT, S])
        rq, rk = sb("rq", [P, KT, S]), sb("rk", [P, KT, S])
        vals, gates, betaT = sb("vals", [S, D]), sb("gates", [S, 2 * H]), sb("betaT", [H, S])
        gpre = sb("gpre", [S, 2 * H])
        entries, decay, weighed = sb("entries", [S, H, S]), sb("decay", [S, H, S]), sb("weighed", [S, H, S])
        o_sb, oT = sb("o_sb", [S, D]), sb("oT", [P, KT, S])
        with stage_sems(nc, ["first_zero"]) as s, nc.Block() as block:
            @block.gpsimd
            def _(pool):
                pool.memset(betaT[:], 0.0).then_inc(s.first_zero, 1)

        sems = ["sq_ready", "ms_ready", "rms_ready", "h_ready", "h_turned", "hT_ready", "beta_ready", "qk_ready", "v_ready", "gates_ready",
                "gpre_ready", "gates_done", "betaT_done", "q_done", "k_done", "v_done", "swap_ready", "rope_step", "rope_ready", "f_ready",
                "entries_ready", "decay_ready", "scores_ready", "weighed_ready", "heads_done", "o_ready", "o_turned", "oT_ready"]
        with nc.Fori(0, B) as b, stage_sems(nc, sems + NORM_SEMS) as s, nc.Block() as block:
            @block.gpsimd
            def _(pool):
                pool.wait_ge(s.sq_ready, 1)
                pool.tensor_scalar(ms[:], ss[:], 1.0 / D, EPS, ALU.mult, ALU.add).then_inc(s.ms_ready, 1)
                pool.wait_ge(s.ms_ready, 1)
                pool.tensor_tensor(st.vareps[:], ms[:], st.minus_half[0:S, :], ALU.pow).then_inc(s.rms_ready, 1)
                pool.wait_ge(s.gates_done, 1)
                pool.tensor_tensor(entries[:], st.ident[0:S, 0:S].unsqueeze(1).to_broadcast([S, H, S]),
                                   gates[:, 0:H].unsqueeze(2).to_broadcast([S, H, S]), ALU.mult).then_inc(s.entries_ready, 1)
                norm_pool(pool, st, s, st.X[:, b, :])

            @block.tensor
            def _(pe):
                pe.wait_ge(s.h_ready, 1)
                for k in range(KT):
                    last = pe.transpose(st.ps[:, 1, k * S:(k + 1) * S], st.xnew[:, k * P:(k + 1) * P], st.ident[0:S, 0:S])
                last.then_inc(s.h_turned, 1)
                pe.wait_ge(s.hT_ready, 1)
                for k in range(KT):
                    last = pe.matmul(st.ps[0:H, 4, 0:S], wbeta[:, k, :], hT[:, k, :], start=(k == 0), stop=(k == KT - 1))
                last.then_inc(s.beta_ready, 1)
                for k in range(KT):
                    last = pe.matmul(st.ps[0:S, 5, 0:2 * H], hT[:, k, :], wgates[:, k, :], start=(k == 0), stop=(k == KT - 1))
                last.then_inc(s.gates_ready, 1)
                for bank, w in ((0, wq), (2, wk)):
                    for m in range(KT):
                        for k in range(KT):
                            last = pe.matmul(st.ps[:, bank, m * S:(m + 1) * S], w[:, k, m * P:(m + 1) * P], hT[:, k, :],
                                             start=(k == 0), stop=(k == KT - 1))
                    last.then_inc(s.qk_ready, 1)
                for k in range(KT):
                    last = pe.matmul(st.ps[0:S, 3, 0:D], hT[:, k, :], wv[:, k, :], start=(k == 0), stop=(k == KT - 1))
                last.then_inc(s.v_ready, 1)
                pe.wait_ge(s.q_done, 1)
                pe.wait_ge(s.k_done, 1)
                for m in range(KT):
                    pe.matmul(st.ps[:, 6, m * S:(m + 1) * S], swap, qT[:, m, :], start=True, stop=True)
                    last = pe.matmul(st.ps[:, 7, m * S:(m + 1) * S], swap, kT[:, m, :], start=True, stop=True)
                last.then_inc(s.swap_ready, 1)
                pe.wait_ge(s.betaT_done, 1)
                pe.wait_ge(s.gpre_ready, 1)
                for h in range(H):
                    last = pe.matmul(st.ps[0:S, 4 + h // 4, (h % 4) * S:(h % 4 + 1) * S],
                                     st.ident[0:H, h:h + 1].to_broadcast([H, S]), betaT[:], start=True, stop=True)
                last.then_inc(s.f_ready, 1)
                pe.wait_ge(s.rope_ready, 2)
                pe.wait_ge(s.v_done, 1)
                for h in range(H):
                    j, r = divmod(h, 4)
                    last = pe.matmul(st.ps[0:S, r, j * S:(j + 1) * S], kT[HD * r:HD * (r + 1), j, :], qT[HD * r:HD * (r + 1), j, :],
                                     start=True, stop=True)
                last.then_inc(s.scores_ready, 1)
                pe.wait_ge(s.weighed_ready, 1)
                for h in range(H):
                    last = pe.matmul(st.ps[0:S, 6, h * HD:(h + 1) * HD], weighed[:, h, :], vals[:, h * HD:(h + 1) * HD], start=True, stop=True)
                last.then_inc(s.heads_done, 1)
                pe.wait_ge(s.o_ready, 1)
                for k in range(KT):
                    last = pe.transpose(st.ps[:, 7, k * S:(k + 1) * S], o_sb[:, k * P:(k + 1) * P], st.ident[0:S, 0:S])
                last.then_inc(s.o_turned, 1)
                pe.wait_ge(s.oT_ready, 1)
                for k in range(KT):
                    last = pe.matmul(st.ps[0:S, 0, 0:D], oT[:, k, :], wout[:, k, :], start=(k == 0), stop=(k == KT - 1))
                last.then_inc(s.y_ready, 1)
                norm_tensor(pe, st, s, 1)

            @block.scalar
            def _(act):
                two = lambda bank: st.ps[:, bank, 0:KT * S].rearrange("p (k t) -> p k t", k=KT)
                act.wait_ge(s.h_turned, 1)
                act.activation(hT[:], two(1), ACT.Copy).then_inc(s.hT_ready, 1)
                act.wait_ge(s.beta_ready, 1)
                act.activation(betaT[:, 1:S], st.ps[0:H, 4, 1:S], ACT.Sigmoid, bias=beta_bias).then_inc(s.betaT_done, 1)
                act.wait_ge(s.gpre_ready, 1)
                act.activation(gates[:], gpre[:], ACT.Sigmoid).then_inc(s.gates_done, 1)
                act.wait_ge(s.qk_ready, 2)
                act.activation(kT[:], two(2), ACT.Copy).then_inc(s.k_done, 1)
                act.wait_ge(s.o_turned, 1)
                act.activation(oT[:], two(7), ACT.Copy).then_inc(s.oT_ready, 1)
                norm_scalar(act, st, s, 1, st.XT[:, :, b, :])

            @block.vector
            def _(dve):
                two = lambda bank: st.ps[:, bank, 0:KT * S].rearrange("p (k t) -> p k t", k=KT)
                wide = lambda t: t[:, 0:S].unsqueeze(1).to_broadcast([P, KT, S])
                x_b = st.X[:, b, :]
                dve.scalar_tensor_tensor(sq[:], x_b, 1.0, x_b, ALU.mult, ALU.mult, accum_out=ss[:, 0:1]).then_inc(s.sq_ready, 1)
                dve.wait_ge(s.rms_ready, 1)
                dve.scalar_tensor_tensor(st.xnew[:], x_b, st.vareps[:, 0:1], norm_w, ALU.mult, ALU.mult).then_inc(s.h_ready, 1)
                dve.wait_ge(s.gates_ready, 1)
                dve.tensor_tensor(gpre[:], st.ps[0:S, 5, 0:2 * H], gate_bias, ALU.add).then_inc(s.gpre_ready, 1)
                dve.wait_ge(s.qk_ready, 1)
                dve.tensor_scalar(qT[:], two(0), float(HD) ** -0.5, None, ALU.mult).then_inc(s.q_done, 1)
                dve.wait_ge(s.v_ready, 1)
                dve.tensor_copy(vals[:], st.ps[0:S, 3, 0:D]).then_inc(s.v_done, 1)
                dve.wait_ge(s.swap_ready, 1)
                dve.tensor_tensor(rq[:], two(6), wide(sin), ALU.mult).then_inc(s.rope_step, 1)
                dve.tensor_tensor(rk[:], two(7), wide(sin), ALU.mult).then_inc(s.rope_step, 1)
                dve.tensor_tensor(qT[:], qT[:], wide(cos), ALU.mult).then_inc(s.rope_step, 1)
                dve.tensor_tensor(kT[:], kT[:], wide(cos), ALU.mult).then_inc(s.rope_step, 1)
                dve.wait_ge(s.rope_step, 4)
                dve.tensor_tensor(qT[:], qT[:], rq[:], ALU.add).then_inc(s.rope_ready, 1)
                dve.tensor_tensor(kT[:], kT[:], rk[:], ALU.add).then_inc(s.rope_ready, 1)
                dve.wait_ge(s.f_ready, 1)
                dve.wait_ge(s.entries_ready, 1)
                for i in range(2):
                    dve.tensor_tensor_scan(decay[:, 4 * i:4 * i + 4, :].rearrange("s h t -> s (h t)"), st.ps[0:S, 4 + i, 0:4 * S],
                                           entries[:, 4 * i:4 * i + 4, :].rearrange("s h t -> s (h t)"), 0.0, ALU.mult, ALU.add).then_inc(s.decay_ready, 1)
                dve.wait_ge(s.decay_ready, 2)
                dve.wait_ge(s.scores_ready, 1)
                for j in range(2):
                    last = dve.tensor_tensor(weighed[:, 4 * j:4 * j + 4, :], st.ps[0:S, 0:4, j * S:(j + 1) * S], decay[:, 4 * j:4 * j + 4, :], ALU.mult)
                last.then_inc(s.weighed_ready, 1)
                dve.wait_ge(s.heads_done, 1)
                dve.tensor_tensor(o_sb[:].rearrange("q (h d) -> q h d", d=HD), st.ps[0:S, 6, 0:D].rearrange("q (h d) -> q h d", d=HD),
                                  gates[:, H:2 * H].unsqueeze(2).to_broadcast([S, H, HD]), ALU.mult).then_inc(s.o_ready, 1)
                norm_vector(dve, st, s, st.ps[0:S, 0, 0:D], x_b, st.w["a6bo"][0:S, :])


def l2_xattn(nc, st, dram):
    H, C, TAPS, NT, EPS = 16, 512, 9, 3, 1e-5
    CT, W2 = C // P, H * TAPS
    w_hist = st.w["a7hw"].rearrange("p (k n) -> p k n", k=KT)
    w_c1 = st.w["a7cw1"].rearrange("p (k n) -> p k n", k=CT)
    w_k1 = st.w["a7kw1"].rearrange("p (k n) -> p k n", k=CT)
    w_k2 = st.w["a7kw2"].rearrange("p (k n) -> p k n", k=KT)
    rows = [min(KROWS, KEYS - t * KROWS) for t in range(NT)]
    with ExitStack() as ctx:
        sb = lambda n, shape, dt=F32: ctx.enter_context(nc.sbuf_tensor(f"l2x_{n}", shape, dt))
        kern = sb("kern", [P, B, W2])
        keep, mask_add = sb("keep", [S, 3, S]), sb("mask_add", [S, S])
        with ExitStack() as ctx2:
            sb2 = lambda n, shape: ctx2.enter_context(nc.sbuf_tensor(f"l2x_{n}", shape, F32))
            ctx_cur, ccT = sb2("hist_cur", [P, KT, KEYS]), sb2("ccT", [P, CT, B])
            eh, ehT, g1T = sb2("eh", [KROWS, NT, C]), sb2("ehT", [P, CT, KEYS]), sb2("g1T", [P, KEYS])
            hstats, hmv = sb2("hstats", [KROWS, NT, 6]), sb2("hmv", [KROWS, NT, 2])
            hvar, hrstd = sb2("hvar", [KROWS, NT]), sb2("hrstd", [KROWS, NT])
            aw, awmax, awsum, awinv = sb2("aw", [1, KEYS]), sb2("awmax", [1, 1]), sb2("awsum", [1, 1]), sb2("awinv", [1, 1])
            pcol = sb2("pcol", [KROWS, NT])
            hist_rows = sb2("hist_rows", [P, 3 * C])
            hb, hg, hs = (hist_rows[:, i * C:(i + 1) * C] for i in range(3))
            with stage_sems(nc, ["buffers_set", "hist_rows_loaded"]) as s, nc.Block() as block:
                @block.sync
                def _(sp):
                    sp.dma_start(hist_rows[:], dram["hist_rows"]).then_inc(s.hist_rows_loaded, 16)
                    sp.wait_ge(s.hist_rows_loaded, 16)

                @block.gpsimd
                def _(pool):
                    pool.memset(eh[:], 0.0).then_inc(s.buffers_set, 1)
                    pool.memset(hmv[:], 1.0).then_inc(s.buffers_set, 1)

            sems = ["cur_ready", "eh_ready", "eh_biased", "stats_done", "mv_done", "var_done", "hrstd_done", "eh_step", "eh_normed", "eh_done",
                    "eh_turned", "ehT_act", "ehT_dve", "g1_ready", "g1_done", "aw_ready", "aw_step", "aw_exp", "p_row", "p_turned", "p_col", "cc_ready", "cc_done"]
            with nc.Fori(0, B) as b, stage_sems(nc, sems) as s, nc.Block() as block:
                @block.gpsimd
                def _(pool):
                    pool.tensor_copy(ctx_cur[:], st.ctxT[:, b, :, :]).then_inc(s.cur_ready, 1)
                    pool.wait_ge(s.mv_done, NT)
                    pool.tensor_scalar(hvar[:], hmv[:, :, 1], EPS, None, ALU.add).then_inc(s.var_done, 1)
                    pool.wait_ge(s.var_done, 1)
                    pool.tensor_tensor(hrstd[:], hvar[:], st.minus_half[0:KROWS, 0:1].to_broadcast([KROWS, NT]), ALU.pow).then_inc(s.hrstd_done, 1)

                @block.tensor
                def _(pe):
                    pe.wait_ge(s.cur_ready, 1)
                    for t in range(NT):
                        for k in range(KT):
                            last = pe.matmul(st.ps[0:rows[t], t, 0:C], ctx_cur[:, k, t * KROWS:t * KROWS + rows[t]], w_hist[:, k, :],
                                             start=(k == 0), stop=(k == KT - 1))
                        last.then_inc(s.eh_ready, 1)
                    for t in range(NT):
                        pe.wait_ge(s.eh_done, t + 1)
                        for c in range(CT):
                            last = pe.transpose(st.ps[:, 4 + c, t * KROWS:t * KROWS + rows[t]], eh[0:rows[t], t, c * P:(c + 1) * P],
                                                st.ident[0:rows[t], 0:rows[t]])
                    last.then_inc(s.eh_turned, 1)
                    for c in range(CT):
                        pe.wait_ge(s.ehT_act if c % 2 == 0 else s.ehT_dve, c // 2 + 1)
                        last = pe.matmul(st.ps[:, 3, 0:KEYS], w_c1[:, c, :], ehT[:, c, :], start=(c == 0), stop=(c == CT - 1))
                    last.then_inc(s.g1_ready, 1)
                    pe.wait_ge(s.g1_done, 1)
                    pe.matmul(st.ps[0:1, 0, 0:KEYS], st.w["a7cw2"], g1T[:], start=True, stop=True).then_inc(s.aw_ready, 1)
                    pe.wait_ge(s.p_row, 1)
                    for t in range(NT):
                        last = pe.matmul(st.ps[0:rows[t], 1, t:t + 1], aw[0:1, t * KROWS:t * KROWS + rows[t]], st.ident[0:1, 0:1], start=True, stop=True)
                    last.then_inc(s.p_turned, 1)
                    pe.wait_ge(s.p_col, NT)
                    for c in range(CT):
                        for t in range(NT):
                            last = pe.matmul(st.ps[:, 2, c:c + 1], eh[0:rows[t], t, c * P:(c + 1) * P], pcol[0:rows[t], t:t + 1],
                                             start=(t == 0), stop=(t == NT - 1))
                    last.then_inc(s.cc_ready, 1)

                @block.scalar
                def _(act):
                    for t in range(NT):
                        act.wait_ge(s.eh_normed, t + 1)
                        act.activation(eh[0:rows[t], t, :], eh[0:rows[t], t, :], ACT.Gelu).then_inc(s.eh_done, 1)
                    act.wait_ge(s.eh_turned, 1)
                    for c in (0, 2):
                        act.activation(ehT[:, c, :], st.ps[:, 4 + c, 0:KEYS], ACT.Copy).then_inc(s.ehT_act, 1)
                    act.wait_ge(s.g1_ready, 1)
                    act.activation(g1T[:], st.ps[:, 3, 0:KEYS], ACT.Gelu, bias=st.w["a7cb1"]).then_inc(s.g1_done, 1)
                    act.wait_ge(s.aw_step, 2)
                    act.activation(aw[:], aw[:], ACT.Exp, bias=awmax[:, 0:1], accum_out=awsum[:, 0:1]).then_inc(s.aw_exp, 1)
                    act.wait_ge(s.cc_ready, 1)
                    act.activation(ccT[:, :, b], st.ps[:, 2, 0:CT], ACT.Copy).then_inc(s.cc_done, 1)

                @block.vector
                def _(dve):
                    for t in range(NT):
                        e = eh[0:rows[t], t, :]
                        dve.wait_ge(s.eh_ready, t + 1)
                        dve.tensor_tensor(e, st.ps[0:rows[t], t, 0:C], hb[0:rows[t], :], ALU.add).then_inc(s.eh_biased, 1)
                        dve.wait_ge(s.eh_biased, t + 1)
                        dve.bn_stats(hstats[0:rows[t], t, :], e).then_inc(s.stats_done, 1)
                        dve.wait_ge(s.stats_done, t + 1)
                        dve.bn_aggr(hmv[0:rows[t], t, :], hstats[0:rows[t], t, :]).then_inc(s.mv_done, 1)
                    dve.wait_ge(s.mv_done, NT)
                    for t in range(NT):
                        e = eh[0:rows[t], t, :]
                        dve.scalar_tensor_tensor(e, e, hmv[0:rows[t], t, 0:1], hg[0:rows[t], :], ALU.subtract, ALU.mult).then_inc(s.eh_step, 1)
                    dve.wait_ge(s.hrstd_done, 1)
                    for t in range(NT):
                        e = eh[0:rows[t], t, :]
                        dve.wait_ge(s.eh_step, t + 1)
                        dve.scalar_tensor_tensor(e, e, hrstd[0:rows[t], t:t + 1], hs[0:rows[t], :], ALU.mult, ALU.add).then_inc(s.eh_normed, 1)
                    dve.wait_ge(s.eh_turned, 1)
                    for c in (1, 3):
                        dve.tensor_copy(ehT[:, c, :], st.ps[:, 4 + c, 0:KEYS]).then_inc(s.ehT_dve, 1)
                    dve.wait_ge(s.aw_ready, 1)
                    dve.tensor_scalar(aw[:], st.ps[0:1, 0, 0:KEYS], st.w["a7cb2"][0:1, 0:1], None, ALU.add).then_inc(s.aw_step, 1)
                    dve.wait_ge(s.aw_step, 1)
                    dve.tensor_reduce(awmax[:], aw[:], AX.X, ALU.max, negate=True).then_inc(s.aw_step, 1)
                    dve.wait_ge(s.aw_exp, 1)
                    dve.reciprocal(awinv[:], awsum[:]).then_inc(s.aw_step, 1)
                    dve.wait_ge(s.aw_step, 3)
                    dve.tensor_scalar(aw[:], aw[:], awinv[:, 0:1], None, ALU.mult).then_inc(s.p_row, 1)
                    dve.wait_ge(s.p_turned, 1)
                    for t in range(NT):
                        dve.tensor_copy(pcol[0:rows[t], t:t + 1], st.ps[0:rows[t], 1, t:t + 1]).then_inc(s.p_col, 1)

            kp, kpT, kern8 = sb2("kp", [B, D]), sb2("kpT", [P, KT, B]), sb2("kern8", [B, H, TAPS])
            kstats, kmv, kvar, krstd = sb2("kstats", [B, 6]), sb2("kmv", [B, 2]), sb2("kvar", [B, 1]), sb2("krstd", [B, 1])
            kmax, ksum = sb2("kmax", [B, H]), sb2("ksum", [B, H])
            net_rows = sb2("net_rows", [B, 3 * D + W2])
            kb1, kg, ks = (net_rows[:, i * D:(i + 1) * D] for i in range(3))
            kb2 = net_rows[:, 3 * D:3 * D + W2]
            m_u8 = ctx2.enter_context(nc.sbuf_tensor("l2x_m_u8", [S, 3, S], U8))
            sems = ["k1_ready", "kp_step", "kvar_done", "krstd_done", "kp_normed", "kp_done", "kp_turned", "kpT_done", "k2_ready", "kern_step",
                    "kern_exp", "kern8_done", "spread_ready", "spread_act", "masks_zero", "masks_loaded", "rows_loaded", "keep_done"]
            with stage_sems(nc, sems) as s, nc.Block() as block:
                @block.sync
                def _(sp):
                    sp.dma_start(net_rows[:], dram["kernel_net_rows"]).then_inc(s.rows_loaded, 16)
                    sp.wait_ge(s.masks_zero, 1)
                    mask = dram["self_mask"]
                    sp.dma_start(m_u8[1:S, 0, :], mask[0:S - 1, :]).then_inc(s.masks_loaded, 16)
                    sp.dma_start(m_u8[:, 1, :], mask).then_inc(s.masks_loaded, 16)
                    sp.dma_start(m_u8[0:S - 1, 2, :], mask[1:S, :]).then_inc(s.masks_loaded, 16)

                @block.gpsimd
                def _(pool):
                    pool.memset(m_u8[:], 0).then_inc(s.masks_zero, 1)
                    pool.wait_ge(s.kp_step, 3)
                    pool.tensor_scalar(kvar[:], kmv[:, 1:2], EPS, None, ALU.add).then_inc(s.kvar_done, 1)
                    pool.wait_ge(s.kvar_done, 1)
                    pool.tensor_tensor(krstd[:], kvar[:], st.minus_half[0:B, :], ALU.pow).then_inc(s.krstd_done, 1)

                @block.tensor
                def _(pe):
                    for c in range(CT):
                        last = pe.matmul(st.ps[0:B, 0, 0:D], ccT[:, c, :], w_k1[:, c, :], start=(c == 0), stop=(c == CT - 1))
                    last.then_inc(s.k1_ready, 1)
                    pe.wait_ge(s.kp_done, 1)
                    for k in range(KT):
                        last = pe.transpose(st.ps[:, 1, k * B:(k + 1) * B], kp[:, k * P:(k + 1) * P], st.ident[0:B, 0:B])
                    last.then_inc(s.kp_turned, 1)
                    pe.wait_ge(s.kpT_done, 1)
                    for k in range(KT):
                        last = pe.matmul(st.ps[0:B, 2, 0:W2], kpT[:, k, :], w_k2[:, k, :], start=(k == 0), stop=(k == KT - 1))
                    last.then_inc(s.k2_ready, 1)
                    pe.wait_ge(s.kern8_done, 1)
                    for b in range(B):
                        last = pe.matmul(st.ps[:, 3 + b // 2, (b % 2) * W2:(b % 2 + 1) * W2], st.ident[0:B, b:b + 1].to_broadcast([B, P]),
                                         kern8[:].rearrange("b h t -> b (h t)"), start=True, stop=True)
                    last.then_inc(s.spread_ready, 1)

                @block.scalar
                def _(act):
                    act.wait_ge(s.kp_normed, 1)
                    act.activation(kp[:], kp[:], ACT.Gelu).then_inc(s.kp_done, 1)
                    act.wait_ge(s.kp_turned, 1)
                    act.activation(kpT[:], st.ps[:, 1, 0:KT * B].rearrange("p (k b) -> p k b", k=KT), ACT.Copy).then_inc(s.kpT_done, 1)
                    act.wait_ge(s.kern_step, 3)
                    act.activation(kern8[:], kern8[:], ACT.Exp).then_inc(s.kern_exp, 1)
                    act.wait_ge(s.spread_ready, 1)
                    act.activation(kern[:].rearrange("p (n b) w -> p n (b w)", b=2), st.ps[:, 3:7, 0:2 * W2], ACT.Copy).then_inc(s.spread_act, 1)

                @block.vector
                def _(dve):
                    dve.wait_ge(s.rows_loaded, 16)
                    dve.wait_ge(s.k1_ready, 1)
                    dve.tensor_tensor(kp[:], st.ps[0:B, 0, 0:D], kb1, ALU.add).then_inc(s.kp_step, 1)
                    dve.wait_ge(s.kp_step, 1)
                    dve.bn_stats(kstats[:], kp[:]).then_inc(s.kp_step, 1)
                    dve.wait_ge(s.kp_step, 2)
                    dve.bn_aggr(kmv[:], kstats[:]).then_inc(s.kp_step, 1)
                    dve.wait_ge(s.kp_step, 3)
                    dve.scalar_tensor_tensor(kp[:], kp[:], kmv[:, 0:1], kg, ALU.subtract, ALU.mult).then_inc(s.kp_step, 1)
                    dve.wait_ge(s.kp_step, 4)
                    dve.wait_ge(s.krstd_done, 1)
                    dve.scalar_tensor_tensor(kp[:], kp[:], krstd[:, 0:1], ks, ALU.mult, ALU.add).then_inc(s.kp_normed, 1)
                    dve.wait_ge(s.k2_ready, 1)
                    dve.tensor_tensor(kern8[:].rearrange("b h t -> b (h t)"), st.ps[0:B, 2, 0:W2], kb2, ALU.add).then_inc(s.kern_step, 1)
                    dve.wait_ge(s.kern_step, 1)
                    dve.tensor_reduce(kmax[:], kern8[:], AX.X, ALU.max).then_inc(s.kern_step, 1)
                    dve.wait_ge(s.kern_step, 2)
                    dve.tensor_tensor(kern8[:], kern8[:], kmax[:].unsqueeze(2).to_broadcast([B, H, TAPS]), ALU.subtract).then_inc(s.kern_step, 1)
                    dve.wait_ge(s.kern_exp, 1)
                    dve.tensor_reduce(ksum[:], kern8[:], AX.X, ALU.add).then_inc(s.kern_step, 1)
                    dve.wait_ge(s.kern_step, 4)
                    dve.reciprocal(kmax[:], ksum[:]).then_inc(s.kern_step, 1)
                    dve.wait_ge(s.kern_step, 5)
                    dve.tensor_tensor(kern8[:], kern8[:], kmax[:].unsqueeze(2).to_broadcast([B, H, TAPS]), ALU.mult).then_inc(s.kern8_done, 1)
                    dve.wait_ge(s.masks_loaded, 48)
                    dve.tensor_scalar(keep[:], m_u8[:], 0, None, ALU.is_equal).then_inc(s.keep_done, 1)
                    dve.wait_ge(s.keep_done, 1)
                    dve.tensor_scalar(mask_add[:], keep[:, 1, :], 1.0, -MASKED, ALU.subtract, ALU.mult).then_inc(s.keep_done, 1)

        conv = Convolution(kern=kern, keep=keep, mask=mask_add[:])
        attention(nc, st, "l2x_a", H, 16, False, weights(st, "a7"), bias={"o": st.w["a7bo"]}, conv=conv)
def k_major(w):
    n_in, n_out = w.shape
    return w.reshape(n_in // P, P, n_out).transpose(1, 0, 2).reshape(P, -1)


def per_partition(v):
    return v.reshape(-1, P).T


def on_all(v):
    return np.broadcast_to(v.reshape(1, -1), (P, v.size))


def spread_heads(w):
    heads = w.reshape(w.shape[0], 2, 4, 2, 16)
    out = np.zeros((w.shape[0], 2, 2, 4, 2, 16), w.dtype)
    for parity in range(2):
        out[:, parity, :, :, parity] = heads[:, :, :, parity]
    return out.reshape(w.shape[0], 512)


def tables():
    out = {}
    out["ident"] = np.eye(P, dtype=np.float32)
    causal = np.triu(np.ones((S, S), bool), 1)
    out["causal"] = np.concatenate([np.where(causal, MASKED, 0.0), np.zeros((P - S, S))]).astype(np.float32)
    return out


def rope_of_16():
    inv = 1.0 / (10000.0 ** (np.arange(0, 16, 2, dtype=np.float32) / np.float32(16)))
    freq = np.outer(np.arange(KEYS, dtype=np.float32), inv.astype(np.float32)).astype(np.float32)
    angle = np.concatenate([freq, freq], 1)[:, np.arange(P) % 16].T
    sign = np.where(np.arange(P) % 16 < 8, -1.0, 1.0).astype(np.float32)[:, None]
    other = np.arange(P) // 16 * 16 + (np.arange(P) % 16 + 8) % 16
    return np.cos(angle).astype(np.float32), (np.sin(angle) * sign).astype(np.float32), np.eye(P, dtype=np.float32)[other]


def rope_of_32():
    half = np.arange(P) % 16
    inv = (np.float32(1.0) / np.power(np.float32(10000.0), np.arange(16, dtype=np.float32) / np.float32(16))).astype(np.float32)
    angle = (np.arange(S, dtype=np.float32)[None, :] * inv[half][:, None]).astype(np.float32)
    sign = np.where(np.arange(P) % 32 < 16, -1.0, 1.0).astype(np.float32)[:, None]
    other = np.arange(P) // 32 * 32 + (np.arange(P) % 32 + 16) % 32
    return np.cos(angle), np.sin(angle) * sign, np.eye(P, dtype=np.float32)[other]


def position_table():
    pos = np.arange(-(S - 1), S, dtype=np.float32)
    inv = (1.0 / np.power(np.float32(10000.0), np.arange(0, D, 2, dtype=np.float32) / np.float32(D))).astype(np.float32)
    ang = (pos[:, None] * inv[None, :]).astype(np.float32)
    return np.stack([np.sin(ang).T, np.cos(ang).T], 1).astype(np.float32).reshape(P, -1)


def rows_on_partitions(*parts):
    rows = np.concatenate(parts)
    return np.concatenate([rows, np.zeros((P - len(rows), rows.shape[1]), rows.dtype)])


def tile_rows(w):
    return np.concatenate([w[..., :P, :], w[..., P:, :]], -1)


def expert_units(a):
    keys, values = a["L1_ffn_keys"], a["L1_ffn_values"]
    first = tile_rows(np.concatenate([keys[0::2], keys[1::2]], -1))
    second = np.concatenate([values[0::2], values[1::2]], -1)
    l1 = np.concatenate([first, second], -1)

    f = 256
    sw, sb, sm = a["L2_ffn_s_fc1_w"], a["L2_ffn_s_fc1_b"], a["L2_ffn_s_geglu_mult"]
    parts = [np.concatenate([sw[c:c + f], sw[2 * f + c:2 * f + c + f]]) for c in (0, f)]
    w1 = np.concatenate([a["L2_ffn_fc1_w"], np.stack(parts)]).transpose(0, 2, 1)
    b1 = np.concatenate([a["L2_ffn_fc1_b"], np.stack([np.concatenate([sb[c:c + f], sb[2 * f + c:2 * f + c + f]]) for c in (0, f)])])
    mult = np.concatenate([a["L2_ffn_geglu_mult"], np.stack([sm[:f], sm[f:]])])
    w2 = np.concatenate([a["L2_ffn_fc2_w"], np.stack([a["L2_ffn_s_fc2_w"][:, :f], a["L2_ffn_s_fc2_w"][:, f:]])]).transpose(0, 2, 1)
    cols = lambda v: v.reshape(len(v), -1, P).transpose(0, 2, 1)
    l2 = np.concatenate([tile_rows(w1), tile_rows(w2), cols(b1), cols(mult)], -1)

    w1 = np.concatenate([a["L3_ffn_W1_s"], a["L3_ffn_W1_r"]])
    b1 = np.concatenate([a["L3_ffn_b1_s"], a["L3_ffn_b1_r"]])
    w2 = np.concatenate([a["L3_ffn_W2_s"], a["L3_ffn_W2_r"]])
    w1 = w1.reshape(10, D, 4, 256).transpose(0, 2, 1, 3).reshape(40, D, 256)
    l3 = np.concatenate([tile_rows(w1), tile_rows(w2.reshape(40, 256, D)), cols(b1.reshape(40, 256))], -1)
    return {"l1_ffn_units": l1, "l2_ffn_units": l2, "l3_ffn_units": l3}


def pack_plan():
    T = lambda n: (lambda a: k_major(a[n].T))
    N = lambda n: (lambda a: k_major(a[n]))
    col = lambda n: (lambda a: per_partition(a[n]))
    row = lambda n: (lambda a: on_all(a[n]))
    plan = [[] for _ in range(12)]
    plan[0] = [("a0q", 1024, lambda a: k_major(spread_heads(a["L0_attn_Wq"].T))), ("a0k", 512, T("L0_attn_Wk")),
               ("a0v", 512, T("L0_attn_Wv")), ("a0o", 512, T("L0_attn_Wo"))]
    plan[1] = [("a1q", 1024, lambda a: k_major(spread_heads(a["L0_xattn_Wq"].T))), ("a1k", 512, T("L0_xattn_Wk")),
               ("a1v", 512, T("L0_xattn_Wv")), ("a1o", 512, T("L0_xattn_Wp")),
               ("a1bq", 4, lambda a: per_partition(spread_heads(a["L0_xattn_bq"].reshape(1, -1)))),
               ("a1bk", 2, col("L0_xattn_bk")), ("a1bv", 256, row("L0_xattn_bv")), ("a1bo", 256, row("L0_xattn_bp"))]
    plan[2] = [("f2w", 512, N("L0_ffn_weight")), ("f2g", 256, row("L0_ffn_ln_gamma")), ("f2b", 256, row("L0_ffn_ln_beta"))]
    plan[3] = [("m_in", 2048, T("L1_attn_w_in")), ("m_conv", 16, lambda a: a["L1_attn_w_conv"].reshape(4, P, 4).transpose(1, 0, 2).reshape(P, 16)),
               ("m_xproj", 384, T("L1_attn_w_xproj")),
               ("m_dt", 512, lambda a: np.concatenate([a["L1_attn_w_dt"].T, np.zeros((64, 512), np.float32)])),
               ("m_bdt", 4, col("L1_attn_b_dt")),
               ("m_alog", 64, lambda a: a["L1_attn_A_log"].reshape(4, P, 16).transpose(1, 0, 2).reshape(P, 64)),
               ("m_d", 4, col("L1_attn_D")), ("m_out", 1024, T("L1_attn_w_out"))]
    plan[4] = [("a4q", 2048, N("L1_xattn_Wq")), ("a4k", 2048, N("L1_xattn_Wk")), ("a4v", 2048, N("L1_xattn_Wv")),
               ("a4o", 2048, N("L1_xattn_Wo")), ("a4bq", 8, col("L1_xattn_bq")), ("a4bk", 8, col("L1_xattn_bk")),
               ("a4bv", 1024, row("L1_xattn_bv")), ("a4bo", 256, row("L1_xattn_bo"))]
    plan[5] = [("f5q", 1024, lambda a: k_major(spread_heads(a["L1_ffn_wq"]))), ("f5k", 512, N("L1_ffn_wk")), ("f5v", 512, N("L1_ffn_wv")),
               ("f5o", 512, N("L1_ffn_wo")), ("f5p", 512, N("L1_ffn_wp")), ("f5pe", 2 * (2 * S - 1), lambda a: position_table()),
               ("f5g1", 256, row("L1_ffn_ln1_g")), ("f5s1", 256, row("L1_ffn_ln1_b")), ("f5g2", 256, row("L1_ffn_ln2_g")),
               ("f5s2", 256, row("L1_ffn_ln2_b")), ("f5sel", 64, N("L1_ffn_sel_w"))]
    plan[6] = [("a6q", 512, T("L2_attn_Wq")), ("a6k", 512, T("L2_attn_Wk")), ("a6v", 512, T("L2_attn_Wv")), ("a6o", 512, T("L2_attn_Wout")),
               ("a6beta", 16, T("L2_attn_Wbeta")), ("a6gates", 32, lambda a: k_major(np.concatenate([a["L2_attn_Wig"], a["L2_attn_Wog"]]).T)),
               ("a6bgates", 16, lambda a: on_all(np.concatenate([a["L2_attn_big"], a["L2_attn_bog"]]))),
               ("a6bbeta", 1, lambda a: rows_on_partitions(a["L2_attn_bbeta"][:, None])), ("a6norm", 256, row("L2_attn_norm_w")),
               ("a6bo", 256, row("L2_attn_bout")), ("a6cos", S, lambda a: rope_of_32()[0]), ("a6sin", S, lambda a: rope_of_32()[1]),
               ("a6swap", P, lambda a: rope_of_32()[2])]
    plan[7] = [("a7q", 1024, lambda a: k_major(spread_heads(a["L2_xattn_Wq"]))), ("a7k", 512, N("L2_xattn_Wk")), ("a7v", 512, N("L2_xattn_Wv")),
               ("a7o", 512, N("L2_xattn_proj_W")), ("a7bo", 256, row("L2_xattn_proj_b")), ("a7hw", 1024, N("L2_xattn_hist_W")),
               ("a7cw1", 512, N("L2_xattn_ctx_W1")), ("a7cb1", 1, col("L2_xattn_ctx_b1")), ("a7cw2", 1, N("L2_xattn_ctx_W2")),
               ("a7cb2", 1, row("L2_xattn_ctx_b2")), ("a7kw1", 1024, N("L2_xattn_kg_W1")), ("a7kw2", 288, N("L2_xattn_kg_W2"))]
    plan[8] = [("f8gate", 30, T("L2_ffn_gate_w")),
               ("f8b2", 256, lambda a: rows_on_partitions(a["L2_ffn_fc2_b"], a["L2_ffn_s_fc2_b"][None]))]
    plan[11] = [("f11gate", 16, N("L3_ffn_centroids")), ("f11gs", 2, col("L3_ffn_g_shared")), ("f11gr", 2, col("L3_ffn_g_routed")),
                ("f11b2", 256, lambda a: rows_on_partitions(a["L3_ffn_b2_s"], a["L3_ffn_b2_r"]))]
    plan[9] = [("a9q", 512, N("L3_attn_wqk")), ("a9o", 512, N("L3_attn_wov"))]
    plan[10] = [("a10q", 1024, lambda a: k_major(spread_heads(a["L3_xattn_W_q"].T))), ("a10k", 512, T("L3_xattn_W_k")),
                ("a10v", 512, T("L3_xattn_W_v")), ("a10o", 512, T("L3_xattn_W_o")),
                ("a10cos", KEYS, lambda a: rope_of_16()[0]), ("a10sin", KEYS, lambda a: rope_of_16()[1]), ("a10swap", P, lambda a: rope_of_16()[2])]
    return plan


TABLES = [("ident", P), ("causal", S)]


def lay_out(a):
    out = {
        "x_tokens": a["x"].transpose(1, 0, 2),
        "x_features": a["x"].reshape(B, S, KT, P).transpose(3, 2, 0, 1),
        "ctx_features": a["ctx_1024"].reshape(B, KEYS, KT, P).transpose(3, 0, 2, 1),
        "key_mask": a["mask_Bx1xSxS2_ik0"].reshape(B, S, KEYS),
        "self_mask": a["mask_SxS_bc0"],
    }
    out["kernel_net_rows"] = on_all(np.concatenate([a["L2_xattn_kg_b1"], a["L2_xattn_kg_ln_g"], a["L2_xattn_kg_ln_b"], a["L2_xattn_kg_b2"]]))[0:B]
    out["hist_rows"] = on_all(np.concatenate([a["L2_xattn_hist_b"], a["L2_xattn_hist_ln_g"], a["L2_xattn_hist_ln_b"]]))
    out.update(expert_units(a))
    made = tables()
    out["tables"] = np.concatenate([made[n] for n, _ in TABLES], 1)
    for i, parts in enumerate(pack_plan()):
        if parts:
            made = [np.broadcast_to(f(a), (P, n)) for _, n, f in parts]
            out[f"pack{i}"] = np.concatenate(made, 1)
    return {k: np.ascontiguousarray(v) for k, v in out.items()}


def program(nc, dram, out, stages):
    plan = pack_plan()
    st = State()
    with ExitStack() as ctx:
        def sb(n, shape, dt=F32):
            return ctx.enter_context(nc.sbuf_tensor(n, shape, dt))

        st.X = sb("X", [S, B, D])
        st.XT = sb("XT", [P, KT, B, S])
        st.ctxT = sb("ctxT", [P, B, KT, KEYS])
        st.ps = ctx.enter_context(nc.psum_tensor("ps", [P, 8, BANK], F32))
        st.resid, st.xnew = sb("resid", [S, D]), sb("xnew", [S, D])
        st.stats, st.meanvar = sb("stats", [S, 6]), sb("meanvar", [S, 2])
        st.vareps, st.rstd = sb("vareps", [S, 1]), sb("rstd", [S, 1])
        st.minus_half = sb("minus_half", [P, 1])
        st.tables = sb("tables_sb", [P, sum(n for _, n in TABLES)])
        ends = np.cumsum([n for _, n in TABLES])
        st.ident, st.causal = (st.tables[:, int(end) - n:int(end)] for (_, n), end in zip(TABLES, ends))
        st.w = {}
        size = [max([sum(n for _, n, _ in plan[i]) for i in stages if i % 2 == r] + [1]) for r in range(2)]
        region = [sb(f"weights{r}", [P, size[r]]) for r in range(2)]
        packs = {}
        for i in stages:
            at = 0
            for n, c, _ in plan[i]:
                st.w[n] = region[i % 2][:, at:at + c]
                at += c
            packs[i] = region[i % 2][:, 0:at]
        start_loaded = ctx.enter_context(nc.semaphore("start_loaded"))
        half_set = ctx.enter_context(nc.semaphore("half_set"))
        pack_loaded = {i: ctx.enter_context(nc.semaphore(f"pack{i}_loaded")) for i in packs}
        x_out = ctx.enter_context(nc.semaphore("x_out"))

        with nc.Block() as block:
            @block.sync
            def _(sp):
                sp.dma_start(st.X[:], dram["x_tokens"]).then_inc(start_loaded, 16)
                sp.dma_start(st.XT[:], dram["x_features"]).then_inc(start_loaded, 16)
                sp.dma_start(st.tables[:], dram["tables"]).then_inc(start_loaded, 16)
                sp.dma_start(packs[stages[0]], dram[f"pack{stages[0]}"]).then_inc(pack_loaded[stages[0]], 16)
                sp.dma_start(st.ctxT[:], dram["ctx_features"]).then_inc(start_loaded, 16)
                sp.wait_ge(start_loaded, 64)

            @block.gpsimd
            def _(pool):
                pool.memset(st.minus_half[:], -0.5).then_inc(half_set, 1)

        for n, i in enumerate(stages):
            with nc.Block() as block:
                @block.sync
                def _(sp, n=n, i=i):
                    if n + 1 < len(stages):
                        nxt = stages[n + 1]
                        sp.dma_start(packs[nxt], dram[f"pack{nxt}"]).then_inc(pack_loaded[nxt], 16)
                    sp.wait_ge(pack_loaded[i], 16)
            STAGES[i](nc, st, dram)

        with nc.Block() as block:
            @block.sync
            def _(sp):
                sp.dma_start(out.rearrange("b t d -> t b d"), st.X[:]).then_inc(x_out, 16)
                sp.wait_ge(x_out, 16)


def weights(st, prefix):
    view = lambda n: st.w[prefix + n].rearrange("p (k n) -> p k n", k=KT) if prefix + n in st.w else None
    return Attention(q=view("q"), k=view("k"), v=view("v"), o=st.w[prefix + "o"].rearrange("p (m n) -> p m n", n=D))


def l0_attn(nc, st, dram):
    attention(nc, st, "l0a", 16, 16, False, weights(st, "a0"), mask=st.causal[0:S, :])


def l0_xattn(nc, st, dram):
    bias = scaled_query_bias(nc, st, "a1", 0.25)
    attention(nc, st, "l0x", 16, 16, True, weights(st, "a1"), bias=bias, plus_one=True)


def l1_xattn(nc, st, dram):
    bias = scaled_query_bias(nc, st, "a4", 0.125)
    attention(nc, st, "l1x", 16, 64, True, weights(st, "a4"), bias=bias)


def l3_xattn(nc, st, dram):
    rope = Rotation(swap=st.w["a10swap"], cos=st.w["a10cos"], sin=st.w["a10sin"])
    attention(nc, st, "l3x", 16, 16, True, weights(st, "a10"), mask_dram=dram["key_mask"], rope=rope)


def scaled_query_bias(nc, st, prefix, scale):
    bq = st.w[prefix + "bq"]
    with stage_sems(nc, ["bias_scaled"]) as s, nc.Block() as block:
        @block.vector
        def _(dve):
            dve.tensor_scalar(bq, bq, scale, None, ALU.mult).then_inc(s.bias_scaled, 1)
    return {"q": bq, "k": st.w[prefix + "bk"], "v": st.w[prefix + "bv"], "o": st.w[prefix + "bo"]}


def l3_attn(nc, st, dram):
    attention(nc, st, "l3a", 1, 256, False, weights(st, "a9"), mask=st.causal[0:S, :])


STAGES = {0: l0_attn, 1: l0_xattn, 2: l0_ffn, 3: l1_attn, 4: l1_xattn, 5: l1_ffn, 6: l2_attn, 7: l2_xattn, 8: l2_ffn, 9: l3_attn, 10: l3_xattn, 11: l3_ffn}


def build(nc, arrays, stages=range(12)):
    dram = {n: nc.dram_tensor(n, v.shape, mybir.dt.from_np(v.dtype), kind="ExternalInput").ap() for n, v in arrays.items()}
    out = nc.dram_tensor("out_0_dram", (B, S, D), F32, kind="ExternalOutput").ap()
    program(nc, dram, out, list(stages))


def kernel(**inputs):
    import concourse.bacc as bacc
    from concourse.bass_utils import run_bass_kernel_spmd

    arrays = lay_out({k: np.asarray(v) for k, v in inputs.items()})
    nc = bacc.Bacc("TRN2", target_bir_lowering=False, num_devices=1)
    build(nc, arrays)
    return run_bass_kernel_spmd(nc, [arrays], core_ids=[0]).results[0]["out_0_dram"]
```

```python
from collections import namedtuple
from contextlib import ExitStack, contextmanager

import numpy as np

import concourse.bass as bass
import concourse.mybir as mybir

F32 = mybir.dt.float32
I32 = mybir.dt.int32
U8 = mybir.dt.uint8
ALU = mybir.AluOpType
ACT = mybir.ActivationFunctionType
AX = mybir.AxisListType

B, S, D = 8, 100, 256
KEYS = 361
P = 128
KT = D // P
TOK = B * S
KROWS = 121
BANK = 512
MASKED = -1.0e30
TURN_LAG = 2
TURN = 4


class State:
    pass


Attention = namedtuple("Attention", "q k v o")
Rotation = namedtuple("Rotation", "cos sin q k")
InnerNorm = namedtuple("InnerNorm", "gain shift turned")
Convolution = namedtuple("Convolution", "kern shift keep mask")


@contextmanager
def stage_sems(nc, names):
    with ExitStack() as ctx:
        handles = {n: ctx.enter_context(nc.semaphore(n)) for n in names}
        yield namedtuple("Semaphores", handles)(**handles)
        for h in handles.values():
            nc.gpsimd.sem_clear(h)
        nc.all_engine_barrier()


NORM_SEMS = ["y_ready", "resid_ready", "stats_ready", "meanvar_ready", "vareps_ready", "rstd_ready",
             "xnew_ready", "xnew_turned", "x_stored", "affine_step"]


def norm_sum_vector(dve, st, s, y, x_b, bias, j=0):
    steps = 1 if bias is None else 2
    dve.wait_ge(s.y_ready, j + 1)
    dve.tensor_tensor(st.resid[:, j, :], y, x_b, ALU.add).then_inc(s.resid_ready, 1)
    if bias is not None:
        dve.wait_ge(s.resid_ready, j * steps + 1)
        dve.tensor_tensor(st.resid[:, j, :], st.resid[:, j, :], bias, ALU.add).then_inc(s.resid_ready, 1)
    dve.wait_ge(s.resid_ready, (j + 1) * steps)
    norm_stats_vector(dve, st, s, j)


def norm_stats_vector(dve, st, s, j=0):
    dve.bn_stats(st.stats[:, j, :], st.resid[:, j, :]).then_inc(s.stats_ready, 1)
    dve.wait_ge(s.stats_ready, j + 1)
    dve.bn_aggr(st.meanvar[:, j, :], st.stats[:, j, :]).then_inc(s.meanvar_ready, 1)


def normalise_vector(dve, st, s, j=0, gain=None, shift=None):
    out = st.xnew[:, j, :]
    dve.wait_ge(s.rstd_ready, j + 1)
    step = dve.tensor_scalar(out, st.resid[:, j, :], st.meanvar[:, j, 0:1], st.rstd[:, j:j + 1], ALU.subtract, ALU.mult)
    if gain is None:
        step.then_inc(s.xnew_ready, 1)
        return
    step.then_inc(s.affine_step, 1)
    dve.wait_ge(s.affine_step, 2 * j + 1)
    dve.tensor_tensor(out, out, gain, ALU.mult).then_inc(s.affine_step, 1)
    dve.wait_ge(s.affine_step, 2 * j + 2)
    dve.tensor_tensor(out, out, shift, ALU.add).then_inc(s.xnew_ready, 1)


def rstd_pool(pool, st, s, j=0, eps=1e-5):
    pool.wait_ge(s.meanvar_ready, j + 1)
    pool.tensor_scalar(st.vareps[:, j:j + 1], st.meanvar[:, j, 1:2], eps, None, ALU.add).then_inc(s.vareps_ready, 1)
    pool.wait_ge(s.vareps_ready, j + 1)
    pool.tensor_tensor(st.rstd[:, j:j + 1], st.vareps[:, j:j + 1], st.minus_half[0:S, 0:1], ALU.pow).then_inc(s.rstd_ready, 1)


def store_pool(pool, st, s, x_b, j=0):
    pool.wait_ge(s.xnew_ready, j + 1)
    pool.tensor_copy(x_b, st.xnew[:, j, :]).then_inc(s.x_stored, 1)


def turn_tensor(pe, st, s, bank, j=0):
    pe.wait_ge(s.xnew_ready, j + 1)
    for k in range(KT):
        last = pe.transpose(st.ps[:, bank, k * S:(k + 1) * S], st.xnew[:, j, k * P:(k + 1) * P], st.ident[0:S, 0:S])
    last.then_inc(s.xnew_turned, 1)


def store_scalar(act, st, s, bank, xt_b, j=0):
    act.wait_ge(s.xnew_turned, j + 1)
    act.activation(xt_b, st.ps[:, bank, 0:KT * S].rearrange("p (k t) -> p k t", k=KT), ACT.Copy)


def attention(nc, st, name, heads, hd, cross, w, bias=None, plus_one=False, mask=None, mask_dram=None,
              rope=None, xT=None, inner=None, bd=None, conv=None):
    nk = KEYS if cross else S
    krows, ktiles = (KROWS, 3) if cross else (S, 1)
    nkp = krows * ktiles
    width = heads * hd
    nf = width // P
    own = w.k is None
    scale = float(hd) ** -0.5 if hd < 256 else 1.0
    pg = min(heads, 1 if cross else 4)
    groups = heads // pg
    steps = groups * TURN
    lag = 2 if conv else 0
    turn_lag, value_lag = lag + TURN_LAG, lag + TURN_LAG + 1
    n_probs = TURN_LAG + 1
    hpt = max(1, P // hd)
    bias = bias or {}
    masked = mask is not None or mask_dram is not None or bd is not None or conv is not None
    xT = st.XT if xT is None else xT
    head_mask = st.head_mask[hd] if hpt > 1 else None
    o_banks = max(1, width // BANK)
    s_banks = 4 if conv else 4 - o_banks
    t_banks = 6 - o_banks - s_banks
    s_bank = lambda n: n % s_banks
    t_bank = lambda n: s_banks + n % t_banks
    o_bank = 6 - o_banks

    qper, vw = min(nf, 4), min(width, BANK)
    q_parts = [m for m in range(0, nf, qper)]
    v_parts = [(t, c) for t in range(ktiles) for c in range(0, width, vw)]
    parts = [("q", m) for m in q_parts] + ([("rq", 0)] if rope else [])
    if not own:
        for m in range(nf):
            parts += [("k", m)] + ([("rk", m)] if rope else [])
        parts += [("v", p) for p in v_parts]
    o_parts = [m for m in range(0, nf, 4)]
    table = {n: [] for n in range(-1, steps + value_lag + 6)}
    for j in range(TURN):
        done = (j + 1) * groups + value_lag - 1
        table[done] += [("o", j, None)]
        table[done + 1] += [("turn_o", j, m) for m in o_parts]
        table[done + 2] += [("y", j, None)]
        table[done + 4] += [("norm", j, None)]
        table[done + 5] += [("turn_x", j, None)]
        for i, (kind, part) in enumerate(parts):
            table[-1 if j == 0 else (j - 1) * groups + i * (groups - 1) // len(parts)].append((kind, j, part))
    through = [x for n in sorted(table) for x in table[n] if x[0] not in ("o", "norm")]
    place = {x: c for c, x in enumerate(through)}
    side_bank = lambda x: 6 + place[x] % 2

    with ExitStack() as ctx:
        def sb(n, shape, dt=F32):
            return ctx.enter_context(nc.sbuf_tensor(f"{name}_{n}", shape, dt))

        q_sb = sb("q_sb", [P, 2, nf, S])
        q_pad = sb("q_pad", [P, 2, heads, S]) if hpt > 1 else None
        kT = sb("kT", [P, 2, nf, nk]) if not own else None
        nv = TURN if width <= D else 2
        vals = sb("vals", [krows, nv, ktiles, width])
        probs = sb("probs", [S, n_probs, pg, nkp])
        probsT = sb("probsT", [krows, 2, pg * ktiles * S])
        nmax, rsum, rinv = sb("nmax", [S, TURN, heads]), sb("rsum", [S, TURN, heads]), sb("rinv", [S, TURN, heads])
        o_sb, oT = sb("o_sb", [S, 2, width]), sb("oT", [P, 2, nf, S])
        xcur = sb("xcur", [P, TURN, KT, S])
        ctx_cur = sb("ctx_cur", [P, TURN, KT, KEYS]) if cross else None
        s_sb = sb("s_sb", [S, 2, pg, nk]) if masked else None
        bd_cur = sb("bd_cur", [S, 2, heads, S]) if bd is not None else None
        sm = sb("sm", [S, 2, pg, S + 2]) if conv else None
        rowsum = sb("rowsum", [S, 3, 3, pg, S]) if conv else None
        product = sb("product", [S, 3, S]) if conv else None
        kern_cur = sb("kern_cur", [S, TURN, heads * 9]) if conv else None
        mask_i = sb("mask_i", [S, 2, KEYS], I32) if mask_dram is not None else None
        mask_b = sb("mask_b", [S, 2, KEYS]) if mask_dram is not None else None
        rq_sb = sb("rq_sb", [P, 2, nf, S]) if rope else None
        rk_sb = sb("rk_sb", [P, 2, nf, nk]) if rope else None

        with stage_sems(nc, ["buffers_cleared"]) as s, nc.Block() as block:
            @block.gpsimd
            def _(pool):
                pool.memset(probs[:], 0.0).then_inc(s.buffers_cleared, 1)
                pool.memset(vals[:], 0.0).then_inc(s.buffers_cleared, 1)
                if conv:
                    pool.memset(sm[:], 0.0).then_inc(s.buffers_cleared, 1)

        sems = ["xcur_ready", "ctx_ready", "kern_ready", "side_ready", "side_copied0", "side_copied1", "q_rotated", "k_rotated", "rope_step",
                "q_spread", "scores_ready", "masked_ready", "max_ready", "exp_done", "probs_turned", "probsT_ready", "values_done",
                "rsum_ready", "rinv_ready", "o_ready", "mask_loaded", "mask_ready", "bd_loaded", "first_tap", "tap_done", "sm_ready",
                "pool_tap", "rows_dve", "summed", "x_summed", "bias_added"]
        with nc.Fori(0, B // TURN) as turn, stage_sems(nc, sems + NORM_SEMS) as s, nc.Block() as block:
            batch = lambda j: turn * TURN + j
            side_copied = [s.side_copied0, s.side_copied1]

            def wait_copied(eng, items):
                for bank in (0, 1):
                    n = max([place[x] // 2 + 1 for x in items if place[x] % 2 == bank], default=0)
                    if n:
                        eng.wait_ge(side_copied[bank], n)

            def copied_by(x):
                kind = x[0]
                if kind in ("q", "v"):
                    return "dve" if kind in bias else "act"
                return "dve" if kind == "y" else "act"

            def items(kind, j):
                return [x for x in through if x[0] == kind and x[1] == j]

            def heads_of(g):
                return range(g * pg, (g + 1) * pg)

            def score_tile(n):
                return st.ps[0:S, s_bank(n), 0:pg * nk].rearrange("q (h k) -> q h k", h=pg)

            def x_b(j):
                return st.X[:, batch(j), :]

            @block.sync
            def _(sp):
                for j in range(TURN):
                    if mask_dram is not None:
                        if j >= 2:
                            sp.wait_ge(s.mask_ready, j - 1)
                        sp.dma_start(mask_i[:, j % 2, :], mask_dram[batch(j)]).then_inc(s.mask_loaded, 16)
                        sp.wait_ge(s.mask_loaded, 16 * (j + 1))
                    if bd is not None:
                        if j >= 2:
                            sp.wait_ge(s.masked_ready, (j - 1) * groups)
                        sp.dma_start(bd_cur[:, j % 2], bd(batch(j))).then_inc(s.bd_loaded, 16)
                        sp.wait_ge(s.bd_loaded, 16 * (j + 1))

            @block.gpsimd
            def _(pool):
                def tokens(j):
                    pool.tensor_copy(xcur[:, j], xT[:, :, batch(j), :]).then_inc(s.xcur_ready, 1)
                    if cross:
                        pool.tensor_copy(ctx_cur[:, j], st.ctxT[:, batch(j), :, :]).then_inc(s.ctx_ready, 1)
                    if own:
                        pool.tensor_copy(vals[:, j % nv, 0, :], x_b(j)).then_inc(s.ctx_ready, 1)
                    if "o" in bias:
                        pool.tensor_tensor(st.resid[:, j, :], x_b(j), bias["o"][0:S, :], ALU.add).then_inc(s.bias_added, 1)
                    if conv:
                        pool.tensor_copy(kern_cur[:, j], conv.kern[0:S, batch(j), :]).then_inc(s.kern_ready, 1)

                def rotate(to, other, n, steps_in_front, done):
                    wide = lambda t: t[:, 0:n].unsqueeze(1).to_broadcast([P, nf, n])
                    pool.tensor_tensor(to, to, wide(rope.cos), ALU.mult).then_inc(s.rope_step, 1)
                    pool.tensor_tensor(other, other, wide(rope.sin), ALU.mult).then_inc(s.rope_step, 1)
                    pool.wait_ge(s.rope_step, steps_in_front + 2)
                    pool.tensor_tensor(to, to, other, ALU.add).then_inc(done, 1)

                def spread(j):
                    wait_copied(pool, items("q", j) + items("rq", j))
                    if rope:
                        rotate(q_sb[:, j % 2], rq_sb[:, j % 2], S, 4 * j, s.q_rotated)
                        pool.wait_ge(s.q_rotated, j + 1)
                    for m in range(nf if hpt > 1 else 0):
                        pool.tensor_tensor(q_pad[:, j % 2, m * hpt:(m + 1) * hpt, :], q_sb[:, j % 2, m, :].unsqueeze(1).to_broadcast([P, hpt, S]),
                                           head_mask.unsqueeze(2).to_broadcast([P, hpt, S]), ALU.mult).then_inc(s.q_spread, 1)

                def pool_taps(n):
                    j, g = divmod(n, groups)
                    i = pg - 1
                    taps = kern_cur[:, j, (g * pg + i) * 9:(g * pg + i + 1) * 9].rearrange("q (r c) -> q r c", c=3)
                    pool.wait_ge(s.sm_ready, n + 1)
                    if n >= 3:
                        pool.wait_ge(s.summed, n - 2)
                    for c in range(3):
                        out = rowsum[:, n % 3, :, i, :]
                        if c >= 1:
                            pool.wait_ge(s.pool_tap, 5 * n + 2 * c - 1)
                        pool.tensor_tensor(out if c == 0 else product[:], sm[:, n % 2, i, c:c + S].unsqueeze(1).to_broadcast([S, 3, S]),
                                           taps[:, :, c].unsqueeze(2).to_broadcast([S, 3, S]), ALU.mult).then_inc(s.pool_tap, 1)
                        if c >= 1:
                            pool.wait_ge(s.pool_tap, 5 * n + 2 * c)
                            pool.tensor_tensor(out, out, product[:], ALU.add).then_inc(s.pool_tap, 1)

                for n in sorted(table):
                    if n == -1:
                        tokens(0)
                    if conv and 0 <= n - 1 < steps:
                        pool_taps(n - 1)
                    if n > 0 and n % groups == 0 and n // groups + 1 < TURN:
                        tokens(n // groups + 1)
                    for x in table[n]:
                        kind, j, part = x
                        if x == (items("rq", j) or items("q", j))[-1]:
                            spread(j)
                        if rope and x == items("rk", j)[-1]:
                            wait_copied(pool, items("k", j) + items("rk", j))
                            rotate(kT[:, j % 2], rk_sb[:, j % 2], nk, 4 * j + 2, s.k_rotated)
                        if kind == "y":
                            rstd_pool(pool, st, s, j)
                            if inner:
                                pool.tensor_tensor(x_b(j), st.resid[:, j, :], x_b(j), ALU.add).then_inc(s.x_summed, 1)
                        if kind == "norm" and not inner:
                            store_pool(pool, st, s, x_b(j), j)
                    if n == -1:
                        tokens(1)

            @block.tensor
            def _(pe):
                def issue(x):
                    kind, j, part = x
                    c, bank = place[x], side_bank(x)
                    if c >= 2:
                        pe.wait_ge(side_copied[c % 2], c // 2)
                    if kind in ("q", "rq"):
                        pe.wait_ge(s.xcur_ready, j + 1)
                        for i, m in enumerate(range(part, part + qper)):
                            for k in range(KT):
                                last = pe.matmul(st.ps[:, bank, i * S:(i + 1) * S], (w.q if kind == "q" else rope.q)[:, k, m * P:(m + 1) * P],
                                                 xcur[:, j, k, :], start=(k == 0), stop=(k == KT - 1))
                    elif kind in ("k", "rk"):
                        if cross:
                            pe.wait_ge(s.ctx_ready, j + 1)
                        src = ctx_cur if cross else xcur
                        for k in range(KT):
                            last = pe.matmul(st.ps[:, bank, 0:nk], (w.k if kind == "k" else rope.k)[:, k, part * P:(part + 1) * P],
                                             src[:, j, k, :], start=(k == 0), stop=(k == KT - 1))
                    elif kind == "v":
                        t, col = part
                        rows = min(krows, nk - t * krows)
                        src = ctx_cur if cross else xcur
                        for k in range(KT):
                            last = pe.matmul(st.ps[0:rows, bank, 0:vw], src[:, j, k, t * krows:t * krows + rows], w.v[:, k, col:col + vw],
                                             start=(k == 0), stop=(k == KT - 1))
                    elif kind == "turn_o":
                        pe.wait_ge(s.o_ready, j + 1)
                        for m in range(part, min(part + 4, nf)):
                            last = pe.transpose(st.ps[:, bank, (m - part) * S:(m - part + 1) * S], o_sb[:, j % 2, m * P:(m + 1) * P], st.ident[0:S, 0:S])
                    elif kind == "y":
                        wait_copied(pe, items("turn_o", j))
                        for m in range(nf):
                            last = pe.matmul(st.ps[0:S, bank, 0:D], oT[:, j % 2, m, :], w.o[:, m, :], start=(m == 0), stop=(m == nf - 1))
                    elif kind == "turn_x":
                        pe.wait_ge(s.xnew_ready, j + 1)
                        for k in range(KT):
                            last = pe.transpose(st.ps[:, bank, k * S:(k + 1) * S], st.xnew[:, j, k * P:(k + 1) * P], st.ident[0:S, 0:S])
                    last.then_inc(s.side_ready, 1)

                def scores(n):
                    j, g = divmod(n, groups)
                    if g * pg % hpt == 0:
                        m = g * pg // hpt
                        if hpt > 1:
                            pe.wait_ge(s.q_spread, j * nf + m + 1)
                        else:
                            wait_copied(pe, items("q", j))
                        if rope:
                            pe.wait_ge(s.k_rotated, j + 1)
                        elif not own:
                            wait_copied(pe, [("k", j, m)])
                    again = n - s_banks
                    if again >= 0:
                        if masked:
                            pe.wait_ge(s.masked_ready, again + 1)
                        else:
                            pe.wait_ge(s.exp_done, (again + 1) * pg)
                    for i, h in enumerate(heads_of(g)):
                        tiles = [h // hpt] if hpt > 1 else range(nf)
                        for m in tiles:
                            q = q_pad[:, j % 2, h, :] if hpt > 1 else q_sb[:, j % 2, m, :]
                            last = pe.matmul(score_tile(n)[:, i, :], q, xcur[:, j, m, :] if own else kT[:, j % 2, m, :],
                                             start=(m == tiles[0]), stop=(m == tiles[-1]))
                    last.then_inc(s.scores_ready, 1)

                def sum_rows(n):
                    pe.wait_ge(s.rows_dve, (n + 1) * 3 * (pg - 1))
                    pe.wait_ge(s.pool_tap, (n + 1) * 5)
                    for r in range(3):
                        last = pe.matmul(st.ps[0:S, s_bank(n), 0:pg * S], conv.shift[r], rowsum[:, n % 3, r].rearrange("q h k -> q (h k)"),
                                         start=(r == 0), stop=(r == 2))
                    last.then_inc(s.summed, 1)

                def turn_probs(n):
                    pe.wait_ge(s.exp_done, (n + 1) * pg)
                    if n >= t_banks:
                        pe.wait_ge(s.probsT_ready, n + 1 - t_banks)
                    for i in range(pg):
                        for t in range(ktiles):
                            c = (i * ktiles + t) * S
                            last = pe.transpose(st.ps[0:krows, t_bank(n), c:c + S], probs[:, n % n_probs, i, t * krows:(t + 1) * krows], st.ident[0:S, 0:S])
                    last.then_inc(s.probs_turned, 1)

                def values(n):
                    j, g = divmod(n, groups)
                    pe.wait_ge(s.probsT_ready, n + 1)
                    if g == 0:
                        if own:
                            pe.wait_ge(s.ctx_ready, j + 1)
                        else:
                            wait_copied(pe, items("v", j))
                        if j >= 1:
                            pe.wait_ge(s.o_ready, j)
                    for i, h in enumerate(heads_of(g)):
                        out = st.ps[0:S, o_bank + h * hd // BANK, h * hd % BANK:h * hd % BANK + hd]
                        for t in range(ktiles):
                            c = (i * ktiles + t) * S
                            last = pe.matmul(out, probsT[:, n % 2, c:c + S], vals[:, j % nv, t, h * hd:(h + 1) * hd],
                                             start=(t == 0), stop=(t == ktiles - 1))
                    last.then_inc(s.values_done, 1)

                for n in sorted(table):
                    if 0 <= n < steps:
                        scores(n)
                    if 0 <= n - turn_lag < steps:
                        turn_probs(n - turn_lag)
                    if 0 <= n - value_lag < steps:
                        values(n - value_lag)
                    if conv and 0 <= n - 2 < steps:
                        sum_rows(n - 2)
                    for x in table[n]:
                        if x in place:
                            issue(x)

            @block.scalar
            def _(act):
                def copy_out(x):
                    kind, j, part = x
                    bank = side_bank(x)
                    act.wait_ge(s.side_ready, place[x] + 1)
                    tiles = lambda n: st.ps[:, bank, 0:n * S].rearrange("p (m t) -> p m t", m=n)
                    if kind in ("q", "rq"):
                        if j >= 2 and hpt > 1:
                            act.wait_ge(s.q_spread, (j - 1) * nf)
                        step = act.activation((q_sb if kind == "q" else rq_sb)[:, j % 2, part:part + qper, :], tiles(qper), ACT.Copy, scale=scale)
                    elif kind in ("k", "rk"):
                        to = (kT if kind == "k" else rk_sb)[:, j % 2, part, :]
                        if rope and j >= 2:
                            act.wait_ge(s.k_rotated, j - 1)
                        if "k" in bias:
                            step = act.activation(to, st.ps[:, bank, 0:nk], ACT.Identity, bias=bias["k"][:, part:part + 1])
                        else:
                            step = act.activation(to, st.ps[:, bank, 0:nk], ACT.Copy)
                    elif kind == "v":
                        t, col = part
                        rows = min(krows, nk - t * krows)
                        step = act.activation(vals[0:rows, j % nv, t, col:col + vw], st.ps[0:rows, bank, 0:vw], ACT.Copy)
                    elif kind == "turn_o":
                        n = min(4, nf - part)
                        step = act.activation(oT[:, j % 2, part:part + n, :], tiles(n), ACT.Copy)
                    elif kind == "turn_x":
                        step = act.activation(inner.turned[:, :, batch(j), :] if inner else st.XT[:, :, batch(j), :], tiles(KT), ACT.Copy)
                    step.then_inc(side_copied[place[x] % 2], 1)

                def first_taps(n):
                    j, g = divmod(n, groups)
                    act.wait_ge(s.sm_ready, n + 1)
                    if g == 0:
                        act.wait_ge(s.kern_ready, j + 1)
                    if n >= 3:
                        act.wait_ge(s.summed, n - 2)
                    for i, h in enumerate(heads_of(g)[:-1]):
                        for r in range(3):
                            act.activation(rowsum[:, n % 3, r, i, :], sm[:, n % 2, i, 0:S], ACT.Copy,
                                           scale=kern_cur[:, j, h * 9 + 3 * r:h * 9 + 3 * r + 1]).then_inc(s.first_tap, 1)

                def exponentials(n):
                    j, g = divmod(n, groups)
                    act.wait_ge(s.max_ready, n + 1)
                    if n >= n_probs:
                        act.wait_ge(s.probs_turned, n + 1 - n_probs)
                    for i, h in enumerate(heads_of(g)):
                        scr = s_sb[:, n % 2, i, :] if masked else score_tile(n)[:, i, :]
                        act.activation(probs[:, n % n_probs, i, 0:nk], scr, ACT.Exp, bias=nmax[:, j, h:h + 1],
                                       accum_out=rsum[:, j, h:h + 1]).then_inc(s.exp_done, 1)

                for n in sorted(table):
                    if conv and 0 <= n < steps:
                        first_taps(n)
                    if 0 <= n - lag < steps:
                        exponentials(n - lag)
                    for x in table[n]:
                        if x in place and copied_by(x) == "act":
                            copy_out(x)

            @block.vector
            def _(dve):
                def copy_out(x):
                    kind, j, part = x
                    bank = side_bank(x)
                    dve.wait_ge(s.side_ready, place[x] + 1)
                    copied = side_copied[place[x] % 2]
                    if kind == "q":
                        if j >= 2 and hpt > 1:
                            dve.wait_ge(s.q_spread, (j - 1) * nf)
                        dve.scalar_tensor_tensor(q_sb[:, j % 2, part:part + qper, :], st.ps[:, bank, 0:qper * S].rearrange("p (m t) -> p m t", m=qper),
                                                 scale, bias["q"][:, part:part + qper].unsqueeze(2).to_broadcast([P, qper, S]),
                                                 ALU.mult, ALU.add).then_inc(copied, 1)
                    elif kind == "v":
                        t, col = part
                        rows = min(krows, nk - t * krows)
                        dve.tensor_tensor(vals[0:rows, j % nv, t, col:col + vw], st.ps[0:rows, bank, 0:vw], bias["v"][0:rows, col:col + vw],
                                          ALU.add).then_inc(copied, 1)
                    else:
                        resid = st.resid[:, j, :]
                        if "o" in bias:
                            dve.wait_ge(s.bias_added, j + 1)
                        dve.tensor_tensor(resid, st.ps[0:S, bank, 0:D], resid if "o" in bias else x_b(j), ALU.add).then_inc(copied, 1)
                        dve.wait_ge(copied, place[x] // 2 + 1)
                        norm_stats_vector(dve, st, s, j)

                def convolve(n):
                    j, g = divmod(n, groups)
                    dve.wait_ge(s.first_tap, (n + 1) * (pg - 1) * 3)
                    mine = pg - 1
                    for tap in (1, 2):
                        for i in range(mine):
                            h = g * pg + i
                            for r in range(3):
                                wt = kern_cur[:, j, h * 9 + 3 * r + tap:h * 9 + 3 * r + tap + 1]
                                acc = rowsum[:, n % 3, r, i, :]
                                if tap == 2:
                                    dve.wait_ge(s.tap_done, (n * mine + i) * 3 + r + 1)
                                dve.scalar_tensor_tensor(acc, sm[:, n % 2, i, tap:tap + S], wt, acc, ALU.mult, ALU.add).then_inc(
                                    s.tap_done if tap == 1 else s.rows_dve, 1)

                def mask_scores(n):
                    dve.wait_ge(s.scores_ready, n + 1)
                    if n >= 2:
                        dve.wait_ge(s.rows_dve, (n - 1) * 3 * (pg - 1))
                        dve.wait_ge(s.pool_tap, (n - 1) * 5)
                    dve.tensor_tensor(sm[:, n % 2, :, 1:S + 1], score_tile(n), conv.keep.unsqueeze(1).to_broadcast([S, pg, S]),
                                      ALU.mult).then_inc(s.sm_ready, 1)

                def maxima(n):
                    j, g = divmod(n, groups)
                    if conv:
                        dve.wait_ge(s.summed, n + 1)
                    else:
                        dve.wait_ge(s.scores_ready, n + 1)
                    rows = score_tile(n)
                    if masked:
                        if n >= 2:
                            dve.wait_ge(s.exp_done, (n - 1) * pg)
                        if bd is not None:
                            if g == 0:
                                dve.wait_ge(s.bd_loaded, 16 * (j + 1))
                            m = bd_cur[:, j % 2, g * pg:(g + 1) * pg, :]
                        else:
                            m = conv.mask if conv else mask if mask is not None else mask_b[:, j % 2, :]
                            m = m.unsqueeze(1).to_broadcast([S, pg, nk])
                        if mask_dram is not None and g == 0:
                            dve.wait_ge(s.mask_loaded, 16 * (j + 1))
                            dve.tensor_scalar(mask_b[:, j % 2, :], mask_i[:, j % 2, :], 0, MASKED, ALU.is_equal, ALU.mult).then_inc(s.mask_ready, 1)
                            dve.wait_ge(s.mask_ready, j + 1)
                        dve.tensor_tensor(s_sb[:, n % 2], rows, m, ALU.add).then_inc(s.masked_ready, 1)
                        dve.wait_ge(s.masked_ready, n + 1)
                        rows = s_sb[:, n % 2]
                    dve.tensor_reduce(nmax[:, j, g * pg:(g + 1) * pg], rows, AX.X, ALU.max, negate=True).then_inc(s.max_ready, 1)

                def copy_probs(n):
                    dve.wait_ge(s.probs_turned, n + 1)
                    if n >= 2:
                        dve.wait_ge(s.values_done, n - 1)
                    dve.tensor_copy(probsT[:, n % 2, :], st.ps[0:krows, t_bank(n), 0:pg * ktiles * S]).then_inc(s.probsT_ready, 1)

                def outputs(j):
                    sums = rsum[:, j, :]
                    dve.wait_ge(s.exp_done, (j + 1) * heads)
                    if plus_one:
                        dve.tensor_scalar(sums, sums, 1.0, None, ALU.add).then_inc(s.rsum_ready, 1)
                        dve.wait_ge(s.rsum_ready, j + 1)
                    dve.reciprocal(rinv[:, j, :], sums).then_inc(s.rinv_ready, 1)
                    dve.wait_ge(s.rinv_ready, j + 1)
                    dve.wait_ge(s.values_done, (j + 1) * groups)
                    hb = heads // o_banks
                    for i in range(o_banks):
                        last = dve.tensor_tensor(o_sb[:, j % 2, i * hb * hd:(i + 1) * hb * hd].rearrange("q (h d) -> q h d", d=hd),
                                                 st.ps[0:S, o_bank + i, 0:hb * hd].rearrange("q (h d) -> q h d", d=hd),
                                                 rinv[:, j, i * hb:(i + 1) * hb].unsqueeze(2).to_broadcast([S, hb, hd]), ALU.mult)
                    last.then_inc(s.o_ready, 1)

                for n in sorted(table):
                    if conv and 0 <= n < steps:
                        mask_scores(n)
                    if not conv and 0 <= n < steps:
                        maxima(n)
                    if 0 <= n - turn_lag < steps:
                        copy_probs(n - turn_lag)
                    if conv and 0 <= n - 1 < steps:
                        convolve(n - 1)
                    if conv and 0 <= n - lag < steps:
                        maxima(n - lag)
                    for x in table[n]:
                        if x[0] == "o":
                            outputs(x[1])
                        elif x[0] == "norm":
                            normalise_vector(dve, st, s, x[1], *((inner.gain, inner.shift) if inner else ()))
                        elif copied_by(x) == "dve":
                            copy_out(x)


def l0_ffn(nc, st, dram):
    QB, EPS, LN_EPS = 128.0, 1e-5, 1e-3
    ROUND = 12582912.0
    wt = st.w["f2w"]
    with ExitStack() as ctx:
        def sb(n, shape, dt=F32):
            return ctx.enter_context(nc.sbuf_tensor(f"l0f_{n}", shape, dt))

        xq = sb("xq", [S, B, D])
        stats, mv = sb("stats", [S, B, 6]), sb("mv", [S, B, 2])
        vareps, rstd = sb("vareps", [S, B]), sb("rstd", [S, B])
        wabs, beta = sb("wabs", [P, 1]), sb("beta", [P, 4])
        ones = sb("ones", [P, P])
        absmax, gmax = sb("absmax", [S, 1]), sb("gmax", [S, 4])
        xq_cur, xqT = sb("xq_cur", [S, TURN, D]), sb("xqT", [P, TURN, KT, S])

        with stage_sems(nc, ["ones_set", "wabs_ready", "wsum_ready", "beta_step", "stats_done", "mv_done",
                             "vareps_done", "rstd_done", "norm_done", "affine_done", "absmax_ready", "gmax_ready",
                             "g_step", "xq_done", "wq_step"]) as s, nc.Block() as block:
            @block.gpsimd
            def _(pool):
                pool.memset(ones[:], 1.0).then_inc(s.ones_set, 1)
                pool.wait_ge(s.mv_done, B)
                pool.tensor_scalar(vareps[:], mv[:, :, 1], LN_EPS, None, ALU.add).then_inc(s.vareps_done, 1)
                pool.wait_ge(s.vareps_done, 1)
                pool.tensor_tensor(rstd[:], vareps[:], st.minus_half[0:S, :].to_broadcast([S, B]), ALU.pow).then_inc(s.rstd_done, 1)
                pool.wait_ge(s.absmax_ready, 1)
                pool.partition_all_reduce(gmax[:, 0:1], absmax[:], S, bass.bass_isa.ReduceOp.max).then_inc(s.gmax_ready, 1)

            @block.tensor
            def _(pe):
                pe.wait_ge(s.ones_set, 1)
                pe.wait_ge(s.wabs_ready, 1)
                pe.matmul(st.ps[:, 0, 0:1], ones[:], wabs[:], start=True, stop=True).then_inc(s.wsum_ready, 1)

            @block.vector
            def _(dve):
                dve.tensor_reduce(wabs[:], wt, AX.X, ALU.add, apply_absolute_value=True).then_inc(s.wabs_ready, 1)
                for b in range(B):
                    dve.bn_stats(stats[:, b, :], st.X[:, b, :]).then_inc(s.stats_done, 1)
                for b in range(B):
                    dve.wait_ge(s.stats_done, b + 1)
                    dve.bn_aggr(mv[:, b, :], stats[:, b, :]).then_inc(s.mv_done, 1)
                dve.wait_ge(s.wsum_ready, 1)
                dve.tensor_scalar(beta[:, 0:1], st.ps[:, 0, 0:1], 1.0 / (D * D), None, ALU.mult).then_inc(s.beta_step, 1)
                dve.wait_ge(s.beta_step, 1)
                dve.tensor_scalar(beta[:, 1:2], beta[:, 0:1], EPS, None, ALU.add).then_inc(s.beta_step, 1)
                dve.wait_ge(s.beta_step, 2)
                dve.reciprocal(beta[:, 2:3], beta[:, 1:2]).then_inc(s.beta_step, 1)
                dve.wait_ge(s.beta_step, 3)
                dve.tensor_scalar(wt, wt, beta[:, 2:3], 1.0, ALU.mult, ALU.min).then_inc(s.wq_step, 1)
                dve.wait_ge(s.wq_step, 1)
                dve.tensor_scalar(wt, wt, -1.0, ROUND, ALU.max, ALU.add).then_inc(s.wq_step, 1)
                dve.wait_ge(s.wq_step, 2)
                dve.tensor_scalar(wt, wt, ROUND, None, ALU.subtract).then_inc(s.wq_step, 1)
                dve.wait_ge(s.rstd_done, 1)
                for b in range(B):
                    dve.tensor_scalar(xq[:, b, :], st.X[:, b, :], mv[:, b, 0:1], rstd[:, b:b + 1],
                                      ALU.subtract, ALU.mult).then_inc(s.norm_done, 1)
                dve.wait_ge(s.norm_done, B)
                dve.tensor_tensor(xq[:], xq[:], st.w["f2g"][0:S, :].unsqueeze(1).to_broadcast([S, B, D]), ALU.mult).then_inc(s.affine_done, 1)
                dve.wait_ge(s.affine_done, 1)
                dve.tensor_tensor(xq[:], xq[:], st.w["f2b"][0:S, :].unsqueeze(1).to_broadcast([S, B, D]), ALU.add).then_inc(s.affine_done, 1)
                dve.wait_ge(s.affine_done, 2)
                dve.tensor_reduce(absmax[:], xq[:], AX.XY, ALU.max, apply_absolute_value=True).then_inc(s.absmax_ready, 1)
                dve.wait_ge(s.gmax_ready, 1)
                dve.reciprocal(gmax[:, 1:2], gmax[:, 0:1]).then_inc(s.g_step, 1)
                dve.tensor_scalar(gmax[:, 3:4], gmax[:, 0:1], beta[0:S, 0:1], 1.0 / QB, ALU.mult, ALU.mult).then_inc(s.g_step, 1)
                dve.wait_ge(s.g_step, 2)
                dve.tensor_scalar(gmax[:, 2:3], gmax[:, 1:2], QB, None, ALU.mult).then_inc(s.g_step, 1)
                dve.wait_ge(s.g_step, 3)
                dve.tensor_scalar(xq[:], xq[:], gmax[:, 2:3], QB - EPS, ALU.mult, ALU.min).then_inc(s.xq_done, 1)
                dve.wait_ge(s.xq_done, 1)
                dve.tensor_scalar(xq[:], xq[:], -QB + EPS, None, ALU.max).then_inc(s.xq_done, 1)

        with nc.Fori(0, B // TURN) as turn, stage_sems(nc, ["cur_ready", "cur_turned", "curT_ready"] + NORM_SEMS) as s, nc.Block() as block:
            x_b = lambda j: st.X[:, turn * TURN + j, :]

            @block.gpsimd
            def _(pool):
                for j in range(TURN):
                    pool.tensor_copy(xq_cur[:, j, :], xq[:, turn * TURN + j, :]).then_inc(s.cur_ready, 1)
                for j in range(TURN):
                    rstd_pool(pool, st, s, j)
                for j in range(TURN):
                    store_pool(pool, st, s, x_b(j), j)

            @block.tensor
            def _(pe):
                for j in range(TURN):
                    pe.wait_ge(s.cur_ready, j + 1)
                    for k in range(KT):
                        last = pe.transpose(st.ps[:, 2 * j, k * S:(k + 1) * S], xq_cur[:, j, k * P:(k + 1) * P], st.ident[0:S, 0:S])
                    last.then_inc(s.cur_turned, 1)
                for j in range(TURN):
                    pe.wait_ge(s.curT_ready, j + 1)
                    for k in range(KT):
                        last = pe.matmul(st.ps[0:S, 2 * j + 1, 0:D], xqT[:, j, k, :], wt[:, k * D:(k + 1) * D], start=(k == 0), stop=(k == KT - 1))
                    last.then_inc(s.y_ready, 1)
                for j in range(TURN):
                    turn_tensor(pe, st, s, 2 * j, j)

            @block.scalar
            def _(act):
                for j in range(TURN):
                    act.wait_ge(s.cur_turned, j + 1)
                    act.activation(xqT[:, j], st.ps[:, 2 * j, 0:KT * S].rearrange("p (k t) -> p k t", k=KT), ACT.Copy).then_inc(s.curT_ready, 1)
                for j in range(TURN):
                    store_scalar(act, st, s, 2 * j, st.XT[:, :, turn * TURN + j, :], j)

            @block.vector
            def _(dve):
                for j in range(TURN):
                    dve.wait_ge(s.y_ready, j + 1)
                    dve.scalar_tensor_tensor(st.resid[:, j, :], st.ps[0:S, 2 * j + 1, 0:D], gmax[:, 3:4], x_b(j),
                                             ALU.mult, ALU.add).then_inc(s.resid_ready, 1)
                    dve.wait_ge(s.resid_ready, j + 1)
                    norm_stats_vector(dve, st, s, j)
                for j in range(TURN):
                    normalise_vector(dve, st, s, j)


def l1_attn(nc, st, dram):
    DIN, NS, R, TAPS = 512, 16, 64, 4
    M = DIN // P
    HALF = TOK // 2
    pad = TAPS - 1
    w_in = st.w["m_in"].rearrange("p (k n) -> p k n", k=KT)
    w_xp = st.w["m_xproj"].rearrange("p (k n) -> p k n", k=M)
    w_out = st.w["m_out"].rearrange("p (k n) -> p k n", k=M)
    w_conv = st.w["m_conv"].rearrange("p (m j) -> p m j", m=M)
    a_log = st.w["m_alog"].rearrange("p (m n) -> p m n", m=M)
    XTf = st.XT[:].rearrange("p k b t -> p k (b t)")
    with ExitStack() as ctx:
        def sb(n, shape, dt=F32):
            return ctx.enter_context(nc.sbuf_tensor(f"l1a_{n}", shape, dt))

        hs = sb("hs", [P, M, TOK])
        gate = sb("gate", [P, M, TOK])
        xdbl = sb("xdbl", [R + 2 * NS, TOK])
        delta = sb("delta", [P, M, TOK])

        with ExitStack() as ctx2:
            def sb2(n, shape, dt=F32):
                return ctx2.enter_context(nc.sbuf_tensor(f"l1a_{n}", shape, dt))

            hpad = sb2("hpad", [P, M, B, pad + S])
            conv = sb2("conv", [P, 2, TOK])
            vraw = sb2("vraw", [P, TOK])
            ev, lg = sb2("ev", [P, TOK]), sb2("lg", [P, TOK])
            er = sb2("er", [P, TOK])
            with stage_sems(nc, ["hpad_zero", "proj_ready", "hs_raw", "gate_done", "conv_step", "hs_done", "xdbl_ready",
                                 "xdbl_done", "dt_ready", "v_done", "abs_done", "exp_done", "log_done", "sp_step",
                                 "delta_done", "a_done", "a_negative"]) as s, nc.Block() as block:
                @block.gpsimd
                def _(pool):
                    pool.memset(hpad[:], 0.0).then_inc(s.hpad_zero, 1)
                    pool.wait_ge(s.a_done, 1)
                    pool.tensor_scalar(st.w["m_alog"], st.w["m_alog"], -1.0, None, ALU.mult).then_inc(s.a_negative, 1)

                @block.tensor
                def _(pe):
                    for m in range(2 * M):
                        if m >= 4:
                            pe.wait_ge(s.hs_raw, m - 3)
                        for j in range(2):
                            for k in range(KT):
                                last = pe.matmul(st.ps[:, 2 * (m % 4) + j, 0:HALF], w_in[:, k, m * P:(m + 1) * P],
                                                 XTf[:, k, j * HALF:(j + 1) * HALF], start=(k == 0), stop=(k == KT - 1))
                        last.then_inc(s.proj_ready, 1)
                    pe.wait_ge(s.hs_raw, M)
                    pe.wait_ge(s.gate_done, 1)
                    pe.wait_ge(s.hs_done, M)
                    for j in range(2):
                        for k in range(M):
                            last = pe.matmul(st.ps[0:R + 2 * NS, j, 0:HALF], w_xp[:, k, :], hs[:, k, j * HALF:(j + 1) * HALF],
                                             start=(k == 0), stop=(k == M - 1))
                    last.then_inc(s.xdbl_ready, 1)
                    pe.wait_ge(s.xdbl_done, 1)
                    for m in range(M):
                        if m >= 2:
                            pe.wait_ge(s.v_done, m - 1)
                        else:
                            pe.wait_ge(s.gate_done, M)
                        for j in range(2):
                            last = pe.matmul(st.ps[:, 4 + 2 * (m % 2) + j, 0:HALF], st.w["m_dt"][0:R + 2 * NS, m * P:(m + 1) * P],
                                             xdbl[:, j * HALF:(j + 1) * HALF], start=True, stop=True)
                        last.then_inc(s.dt_ready, 1)

                @block.scalar
                def _(act):
                    act.wait_ge(s.hpad_zero, 1)
                    for m in range(2 * M):
                        act.wait_ge(s.proj_ready, m + 1)
                        for j in range(2):
                            ps = st.ps[:, 2 * (m % 4) + j, 0:HALF]
                            if m < M:
                                last = act.activation(hpad[:, m, j * B // 2:(j + 1) * B // 2, pad:],
                                                      ps.rearrange("p (b t) -> p b t", t=S), ACT.Copy)
                            else:
                                last = act.activation(gate[:, m - M, j * HALF:(j + 1) * HALF], ps, ACT.Silu)
                        last.then_inc(s.hs_raw if m < M else s.gate_done, 1)
                    for m in range(M):
                        act.wait_ge(s.conv_step, TAPS * (m + 1))
                        act.activation(hs[:, m, :], conv[:, m % 2, :], ACT.Silu).then_inc(s.hs_done, 1)
                    act.wait_ge(s.xdbl_ready, 1)
                    act.activation(xdbl[:].rearrange("p (j t) -> p j t", j=2), st.ps[0:R + 2 * NS, 0:2, 0:HALF], ACT.Copy).then_inc(s.xdbl_done, 1)
                    act.activation(st.w["m_alog"], st.w["m_alog"], ACT.Exp).then_inc(s.a_done, 1)
                    for m in range(M):
                        act.wait_ge(s.dt_ready, m + 1)
                        if m >= 1:
                            act.wait_ge(s.delta_done, m)
                        act.activation(vraw[:].rearrange("p (j t) -> p j t", j=2), st.ps[:, 4 + 2 * (m % 2):6 + 2 * (m % 2), 0:HALF],
                                       ACT.Identity, bias=st.w["m_bdt"][:, m:m + 1]).then_inc(s.v_done, 1)
                        act.wait_ge(s.v_done, m + 1)
                        act.activation(ev[:], vraw[:], ACT.Abs).then_inc(s.abs_done, 1)
                        act.wait_ge(s.abs_done, m + 1)
                        act.activation(ev[:], ev[:], ACT.Exp, scale=-1.0).then_inc(s.exp_done, 1)
                        act.wait_ge(s.exp_done, m + 1)
                        act.activation(lg[:], ev[:], ACT.Ln, bias=1.0).then_inc(s.log_done, 1)

                @block.vector
                def _(dve):
                    for m in range(M):
                        dve.wait_ge(s.hs_raw, m + 1)
                        if m >= 2:
                            dve.wait_ge(s.hs_done, m - 1)
                        acc = conv[:, m % 2, :].rearrange("p (b t) -> p b t", t=S)
                        dve.tensor_scalar(acc, hpad[:, m, :, 0:S], w_conv[:, m, 0:1], None, ALU.mult).then_inc(s.conv_step, 1)
                        for j in range(1, TAPS):
                            dve.wait_ge(s.conv_step, TAPS * m + j)
                            dve.scalar_tensor_tensor(acc, hpad[:, m, :, j:j + S], w_conv[:, m, j:j + 1], acc,
                                                     ALU.mult, ALU.add).then_inc(s.conv_step, 1)
                    for m in range(M):
                        dve.wait_ge(s.exp_done, m + 1)
                        dve.tensor_scalar(er[:], ev[:], 1.0, 1.0, ALU.add, ALU.subtract).then_inc(s.sp_step, 1)
                        dve.wait_ge(s.sp_step, 3 * m + 1)
                        dve.tensor_tensor(er[:], ev[:], er[:], ALU.subtract).then_inc(s.sp_step, 1)
                        dve.wait_ge(s.sp_step, 3 * m + 2)
                        dve.scalar_tensor_tensor(er[:], vraw[:], 0.0, er[:], ALU.max, ALU.add).then_inc(s.sp_step, 1)
                        dve.wait_ge(s.sp_step, 3 * m + 3)
                        dve.wait_ge(s.log_done, m + 1)
                        dve.tensor_tensor(delta[:, m, :], lg[:], er[:], ALU.add).then_inc(s.delta_done, 1)

        halves = lambda t: t[:].rearrange("p m (j t) -> p m j t", j=2)
        hs_h, gate_h, delta_h = halves(hs), halves(gate), halves(delta)
        xdbl_h = xdbl[:].rearrange("p (j t) -> p j t", j=2)
        with ExitStack() as ctx2:
            def sb2(n, shape):
                return ctx2.enter_context(nc.sbuf_tensor(f"l1a_{n}", shape, F32))

            bcs = sb2("bcs", [P, 2 * NS, HALF])
            da = st.w["m_in"][:, 0:3 * HALF].rearrange("p (i c) -> p i c", i=3)
            dbx = sb2("dbx", [P, 3, HALF])
            z = sb2("z", [P, 3, HALF])
            dx = sb2("dx", [P, HALF])
            steps = M * NS
            with nc.Fori(0, 2) as j, stage_sems(nc, ["bc_ready", "bc_copied", "dx_ready", "da_ready", "da_reset", "dbx_ready", "scan_done",
                                                     "zc_ready", "sum_done", "skip_done", "tile_done"]) as s, nc.Block() as block:
                @block.gpsimd
                def _(pool):
                    for m in range(M):
                        if m >= 1:
                            pool.wait_ge(s.dbx_ready, m * NS)
                        pool.tensor_tensor(dx[:], delta_h[:, m, j, :], hs_h[:, m, j, :], ALU.mult).then_inc(s.dx_ready, 1)
                        pool.wait_ge(s.dx_ready, m + 1)
                        for i in range(NS):
                            n = m * NS + i
                            if m == 0:
                                pool.wait_ge(s.bc_copied, 2 * i + 1)
                            if n >= 3:
                                pool.wait_ge(s.scan_done, n - 2)
                            pool.tensor_tensor(dbx[:, n % 3, :], dx[:], bcs[:, i, :], ALU.mult).then_inc(s.dbx_ready, 1)

                @block.scalar
                def _(act):
                    for n in range(steps):
                        m, i = divmod(n, NS)
                        if m == 0:
                            for c in (2 * i, 2 * i + 1):
                                act.wait_ge(s.bc_ready, c + 1)
                                act.activation(bcs[:, c % 2 * NS + i, :], st.ps[:, 4 + c % 4, 0:HALF], ACT.Copy).then_inc(s.bc_copied, 1)
                        if n >= 3:
                            act.wait_ge(s.scan_done, n - 2)
                        act.activation(da[:, n % 3, :], delta_h[:, m, j, :], ACT.Exp, scale=a_log[:, m, i:i + 1]).then_inc(s.da_ready, 1)
                        act.wait_ge(s.da_ready, n + 1)
                        act.mul(da[:, n % 3, 0:HALF:S], da[:, n % 3, 0:HALF:S], 0.0).then_inc(s.da_reset, 1)

                @block.vector
                def _(dve):
                    def times_c(n):
                        m, i = divmod(n, NS)
                        if m == 0:
                            dve.wait_ge(s.bc_copied, 2 * i + 2)
                        dve.wait_ge(s.scan_done, n + 1)
                        dve.tensor_tensor(z[:, n % 3, :], z[:, n % 3, :], bcs[:, NS + i, :], ALU.mult).then_inc(s.zc_ready, 1)

                    def finish(m):
                        tile = gate_h[:, m, j, :]
                        dve.wait_ge(s.sum_done, (m + 1) * NS)
                        dve.scalar_tensor_tensor(hs_h[:, m, j, :], hs_h[:, m, j, :], st.w["m_d"][:, m:m + 1], st.ps[:, m % 2, 0:HALF],
                                                 ALU.mult, ALU.add).then_inc(s.skip_done, 1)
                        dve.wait_ge(s.skip_done, m + 1)
                        dve.tensor_tensor(tile, hs_h[:, m, j, :], tile, ALU.mult).then_inc(s.tile_done, 1)

                    for n in range(steps):
                        dve.wait_ge(s.da_reset, n + 1)
                        dve.wait_ge(s.dbx_ready, n + 1)
                        if n >= 3:
                            dve.wait_ge(s.sum_done, n - 2)
                        dve.tensor_tensor_scan(z[:, n % 3, :], da[:, n % 3, :], dbx[:, n % 3, :], 0.0, ALU.mult, ALU.add).then_inc(s.scan_done, 1)
                        if n >= 1:
                            times_c(n - 1)
                        if n % NS == 3 and n > NS:
                            finish(n // NS - 1)
                    times_c(steps - 1)
                    finish(M - 1)

                @block.tensor
                def _(pe):
                    def spread(i):
                        for c in (2 * i, 2 * i + 1):
                            if c >= 4:
                                pe.wait_ge(s.bc_copied, c - 3)
                            row = R + c % 2 * NS + i
                            pe.matmul(st.ps[:, 4 + c % 4, 0:HALF], st.ident[0:R + 2 * NS, row:row + 1].to_broadcast([R + 2 * NS, P]),
                                      xdbl_h[:, j, :], start=True, stop=True).then_inc(s.bc_ready, 1)

                    spread(0)
                    spread(1)
                    for n in range(steps):
                        m, i = divmod(n, NS)
                        if n + 2 < NS:
                            spread(n + 2)
                        if m >= 2 and i == 0:
                            pe.wait_ge(s.tile_done, m - 1)
                        pe.wait_ge(s.zc_ready, n + 1)
                        pe.matmul(st.ps[:, m % 2, 0:HALF], st.ident, z[:, n % 3, :],
                                  start=(i == 0), stop=(i == NS - 1)).then_inc(s.sum_done, 1)

        y_cur = sb("y_cur", [P, TURN, M, S])
        with nc.Fori(0, B // TURN) as turn, stage_sems(nc, ["cur_ready"] + NORM_SEMS) as s, nc.Block() as block:
            x_b = lambda j: st.X[:, turn * TURN + j, :]

            @block.gpsimd
            def _(pool):
                for j in range(TURN):
                    pool.tensor_copy(y_cur[:, j], gate[:].rearrange("p m (b t) -> p m b t", b=B)[:, :, turn * TURN + j, :]).then_inc(s.cur_ready, 1)
                for j in range(TURN):
                    rstd_pool(pool, st, s, j)
                for j in range(TURN):
                    store_pool(pool, st, s, x_b(j), j)

            @block.tensor
            def _(pe):
                for j in range(TURN):
                    pe.wait_ge(s.cur_ready, j + 1)
                    for k in range(M):
                        last = pe.matmul(st.ps[0:S, j, 0:D], y_cur[:, j, k, :], w_out[:, k, :], start=(k == 0), stop=(k == M - 1))
                    last.then_inc(s.y_ready, 1)
                for j in range(TURN):
                    turn_tensor(pe, st, s, TURN + j, j)

            @block.scalar
            def _(act):
                for j in range(TURN):
                    store_scalar(act, st, s, TURN + j, st.XT[:, :, turn * TURN + j, :], j)

            @block.vector
            def _(dve):
                for j in range(TURN):
                    norm_sum_vector(dve, st, s, st.ps[0:S, j, 0:D], x_b(j), None, j)
                for j in range(TURN):
                    normalise_vector(dve, st, s, j)


GATE_SEMS = ["logits_ready", "score_ready", "score_step", "top_ready", "picked_ready", "left_ready", "gate_step",
             "gate_ready", "gate_turned", "gateT_stored"]


class Gate:

    def __init__(self, nc, ctx, name, experts, top, ones_in_front, ones_behind, turns_per_gate=1):
        def sb(n, shape):
            return ctx.enter_context(nc.sbuf_tensor(f"{name}_{n}", shape, F32))

        self.experts, self.top, self.front = experts, top, ones_in_front
        self.marks = 8 - top
        self.width = ones_in_front + experts + ones_behind
        self.scores = sb("scores", [S, B, experts + self.marks])
        self.left = sb("left", [S, B, experts + self.marks])
        self.top8, self.picked = sb("top8", [S, B, 8]), sb("picked", [S, B, 8])
        self.gate = sb("gate", [S, B, self.width])
        self.total, self.rtotal = sb("total", [S, B]), sb("rtotal", [S, B])
        self.gateT = sb("gateT", [self.width, B, S])
        self.dram = nc.dram_tensor(f"{name}_gates", (self.width, turns_per_gate, TOK), F32).ap()
        self.repeats = turns_per_gate

    def wide(self, t):
        return t[:].unsqueeze(2).to_broadcast([S, B, self.experts])

    def logits(self, st):
        return st.ps[0:S, 0, 0:B * self.experts].rearrange("s (b e) -> s b e", b=B)

    def pool_marks(self, pool, s):
        pool.memset(self.scores[:], -1.0)
        pool.memset(self.picked[:], -1.0)
        pool.memset(self.gate[:], 1.0).then_inc(s.marks_set, 1)

    def tensor_logits(self, pe, st, s, x, wg):
        for b in range(B):
            for k in range(KT):
                last = pe.matmul(self.logits(st)[:, b, :], x[:, k, b, :], wg[:, k, :], start=(k == 0), stop=(k == KT - 1))
        last.then_inc(s.logits_ready, 1)

    def vector_pick(self, dve, s):
        e = self.experts
        dve.wait_ge(s.score_ready, 1)
        for b in range(B):
            dve.max(self.top8[:, b, :], self.scores[:, b, 0:e]).then_inc(s.top_ready, 1)
        dve.wait_ge(s.top_ready, B)
        dve.tensor_copy(self.picked[:, :, 0:self.top], self.top8[:, :, 0:self.top]).then_inc(s.picked_ready, 1)
        dve.wait_ge(s.picked_ready, 1)
        for b in range(B):
            dve.match_replace(self.left[:, b, :], self.picked[:, b, :], self.scores[:, b, :], 0.0).then_inc(s.left_ready, 1)
        dve.wait_ge(s.left_ready, B)
        return self.gate[:, :, self.front:self.front + e], self.scores[:, :, 0:e], self.left[:, :, 0:e]

    def tensor_turn(self, pe, st, s):
        pe.wait_ge(s.gate_ready, 1)
        for b in range(B):
            last = pe.transpose(st.ps[0:self.width, 2 + b // 4, (b % 4) * S:(b % 4 + 1) * S], self.gate[:, b, :], st.ident[0:S, 0:S])
        last.then_inc(s.gate_turned, 1)

    def scalar_store(self, act, st, s):
        act.wait_ge(s.gate_turned, 1)
        act.activation(self.gateT[:].rearrange("e (i b) t -> e i (b t)", i=2), st.ps[0:self.width, 2:4, 0:4 * S], ACT.Copy).then_inc(s.gateT_stored, 1)


def experts(nc, st, name, kind, units, unit_cols, dram_w, gate, gate_row, inputs, b2):
    HALF = TOK // 2
    geglu = kind == "geglu"
    up = 4 if geglu else 2
    n_gates = 2 if kind == "relu" else 1
    off2 = KT * up * P
    offb = off2 + 2 * D
    yT = st.yT
    with ExitStack() as ctx:
        def sb(n, shape, dt=F32):
            return ctx.enter_context(nc.sbuf_tensor(f"{name}_{n}", shape, dt))

        slot = [sb(f"slot{i}", [P, unit_cols]) for i in range(2)]
        gates = [sb(f"gates{i}", [P, n_gates, TOK]) for i in range(2)]
        act_out = sb("act_out", [P, 2, TOK]) if kind != "relu" else None
        prod = sb("prod", [P, 2, TOK]) if geglu else None
        hg = sb("hg", [P, 2, TOK])
        sems = ["gates_stored", "weights_loaded0", "weights_loaded1", "h_ready", "gelu_done", "prod_done", "hg_ready",
                "y_done", "y_copied"]
        with stage_sems(nc, sems) as s, nc.Block() as block:
            loaded = [s.weights_loaded0, s.weights_loaded1]
            gate_rows = gate.dram.rearrange("e r t -> (e r) t").rearrange("(u g) t -> u g t", g=n_gates)

            def w1(sl, k, m):
                return slot[sl][:, k * up * P + m * P:k * up * P + (m + 1) * P]

            def w2(sl, t, m):
                return slot[sl][:, off2 + t * D + m * P:off2 + t * D + (m + 1) * P]

            def col(sl, i):
                return slot[sl][:, offb + i:offb + i + 1]

            def halves(t, i):
                return t[:, i, :].rearrange("p (j c) -> p j c", j=2)

            turns = (units + 1) // 2
            cuts = sorted({1, turns - 1} | {u // 2 for u, _ in inputs if u // 2 > 0})

            def run(eng, body):
                body(0, inputs[0][1])
                for lo, hi in zip(cuts[:-1], cuts[1:]):
                    x = [x for u, x in inputs if u // 2 <= lo][-1]
                    with eng.Fori(lo, hi) as i:
                        body(i, x)
                body(turns - 1, inputs[-1][1])

            def tiles_of(i):
                n = 2 if type(i) is int and 2 * i + 1 >= units else 4
                return [(c, c // 2, c % 2) for c in range(n)]

            def after(eng, sem, value, least=1):
                if type(value) is not int or value >= least:
                    eng.wait_ge(sem, value)

            @block.sync
            def _(sp):
                for r in range(gate.repeats):
                    sp.dma_start(gate.dram[:, r, :], gate.gateT[:].rearrange("e b t -> e (b t)")).then_inc(s.gates_stored, 16)
                sp.wait_ge(s.gates_stored, 16 * gate.repeats)

                def body(i, _):
                    for sl in sorted({sl for _, sl, _ in tiles_of(i)}):
                        u = i * 2 + sl
                        after(sp, s.y_done, 4 * i + 2 * sl - 2)
                        sp.dma_start(slot[sl][:], dram_w[u]).then_inc(loaded[sl], 16)
                        sp.dma_start(gates[sl][:], gate_rows[gate_row(i, sl)].partition_broadcast(P)).then_inc(loaded[sl], 16)
                run(sp, body)

            @block.tensor
            def _(pe):
                if b2 is not None:
                    for m in range(2):
                        for j in range(2):
                            pe.matmul(st.ps[:, 2 * m + j, 0:HALF], b2[0:gate.width, m * P:(m + 1) * P],
                                      gate.gateT[:].rearrange("e b t -> e (b t)")[:, j * HALF:(j + 1) * HALF], start=True, stop=False)

                def down(n, sl, t, first, last_tile):
                    pe.wait_ge(s.hg_ready, n + 1)
                    for m in range(2):
                        for j in range(2):
                            last = pe.matmul(st.ps[:, 2 * m + j, 0:HALF], w2(sl, t, m), hg[:, t, j * HALF:(j + 1) * HALF],
                                             start=first, stop=last_tile)
                    last.then_inc(s.y_done, 1)

                def body(i, x):
                    tiles = tiles_of(i)
                    for c, sl, t in tiles:
                        n = i * 4 + c
                        if t == 0:
                            pe.wait_ge(loaded[sl], i * 32 + 32)
                        if geglu:
                            after(pe, s.gelu_done, n)
                            after(pe, s.prod_done, n)
                        elif kind == "gelu":
                            after(pe, s.gelu_done, n - 1)
                        else:
                            after(pe, s.hg_ready, n - 1)
                        for half in range(2 if geglu else 1):
                            for j in range(2):
                                bank = 4 + 2 * half + j if geglu else 4 + 2 * t + j
                                for k in range(KT):
                                    last = pe.matmul(st.ps[:, bank, 0:HALF], w1(sl, k, t + 2 * half), x[:, k, j * HALF:(j + 1) * HALF],
                                                     start=(k == 0), stop=(k == KT - 1))
                        last.then_inc(s.h_ready, 1)
                        if not (type(i) is int and i == 0 and c == 0):
                            down(n - 1, 1 - sl if t == 0 else sl, 1 - t, b2 is None and type(i) is int and n == 1, False)
                run(pe, body)
                c, sl, t = tiles_of(turns - 1)[-1]
                down(2 * units - 1, sl, t, False, True)

            if kind != "relu":
                @block.scalar
                def _(act):
                    def body(i, _):
                        for c, sl, t in tiles_of(i):
                            n = i * 4 + c
                            act.wait_ge(s.h_ready, n + 1)
                            after(act, s.hg_ready, n - 1)
                            bank = 6 if geglu else 4 + 2 * t
                            act.activation(halves(act_out, t), st.ps[:, bank:bank + 2, 0:HALF], ACT.Gelu,
                                           bias=col(sl, 2 + t if geglu else t)).then_inc(s.gelu_done, 1)
                    run(act, body)

            @block.vector
            def _(dve):
                def body(i, _):
                    for c, sl, t in tiles_of(i):
                        n = i * 4 + c
                        if kind == "relu":
                            dve.wait_ge(s.h_ready, n + 1)
                            if t == 0:
                                dve.wait_ge(loaded[sl], i * 32 + 32)
                            after(dve, s.y_done, n - 1)
                            dve.scalar_tensor_tensor(halves(hg, t), st.ps[:, 4 + 2 * t:6 + 2 * t, 0:HALF], 0.0, halves(gates[sl], t),
                                                     ALU.max, ALU.mult).then_inc(s.hg_ready, 1)
                            continue
                        if t == 0:
                            dve.wait_ge(loaded[sl], i * 32 + 32)
                        if geglu:
                            dve.wait_ge(s.gelu_done, n + 1)
                            dve.scalar_tensor_tensor(halves(prod, t), st.ps[:, 4:6, 0:HALF], col(sl, t), halves(act_out, t),
                                                     ALU.add, ALU.mult).then_inc(s.prod_done, 1)
                            after(dve, s.y_done, n - 1)
                            dve.wait_ge(s.prod_done, n + 1)
                            dve.scalar_tensor_tensor(hg[:, t, :], prod[:, t, :], col(sl, 4 + t), gates[sl][:, 0, :],
                                                     ALU.mult, ALU.mult).then_inc(s.hg_ready, 1)
                        else:
                            dve.wait_ge(s.gelu_done, n + 1)
                            after(dve, s.y_done, n - 1)
                            dve.tensor_tensor(hg[:, t, :], act_out[:, t, :], gates[sl][:, 0, :], ALU.mult).then_inc(s.hg_ready, 1)
                run(dve, body)
                dve.wait_ge(s.y_done, 2 * units)
                for m in range(2):
                    dve.tensor_copy(halves(yT, m), st.ps[:, 2 * m:2 * m + 2, 0:HALF]).then_inc(s.y_copied, 1)


def experts_tail(nc, st):
    with nc.Fori(0, B // TURN) as turn, stage_sems(nc, ["cur_ready"] + NORM_SEMS) as s, nc.Block() as block:
        y = st.yT[:].rearrange("p m (b t) -> p m b t", b=B)

        @block.gpsimd
        def _(pool):
            for j in range(TURN):
                pool.tensor_copy(st.ycur[:, j], y[:, :, turn * TURN + j, :]).then_inc(s.cur_ready, 1)
            for j in range(TURN):
                rstd_pool(pool, st, s, j)
            for j in range(TURN):
                store_pool(pool, st, s, st.X[:, turn * TURN + j, :], j)

        @block.tensor
        def _(pe):
            for j in range(TURN):
                pe.wait_ge(s.cur_ready, j + 1)
                for m in range(KT):
                    last = pe.transpose(st.ps[0:S, j, m * P:(m + 1) * P], st.ycur[:, j, m, :], st.ident)
                last.then_inc(s.y_ready, 1)
            for j in range(TURN):
                turn_tensor(pe, st, s, TURN + j, j)

        @block.scalar
        def _(act):
            for j in range(TURN):
                store_scalar(act, st, s, TURN + j, st.XT[:, :, turn * TURN + j, :], j)

        @block.vector
        def _(dve):
            for j in range(TURN):
                norm_sum_vector(dve, st, s, st.ps[0:S, j, 0:D], st.X[:, turn * TURN + j, :], None, j)
            for j in range(TURN):
                normalise_vector(dve, st, s, j)


def l2_ffn(nc, st, dram):
    E, TOP, EPS = 15, 3, 1e-20
    with ExitStack() as ctx:
        sb = lambda n, shape: ctx.enter_context(nc.sbuf_tensor(f"l2f_{n}", shape, F32))
        st.yT, st.ycur = sb("yT", [P, KT, TOK]), sb("ycur", [P, TURN, KT, S])
        raw, expsum, rexpsum = sb("raw", [S, B, E]), sb("expsum", [S, B]), sb("rexpsum", [S, B])
        gate = Gate(nc, ctx, "l2f", E, TOP, 0, 2)
        with stage_sems(nc, GATE_SEMS + ["marks_set", "exp_done"]) as s, nc.Block() as block:
            @block.gpsimd
            def _(pool):
                gate.pool_marks(pool, s)

            @block.tensor
            def _(pe):
                gate.tensor_logits(pe, st, s, st.XT, st.w["f8gate"].rearrange("p (k e) -> p k e", k=KT))
                gate.tensor_turn(pe, st, s)

            @block.scalar
            def _(act):
                act.wait_ge(s.score_step, 2)
                act.activation(raw[:], raw[:], ACT.Exp).then_inc(s.exp_done, 1)
                gate.scalar_store(act, st, s)

            @block.vector
            def _(dve):
                dve.wait_ge(s.logits_ready, 1)
                dve.tensor_reduce(expsum[:], gate.logits(st), AX.X, ALU.max).then_inc(s.score_step, 1)
                dve.wait_ge(s.score_step, 1)
                dve.tensor_tensor(raw[:], gate.logits(st), gate.wide(expsum), ALU.subtract).then_inc(s.score_step, 1)
                dve.wait_ge(s.exp_done, 1)
                dve.tensor_reduce(expsum[:], raw[:], AX.X, ALU.add).then_inc(s.score_step, 1)
                dve.wait_ge(s.score_step, 3)
                dve.reciprocal(rexpsum[:], expsum[:]).then_inc(s.score_step, 1)
                dve.wait_ge(s.score_step, 4)
                dve.wait_ge(s.marks_set, 1)
                dve.tensor_tensor(gate.scores[:, :, 0:E], raw[:], gate.wide(rexpsum), ALU.mult).then_inc(s.score_ready, 1)
                out, scores, left = gate.vector_pick(dve, s)
                dve.tensor_tensor(raw[:], scores, left, ALU.subtract).then_inc(s.gate_step, 1)
                dve.tensor_reduce(gate.total[:], gate.top8[:, :, 0:TOP], AX.X, ALU.add).then_inc(s.gate_step, 1)
                dve.wait_ge(s.gate_step, 2)
                dve.tensor_scalar(gate.total[:], gate.total[:], EPS, None, ALU.add).then_inc(s.gate_step, 1)
                dve.wait_ge(s.gate_step, 3)
                dve.reciprocal(gate.rtotal[:], gate.total[:]).then_inc(s.gate_step, 1)
                dve.wait_ge(s.gate_step, 4)
                dve.tensor_tensor(out, raw[:], gate.wide(gate.rtotal), ALU.mult).then_inc(s.gate_ready, 1)

        xf = st.XT[:].rearrange("p k b t -> p k (b t)")
        experts(nc, st, "l2f", "geglu", E + 2, KT * 4 * P + 2 * D + 6, dram["l2_ffn_units"], gate,
                lambda i, sl: i * 2 + sl, [(0, xf)], st.w["f8b2"])
        experts_tail(nc, st)


def l3_ffn(nc, st, dram):
    E, TOP, EPS = 8, 2, float(np.finfo(np.float32).eps)
    with ExitStack() as ctx:
        sb = lambda n, shape: ctx.enter_context(nc.sbuf_tensor(f"l3f_{n}", shape, F32))
        st.yT, st.ycur = sb("yT", [P, KT, TOK]), sb("ycur", [P, TURN, KT, S])
        xs, xr = sb("xs", [P, KT, B, S]), sb("xr", [P, KT, B, S])
        ss, ms = sb("ss", [S, TURN]), sb("ms", [S, TURN])
        gate = Gate(nc, ctx, "l3f", E, TOP, 2, 0, turns_per_gate=2)
        with stage_sems(nc, GATE_SEMS + ["marks_set"]) as s, nc.Block() as block:
            @block.gpsimd
            def _(pool):
                gate.pool_marks(pool, s)

            @block.tensor
            def _(pe):
                gate.tensor_logits(pe, st, s, st.XT, st.w["f11gate"].rearrange("p (k e) -> p k e", k=KT))
                gate.tensor_turn(pe, st, s)

            @block.scalar
            def _(act):
                act.wait_ge(s.logits_ready, 1)
                act.wait_ge(s.marks_set, 1)
                act.activation(gate.scores[:, :, 0:E], gate.logits(st), ACT.Sigmoid).then_inc(s.score_ready, 1)
                gate.scalar_store(act, st, s)

            @block.vector
            def _(dve):
                out, scores, left = gate.vector_pick(dve, s)
                dve.tensor_reduce(gate.total[:], scores, AX.X, ALU.add).then_inc(s.gate_step, 1)
                dve.wait_ge(s.gate_step, 1)
                dve.reciprocal(gate.rtotal[:], gate.total[:]).then_inc(s.gate_step, 1)
                dve.tensor_tensor(out, scores, left, ALU.subtract).then_inc(s.gate_step, 1)
                dve.wait_ge(s.gate_step, 3)
                dve.tensor_tensor(out, out, gate.wide(gate.rtotal), ALU.mult).then_inc(s.gate_ready, 1)

        with nc.Fori(0, B // TURN) as turn, stage_sems(nc, ["sq_ready", "ms_ready", "rms_ready", "xn_ready", "xn_turned", "xs_done",
                                                            "twice_done"]) as s, nc.Block() as block:
            @block.gpsimd
            def _(pool):
                for j in range(TURN):
                    pool.wait_ge(s.sq_ready, j + 1)
                    pool.tensor_scalar(ms[:, j:j + 1], ss[:, j:j + 1], 1.0 / D, EPS, ALU.mult, ALU.add).then_inc(s.ms_ready, 1)
                    pool.wait_ge(s.ms_ready, j + 1)
                    pool.tensor_tensor(st.rstd[:, j:j + 1], ms[:, j:j + 1], st.minus_half[0:S, :], ALU.pow).then_inc(s.rms_ready, 1)

            @block.tensor
            def _(pe):
                for j in range(TURN):
                    pe.wait_ge(s.xn_ready, j + 1)
                    for k in range(KT):
                        last = pe.transpose(st.ps[:, j, k * S:(k + 1) * S], st.xnew[:, j, k * P:(k + 1) * P], st.ident[0:S, 0:S])
                    last.then_inc(s.xn_turned, 1)

            @block.scalar
            def _(act):
                for j in range(TURN):
                    act.wait_ge(s.xn_turned, j + 1)
                    for k in range(KT):
                        ps = st.ps[:, j, k * S:(k + 1) * S]
                        act.activation(xs[:, k, turn * TURN + j, :], ps, ACT.Copy, scale=st.w["f11gs"][:, k:k + 1]).then_inc(s.xs_done, 1)
                        act.activation(xr[:, k, turn * TURN + j, :], ps, ACT.Copy, scale=st.w["f11gr"][:, k:k + 1]).then_inc(s.xs_done, 1)

            @block.vector
            def _(dve):
                for j in range(TURN):
                    x_b = st.X[:, turn * TURN + j, :]
                    dve.scalar_tensor_tensor(st.resid[:, j, :], x_b, 1.0, x_b, ALU.mult, ALU.mult, accum_out=ss[:, j:j + 1]).then_inc(s.sq_ready, 1)
                for j in range(TURN):
                    x_b = st.X[:, turn * TURN + j, :]
                    dve.wait_ge(s.rms_ready, j + 1)
                    dve.tensor_scalar(st.xnew[:, j, :], x_b, st.rstd[:, j:j + 1], None, ALU.mult).then_inc(s.xn_ready, 1)
                    dve.wait_ge(s.xn_ready, j + 1)
                    dve.tensor_tensor(x_b, x_b, x_b, ALU.add).then_inc(s.twice_done, 1)

        flat = lambda t: t[:].rearrange("p k b t -> p k (b t)")
        experts(nc, st, "l3f", "gelu", 40, KT * 2 * P + 2 * D + 2, dram["l3_ffn_units"], gate,
                lambda i, sl: i, [(0, flat(xs)), (8, flat(xr))], st.w["f11b2"])
        experts_tail(nc, st)


def l1_ffn(nc, st, dram):
    E, TOP, H = 32, 4, 16
    REL = 2 * S - 1
    ROW, PITCH = 200, 3300
    scratch = nc.dram_tensor("l1f_positions", (B, S * PITCH), F32).ap()
    wq = st.w["f5q"].rearrange("p (k n) -> p k n", k=KT)
    wp = st.w["f5p"].rearrange("p (k n) -> p k n", k=KT)
    pe_table = st.w["f5pe"].rearrange("p (k n) -> p k n", k=KT)
    with ExitStack() as ctx:
        sb = lambda n, shape: ctx.enter_context(nc.sbuf_tensor(f"l1f_{n}", shape, F32))
        st.yT, st.ycur = sb("yT", [P, KT, TOK]), sb("ycur", [P, TURN, KT, S])
        x2T = sb("x2T", [P, KT, B, S])
        with ExitStack() as ctx2:
            sb2 = lambda n, shape: ctx2.enter_context(nc.sbuf_tensor(f"l1f_{n}", shape, F32))
            x1T = sb2("x1T", [P, KT, B, S])
            with ExitStack() as ctx3:
                sb3 = lambda n, shape: ctx3.enter_context(nc.sbuf_tensor(f"l1f_{n}", shape, F32))
                pT = sb3("pT", [P, KT, REL])
                q1, x1_cur = sb3("q1", [P, TURN, KT, S]), sb3("x1_cur", [P, TURN, KT, S])
                q_pad = sb3("q_between", [P, 2, H, S])
                bd = sb3("bd", [S, H, REL])
                with stage_sems(nc, ["p_ready", "p_done"]) as s, nc.Block() as block:
                    @block.tensor
                    def _(pe):
                        for m in range(KT):
                            for k in range(KT):
                                last = pe.matmul(st.ps[:, m, 0:REL], wp[:, k, m * P:(m + 1) * P], pe_table[:, k, :], start=(k == 0), stop=(k == KT - 1))
                        last.then_inc(s.p_ready, 1)

                    @block.scalar
                    def _(act):
                        act.wait_ge(s.p_ready, 1)
                        act.activation(pT[:], st.ps[:, 0:KT, 0:REL], ACT.Copy).then_inc(s.p_done, 1)

                with nc.Fori(0, B // TURN) as turn, stage_sems(nc, NORM_SEMS + ["x1_stored", "q_ready", "q_copied", "q_spread", "bd_ready", "bd_copied0",
                                                                               "bd_copied1", "bd_stored"]) as s, nc.Block() as block:
                    pairs = H // 2

                    def copy_bd(eng, n):
                        j, g = divmod(n, pairs)
                        eng.wait_ge(s.bd_ready, n + 1)
                        if j >= 1:
                            eng.wait_ge(s.bd_stored, 16 * j)
                        out, ps = bd[:, 2 * g:2 * g + 2, :], st.ps[0:S, n % 4, 0:2 * REL].rearrange("p (h r) -> p h r", h=2)
                        if n % 2 == 0:
                            eng.tensor_copy(out, ps).then_inc(s.bd_copied0, 1)
                        else:
                            eng.activation(out, ps, ACT.Copy).then_inc(s.bd_copied1, 1)

                    @block.gpsimd
                    def _(pool):
                        for j in range(TURN):
                            pool.tensor_copy(st.resid[:, j, :], st.X[:, turn * TURN + j, :]).then_inc(s.resid_ready, 1)
                        for j in range(TURN):
                            rstd_pool(pool, st, s, j)
                        for j in range(TURN):
                            pool.wait_ge(s.q_copied, j + 1)
                            if j >= 2:
                                pool.wait_ge(s.bd_ready, (j - 1) * pairs)
                            for m in range(KT):
                                pool.tensor_tensor(q_pad[:, j % 2, 8 * m:8 * m + 8, :], q1[:, j, m, :].unsqueeze(1).to_broadcast([P, 8, S]),
                                                   st.head_mask[16].unsqueeze(2).to_broadcast([P, 8, S]), ALU.mult).then_inc(s.q_spread, 1)

                    @block.vector
                    def _(dve):
                        for j in range(TURN):
                            dve.wait_ge(s.resid_ready, j + 1)
                            norm_stats_vector(dve, st, s, j)
                        for j in range(TURN):
                            normalise_vector(dve, st, s, j, st.w["f5g1"][0:S, :], st.w["f5s1"][0:S, :])
                        for n in range(0, TURN * pairs, 2):
                            copy_bd(dve, n)

                    @block.tensor
                    def _(pe):
                        for j in range(TURN):
                            turn_tensor(pe, st, s, 4 + j, j)
                        for j in range(TURN):
                            pe.wait_ge(s.x1_stored, 2 * (j + 1))
                            for m in range(KT):
                                for k in range(KT):
                                    last = pe.matmul(st.ps[:, 4 + j, m * S:(m + 1) * S], wq[:, k, m * P:(m + 1) * P], x1_cur[:, j, k, :],
                                                     start=(k == 0), stop=(k == KT - 1))
                            last.then_inc(s.q_ready, 1)
                        for n in range(TURN * pairs):
                            j, g = divmod(n, pairs)
                            if g == 0:
                                pe.wait_ge(s.q_spread, (j + 1) * KT)
                            if n >= 4:
                                pe.wait_ge(s.bd_copied0 if n % 2 == 0 else s.bd_copied1, n // 2 - 1)
                            for i in range(2):
                                h = 2 * g + i
                                last = pe.matmul(st.ps[0:S, n % 4, i * REL:(i + 1) * REL], q_pad[:, j % 2, h, :], pT[:, h // 8, :], start=True, stop=True)
                            last.then_inc(s.bd_ready, 1)

                    @block.scalar
                    def _(act):
                        for j in range(TURN):
                            act.wait_ge(s.xnew_turned, j + 1)
                            ps = st.ps[:, 4 + j, 0:KT * S].rearrange("p (k t) -> p k t", k=KT)
                            act.activation(x1_cur[:, j], ps, ACT.Copy).then_inc(s.x1_stored, 1)
                            act.activation(x1T[:, :, turn * TURN + j, :], ps, ACT.Copy).then_inc(s.x1_stored, 1)
                        for j in range(TURN):
                            act.wait_ge(s.q_ready, j + 1)
                            act.activation(q1[:, j], st.ps[:, 4 + j, 0:KT * S].rearrange("p (m t) -> p m t", m=KT), ACT.Copy, scale=0.25).then_inc(s.q_copied, 1)
                        for n in range(1, TURN * pairs, 2):
                            copy_bd(act, n)

                    @block.sync
                    def _(sp):
                        for j in range(TURN):
                            sp.wait_ge(s.bd_copied0, (j + 1) * pairs // 2)
                            sp.wait_ge(s.bd_copied1, (j + 1) * pairs // 2)
                            rows = scratch[turn * TURN + j, :].rearrange("(i c) -> i c", c=PITCH)[:, 0:H * ROW].rearrange("i (h r) -> i h r", r=ROW)
                            sp.dma_start(rows[:, :, 0:REL], bd[:]).then_inc(s.bd_stored, 16)
                            sp.wait_ge(s.bd_stored, 16 * (j + 1))

            def skewed(b):
                rows = scratch[b, S - 1:S - 1 + S * (PITCH - 1)].rearrange("(i c) -> i c", c=PITCH - 1)
                return rows[:, 0:H * ROW].rearrange("i (h r) -> i h r", r=ROW)[:, :, 0:S]

            w = weights(st, "f5")
            attention(nc, st, "l1f", H, 16, False, w, xT=x1T, inner=InnerNorm(st.w["f5g2"][0:S, :], st.w["f5s2"][0:S, :], x2T), bd=skewed)

        gate = Gate(nc, ctx, "l1f", E, TOP, 0, 0)
        with stage_sems(nc, GATE_SEMS + ["marks_set"]) as s, nc.Block() as block:
            @block.gpsimd
            def _(pool):
                gate.pool_marks(pool, s)

            @block.tensor
            def _(pe):
                gate.tensor_logits(pe, st, s, x2T, st.w["f5sel"].rearrange("p (k e) -> p k e", k=KT))
                gate.tensor_turn(pe, st, s)

            @block.scalar
            def _(act):
                act.wait_ge(s.logits_ready, 1)
                act.wait_ge(s.marks_set, 1)
                act.activation(gate.scores[:, :, 0:E], gate.logits(st), ACT.Sigmoid).then_inc(s.score_ready, 1)
                gate.scalar_store(act, st, s)

            @block.vector
            def _(dve):
                out, scores, left = gate.vector_pick(dve, s)
                dve.tensor_tensor(out, scores, left, ALU.subtract).then_inc(s.gate_ready, 1)

        experts(nc, st, "l1f", "relu", E // 2, KT * 2 * P + 2 * D, dram["l1_ffn_units"], gate,
                lambda i, sl: i * 2 + sl, [(0, x2T[:].rearrange("p k b t -> p k (b t)"))], None)
        experts_tail(nc, st)


def l2_attn(nc, st, dram):
    H, HD, EPS = 8, 32, 1e-6
    HPT = P // HD
    view = lambda n: st.w[n].rearrange("p (k n) -> p k n", k=KT)
    wq, wk, wrq, wrk = view("a6q"), view("a6k"), view("a6rq"), view("a6rk")
    wvg, wout = view("a6vg"), view("a6o")
    VG = D + 3 * H
    norm_w, gate_bias = st.w["a6norm"][0:S, :], st.w["a6bgates"][0:S, :]
    cos, sin, head_mask = st.w["a6cos"], st.w["a6sin"], st.w["a6heads"]
    js = range(TURN)
    with ExitStack() as ctx:
        def sb(n, shape):
            return ctx.enter_context(nc.sbuf_tensor(f"l2a_{n}", shape, F32))

        ss, ms = sb("ss", [S, TURN]), sb("ms", [S, TURN])
        hT = sb("hT", [P, TURN, KT, S])
        qk, rqk = sb("qk", [P, TURN, 2 * KT, S]), sb("rqk", [P, TURN, 2 * KT, S])
        q_pad = sb("q_pad", [P, TURN, H, S])
        vg = sb("vg", [S, TURN, VG])
        beta_pad = sb("beta_pad", [P, TURN, S])
        entries, decay = sb("entries", [S, TURN, H, S]), sb("decay", [S, TURN, H, S])
        o_sb, oT = sb("o_sb", [S, TURN, D]), sb("oT", [P, TURN, KT, S])
        with stage_sems(nc, ["first_zero"]) as s, nc.Block() as block:
            @block.gpsimd
            def _(pool):
                pool.memset(beta_pad[:], 0.0).then_inc(s.first_zero, 1)

        sems = ["sq_ready", "ms_ready", "rms_ready", "h_ready", "h_turned", "hT_ready", "vg_ready", "qk_ready", "rqk_ready",
                "vg_done", "gates_done", "qk_done", "rope_step", "rotated", "q_spread", "beta_turned", "beta_done", "f_ready",
                "entries_ready", "decay_ready", "scores_ready", "weighed_ready", "heads_done", "o_ready", "o_turned", "oT_ready"]
        with nc.Fori(0, B // TURN) as turn, stage_sems(nc, sems + NORM_SEMS) as s, nc.Block() as block:
            x_b = lambda j: st.X[:, turn * TURN + j, :]
            tiles = lambda bank, n: st.ps[:, bank, 0:n * S].rearrange("p (m t) -> p m t", m=n)
            wide = lambda t, n: t.unsqueeze(1).to_broadcast([P, n, S])

            @block.gpsimd
            def _(pool):
                for j in js:
                    pool.wait_ge(s.sq_ready, j + 1)
                    pool.tensor_scalar(ms[:, j:j + 1], ss[:, j:j + 1], 1.0 / D, EPS, ALU.mult, ALU.add).then_inc(s.ms_ready, 1)
                    pool.wait_ge(s.ms_ready, j + 1)
                    pool.tensor_tensor(st.vareps[:, j:j + 1], ms[:, j:j + 1], st.minus_half[0:S, :], ALU.pow).then_inc(s.rms_ready, 1)
                for j in js:
                    pool.wait_ge(s.gates_done, j + 1)
                    pool.tensor_tensor(entries[:, j], st.ident[0:S, 0:S].unsqueeze(1).to_broadcast([S, H, S]),
                                       vg[:, j, D:D + H].unsqueeze(2).to_broadcast([S, H, S]), ALU.mult).then_inc(s.entries_ready, 1)
                    pool.wait_ge(s.rotated, j + 1)
                    for m in range(KT):
                        pool.tensor_tensor(q_pad[:, j, m * HPT:(m + 1) * HPT, :], wide(qk[:, j, m, :], HPT),
                                           head_mask.unsqueeze(2).to_broadcast([P, HPT, S]), ALU.mult).then_inc(s.q_spread, 1)
                for j in js:
                    rstd_pool(pool, st, s, j)
                for j in js:
                    store_pool(pool, st, s, x_b(j), j)

            @block.tensor
            def _(pe):
                for j in js:
                    pe.wait_ge(s.h_ready, j + 1)
                    for k in range(KT):
                        last = pe.transpose(st.ps[:, 2 * j, k * S:(k + 1) * S], st.xnew[:, j, k * P:(k + 1) * P], st.ident[0:S, 0:S])
                    last.then_inc(s.h_turned, 1)
                for j in js:
                    pe.wait_ge(s.hT_ready, j + 1)
                    for k in range(KT):
                        last = pe.matmul(st.ps[0:S, 2 * j, 0:VG], hT[:, j, k, :], wvg[:, k, :], start=(k == 0), stop=(k == KT - 1))
                    last.then_inc(s.vg_ready, 1)
                    for i in range(2 * KT):
                        w, m = (wq, wk)[i // KT], i % KT
                        for k in range(KT):
                            last = pe.matmul(st.ps[:, 2 * j + 1, i * S:(i + 1) * S], w[:, k, m * P:(m + 1) * P], hT[:, j, k, :],
                                             start=(k == 0), stop=(k == KT - 1))
                    last.then_inc(s.qk_ready, 1)
                for j in js:
                    pe.wait_ge(s.vg_done, 2 * (j + 1))
                    for i in range(2 * KT):
                        w, m = (wrq, wrk)[i // KT], i % KT
                        for k in range(KT):
                            last = pe.matmul(st.ps[:, 2 * j, i * S:(i + 1) * S], w[:, k, m * P:(m + 1) * P], hT[:, j, k, :],
                                             start=(k == 0), stop=(k == KT - 1))
                    last.then_inc(s.rqk_ready, 1)
                for j in js:
                    pe.wait_ge(s.gates_done, j + 1)
                    pe.wait_ge(s.qk_done, j + 1)
                    pe.transpose(st.ps[0:H, 2 * j + 1, 0:S], vg[:, j, D + 2 * H:VG], st.ident[0:S, 0:S]).then_inc(s.beta_turned, 1)
                for j in js:
                    pe.wait_ge(s.beta_done, j + 1)
                    pe.wait_ge(s.rotated, j + 1)
                    for h in range(H):
                        last = pe.matmul(st.ps[0:S, 2 * j + h // 4, (h % 4) * S:(h % 4 + 1) * S],
                                         st.ident[:, h:h + 1].to_broadcast([P, S]), beta_pad[:, j, :], start=True, stop=True)
                    last.then_inc(s.f_ready, 1)
                for j in js:
                    pe.wait_ge(s.decay_ready, 2 * (j + 1))
                    pe.wait_ge(s.q_spread, KT * (j + 1))
                    for h in range(H):
                        last = pe.matmul(st.ps[0:S, 2 * j + h // 4, (h % 4) * S:(h % 4 + 1) * S], qk[:, j, KT + h // HPT, :], q_pad[:, j, h, :],
                                         start=True, stop=True)
                    last.then_inc(s.scores_ready, 1)
                for j in js:
                    pe.wait_ge(s.weighed_ready, 2 * (j + 1))
                    for h in range(H):
                        last = pe.matmul(st.ps[0:S, 2 * j, h * HD:(h + 1) * HD], decay[:, j, h, :], vg[:, j, h * HD:(h + 1) * HD], start=True, stop=True)
                    last.then_inc(s.heads_done, 1)
                for j in js:
                    pe.wait_ge(s.o_ready, j + 1)
                    for k in range(KT):
                        last = pe.transpose(st.ps[:, 2 * j + 1, k * S:(k + 1) * S], o_sb[:, j, k * P:(k + 1) * P], st.ident[0:S, 0:S])
                    last.then_inc(s.o_turned, 1)
                for j in js:
                    pe.wait_ge(s.oT_ready, j + 1)
                    for k in range(KT):
                        last = pe.matmul(st.ps[0:S, 2 * j, 0:D], oT[:, j, k, :], wout[:, k, :], start=(k == 0), stop=(k == KT - 1))
                    last.then_inc(s.y_ready, 1)
                for j in js:
                    turn_tensor(pe, st, s, 2 * j + 1, j)

            @block.scalar
            def _(act):
                for j in js:
                    act.wait_ge(s.h_turned, j + 1)
                    act.activation(hT[:, j], tiles(2 * j, KT), ACT.Copy).then_inc(s.hT_ready, 1)
                for j in js:
                    act.wait_ge(s.qk_ready, j + 1)
                    act.activation(qk[:, j], tiles(2 * j + 1, 2 * KT), ACT.Copy).then_inc(s.qk_done, 1)
                    act.wait_ge(s.vg_done, 2 * (j + 1))
                    act.activation(vg[:, j, D:VG], vg[:, j, D:VG], ACT.Sigmoid).then_inc(s.gates_done, 1)
                for j in js:
                    act.wait_ge(s.beta_turned, j + 1)
                    act.activation(beta_pad[0:H, j, 1:S], st.ps[0:H, 2 * j + 1, 1:S], ACT.Copy).then_inc(s.beta_done, 1)
                for j in js:
                    act.wait_ge(s.o_turned, j + 1)
                    act.activation(oT[:, j], tiles(2 * j + 1, KT), ACT.Copy).then_inc(s.oT_ready, 1)
                for j in js:
                    store_scalar(act, st, s, 2 * j + 1, st.XT[:, :, turn * TURN + j, :], j)

            @block.vector
            def _(dve):
                for j in js:
                    dve.scalar_tensor_tensor(st.resid[:, j, :], x_b(j), 1.0, x_b(j), ALU.mult, ALU.mult, accum_out=ss[:, j:j + 1]).then_inc(s.sq_ready, 1)
                for j in js:
                    dve.wait_ge(s.rms_ready, j + 1)
                    dve.scalar_tensor_tensor(st.xnew[:, j, :], x_b(j), st.vareps[:, j:j + 1], norm_w, ALU.mult, ALU.mult).then_inc(s.h_ready, 1)
                for j in js:
                    dve.wait_ge(s.vg_ready, j + 1)
                    dve.tensor_copy(vg[:, j, 0:D], st.ps[0:S, 2 * j, 0:D]).then_inc(s.vg_done, 1)
                    dve.tensor_tensor(vg[:, j, D:VG], st.ps[0:S, 2 * j, D:VG], gate_bias, ALU.add).then_inc(s.vg_done, 1)
                for j in js:
                    dve.wait_ge(s.rqk_ready, j + 1)
                    dve.tensor_tensor(rqk[:, j], tiles(2 * j, 2 * KT), wide(sin, 2 * KT), ALU.mult).then_inc(s.rope_step, 1)
                    dve.wait_ge(s.qk_done, j + 1)
                    dve.tensor_tensor(qk[:, j], qk[:, j], wide(cos, 2 * KT), ALU.mult).then_inc(s.rope_step, 1)
                    dve.wait_ge(s.rope_step, 2 * (j + 1))
                    dve.tensor_tensor(qk[:, j], qk[:, j], rqk[:, j], ALU.add).then_inc(s.rotated, 1)
                for j in js:
                    dve.wait_ge(s.f_ready, j + 1)
                    dve.wait_ge(s.entries_ready, j + 1)
                    for i in range(2):
                        dve.tensor_tensor_scan(decay[:, j, 4 * i:4 * i + 4, :].rearrange("s h t -> s (h t)"), st.ps[0:S, 2 * j + i, 0:4 * S],
                                               entries[:, j, 4 * i:4 * i + 4, :].rearrange("s h t -> s (h t)"), 0.0, ALU.mult, ALU.add).then_inc(s.decay_ready, 1)
                for j in js:
                    dve.wait_ge(s.decay_ready, 2 * (j + 1))
                    dve.wait_ge(s.scores_ready, j + 1)
                    for i in range(2):
                        part = decay[:, j, 4 * i:4 * i + 4, :]
                        dve.scalar_tensor_tensor(part, st.ps[0:S, 2 * j + i, 0:4 * S].rearrange("s (h t) -> s h t", h=4), float(HD) ** -0.5, part,
                                                 ALU.mult, ALU.mult).then_inc(s.weighed_ready, 1)
                for j in js:
                    dve.wait_ge(s.heads_done, j + 1)
                    dve.tensor_tensor(o_sb[:, j, :].rearrange("q (h d) -> q h d", d=HD), st.ps[0:S, 2 * j, 0:D].rearrange("q (h d) -> q h d", d=HD),
                                      vg[:, j, D + H:D + 2 * H].unsqueeze(2).to_broadcast([S, H, HD]), ALU.mult).then_inc(s.o_ready, 1)
                for j in js:
                    norm_sum_vector(dve, st, s, st.ps[0:S, 2 * j, 0:D], x_b(j), st.w["a6bo"][0:S, :], j)
                for j in js:
                    normalise_vector(dve, st, s, j)


def l2_xattn(nc, st, dram):
    H, C, TAPS, NT, EPS = 16, 512, 9, 3, 1e-5
    CT, W2 = C // P, H * TAPS
    w_hist = st.w["a7hw"].rearrange("p (k n) -> p k n", k=KT)
    w_c1 = st.w["a7cw1"].rearrange("p (k n) -> p k n", k=CT)
    w_k1 = st.w["a7kw1"].rearrange("p (k n) -> p k n", k=CT)
    w_k2 = st.w["a7kw2"].rearrange("p (k n) -> p k n", k=KT)
    rows = [min(KROWS, KEYS - t * KROWS) for t in range(NT)]
    with ExitStack() as ctx:
        sb = lambda n, shape, dt=F32: ctx.enter_context(nc.sbuf_tensor(f"l2x_{n}", shape, dt))
        kern = sb("kern", [P, B, W2])
        keep, mask_add = sb("keep", [S, S]), sb("mask_add", [S, S])
        with ExitStack() as ctx2:
            sb2 = lambda n, shape: ctx2.enter_context(nc.sbuf_tensor(f"l2x_{n}", shape, F32))
            ctx_cur, ccT = sb2("hist_cur", [P, TURN, KT, KEYS]), sb2("ccT", [P, CT, B])
            eh, ehT, g1T = sb2("eh", [KROWS, TURN, NT, C]), sb2("ehT", [P, TURN, CT, KEYS]), sb2("g1T", [P, TURN, KEYS])
            hstats, hmv = sb2("hstats", [KROWS, NT, TURN, 6]), sb2("hmv", [KROWS, NT, TURN, 2])
            hvar, hrstd = sb2("hvar", [KROWS, NT, TURN]), sb2("hrstd", [KROWS, NT, TURN])
            aw, awmax, awsum, awinv = sb2("aw", [1, TURN, KEYS]), sb2("awmax", [1, TURN]), sb2("awsum", [1, TURN]), sb2("awinv", [1, TURN])
            pcol = sb2("pcol", [KROWS, TURN, NT])
            hist_rows = sb2("hist_rows", [P, 3 * C])
            hb, hg, hs = (hist_rows[:, i * C:(i + 1) * C] for i in range(3))
            with stage_sems(nc, ["buffers_set", "hist_rows_loaded"]) as s, nc.Block() as block:
                @block.sync
                def _(sp):
                    sp.dma_start(hist_rows[:], dram["hist_rows"]).then_inc(s.hist_rows_loaded, 16)
                    sp.wait_ge(s.hist_rows_loaded, 16)

                @block.gpsimd
                def _(pool):
                    pool.memset(eh[:], 0.0).then_inc(s.buffers_set, 1)
                    pool.memset(hmv[:], 1.0).then_inc(s.buffers_set, 1)

            sems = ["cur_ready", "eh_ready", "eh_biased", "stats_done", "mv_done", "var_done", "hrstd_done", "eh_step", "eh_normed", "eh_done",
                    "turned_act", "turned_dve", "ehT_act", "ehT_dve", "g1_ready", "g1_done", "aw_ready", "aw_shifted", "aw_max", "aw_exp", "aw_inverse",
                    "p_row", "p_turned", "p_col", "cc_ready", "cc_done"]
            js = range(TURN)
            tiles = [(j, t) for t in range(NT) for j in js]
            with nc.Fori(0, B // TURN) as turn, stage_sems(nc, sems) as s, nc.Block() as block:
                bank = lambda j, i: 2 * j + i % 2
                part = lambda j, t: eh[0:rows[t], j, t, :]

                @block.gpsimd
                def _(pool):
                    for j in js:
                        pool.tensor_copy(ctx_cur[:, j], st.ctxT[:, turn * TURN + j, :, :]).then_inc(s.cur_ready, 1)
                    for t in range(NT):
                        pool.wait_ge(s.mv_done, TURN * (t + 1))
                        pool.tensor_scalar(hvar[:, t, :], hmv[:, t, :, 1], EPS, None, ALU.add).then_inc(s.var_done, 1)
                        pool.wait_ge(s.var_done, t + 1)
                        pool.tensor_tensor(hrstd[:, t, :], hvar[:, t, :], st.minus_half[0:KROWS, 0:1].to_broadcast([KROWS, TURN]), ALU.pow).then_inc(s.hrstd_done, 1)

                @block.tensor
                def _(pe):
                    for n, (j, t) in enumerate(tiles):
                        if t == 0:
                            pe.wait_ge(s.cur_ready, j + 1)
                        if t == 2:
                            pe.wait_ge(s.eh_biased, j + 1)
                        for k in range(KT):
                            last = pe.matmul(st.ps[0:rows[t], bank(j, t), 0:C], ctx_cur[:, j, k, t * KROWS:t * KROWS + rows[t]], w_hist[:, k, :],
                                             start=(k == 0), stop=(k == KT - 1))
                        last.then_inc(s.eh_ready, 1)
                    pe.wait_ge(s.eh_done, len(tiles))
                    for c in range(CT):
                        copied = (s.ehT_act, s.ehT_dve)[c % 2]
                        for j in js:
                            if c >= 2:
                                pe.wait_ge(copied, j + 1)
                            for t in range(NT):
                                last = pe.transpose(st.ps[:, bank(j, c), t * KROWS:t * KROWS + rows[t]], part(j, t)[:, c * P:(c + 1) * P],
                                                    st.ident[0:rows[t], 0:rows[t]])
                            last.then_inc((s.turned_act, s.turned_dve)[c % 2], 1)
                    for j in js:
                        pe.wait_ge(s.ehT_act, TURN + j + 1)
                        pe.wait_ge(s.ehT_dve, TURN + j + 1)
                        for c in range(CT):
                            last = pe.matmul(st.ps[:, bank(j, 0), 0:KEYS], w_c1[:, c, :], ehT[:, j, c, :], start=(c == 0), stop=(c == CT - 1))
                        last.then_inc(s.g1_ready, 1)
                    for j in js:
                        pe.wait_ge(s.g1_done, j + 1)
                        pe.matmul(st.ps[0:1, bank(j, 1), 0:KEYS], st.w["a7cw2"], g1T[:, j, :], start=True, stop=True).then_inc(s.aw_ready, 1)
                    for j in js:
                        pe.wait_ge(s.p_row, j + 1)
                        for t in range(NT):
                            last = pe.matmul(st.ps[0:rows[t], bank(j, 0), t:t + 1], aw[0:1, j, t * KROWS:t * KROWS + rows[t]], st.ident[0:1, 0:1], start=True, stop=True)
                        last.then_inc(s.p_turned, 1)
                    for j in js:
                        pe.wait_ge(s.p_col, NT * (j + 1))
                        for c in range(CT):
                            for t in range(NT):
                                last = pe.matmul(st.ps[:, bank(j, 1), c:c + 1], part(j, t)[:, c * P:(c + 1) * P], pcol[0:rows[t], j, t:t + 1],
                                                 start=(t == 0), stop=(t == NT - 1))
                        last.then_inc(s.cc_ready, 1)

                @block.scalar
                def _(act):
                    for n, (j, t) in enumerate(tiles):
                        act.wait_ge(s.eh_normed, n + 1)
                        act.activation(part(j, t), part(j, t), ACT.Gelu).then_inc(s.eh_done, 1)
                    for n, (c, j) in enumerate([(c, j) for c in (0, 2) for j in js]):
                        act.wait_ge(s.turned_act, n + 1)
                        act.activation(ehT[:, j, c, :], st.ps[:, bank(j, c), 0:KEYS], ACT.Copy).then_inc(s.ehT_act, 1)
                    for j in js:
                        act.wait_ge(s.g1_ready, j + 1)
                        act.activation(g1T[:, j, :], st.ps[:, bank(j, 0), 0:KEYS], ACT.Gelu, bias=st.w["a7cb1"]).then_inc(s.g1_done, 1)
                    for j in js:
                        act.wait_ge(s.aw_max, j + 1)
                        act.activation(aw[:, j, :], aw[:, j, :], ACT.Exp, bias=awmax[:, j:j + 1], accum_out=awsum[:, j:j + 1]).then_inc(s.aw_exp, 1)
                    for j in js:
                        act.wait_ge(s.cc_ready, j + 1)
                        act.activation(ccT[:, :, turn * TURN + j], st.ps[:, bank(j, 1), 0:CT], ACT.Copy).then_inc(s.cc_done, 1)

                @block.vector
                def _(dve):
                    for t in range(NT):
                        for j in js:
                            n = t * TURN + j
                            dve.wait_ge(s.eh_ready, n + 1)
                            dve.tensor_tensor(part(j, t), st.ps[0:rows[t], bank(j, t), 0:C], hb[0:rows[t], :], ALU.add).then_inc(s.eh_biased, 1)
                            dve.wait_ge(s.eh_biased, n + 1)
                            dve.bn_stats(hstats[0:rows[t], t, j, :], part(j, t)).then_inc(s.stats_done, 1)
                            dve.wait_ge(s.stats_done, n + 1)
                            dve.bn_aggr(hmv[0:rows[t], t, j, :], hstats[0:rows[t], t, j, :]).then_inc(s.mv_done, 1)
                        for j in js:
                            dve.wait_ge(s.mv_done, t * TURN + j + 1)
                            dve.scalar_tensor_tensor(part(j, t), part(j, t), hmv[0:rows[t], t, j, 0:1], hg[0:rows[t], :], ALU.subtract, ALU.mult).then_inc(s.eh_step, 1)
                        dve.wait_ge(s.hrstd_done, t + 1)
                        for j in js:
                            dve.wait_ge(s.eh_step, t * TURN + j + 1)
                            dve.scalar_tensor_tensor(part(j, t), part(j, t), hrstd[0:rows[t], t, j:j + 1], hs[0:rows[t], :], ALU.mult, ALU.add).then_inc(s.eh_normed, 1)
                    for n, (c, j) in enumerate([(c, j) for c in (1, 3) for j in js]):
                        dve.wait_ge(s.turned_dve, n + 1)
                        dve.tensor_copy(ehT[:, j, c, :], st.ps[:, bank(j, c), 0:KEYS]).then_inc(s.ehT_dve, 1)
                    for j in js:
                        dve.wait_ge(s.aw_ready, j + 1)
                        dve.tensor_scalar(aw[:, j, :], st.ps[0:1, bank(j, 1), 0:KEYS], st.w["a7cb2"][0:1, 0:1], None, ALU.add).then_inc(s.aw_shifted, 1)
                        dve.wait_ge(s.aw_shifted, j + 1)
                        dve.tensor_reduce(awmax[:, j:j + 1], aw[:, j, :], AX.X, ALU.max, negate=True).then_inc(s.aw_max, 1)
                    for j in js:
                        dve.wait_ge(s.aw_exp, j + 1)
                        dve.reciprocal(awinv[:, j:j + 1], awsum[:, j:j + 1]).then_inc(s.aw_inverse, 1)
                        dve.wait_ge(s.aw_inverse, j + 1)
                        dve.tensor_scalar(aw[:, j, :], aw[:, j, :], awinv[:, j:j + 1], None, ALU.mult).then_inc(s.p_row, 1)
                    for j in js:
                        dve.wait_ge(s.p_turned, j + 1)
                        for t in range(NT):
                            dve.tensor_copy(pcol[0:rows[t], j, t:t + 1], st.ps[0:rows[t], bank(j, 0), t:t + 1]).then_inc(s.p_col, 1)

            kp, kpT, kern8 = sb2("kp", [B, D]), sb2("kpT", [P, KT, B]), sb2("kern8", [B, H, TAPS])
            kstats, kmv, kvar, krstd = sb2("kstats", [B, 6]), sb2("kmv", [B, 2]), sb2("kvar", [B, 1]), sb2("krstd", [B, 1])
            kmax, ksum = sb2("kmax", [B, H]), sb2("ksum", [B, H])
            net_rows = sb2("net_rows", [B, 3 * D + W2])
            kb1, kg, ks = (net_rows[:, i * D:(i + 1) * D] for i in range(3))
            kb2 = net_rows[:, 3 * D:3 * D + W2]
            m_u8 = ctx2.enter_context(nc.sbuf_tensor("l2x_m_u8", [S, S], U8))
            sems = ["k1_ready", "kp_step", "kvar_done", "krstd_done", "kp_normed", "kp_done", "kp_turned", "kpT_done", "k2_ready", "kern_step",
                    "kern_exp", "kern8_done", "spread_ready", "spread_act", "mask_loaded", "rows_loaded", "keep_done"]
            with stage_sems(nc, sems) as s, nc.Block() as block:
                @block.sync
                def _(sp):
                    sp.dma_start(net_rows[:], dram["kernel_net_rows"]).then_inc(s.rows_loaded, 16)
                    sp.dma_start(m_u8[:], dram["self_mask"]).then_inc(s.mask_loaded, 16)

                @block.gpsimd
                def _(pool):
                    pool.wait_ge(s.kp_step, 3)
                    pool.tensor_scalar(kvar[:], kmv[:, 1:2], EPS, None, ALU.add).then_inc(s.kvar_done, 1)
                    pool.wait_ge(s.kvar_done, 1)
                    pool.tensor_tensor(krstd[:], kvar[:], st.minus_half[0:B, :], ALU.pow).then_inc(s.krstd_done, 1)

                @block.tensor
                def _(pe):
                    for c in range(CT):
                        last = pe.matmul(st.ps[0:B, 0, 0:D], ccT[:, c, :], w_k1[:, c, :], start=(c == 0), stop=(c == CT - 1))
                    last.then_inc(s.k1_ready, 1)
                    pe.wait_ge(s.kp_done, 1)
                    for k in range(KT):
                        last = pe.transpose(st.ps[:, 1, k * B:(k + 1) * B], kp[:, k * P:(k + 1) * P], st.ident[0:B, 0:B])
                    last.then_inc(s.kp_turned, 1)
                    pe.wait_ge(s.kpT_done, 1)
                    for k in range(KT):
                        last = pe.matmul(st.ps[0:B, 2, 0:W2], kpT[:, k, :], w_k2[:, k, :], start=(k == 0), stop=(k == KT - 1))
                    last.then_inc(s.k2_ready, 1)
                    pe.wait_ge(s.kern8_done, 1)
                    for b in range(B):
                        last = pe.matmul(st.ps[:, 3 + b // 2, (b % 2) * W2:(b % 2 + 1) * W2], st.ident[0:B, b:b + 1].to_broadcast([B, P]),
                                         kern8[:].rearrange("b h t -> b (h t)"), start=True, stop=True)
                    last.then_inc(s.spread_ready, 1)

                @block.scalar
                def _(act):
                    act.wait_ge(s.kp_normed, 1)
                    act.activation(kp[:], kp[:], ACT.Gelu).then_inc(s.kp_done, 1)
                    act.wait_ge(s.kp_turned, 1)
                    act.activation(kpT[:], st.ps[:, 1, 0:KT * B].rearrange("p (k b) -> p k b", k=KT), ACT.Copy).then_inc(s.kpT_done, 1)
                    act.wait_ge(s.kern_step, 3)
                    act.activation(kern8[:], kern8[:], ACT.Exp).then_inc(s.kern_exp, 1)
                    act.wait_ge(s.spread_ready, 1)
                    act.activation(kern[:].rearrange("p (n b) w -> p n (b w)", b=2), st.ps[:, 3:7, 0:2 * W2], ACT.Copy).then_inc(s.spread_act, 1)

                @block.vector
                def _(dve):
                    dve.wait_ge(s.rows_loaded, 16)
                    dve.wait_ge(s.k1_ready, 1)
                    dve.tensor_tensor(kp[:], st.ps[0:B, 0, 0:D], kb1, ALU.add).then_inc(s.kp_step, 1)
                    dve.wait_ge(s.kp_step, 1)
                    dve.bn_stats(kstats[:], kp[:]).then_inc(s.kp_step, 1)
                    dve.wait_ge(s.kp_step, 2)
                    dve.bn_aggr(kmv[:], kstats[:]).then_inc(s.kp_step, 1)
                    dve.wait_ge(s.kp_step, 3)
                    dve.scalar_tensor_tensor(kp[:], kp[:], kmv[:, 0:1], kg, ALU.subtract, ALU.mult).then_inc(s.kp_step, 1)
                    dve.wait_ge(s.kp_step, 4)
                    dve.wait_ge(s.krstd_done, 1)
                    dve.scalar_tensor_tensor(kp[:], kp[:], krstd[:, 0:1], ks, ALU.mult, ALU.add).then_inc(s.kp_normed, 1)
                    dve.wait_ge(s.k2_ready, 1)
                    dve.tensor_tensor(kern8[:].rearrange("b h t -> b (h t)"), st.ps[0:B, 2, 0:W2], kb2, ALU.add).then_inc(s.kern_step, 1)
                    dve.wait_ge(s.kern_step, 1)
                    dve.tensor_reduce(kmax[:], kern8[:], AX.X, ALU.max).then_inc(s.kern_step, 1)
                    dve.wait_ge(s.kern_step, 2)
                    dve.tensor_tensor(kern8[:], kern8[:], kmax[:].unsqueeze(2).to_broadcast([B, H, TAPS]), ALU.subtract).then_inc(s.kern_step, 1)
                    dve.wait_ge(s.kern_exp, 1)
                    dve.tensor_reduce(ksum[:], kern8[:], AX.X, ALU.add).then_inc(s.kern_step, 1)
                    dve.wait_ge(s.kern_step, 4)
                    dve.reciprocal(kmax[:], ksum[:]).then_inc(s.kern_step, 1)
                    dve.wait_ge(s.kern_step, 5)
                    dve.tensor_tensor(kern8[:], kern8[:], kmax[:].unsqueeze(2).to_broadcast([B, H, TAPS]), ALU.mult).then_inc(s.kern8_done, 1)
                    dve.wait_ge(s.mask_loaded, 16)
                    dve.tensor_scalar(keep[:], m_u8[:], 0, None, ALU.is_equal).then_inc(s.keep_done, 1)
                    dve.wait_ge(s.keep_done, 1)
                    dve.tensor_scalar(mask_add[:], keep[:], 1.0, -MASKED, ALU.subtract, ALU.mult).then_inc(s.keep_done, 1)

        shift = [st.shift[0:S, r:r + S] for r in range(3)]
        conv = Convolution(kern=kern, shift=shift, keep=keep[:], mask=mask_add[:])
        attention(nc, st, "l2x_a", H, 16, False, weights(st, "a7"), bias={"o": st.w["a7bo"]}, conv=conv)
def k_major(w):
    n_in, n_out = w.shape
    return w.reshape(n_in // P, P, n_out).transpose(1, 0, 2).reshape(P, -1)


def per_partition(v):
    return v.reshape(-1, P).T


def on_all(v):
    return np.broadcast_to(v.reshape(1, -1), (P, v.size))


def tables():
    out = {}
    out["ident"] = np.eye(P, dtype=np.float32)
    causal = np.triu(np.ones((S, S), bool), 1)
    out["shift"] = np.eye(P, S + 2, 1, dtype=np.float32)
    for hd in (16, 64):
        out[f"head_mask{hd}"] = (np.arange(P)[:, None] // hd == np.arange(P // hd)[None, :]).astype(np.float32)
    out["causal"] = np.concatenate([np.where(causal, MASKED, 0.0), np.zeros((P - S, S))]).astype(np.float32)
    return out


def rope_of_16():
    inv = 1.0 / (10000.0 ** (np.arange(0, 16, 2, dtype=np.float32) / np.float32(16)))
    freq = np.outer(np.arange(KEYS, dtype=np.float32), inv.astype(np.float32)).astype(np.float32)
    angle = np.concatenate([freq, freq], 1)[:, np.arange(P) % 16].T
    sign = np.where(np.arange(P) % 16 < 8, -1.0, 1.0).astype(np.float32)[:, None]
    return np.cos(angle).astype(np.float32), (np.sin(angle) * sign).astype(np.float32)


def swap_halves(w, heads):
    return w.reshape(D, heads, 2, D // heads // 2)[:, :, ::-1].reshape(D, D)


def rope_of_32():
    half = np.arange(P) % 16
    inv = (np.float32(1.0) / np.power(np.float32(10000.0), np.arange(16, dtype=np.float32) / np.float32(16))).astype(np.float32)
    angle = (np.arange(S, dtype=np.float32)[None, :] * inv[half][:, None]).astype(np.float32)
    sign = np.where(np.arange(P) % 32 < 16, -1.0, 1.0).astype(np.float32)[:, None]
    return np.cos(angle), np.sin(angle) * sign


def position_table():
    pos = np.arange(-(S - 1), S, dtype=np.float32)
    inv = (1.0 / np.power(np.float32(10000.0), np.arange(0, D, 2, dtype=np.float32) / np.float32(D))).astype(np.float32)
    ang = (pos[:, None] * inv[None, :]).astype(np.float32)
    return np.stack([np.sin(ang).T, np.cos(ang).T], 1).astype(np.float32).reshape(P, -1)


def rows_on_partitions(*parts):
    rows = np.concatenate(parts)
    return np.concatenate([rows, np.zeros((P - len(rows), rows.shape[1]), rows.dtype)])


def tile_rows(w):
    return np.concatenate([w[..., :P, :], w[..., P:, :]], -1)


def expert_units(a):
    keys, values = a["L1_ffn_keys"], a["L1_ffn_values"]
    first = tile_rows(np.concatenate([keys[0::2], keys[1::2]], -1))
    second = np.concatenate([values[0::2], values[1::2]], -1)
    l1 = np.concatenate([first, second], -1)

    f = 256
    sw, sb, sm = a["L2_ffn_s_fc1_w"], a["L2_ffn_s_fc1_b"], a["L2_ffn_s_geglu_mult"]
    parts = [np.concatenate([sw[c:c + f], sw[2 * f + c:2 * f + c + f]]) for c in (0, f)]
    w1 = np.concatenate([a["L2_ffn_fc1_w"], np.stack(parts)]).transpose(0, 2, 1)
    b1 = np.concatenate([a["L2_ffn_fc1_b"], np.stack([np.concatenate([sb[c:c + f], sb[2 * f + c:2 * f + c + f]]) for c in (0, f)])])
    mult = np.concatenate([a["L2_ffn_geglu_mult"], np.stack([sm[:f], sm[f:]])])
    w2 = np.concatenate([a["L2_ffn_fc2_w"], np.stack([a["L2_ffn_s_fc2_w"][:, :f], a["L2_ffn_s_fc2_w"][:, f:]])]).transpose(0, 2, 1)
    cols = lambda v: v.reshape(len(v), -1, P).transpose(0, 2, 1)
    l2 = np.concatenate([tile_rows(w1), tile_rows(w2), cols(b1), cols(mult)], -1)

    w1 = np.concatenate([a["L3_ffn_W1_s"], a["L3_ffn_W1_r"]])
    b1 = np.concatenate([a["L3_ffn_b1_s"], a["L3_ffn_b1_r"]])
    w2 = np.concatenate([a["L3_ffn_W2_s"], a["L3_ffn_W2_r"]])
    w1 = w1.reshape(10, D, 4, 256).transpose(0, 2, 1, 3).reshape(40, D, 256)
    l3 = np.concatenate([tile_rows(w1), tile_rows(w2.reshape(40, 256, D)), cols(b1.reshape(40, 256))], -1)
    return {"l1_ffn_units": l1, "l2_ffn_units": l2, "l3_ffn_units": l3}


def pack_plan():
    T = lambda n: (lambda a: k_major(a[n].T))
    N = lambda n: (lambda a: k_major(a[n]))
    col = lambda n: (lambda a: per_partition(a[n]))
    row = lambda n: (lambda a: on_all(a[n]))
    plan = [[] for _ in range(12)]
    plan[0] = [("a0q", 512, T("L0_attn_Wq")), ("a0k", 512, T("L0_attn_Wk")),
               ("a0v", 512, T("L0_attn_Wv")), ("a0o", 512, T("L0_attn_Wo"))]
    plan[1] = [("a1q", 512, T("L0_xattn_Wq")), ("a1k", 512, T("L0_xattn_Wk")),
               ("a1v", 512, T("L0_xattn_Wv")), ("a1o", 512, T("L0_xattn_Wp")),
               ("a1bq", 2, col("L0_xattn_bq")),
               ("a1bk", 2, col("L0_xattn_bk")), ("a1bv", 256, row("L0_xattn_bv")), ("a1bo", 256, row("L0_xattn_bp"))]
    plan[2] = [("f2w", 512, N("L0_ffn_weight")), ("f2g", 256, row("L0_ffn_ln_gamma")), ("f2b", 256, row("L0_ffn_ln_beta"))]
    plan[3] = [("m_in", 2048, T("L1_attn_w_in")), ("m_conv", 16, lambda a: a["L1_attn_w_conv"].reshape(4, P, 4).transpose(1, 0, 2).reshape(P, 16)),
               ("m_xproj", 384, T("L1_attn_w_xproj")),
               ("m_dt", 512, lambda a: np.concatenate([a["L1_attn_w_dt"].T, np.zeros((64, 512), np.float32)])),
               ("m_bdt", 4, col("L1_attn_b_dt")),
               ("m_alog", 64, lambda a: a["L1_attn_A_log"].reshape(4, P, 16).transpose(1, 0, 2).reshape(P, 64)),
               ("m_d", 4, col("L1_attn_D")), ("m_out", 1024, T("L1_attn_w_out"))]
    plan[4] = [("a4q", 2048, N("L1_xattn_Wq")), ("a4k", 2048, N("L1_xattn_Wk")), ("a4v", 2048, N("L1_xattn_Wv")),
               ("a4o", 2048, N("L1_xattn_Wo")), ("a4bq", 8, col("L1_xattn_bq")), ("a4bk", 8, col("L1_xattn_bk")),
               ("a4bv", 1024, row("L1_xattn_bv")), ("a4bo", 256, row("L1_xattn_bo"))]
    plan[5] = [("f5q", 512, N("L1_ffn_wq")), ("f5k", 512, N("L1_ffn_wk")), ("f5v", 512, N("L1_ffn_wv")),
               ("f5o", 512, N("L1_ffn_wo")), ("f5p", 512, N("L1_ffn_wp")), ("f5pe", 2 * (2 * S - 1), lambda a: position_table()),
               ("f5g1", 256, row("L1_ffn_ln1_g")), ("f5s1", 256, row("L1_ffn_ln1_b")), ("f5g2", 256, row("L1_ffn_ln2_g")),
               ("f5s2", 256, row("L1_ffn_ln2_b")), ("f5sel", 64, N("L1_ffn_sel_w"))]
    plan[6] = [("a6q", 512, T("L2_attn_Wq")), ("a6k", 512, T("L2_attn_Wk")), ("a6o", 512, T("L2_attn_Wout")),
               ("a6rq", 512, lambda a: k_major(swap_halves(a["L2_attn_Wq"].T, 8))), ("a6rk", 512, lambda a: k_major(swap_halves(a["L2_attn_Wk"].T, 8))),
               ("a6vg", 560, lambda a: k_major(np.concatenate([a[f"L2_attn_W{n}"] for n in ("v", "ig", "og", "beta")]).T)),
               ("a6bgates", 24, lambda a: on_all(np.concatenate([a[f"L2_attn_b{n}"] for n in ("ig", "og", "beta")]))),
               ("a6norm", 256, row("L2_attn_norm_w")), ("a6bo", 256, row("L2_attn_bout")),
               ("a6cos", S, lambda a: rope_of_32()[0]), ("a6sin", S, lambda a: rope_of_32()[1]),
               ("a6heads", P // 32, lambda a: (np.arange(P)[:, None] // 32 == np.arange(P // 32)[None, :]).astype(np.float32))]
    plan[7] = [("a7q", 512, N("L2_xattn_Wq")), ("a7k", 512, N("L2_xattn_Wk")), ("a7v", 512, N("L2_xattn_Wv")),
               ("a7o", 512, N("L2_xattn_proj_W")), ("a7bo", 256, row("L2_xattn_proj_b")), ("a7hw", 1024, N("L2_xattn_hist_W")),
               ("a7cw1", 512, N("L2_xattn_ctx_W1")), ("a7cb1", 1, col("L2_xattn_ctx_b1")), ("a7cw2", 1, N("L2_xattn_ctx_W2")),
               ("a7cb2", 1, row("L2_xattn_ctx_b2")), ("a7kw1", 1024, N("L2_xattn_kg_W1")), ("a7kw2", 288, N("L2_xattn_kg_W2"))]
    plan[8] = [("f8gate", 30, T("L2_ffn_gate_w")),
               ("f8b2", 256, lambda a: rows_on_partitions(a["L2_ffn_fc2_b"], a["L2_ffn_s_fc2_b"][None]))]
    plan[11] = [("f11gate", 16, N("L3_ffn_centroids")), ("f11gs", 2, col("L3_ffn_g_shared")), ("f11gr", 2, col("L3_ffn_g_routed")),
                ("f11b2", 256, lambda a: rows_on_partitions(a["L3_ffn_b2_s"], a["L3_ffn_b2_r"]))]
    plan[9] = [("a9q", 512, N("L3_attn_wqk")), ("a9o", 512, N("L3_attn_wov"))]
    plan[10] = [("a10q", 512, T("L3_xattn_W_q")), ("a10k", 512, T("L3_xattn_W_k")),
                ("a10v", 512, T("L3_xattn_W_v")), ("a10o", 512, T("L3_xattn_W_o")),
                ("a10cos", KEYS, lambda a: rope_of_16()[0]), ("a10sin", KEYS, lambda a: rope_of_16()[1]), ("a10rq", 512, lambda a: k_major(swap_halves(a["L3_xattn_W_q"].T, 16))), ("a10rk", 512, lambda a: k_major(swap_halves(a["L3_xattn_W_k"].T, 16)))]
    return plan


TABLES = [("ident", P), ("causal", S), ("shift", S + 2), ("head_mask16", P // 16), ("head_mask64", P // 64)]


def lay_out(a):
    out = {
        "x_tokens": a["x"].transpose(1, 0, 2),
        "x_features": a["x"].reshape(B, S, KT, P).transpose(3, 2, 0, 1),
        "ctx_features": a["ctx_1024"].reshape(B, KEYS, KT, P).transpose(3, 0, 2, 1),
        "key_mask": a["mask_Bx1xSxS2_ik0"].reshape(B, S, KEYS),
        "self_mask": a["mask_SxS_bc0"],
    }
    out["kernel_net_rows"] = on_all(np.concatenate([a["L2_xattn_kg_b1"], a["L2_xattn_kg_ln_g"], a["L2_xattn_kg_ln_b"], a["L2_xattn_kg_b2"]]))[0:B]
    out["hist_rows"] = on_all(np.concatenate([a["L2_xattn_hist_b"], a["L2_xattn_hist_ln_g"], a["L2_xattn_hist_ln_b"]]))
    out.update(expert_units(a))
    made = tables()
    out["tables"] = np.concatenate([made[n] for n, _ in TABLES], 1)
    for i, parts in enumerate(pack_plan()):
        if parts:
            made = [np.broadcast_to(f(a), (P, n)) for _, n, f in parts]
            out[f"pack{i}"] = np.concatenate(made, 1)
    return {k: np.ascontiguousarray(v) for k, v in out.items()}


def program(nc, dram, out, stages):
    plan = pack_plan()
    st = State()
    with ExitStack() as ctx:
        def sb(n, shape, dt=F32):
            return ctx.enter_context(nc.sbuf_tensor(n, shape, dt))

        st.X = sb("X", [S, B, D])
        st.XT = sb("XT", [P, KT, B, S])
        st.ctxT = sb("ctxT", [P, B, KT, KEYS])
        st.ps = ctx.enter_context(nc.psum_tensor("ps", [P, 8, BANK], F32))
        st.resid, st.xnew = sb("resid", [S, TURN, D]), sb("xnew", [S, TURN, D])
        st.stats, st.meanvar = sb("stats", [S, TURN, 6]), sb("meanvar", [S, TURN, 2])
        st.vareps, st.rstd = sb("vareps", [S, TURN]), sb("rstd", [S, TURN])
        st.minus_half = sb("minus_half", [P, 1])
        st.tables = sb("tables_sb", [P, sum(n for _, n in TABLES)])
        ends = np.cumsum([n for _, n in TABLES])
        st.ident, st.causal, st.shift, heads16, heads64 = (st.tables[:, int(end) - n:int(end)] for (_, n), end in zip(TABLES, ends))
        st.head_mask = {16: heads16, 64: heads64}
        st.w = {}
        size = [max([sum(n for _, n, _ in plan[i]) for i in stages if i % 2 == r] + [1]) for r in range(2)]
        region = [sb(f"weights{r}", [P, size[r]]) for r in range(2)]
        packs = {}
        for i in stages:
            at = 0
            for n, c, _ in plan[i]:
                st.w[n] = region[i % 2][:, at:at + c]
                at += c
            packs[i] = region[i % 2][:, 0:at]
        start_loaded = ctx.enter_context(nc.semaphore("start_loaded"))
        half_set = ctx.enter_context(nc.semaphore("half_set"))
        pack_loaded = {i: ctx.enter_context(nc.semaphore(f"pack{i}_loaded")) for i in packs}
        x_out = ctx.enter_context(nc.semaphore("x_out"))

        with nc.Block() as block:
            @block.sync
            def _(sp):
                sp.dma_start(st.X[:], dram["x_tokens"]).then_inc(start_loaded, 16)
                sp.dma_start(st.XT[:], dram["x_features"]).then_inc(start_loaded, 16)
                sp.dma_start(st.tables[:], dram["tables"]).then_inc(start_loaded, 16)
                sp.dma_start(packs[stages[0]], dram[f"pack{stages[0]}"]).then_inc(pack_loaded[stages[0]], 16)
                sp.dma_start(st.ctxT[:], dram["ctx_features"]).then_inc(start_loaded, 16)
                sp.wait_ge(start_loaded, 64)

            @block.gpsimd
            def _(pool):
                pool.memset(st.minus_half[:], -0.5).then_inc(half_set, 1)

        for n, i in enumerate(stages):
            with nc.Block() as block:
                @block.sync
                def _(sp, n=n, i=i):
                    if n + 1 < len(stages):
                        nxt = stages[n + 1]
                        sp.dma_start(packs[nxt], dram[f"pack{nxt}"]).then_inc(pack_loaded[nxt], 16)
                    sp.wait_ge(pack_loaded[i], 16)
            STAGES[i](nc, st, dram)

        with nc.Block() as block:
            @block.sync
            def _(sp):
                sp.dma_start(out.rearrange("b t d -> t b d"), st.X[:]).then_inc(x_out, 16)
                sp.wait_ge(x_out, 16)


def weights(st, prefix):
    view = lambda n: st.w[prefix + n].rearrange("p (k n) -> p k n", k=KT) if prefix + n in st.w else None
    return Attention(q=view("q"), k=view("k"), v=view("v"), o=st.w[prefix + "o"].rearrange("p (m n) -> p m n", n=D))


def l0_attn(nc, st, dram):
    attention(nc, st, "l0a", 16, 16, False, weights(st, "a0"), mask=st.causal[0:S, :])


def l0_xattn(nc, st, dram):
    bias = scaled_query_bias(nc, st, "a1", 0.25)
    attention(nc, st, "l0x", 16, 16, True, weights(st, "a1"), bias=bias, plus_one=True)


def l1_xattn(nc, st, dram):
    bias = scaled_query_bias(nc, st, "a4", 0.125)
    attention(nc, st, "l1x", 16, 64, True, weights(st, "a4"), bias=bias)


def l3_xattn(nc, st, dram):
    view = lambda n: st.w[n].rearrange("p (k n) -> p k n", k=KT)
    rope = Rotation(cos=st.w["a10cos"], sin=st.w["a10sin"], q=view("a10rq"), k=view("a10rk"))
    attention(nc, st, "l3x", 16, 16, True, weights(st, "a10"), mask_dram=dram["key_mask"], rope=rope)


def scaled_query_bias(nc, st, prefix, scale):
    bq = st.w[prefix + "bq"]
    with stage_sems(nc, ["bias_scaled"]) as s, nc.Block() as block:
        @block.vector
        def _(dve):
            dve.tensor_scalar(bq, bq, scale, None, ALU.mult).then_inc(s.bias_scaled, 1)
    return {"q": bq, "k": st.w[prefix + "bk"], "v": st.w[prefix + "bv"], "o": st.w[prefix + "bo"]}


def l3_attn(nc, st, dram):
    attention(nc, st, "l3a", 1, 256, False, weights(st, "a9"), mask=st.causal[0:S, :])


STAGES = {0: l0_attn, 1: l0_xattn, 2: l0_ffn, 3: l1_attn, 4: l1_xattn, 5: l1_ffn, 6: l2_attn, 7: l2_xattn, 8: l2_ffn, 9: l3_attn, 10: l3_xattn, 11: l3_ffn}


def build(nc, arrays, stages=range(12)):
    dram = {n: nc.dram_tensor(n, v.shape, mybir.dt.from_np(v.dtype), kind="ExternalInput").ap() for n, v in arrays.items()}
    out = nc.dram_tensor("out_0_dram", (B, S, D), F32, kind="ExternalOutput").ap()
    program(nc, dram, out, list(stages))


def kernel(**inputs):
    import concourse.bacc as bacc
    from concourse.bass_utils import run_bass_kernel_spmd

    arrays = lay_out({k: np.asarray(v) for k, v in inputs.items()})
    nc = bacc.Bacc("TRN2", target_bir_lowering=False, num_devices=1)
    build(nc, arrays)
    return run_bass_kernel_spmd(nc, [arrays], core_ids=[0]).results[0]["out_0_dram"]
```

```python
from collections import namedtuple
from contextlib import ExitStack, contextmanager

import numpy as np

import concourse.bass as bass
import concourse.mybir as mybir

F32 = mybir.dt.float32
F32R = mybir.dt.float32r
I32 = mybir.dt.int32
U8 = mybir.dt.uint8
ALU = mybir.AluOpType
ACT = mybir.ActivationFunctionType
AX = mybir.AxisListType

B, S, D = 8, 100, 256
KEYS = 361
P = 128
KT = D // P
TOK = B * S
KROWS = 121
BANK = 512
MASKED = -1.0e30
TURN_LAG = 2
TURN = 4


class State:
    pass


Attention = namedtuple("Attention", "q k v o")
Rotation = namedtuple("Rotation", "cos sin q k")
InnerNorm = namedtuple("InnerNorm", "gain shift turned")
Convolution = namedtuple("Convolution", "kern shift keep mask")


@contextmanager
def stage_sems(nc, names):
    with ExitStack() as ctx:
        handles = {n: ctx.enter_context(nc.semaphore(n)) for n in names}
        yield namedtuple("Semaphores", handles)(**handles)
        for h in handles.values():
            nc.gpsimd.sem_clear(h)
        nc.all_engine_barrier()


NORM_SEMS = ["y_ready", "resid_ready", "stats_ready", "meanvar_ready", "vareps_ready", "rstd_ready",
             "xnew_ready", "xnew_turned", "x_stored", "affine_step"]


def norm_sum_vector(dve, st, s, y, x_b, bias, j=0):
    steps = 1 if bias is None else 2
    dve.wait_ge(s.y_ready, j + 1)
    dve.tensor_tensor(st.resid[:, j, :], y, x_b, ALU.add).then_inc(s.resid_ready, 1)
    if bias is not None:
        dve.wait_ge(s.resid_ready, j * steps + 1)
        dve.tensor_tensor(st.resid[:, j, :], st.resid[:, j, :], bias, ALU.add).then_inc(s.resid_ready, 1)
    dve.wait_ge(s.resid_ready, (j + 1) * steps)
    norm_stats_vector(dve, st, s, j)


def norm_stats_vector(dve, st, s, j=0):
    dve.bn_stats(st.stats[:, j, :], st.resid[:, j, :]).then_inc(s.stats_ready, 1)
    dve.wait_ge(s.stats_ready, j + 1)
    dve.bn_aggr(st.meanvar[:, j, :], st.stats[:, j, :]).then_inc(s.meanvar_ready, 1)


def normalise_vector(dve, st, s, j=0, gain=None, shift=None):
    out = st.xnew[:, j, :]
    dve.wait_ge(s.rstd_ready, j + 1)
    step = dve.tensor_scalar(out, st.resid[:, j, :], st.meanvar[:, j, 0:1], st.rstd[:, j:j + 1], ALU.subtract, ALU.mult)
    if gain is None:
        step.then_inc(s.xnew_ready, 1)
        return
    step.then_inc(s.affine_step, 1)
    dve.wait_ge(s.affine_step, 2 * j + 1)
    dve.tensor_tensor(out, out, gain, ALU.mult).then_inc(s.affine_step, 1)
    dve.wait_ge(s.affine_step, 2 * j + 2)
    dve.tensor_tensor(out, out, shift, ALU.add).then_inc(s.xnew_ready, 1)


def rstd_pool(pool, st, s, j=0, eps=1e-5):
    pool.wait_ge(s.meanvar_ready, j + 1)
    pool.tensor_scalar(st.vareps[:, j:j + 1], st.meanvar[:, j, 1:2], eps, None, ALU.add).then_inc(s.vareps_ready, 1)
    pool.wait_ge(s.vareps_ready, j + 1)
    pool.tensor_tensor(st.rstd[:, j:j + 1], st.vareps[:, j:j + 1], st.minus_half[0:S, 0:1], ALU.pow).then_inc(s.rstd_ready, 1)


def store_pool(pool, st, s, x_b, j=0):
    pool.wait_ge(s.xnew_ready, j + 1)
    pool.tensor_copy(x_b, st.xnew[:, j, :]).then_inc(s.x_stored, 1)


def turn_tensor(pe, st, s, bank, j=0):
    pe.wait_ge(s.xnew_ready, j + 1)
    for k in range(KT):
        last = pe.transpose(st.ps[:, bank, k * S:(k + 1) * S], st.xnew[:, j, k * P:(k + 1) * P], st.ident[0:S, 0:S])
    last.then_inc(s.xnew_turned, 1)


def store_scalar(act, st, s, bank, xt_b, j=0):
    act.wait_ge(s.xnew_turned, j + 1)
    act.activation(xt_b, st.ps[:, bank, 0:KT * S].rearrange("p (k t) -> p k t", k=KT), ACT.Copy)


def attention(nc, st, name, heads, hd, cross, w, bias=None, plus_one=False, mask=None, mask_dram=None,
              rope=None, xT=None, inner=None, bd=None, conv=None):
    nk = KEYS if cross else S
    krows, ktiles = (KROWS, 3) if cross else (S, 1)
    nkp = krows * ktiles
    width = heads * hd
    nf = width // P
    own = w.k is None
    scale = float(hd) ** -0.5 if hd < 256 else 1.0
    pg = min(heads, 1 if cross else 4)
    groups = heads // pg
    steps = groups * TURN
    lag = 2 if conv else 0
    turn_lag, value_lag = lag + TURN_LAG, lag + TURN_LAG + 1
    n_probs = TURN_LAG + 1
    hpt = max(1, P // hd)
    bias = bias or {}
    masked = mask is not None or mask_dram is not None or bd is not None or conv is not None
    xT = st.XT if xT is None else xT
    head_mask = st.head_mask[hd] if hpt > 1 else None
    o_banks = max(1, width // BANK)
    s_banks = 4 if conv else 4 - o_banks
    t_banks = 6 - o_banks - s_banks
    s_bank = lambda n: n % s_banks
    t_bank = lambda n: s_banks + n % t_banks
    o_bank = 6 - o_banks

    qper, vw = min(nf, 4), min(width, BANK)
    q_parts = [m for m in range(0, nf, qper)]
    v_parts = [(t, c) for t in range(ktiles) for c in range(0, width, vw)]
    parts = [("q", m) for m in q_parts] + ([("rq", 0)] if rope else [])
    if not own:
        for m in range(nf):
            parts += [("k", m)] + ([("rk", m)] if rope else [])
        parts += [("v", p) for p in v_parts]
    o_parts = [m for m in range(0, nf, 4)]
    table = {n: [] for n in range(-1, steps + value_lag + 6)}
    for j in range(TURN):
        done = (j + 1) * groups + value_lag - 1
        table[done] += [("o", j, None)]
        table[done + 1] += [("turn_o", j, m) for m in o_parts]
        table[done + 2] += [("y", j, None)]
        table[done + 4] += [("norm", j, None)]
        table[done + 5] += [("turn_x", j, None)]
        for i, (kind, part) in enumerate(parts):
            table[-1 if j == 0 else (j - 1) * groups + i * (groups - 1) // len(parts)].append((kind, j, part))
    through = [x for n in sorted(table) for x in table[n] if x[0] not in ("o", "norm")]
    place = {x: c for c, x in enumerate(through)}
    side_bank = lambda x: 6 + place[x] % 2

    with ExitStack() as ctx:
        def sb(n, shape, dt=F32):
            return ctx.enter_context(nc.sbuf_tensor(f"{name}_{n}", shape, dt))

        q_sb = sb("q_sb", [P, 2, nf, S])
        q_pad = sb("q_pad", [P, 2, heads, S]) if hpt > 1 else None
        kT = sb("kT", [P, 2, nf, nk]) if not own else None
        nv = TURN if width <= D else 2
        vals = sb("vals", [krows, nv, ktiles, width])
        probs = sb("probs", [S, n_probs, pg, nkp])
        probsT = sb("probsT", [krows, 2, pg * ktiles * S])
        nmax, rsum, rinv = sb("nmax", [S, TURN, heads]), sb("rsum", [S, TURN, heads]), sb("rinv", [S, TURN, heads])
        o_sb, oT = sb("o_sb", [S, 2, width]), sb("oT", [P, 2, nf, S])
        xcur = sb("xcur", [P, TURN, KT, S])
        ctx_cur = sb("ctx_cur", [P, TURN, KT, KEYS]) if cross else None
        s_sb = sb("s_sb", [S, 2, pg, nk]) if masked else None
        bd_cur = sb("bd_cur", [S, 2, heads, S]) if bd is not None else None
        sm = sb("sm", [S, 3, pg, S + 2]) if conv else None
        rowsum = sb("rowsum", [S, 3, 3, pg, S]) if conv else None
        product = sb("product", [S, 3, S]) if conv else None
        kern_cur = sb("kern_cur", [S, TURN, heads * 9]) if conv else None
        mask_i = sb("mask_i", [S, 2, KEYS], I32) if mask_dram is not None else None
        mask_b = sb("mask_b", [S, 2, KEYS]) if mask_dram is not None else None
        rq_sb = sb("rq_sb", [P, 2, nf, S]) if rope else None
        rk_sb = sb("rk_sb", [P, 2, nf, nk]) if rope else None

        with stage_sems(nc, ["buffers_cleared"]) as s, nc.Block() as block:
            @block.gpsimd
            def _(pool):
                pool.memset(probs[:], 0.0).then_inc(s.buffers_cleared, 1)
                pool.memset(vals[:], 0.0).then_inc(s.buffers_cleared, 1)
                if conv:
                    pool.memset(sm[:], 0.0).then_inc(s.buffers_cleared, 1)

        sems = ["xcur_ready", "ctx_ready", "kern_ready", "side_ready", "side_copied0", "side_copied1", "q_rotated", "k_rotated", "rope_step",
                "q_spread", "scores_ready", "masked_ready", "max_ready", "exp_done", "probs_turned", "probsT_ready", "values_done",
                "rsum_ready", "rinv_ready", "o_ready", "mask_loaded", "mask_ready", "bd_loaded", "first_tap", "tap_done", "sm_ready",
                "pool_tap", "rows_dve", "summed", "x_summed", "bias_added"]
        with nc.Fori(0, B // TURN) as turn, stage_sems(nc, sems + NORM_SEMS) as s, nc.Block() as block:
            batch = lambda j: turn * TURN + j
            side_copied = [s.side_copied0, s.side_copied1]

            def wait_copied(eng, items):
                for bank in (0, 1):
                    n = max([place[x] // 2 + 1 for x in items if place[x] % 2 == bank], default=0)
                    if n:
                        eng.wait_ge(side_copied[bank], n)

            def copied_by(x):
                kind = x[0]
                if kind in ("q", "v"):
                    return "dve" if kind in bias else "act"
                return "dve" if kind == "y" else "act"

            def items(kind, j):
                return [x for x in through if x[0] == kind and x[1] == j]

            def heads_of(g):
                return range(g * pg, (g + 1) * pg)

            def score_tile(n):
                return st.ps[0:S, s_bank(n), 0:pg * nk].rearrange("q (h k) -> q h k", h=pg)

            def copy_probs(eng, n):
                eng.wait_ge(s.probs_turned, n + 1)
                if n >= 2:
                    eng.wait_ge(s.values_done, n - 1)
                out, ps = probsT[:, n % 2, :], st.ps[0:krows, t_bank(n), 0:pg * ktiles * S]
                step = eng.activation(out, ps, ACT.Copy) if conv else eng.tensor_copy(out, ps)
                step.then_inc(s.probsT_ready, 1)

            def x_b(j):
                return st.X[:, batch(j), :]

            @block.sync
            def _(sp):
                for j in range(TURN):
                    if mask_dram is not None:
                        if j >= 2:
                            sp.wait_ge(s.mask_ready, j - 1)
                        sp.dma_start(mask_i[:, j % 2, :], mask_dram[batch(j)]).then_inc(s.mask_loaded, 16)
                        sp.wait_ge(s.mask_loaded, 16 * (j + 1))
                    if bd is not None:
                        if j >= 2:
                            sp.wait_ge(s.masked_ready, (j - 1) * groups)
                        sp.dma_start(bd_cur[:, j % 2], bd(batch(j))).then_inc(s.bd_loaded, 16)
                        sp.wait_ge(s.bd_loaded, 16 * (j + 1))

            @block.gpsimd
            def _(pool):
                def tokens(j):
                    pool.tensor_copy(xcur[:, j], xT[:, :, batch(j), :]).then_inc(s.xcur_ready, 1)
                    if cross:
                        pool.tensor_copy(ctx_cur[:, j], st.ctxT[:, batch(j), :, :]).then_inc(s.ctx_ready, 1)
                    if own:
                        pool.tensor_copy(vals[:, j % nv, 0, :], x_b(j)).then_inc(s.ctx_ready, 1)
                    if "o" in bias:
                        pool.tensor_tensor(st.resid[:, j, :], x_b(j), bias["o"][0:S, :], ALU.add).then_inc(s.bias_added, 1)
                    if conv:
                        pool.tensor_copy(kern_cur[:, j], conv.kern[0:S, batch(j), :]).then_inc(s.kern_ready, 1)

                def rotate(to, other, n, steps_in_front, done):
                    wide = lambda t: t[:, 0:n].unsqueeze(1).to_broadcast([P, nf, n])
                    pool.tensor_tensor(to, to, wide(rope.cos), ALU.mult).then_inc(s.rope_step, 1)
                    pool.tensor_tensor(other, other, wide(rope.sin), ALU.mult).then_inc(s.rope_step, 1)
                    pool.wait_ge(s.rope_step, steps_in_front + 2)
                    pool.tensor_tensor(to, to, other, ALU.add).then_inc(done, 1)

                def spread(j):
                    wait_copied(pool, items("q", j) + items("rq", j))
                    if rope:
                        rotate(q_sb[:, j % 2], rq_sb[:, j % 2], S, 4 * j, s.q_rotated)
                        pool.wait_ge(s.q_rotated, j + 1)
                    for m in range(nf if hpt > 1 else 0):
                        pool.tensor_tensor(q_pad[:, j % 2, m * hpt:(m + 1) * hpt, :], q_sb[:, j % 2, m, :].unsqueeze(1).to_broadcast([P, hpt, S]),
                                           head_mask.unsqueeze(2).to_broadcast([P, hpt, S]), ALU.mult).then_inc(s.q_spread, 1)

                def pool_taps(n):
                    j, g = divmod(n, groups)
                    i = pg - 1
                    taps = kern_cur[:, j, (g * pg + i) * 9:(g * pg + i + 1) * 9].rearrange("q (r c) -> q r c", c=3)
                    pool.wait_ge(s.first_tap, (n + 1) * pg * 3)
                    for c in (1, 2):
                        out = rowsum[:, n % 3, :, i, :]
                        if n > 0 or c == 2:
                            pool.wait_ge(s.pool_tap, 4 * n + 2 * c - 2)
                        pool.tensor_tensor(product[:], sm[:, n % 3, i, c:c + S].unsqueeze(1).to_broadcast([S, 3, S]),
                                           taps[:, :, c].unsqueeze(2).to_broadcast([S, 3, S]), ALU.mult).then_inc(s.pool_tap, 1)
                        pool.wait_ge(s.pool_tap, 4 * n + 2 * c - 1)
                        pool.tensor_tensor(out, out, product[:], ALU.add).then_inc(s.pool_tap, 1)

                for n in sorted(table):
                    if n == -1:
                        tokens(0)
                    if conv and 0 <= n - 1 < steps:
                        pool_taps(n - 1)
                    if n > 0 and n % groups == 0 and n // groups + 1 < TURN:
                        tokens(n // groups + 1)
                    for x in table[n]:
                        kind, j, part = x
                        if x == (items("rq", j) or items("q", j))[-1]:
                            spread(j)
                        if rope and x == items("rk", j)[-1]:
                            wait_copied(pool, items("k", j) + items("rk", j))
                            rotate(kT[:, j % 2], rk_sb[:, j % 2], nk, 4 * j + 2, s.k_rotated)
                        if kind == "y":
                            rstd_pool(pool, st, s, j)
                            if inner:
                                pool.tensor_tensor(x_b(j), st.resid[:, j, :], x_b(j), ALU.add).then_inc(s.x_summed, 1)
                        if kind == "norm" and not inner:
                            store_pool(pool, st, s, x_b(j), j)
                    if n == -1:
                        tokens(1)

            @block.tensor
            def _(pe):
                def issue(x):
                    kind, j, part = x
                    c, bank = place[x], side_bank(x)
                    if c >= 2:
                        pe.wait_ge(side_copied[c % 2], c // 2)
                    if kind in ("q", "rq"):
                        pe.wait_ge(s.xcur_ready, j + 1)
                        for i, m in enumerate(range(part, part + qper)):
                            for k in range(KT):
                                last = pe.matmul(st.ps[:, bank, i * S:(i + 1) * S], (w.q if kind == "q" else rope.q)[:, k, m * P:(m + 1) * P],
                                                 xcur[:, j, k, :], start=(k == 0), stop=(k == KT - 1))
                    elif kind in ("k", "rk"):
                        if cross:
                            pe.wait_ge(s.ctx_ready, j + 1)
                        src = ctx_cur if cross else xcur
                        for k in range(KT):
                            last = pe.matmul(st.ps[:, bank, 0:nk], (w.k if kind == "k" else rope.k)[:, k, part * P:(part + 1) * P],
                                             src[:, j, k, :], start=(k == 0), stop=(k == KT - 1))
                    elif kind == "v":
                        t, col = part
                        rows = min(krows, nk - t * krows)
                        src = ctx_cur if cross else xcur
                        for k in range(KT):
                            last = pe.matmul(st.ps[0:rows, bank, 0:vw], src[:, j, k, t * krows:t * krows + rows], w.v[:, k, col:col + vw],
                                             start=(k == 0), stop=(k == KT - 1))
                    elif kind == "turn_o":
                        pe.wait_ge(s.o_ready, j + 1)
                        for m in range(part, min(part + 4, nf)):
                            last = pe.transpose(st.ps[:, bank, (m - part) * S:(m - part + 1) * S], o_sb[:, j % 2, m * P:(m + 1) * P], st.ident[0:S, 0:S])
                    elif kind == "y":
                        wait_copied(pe, items("turn_o", j))
                        for m in range(nf):
                            last = pe.matmul(st.ps[0:S, bank, 0:D], oT[:, j % 2, m, :], w.o[:, m, :], start=(m == 0), stop=(m == nf - 1))
                    elif kind == "turn_x":
                        pe.wait_ge(s.xnew_ready, j + 1)
                        for k in range(KT):
                            last = pe.transpose(st.ps[:, bank, k * S:(k + 1) * S], st.xnew[:, j, k * P:(k + 1) * P], st.ident[0:S, 0:S])
                    last.then_inc(s.side_ready, 1)

                def scores(n):
                    j, g = divmod(n, groups)
                    if g * pg % hpt == 0:
                        m = g * pg // hpt
                        if hpt > 1:
                            pe.wait_ge(s.q_spread, j * nf + m + 1)
                        else:
                            wait_copied(pe, items("q", j))
                        if rope:
                            pe.wait_ge(s.k_rotated, j + 1)
                        elif not own:
                            wait_copied(pe, [("k", j, m)])
                    again = n - s_banks
                    if again >= 0:
                        if masked:
                            pe.wait_ge(s.masked_ready, again + 1)
                        else:
                            pe.wait_ge(s.exp_done, (again + 1) * pg)
                    for i, h in enumerate(heads_of(g)):
                        tiles = [h // hpt] if hpt > 1 else range(nf)
                        for m in tiles:
                            q = q_pad[:, j % 2, h, :] if hpt > 1 else q_sb[:, j % 2, m, :]
                            last = pe.matmul(score_tile(n)[:, i, :], q, xcur[:, j, m, :] if own else kT[:, j % 2, m, :],
                                             start=(m == tiles[0]), stop=(m == tiles[-1]))
                    last.then_inc(s.scores_ready, 1)

                def sum_rows(n):
                    pe.wait_ge(s.rows_dve, (n + 1) * 3 * (pg - 1))
                    pe.wait_ge(s.pool_tap, (n + 1) * 4)
                    for r in range(3):
                        last = pe.matmul(st.ps[0:S, s_bank(n), 0:pg * S], conv.shift[r], rowsum[:, n % 3, r].rearrange("q h k -> q (h k)"),
                                         start=(r == 0), stop=(r == 2))
                    last.then_inc(s.summed, 1)

                def turn_probs(n):
                    pe.wait_ge(s.exp_done, (n + 1) * pg)
                    if n >= t_banks:
                        pe.wait_ge(s.probsT_ready, n + 1 - t_banks)
                    for i in range(pg):
                        for t in range(ktiles):
                            c = (i * ktiles + t) * S
                            last = pe.transpose(st.ps[0:krows, t_bank(n), c:c + S], probs[:, n % n_probs, i, t * krows:(t + 1) * krows], st.ident[0:S, 0:S])
                    last.then_inc(s.probs_turned, 1)

                def values(n):
                    j, g = divmod(n, groups)
                    pe.wait_ge(s.probsT_ready, n + 1)
                    if g == 0:
                        if own:
                            pe.wait_ge(s.ctx_ready, j + 1)
                        else:
                            wait_copied(pe, items("v", j))
                        if j >= 1:
                            pe.wait_ge(s.o_ready, j)
                    for i, h in enumerate(heads_of(g)):
                        out = st.ps[0:S, o_bank + h * hd // BANK, h * hd % BANK:h * hd % BANK + hd]
                        for t in range(ktiles):
                            c = (i * ktiles + t) * S
                            last = pe.matmul(out, probsT[:, n % 2, c:c + S], vals[:, j % nv, t, h * hd:(h + 1) * hd],
                                             start=(t == 0), stop=(t == ktiles - 1))
                    last.then_inc(s.values_done, 1)

                for n in sorted(table):
                    if n == 0 or not conv and 0 < n < steps:
                        scores(n)
                    if 0 <= n - turn_lag < steps:
                        turn_probs(n - turn_lag)
                    if 0 <= n - value_lag < steps:
                        values(n - value_lag)
                    if conv and 0 <= n < steps - 1:
                        scores(n + 1)
                    if conv and 0 <= n - 2 < steps:
                        sum_rows(n - 2)
                    for x in table[n]:
                        if x in place:
                            issue(x)

            @block.scalar
            def _(act):
                def copy_out(x):
                    kind, j, part = x
                    bank = side_bank(x)
                    act.wait_ge(s.side_ready, place[x] + 1)
                    tiles = lambda n: st.ps[:, bank, 0:n * S].rearrange("p (m t) -> p m t", m=n)
                    if kind in ("q", "rq"):
                        if j >= 2 and hpt > 1:
                            act.wait_ge(s.q_spread, (j - 1) * nf)
                        step = act.activation((q_sb if kind == "q" else rq_sb)[:, j % 2, part:part + qper, :], tiles(qper), ACT.Copy, scale=scale)
                    elif kind in ("k", "rk"):
                        to = (kT if kind == "k" else rk_sb)[:, j % 2, part, :]
                        if rope and j >= 2:
                            act.wait_ge(s.k_rotated, j - 1)
                        if "k" in bias:
                            step = act.activation(to, st.ps[:, bank, 0:nk], ACT.Identity, bias=bias["k"][:, part:part + 1])
                        else:
                            step = act.activation(to, st.ps[:, bank, 0:nk], ACT.Copy)
                    elif kind == "v":
                        t, col = part
                        rows = min(krows, nk - t * krows)
                        step = act.activation(vals[0:rows, j % nv, t, col:col + vw], st.ps[0:rows, bank, 0:vw], ACT.Copy)
                    elif kind == "turn_o":
                        n = min(4, nf - part)
                        step = act.activation(oT[:, j % 2, part:part + n, :], tiles(n), ACT.Copy)
                    elif kind == "turn_x":
                        step = act.activation(inner.turned[:, :, batch(j), :] if inner else st.XT[:, :, batch(j), :], tiles(KT), ACT.Copy)
                    step.then_inc(side_copied[place[x] % 2], 1)

                def first_taps(n):
                    j, g = divmod(n, groups)
                    act.wait_ge(s.sm_ready, n + 1)
                    if g == 0:
                        act.wait_ge(s.kern_ready, j + 1)
                    if n >= 3:
                        act.wait_ge(s.summed, n - 2)
                    for i, h in enumerate(heads_of(g)):
                        for r in range(3):
                            act.activation(rowsum[:, n % 3, r, i, :], sm[:, n % 3, i, 0:S], ACT.Copy,
                                           scale=kern_cur[:, j, h * 9 + 3 * r:h * 9 + 3 * r + 1]).then_inc(s.first_tap, 1)

                def exponentials(n):
                    j, g = divmod(n, groups)
                    act.wait_ge(s.max_ready, n + 1)
                    if n >= n_probs:
                        act.wait_ge(s.probs_turned, n + 1 - n_probs)
                    for i, h in enumerate(heads_of(g)):
                        scr = s_sb[:, n % 2, i, :] if masked else score_tile(n)[:, i, :]
                        act.activation(probs[:, n % n_probs, i, 0:nk], scr, ACT.Exp, bias=nmax[:, j, h:h + 1],
                                       accum_out=rsum[:, j, h:h + 1]).then_inc(s.exp_done, 1)

                for n in sorted(table):
                    if conv and 0 <= n < steps:
                        first_taps(n)
                    if conv and 0 <= n - turn_lag < steps:
                        copy_probs(act, n - turn_lag)
                    if 0 <= n - lag < steps:
                        exponentials(n - lag)
                    for x in table[n]:
                        if x in place and copied_by(x) == "act":
                            copy_out(x)

            @block.vector
            def _(dve):
                def copy_out(x):
                    kind, j, part = x
                    bank = side_bank(x)
                    dve.wait_ge(s.side_ready, place[x] + 1)
                    copied = side_copied[place[x] % 2]
                    if kind == "q":
                        if j >= 2 and hpt > 1:
                            dve.wait_ge(s.q_spread, (j - 1) * nf)
                        dve.scalar_tensor_tensor(q_sb[:, j % 2, part:part + qper, :], st.ps[:, bank, 0:qper * S].rearrange("p (m t) -> p m t", m=qper),
                                                 scale, bias["q"][:, part:part + qper].unsqueeze(2).to_broadcast([P, qper, S]),
                                                 ALU.mult, ALU.add).then_inc(copied, 1)
                    elif kind == "v":
                        t, col = part
                        rows = min(krows, nk - t * krows)
                        dve.tensor_tensor(vals[0:rows, j % nv, t, col:col + vw], st.ps[0:rows, bank, 0:vw], bias["v"][0:rows, col:col + vw],
                                          ALU.add).then_inc(copied, 1)
                    else:
                        resid = st.resid[:, j, :]
                        if "o" in bias:
                            dve.wait_ge(s.bias_added, j + 1)
                        dve.tensor_tensor(resid, st.ps[0:S, bank, 0:D], resid if "o" in bias else x_b(j), ALU.add).then_inc(copied, 1)
                        dve.wait_ge(copied, place[x] // 2 + 1)
                        norm_stats_vector(dve, st, s, j)

                def convolve(n):
                    j, g = divmod(n, groups)
                    dve.wait_ge(s.first_tap, n * pg * 3 + (pg - 1) * 3)
                    mine = pg - 1
                    for tap in (1, 2):
                        for i in range(mine):
                            h = g * pg + i
                            for r in range(3):
                                wt = kern_cur[:, j, h * 9 + 3 * r + tap:h * 9 + 3 * r + tap + 1]
                                acc = rowsum[:, n % 3, r, i, :]
                                if tap == 2:
                                    dve.wait_ge(s.tap_done, (n * mine + i) * 3 + r + 1)
                                dve.scalar_tensor_tensor(acc, sm[:, n % 3, i, tap:tap + S], wt, acc, ALU.mult, ALU.add).then_inc(
                                    s.tap_done if tap == 1 else s.rows_dve, 1)

                def mask_scores(n):
                    dve.wait_ge(s.scores_ready, n + 1)
                    if n >= 3:
                        dve.wait_ge(s.rows_dve, (n - 2) * 3 * (pg - 1))
                        dve.wait_ge(s.pool_tap, (n - 2) * 4)
                    dve.tensor_tensor(sm[:, n % 3, :, 1:S + 1], score_tile(n), conv.keep.unsqueeze(1).to_broadcast([S, pg, S]),
                                      ALU.mult).then_inc(s.sm_ready, 1)

                def maxima(n):
                    j, g = divmod(n, groups)
                    if conv:
                        dve.wait_ge(s.summed, n + 1)
                    else:
                        dve.wait_ge(s.scores_ready, n + 1)
                    rows = score_tile(n)
                    if masked:
                        if n >= 2:
                            dve.wait_ge(s.exp_done, (n - 1) * pg)
                        if bd is not None:
                            if g == 0:
                                dve.wait_ge(s.bd_loaded, 16 * (j + 1))
                            m = bd_cur[:, j % 2, g * pg:(g + 1) * pg, :]
                        else:
                            m = conv.mask if conv else mask if mask is not None else mask_b[:, j % 2, :]
                            m = m.unsqueeze(1).to_broadcast([S, pg, nk])
                        if mask_dram is not None and g == 0:
                            dve.wait_ge(s.mask_loaded, 16 * (j + 1))
                            dve.tensor_scalar(mask_b[:, j % 2, :], mask_i[:, j % 2, :], 0, MASKED, ALU.is_equal, ALU.mult).then_inc(s.mask_ready, 1)
                            dve.wait_ge(s.mask_ready, j + 1)
                        dve.tensor_tensor(s_sb[:, n % 2], rows, m, ALU.add).then_inc(s.masked_ready, 1)
                        dve.wait_ge(s.masked_ready, n + 1)
                        rows = s_sb[:, n % 2]
                    dve.tensor_reduce(nmax[:, j, g * pg:(g + 1) * pg], rows, AX.X, ALU.max, negate=True).then_inc(s.max_ready, 1)

                def outputs(j):
                    sums = rsum[:, j, :]
                    dve.wait_ge(s.exp_done, (j + 1) * heads)
                    if plus_one:
                        dve.tensor_scalar(sums, sums, 1.0, None, ALU.add).then_inc(s.rsum_ready, 1)
                        dve.wait_ge(s.rsum_ready, j + 1)
                    dve.reciprocal(rinv[:, j, :], sums).then_inc(s.rinv_ready, 1)
                    dve.wait_ge(s.rinv_ready, j + 1)
                    dve.wait_ge(s.values_done, (j + 1) * groups)
                    hb = heads // o_banks
                    for i in range(o_banks):
                        last = dve.tensor_tensor(o_sb[:, j % 2, i * hb * hd:(i + 1) * hb * hd].rearrange("q (h d) -> q h d", d=hd),
                                                 st.ps[0:S, o_bank + i, 0:hb * hd].rearrange("q (h d) -> q h d", d=hd),
                                                 rinv[:, j, i * hb:(i + 1) * hb].unsqueeze(2).to_broadcast([S, hb, hd]), ALU.mult)
                    last.then_inc(s.o_ready, 1)

                for n in sorted(table):
                    if conv and 0 <= n < steps:
                        mask_scores(n)
                    if not conv and 0 <= n < steps:
                        maxima(n)
                    if not conv and 0 <= n - turn_lag < steps:
                        copy_probs(dve, n - turn_lag)
                    if conv and 0 <= n - 1 < steps:
                        convolve(n - 1)
                    if conv and 0 <= n - lag < steps:
                        maxima(n - lag)
                    for x in table[n]:
                        if x[0] == "o":
                            outputs(x[1])
                        elif x[0] == "norm":
                            normalise_vector(dve, st, s, x[1], *((inner.gain, inner.shift) if inner else ()))
                        elif copied_by(x) == "dve":
                            copy_out(x)


def l0_ffn(nc, st, dram):
    QB, EPS, LN_EPS = 128.0, 1e-5, 1e-3
    ROUND = 12582912.0
    wt = st.w["f2w"]
    with ExitStack() as ctx:
        def sb(n, shape, dt=F32):
            return ctx.enter_context(nc.sbuf_tensor(f"l0f_{n}", shape, dt))

        xq = sb("xq", [S, B, D])
        stats, mv = sb("stats", [S, B, 6]), sb("mv", [S, B, 2])
        vareps, rstd = sb("vareps", [S, B]), sb("rstd", [S, B])
        wabs, beta = sb("wabs", [P, 1]), sb("beta", [P, 4])
        ones = sb("ones", [P, P])
        absmax, gmax = sb("absmax", [S, 1]), sb("gmax", [S, 4])
        xq_cur, xqT = sb("xq_cur", [S, TURN, D]), sb("xqT", [P, TURN, KT, S])

        with stage_sems(nc, ["ones_set", "wabs_ready", "wsum_ready", "beta_step", "stats_done", "mv_done",
                             "vareps_done", "rstd_done", "norm_done", "affine_done", "absmax_ready", "gmax_ready",
                             "g_step", "xq_done", "wq_step"]) as s, nc.Block() as block:
            @block.gpsimd
            def _(pool):
                pool.memset(ones[:], 1.0).then_inc(s.ones_set, 1)
                pool.wait_ge(s.mv_done, B)
                pool.tensor_scalar(vareps[:], mv[:, :, 1], LN_EPS, None, ALU.add).then_inc(s.vareps_done, 1)
                pool.wait_ge(s.vareps_done, 1)
                pool.tensor_tensor(rstd[:], vareps[:], st.minus_half[0:S, :].to_broadcast([S, B]), ALU.pow).then_inc(s.rstd_done, 1)
                pool.wait_ge(s.absmax_ready, 1)
                pool.partition_all_reduce(gmax[:, 0:1], absmax[:], S, bass.bass_isa.ReduceOp.max).then_inc(s.gmax_ready, 1)

            @block.tensor
            def _(pe):
                pe.wait_ge(s.ones_set, 1)
                pe.wait_ge(s.wabs_ready, 1)
                pe.matmul(st.ps[:, 0, 0:1], ones[:], wabs[:], start=True, stop=True).then_inc(s.wsum_ready, 1)

            @block.vector
            def _(dve):
                dve.tensor_reduce(wabs[:], wt, AX.X, ALU.add, apply_absolute_value=True).then_inc(s.wabs_ready, 1)
                for b in range(B):
                    dve.bn_stats(stats[:, b, :], st.X[:, b, :]).then_inc(s.stats_done, 1)
                for b in range(B):
                    dve.wait_ge(s.stats_done, b + 1)
                    dve.bn_aggr(mv[:, b, :], stats[:, b, :]).then_inc(s.mv_done, 1)
                dve.wait_ge(s.wsum_ready, 1)
                dve.tensor_scalar(beta[:, 0:1], st.ps[:, 0, 0:1], 1.0 / (D * D), None, ALU.mult).then_inc(s.beta_step, 1)
                dve.wait_ge(s.beta_step, 1)
                dve.tensor_scalar(beta[:, 1:2], beta[:, 0:1], EPS, None, ALU.add).then_inc(s.beta_step, 1)
                dve.wait_ge(s.beta_step, 2)
                dve.reciprocal(beta[:, 2:3], beta[:, 1:2]).then_inc(s.beta_step, 1)
                dve.wait_ge(s.beta_step, 3)
                dve.tensor_scalar(wt, wt, beta[:, 2:3], 1.0, ALU.mult, ALU.min).then_inc(s.wq_step, 1)
                dve.wait_ge(s.wq_step, 1)
                dve.tensor_scalar(wt, wt, -1.0, ROUND, ALU.max, ALU.add).then_inc(s.wq_step, 1)
                dve.wait_ge(s.wq_step, 2)
                dve.tensor_scalar(wt, wt, ROUND, None, ALU.subtract).then_inc(s.wq_step, 1)
                dve.wait_ge(s.rstd_done, 1)
                for b in range(B):
                    dve.tensor_scalar(xq[:, b, :], st.X[:, b, :], mv[:, b, 0:1], rstd[:, b:b + 1],
                                      ALU.subtract, ALU.mult).then_inc(s.norm_done, 1)
                dve.wait_ge(s.norm_done, B)
                dve.tensor_tensor(xq[:], xq[:], st.w["f2g"][0:S, :].unsqueeze(1).to_broadcast([S, B, D]), ALU.mult).then_inc(s.affine_done, 1)
                dve.wait_ge(s.affine_done, 1)
                dve.tensor_tensor(xq[:], xq[:], st.w["f2b"][0:S, :].unsqueeze(1).to_broadcast([S, B, D]), ALU.add).then_inc(s.affine_done, 1)
                dve.wait_ge(s.affine_done, 2)
                dve.tensor_reduce(absmax[:], xq[:], AX.XY, ALU.max, apply_absolute_value=True).then_inc(s.absmax_ready, 1)
                dve.wait_ge(s.gmax_ready, 1)
                dve.reciprocal(gmax[:, 1:2], gmax[:, 0:1]).then_inc(s.g_step, 1)
                dve.tensor_scalar(gmax[:, 3:4], gmax[:, 0:1], beta[0:S, 0:1], 1.0 / QB, ALU.mult, ALU.mult).then_inc(s.g_step, 1)
                dve.wait_ge(s.g_step, 2)
                dve.tensor_scalar(gmax[:, 2:3], gmax[:, 1:2], QB, None, ALU.mult).then_inc(s.g_step, 1)
                dve.wait_ge(s.g_step, 3)
                dve.tensor_scalar(xq[:], xq[:], gmax[:, 2:3], QB - EPS, ALU.mult, ALU.min).then_inc(s.xq_done, 1)
                dve.wait_ge(s.xq_done, 1)
                dve.tensor_scalar(xq[:], xq[:], -QB + EPS, None, ALU.max).then_inc(s.xq_done, 1)

        with nc.Fori(0, B // TURN) as turn, stage_sems(nc, ["cur_ready", "cur_turned", "curT_ready"] + NORM_SEMS) as s, nc.Block() as block:
            x_b = lambda j: st.X[:, turn * TURN + j, :]

            @block.gpsimd
            def _(pool):
                for j in range(TURN):
                    pool.tensor_copy(xq_cur[:, j, :], xq[:, turn * TURN + j, :]).then_inc(s.cur_ready, 1)
                for j in range(TURN):
                    rstd_pool(pool, st, s, j)
                for j in range(TURN):
                    store_pool(pool, st, s, x_b(j), j)

            @block.tensor
            def _(pe):
                for j in range(TURN):
                    pe.wait_ge(s.cur_ready, j + 1)
                    for k in range(KT):
                        last = pe.transpose(st.ps[:, 2 * j, k * S:(k + 1) * S], xq_cur[:, j, k * P:(k + 1) * P], st.ident[0:S, 0:S])
                    last.then_inc(s.cur_turned, 1)
                for j in range(TURN):
                    pe.wait_ge(s.curT_ready, j + 1)
                    for k in range(KT):
                        last = pe.matmul(st.ps[0:S, 2 * j + 1, 0:D], xqT[:, j, k, :], wt[:, k * D:(k + 1) * D], start=(k == 0), stop=(k == KT - 1))
                    last.then_inc(s.y_ready, 1)
                for j in range(TURN):
                    turn_tensor(pe, st, s, 2 * j, j)

            @block.scalar
            def _(act):
                for j in range(TURN):
                    act.wait_ge(s.cur_turned, j + 1)
                    act.activation(xqT[:, j], st.ps[:, 2 * j, 0:KT * S].rearrange("p (k t) -> p k t", k=KT), ACT.Copy).then_inc(s.curT_ready, 1)
                for j in range(TURN):
                    store_scalar(act, st, s, 2 * j, st.XT[:, :, turn * TURN + j, :], j)

            @block.vector
            def _(dve):
                for j in range(TURN):
                    dve.wait_ge(s.y_ready, j + 1)
                    dve.scalar_tensor_tensor(st.resid[:, j, :], st.ps[0:S, 2 * j + 1, 0:D], gmax[:, 3:4], x_b(j),
                                             ALU.mult, ALU.add).then_inc(s.resid_ready, 1)
                    dve.wait_ge(s.resid_ready, j + 1)
                    norm_stats_vector(dve, st, s, j)
                for j in range(TURN):
                    normalise_vector(dve, st, s, j)


def l1_attn(nc, st, dram):
    DIN, NS, R, TAPS = 512, 16, 64, 4
    M = DIN // P
    HALF = TOK // 2
    pad = TAPS - 1
    w_in = st.w["m_in"].rearrange("p (k n) -> p k n", k=KT)
    w_xp = st.w["m_xproj"].rearrange("p (k n) -> p k n", k=M)
    w_out = st.w["m_out"].rearrange("p (k n) -> p k n", k=M)
    w_conv = st.w["m_conv"].rearrange("p (m j) -> p m j", m=M)
    a_log = st.w["m_alog"].rearrange("p (m n) -> p m n", m=M)
    XTf = st.XT[:].rearrange("p k b t -> p k (b t)")
    with ExitStack() as ctx:
        def sb(n, shape, dt=F32):
            return ctx.enter_context(nc.sbuf_tensor(f"l1a_{n}", shape, dt))

        hs = sb("hs", [P, M, TOK])
        gate = sb("gate", [P, M, TOK])
        xdbl = sb("xdbl", [R + 2 * NS, TOK])
        delta = sb("delta", [P, M, TOK])

        with ExitStack() as ctx2:
            def sb2(n, shape, dt=F32):
                return ctx2.enter_context(nc.sbuf_tensor(f"l1a_{n}", shape, dt))

            hpad = sb2("hpad", [P, M, B, pad + S])
            vraw, ev, lg = (sb2(n, [P, M, TOK]) for n in ("vraw", "ev", "lg"))
            er = sb2("er", [P, M, TOK])
            with stage_sems(nc, ["hpad_zero", "proj_ready", "hs_raw", "gate_done", "conv_step", "hs_done", "xdbl_ready",
                                 "xdbl_done", "dt_ready", "v_done", "abs_done", "exp_done", "log_done", "sp_step",
                                 "delta_done", "a_done", "a_negative"]) as s, nc.Block() as block:
                @block.gpsimd
                def _(pool):
                    pool.memset(hpad[:], 0.0).then_inc(s.hpad_zero, 1)
                    pool.wait_ge(s.a_done, 1)
                    pool.tensor_scalar(st.w["m_alog"], st.w["m_alog"], -1.0, None, ALU.mult).then_inc(s.a_negative, 1)

                @block.tensor
                def _(pe):
                    for m in range(2 * M):
                        if m >= 4:
                            pe.wait_ge(s.hs_raw, m - 3)
                        for j in range(2):
                            for k in range(KT):
                                last = pe.matmul(st.ps[:, 2 * (m % 4) + j, 0:HALF], w_in[:, k, m * P:(m + 1) * P],
                                                 XTf[:, k, j * HALF:(j + 1) * HALF], start=(k == 0), stop=(k == KT - 1))
                        last.then_inc(s.proj_ready, 1)
                    pe.wait_ge(s.hs_raw, M)
                    pe.wait_ge(s.gate_done, 1)
                    pe.wait_ge(s.hs_done, M)
                    for j in range(2):
                        for k in range(M):
                            last = pe.matmul(st.ps[0:R + 2 * NS, j, 0:HALF], w_xp[:, k, :], hs[:, k, j * HALF:(j + 1) * HALF],
                                             start=(k == 0), stop=(k == M - 1))
                    last.then_inc(s.xdbl_ready, 1)
                    pe.wait_ge(s.xdbl_done, 1)
                    for m in range(M):
                        if m >= 2:
                            pe.wait_ge(s.v_done, m - 1)
                        else:
                            pe.wait_ge(s.gate_done, M)
                        for j in range(2):
                            last = pe.matmul(st.ps[:, 4 + 2 * (m % 2) + j, 0:HALF], st.w["m_dt"][0:R + 2 * NS, m * P:(m + 1) * P],
                                             xdbl[:, j * HALF:(j + 1) * HALF], start=True, stop=True)
                        last.then_inc(s.dt_ready, 1)

                @block.scalar
                def _(act):
                    act.wait_ge(s.hpad_zero, 1)
                    for m in range(2 * M):
                        act.wait_ge(s.proj_ready, m + 1)
                        for j in range(2):
                            ps = st.ps[:, 2 * (m % 4) + j, 0:HALF]
                            if m < M:
                                last = act.activation(hpad[:, m, j * B // 2:(j + 1) * B // 2, pad:],
                                                      ps.rearrange("p (b t) -> p b t", t=S), ACT.Copy)
                            else:
                                last = act.activation(gate[:, m - M, j * HALF:(j + 1) * HALF], ps, ACT.Silu)
                        last.then_inc(s.hs_raw if m < M else s.gate_done, 1)
                    for m in range(M):
                        act.wait_ge(s.conv_step, TAPS * (m + 1))
                        act.activation(hs[:, m, :], hs[:, m, :], ACT.Silu).then_inc(s.hs_done, 1)
                    act.wait_ge(s.xdbl_ready, 1)
                    act.activation(xdbl[:].rearrange("p (j t) -> p j t", j=2), st.ps[0:R + 2 * NS, 0:2, 0:HALF], ACT.Copy).then_inc(s.xdbl_done, 1)
                    act.activation(st.w["m_alog"], st.w["m_alog"], ACT.Exp).then_inc(s.a_done, 1)
                    for m in range(M):
                        act.wait_ge(s.dt_ready, m + 1)
                        ps = st.ps[:, 4 + 2 * (m % 2):6 + 2 * (m % 2), 0:HALF]
                        by_bank = lambda t: t[:, m, :].rearrange("p (j t) -> p j t", j=2)
                        act.activation(by_bank(ev), ps, ACT.Abs, bias=st.w["m_bdt"][:, m:m + 1]).then_inc(s.abs_done, 1)
                        act.activation(by_bank(vraw), ps, ACT.Identity, bias=st.w["m_bdt"][:, m:m + 1]).then_inc(s.v_done, 1)
                    for m in range(M):
                        act.wait_ge(s.abs_done, m + 1)
                        act.activation(ev[:, m, :], ev[:, m, :], ACT.Exp, scale=-1.0).then_inc(s.exp_done, 1)
                    for m in range(M):
                        act.wait_ge(s.exp_done, m + 1)
                        act.activation(lg[:, m, :], ev[:, m, :], ACT.Ln, bias=1.0).then_inc(s.log_done, 1)

                @block.vector
                def _(dve):
                    for m in range(M):
                        dve.wait_ge(s.hs_raw, m + 1)
                        acc = hs[:, m, :].rearrange("p (b t) -> p b t", t=S)
                        dve.tensor_scalar(acc, hpad[:, m, :, 0:S], w_conv[:, m, 0:1], None, ALU.mult).then_inc(s.conv_step, 1)
                        for j in range(1, TAPS):
                            dve.wait_ge(s.conv_step, TAPS * m + j)
                            dve.scalar_tensor_tensor(acc, hpad[:, m, :, j:j + S], w_conv[:, m, j:j + 1], acc,
                                                     ALU.mult, ALU.add).then_inc(s.conv_step, 1)
                    for m in range(M):
                        rest = er[:, m, :]
                        dve.wait_ge(s.exp_done, m + 1)
                        dve.tensor_scalar(rest, ev[:, m, :], 1.0, 1.0, ALU.add, ALU.subtract).then_inc(s.sp_step, 1)
                        dve.wait_ge(s.sp_step, 3 * m + 1)
                        dve.tensor_tensor(rest, ev[:, m, :], rest, ALU.subtract).then_inc(s.sp_step, 1)
                        dve.wait_ge(s.sp_step, 3 * m + 2)
                        dve.wait_ge(s.v_done, m + 1)
                        dve.scalar_tensor_tensor(rest, vraw[:, m, :], 0.0, rest, ALU.max, ALU.add).then_inc(s.sp_step, 1)
                    for m in range(M):
                        dve.wait_ge(s.sp_step, 3 * m + 3)
                        dve.wait_ge(s.log_done, m + 1)
                        dve.tensor_tensor(delta[:, m, :], lg[:, m, :], er[:, m, :], ALU.add).then_inc(s.delta_done, 1)

        halves = lambda t: t[:].rearrange("p m (j t) -> p m j t", j=2)
        hs_h, gate_h, delta_h = halves(hs), halves(gate), halves(delta)
        xdbl_h = xdbl[:].rearrange("p (j t) -> p j t", j=2)
        with ExitStack() as ctx2:
            def sb2(n, shape):
                return ctx2.enter_context(nc.sbuf_tensor(f"l1a_{n}", shape, F32))

            BUFS = 4
            bcs = sb2("bcs", [P, 4, HALF])
            da, dbx = sb2("da", [P, BUFS, HALF]), sb2("dbx", [P, BUFS, HALF])
            z = sb2("z", [P, BUFS, HALF])
            dx = sb2("dx", [P, M, HALF])
            steps = M * NS
            with nc.Fori(0, 2) as j, stage_sems(nc, ["bc_ready", "bc_copied", "dx_ready", "da_ready", "da_reset", "dbx_ready", "scan_done",
                                                     "zc_ready", "sum_done", "skip_done", "tile_done"]) as s, nc.Block() as block:
                @block.gpsimd
                def _(pool):
                    for n in range(steps):
                        i, m = divmod(n, M)
                        if i == 0:
                            pool.tensor_tensor(dx[:, m, :], delta_h[:, m, j, :], hs_h[:, m, j, :], ALU.mult).then_inc(s.dx_ready, 1)
                            pool.wait_ge(s.dx_ready, m + 1)
                        if m == 0:
                            pool.wait_ge(s.bc_copied, 2 * i + 1)
                        if n >= BUFS:
                            pool.wait_ge(s.scan_done, n - BUFS + 1)
                        pool.tensor_tensor(dbx[:, n % BUFS, :], dx[:, m, :], bcs[:, 2 * i % 4, :], ALU.mult).then_inc(s.dbx_ready, 1)

                @block.scalar
                def _(act):
                    def copy_row(c):
                        i = c // 2
                        act.wait_ge(s.bc_ready, c + 1)
                        if i >= 2:
                            act.wait_ge(s.dbx_ready if c % 2 == 0 else s.zc_ready, (i - 1) * M)
                        act.activation(bcs[:, c % 4, :], st.ps[:, 4 + c % 4, 0:HALF], ACT.Copy).then_inc(s.bc_copied, 1)

                    copy_row(0)
                    copy_row(1)
                    for n in range(steps):
                        i, m = divmod(n, M)
                        if i + 1 < NS and m in (1, 3):
                            copy_row(2 * (i + 1) + m // 2)
                        if n >= BUFS:
                            act.wait_ge(s.scan_done, n - BUFS + 1)
                        act.activation(da[:, n % BUFS, :], delta_h[:, m, j, :], ACT.Exp, scale=a_log[:, m, i:i + 1]).then_inc(s.da_ready, 1)
                        act.wait_ge(s.da_ready, n + 1)
                        act.mul(da[:, n % BUFS, 0:HALF:S], da[:, n % BUFS, 0:HALF:S], 0.0).then_inc(s.da_reset, 1)

                @block.vector
                def _(dve):
                    def times_c(n):
                        i, m = divmod(n, M)
                        if m == 0:
                            dve.wait_ge(s.bc_copied, 2 * i + 2)
                        dve.wait_ge(s.scan_done, n + 1)
                        dve.tensor_tensor(z[:, n % BUFS, :], z[:, n % BUFS, :], bcs[:, (2 * i + 1) % 4, :], ALU.mult).then_inc(s.zc_ready, 1)

                    for n in range(steps):
                        dve.wait_ge(s.da_reset, n + 1)
                        dve.wait_ge(s.dbx_ready, n + 1)
                        if n >= BUFS:
                            dve.wait_ge(s.sum_done, n - BUFS + 1)
                        dve.tensor_tensor_scan(z[:, n % BUFS, :], da[:, n % BUFS, :], dbx[:, n % BUFS, :], 0.0, ALU.mult, ALU.add).then_inc(s.scan_done, 1)
                        if n >= 1:
                            times_c(n - 1)
                    times_c(steps - 1)
                    for m in range(M):
                        tile = gate_h[:, m, j, :]
                        dve.wait_ge(s.sum_done, steps - M + m + 1)
                        dve.scalar_tensor_tensor(hs_h[:, m, j, :], hs_h[:, m, j, :], st.w["m_d"][:, m:m + 1], st.ps[:, m, 0:HALF],
                                                 ALU.mult, ALU.add).then_inc(s.skip_done, 1)
                        dve.wait_ge(s.skip_done, m + 1)
                        dve.tensor_tensor(tile, hs_h[:, m, j, :], tile, ALU.mult).then_inc(s.tile_done, 1)

                @block.tensor
                def _(pe):
                    def spread(i):
                        for c in (2 * i, 2 * i + 1):
                            if c >= 4:
                                pe.wait_ge(s.bc_copied, c - 3)
                            row = R + c % 2 * NS + i
                            pe.matmul(st.ps[:, 4 + c % 4, 0:HALF], st.ident[0:R + 2 * NS, row:row + 1].to_broadcast([R + 2 * NS, P]),
                                      xdbl_h[:, j, :], start=True, stop=True).then_inc(s.bc_ready, 1)

                    spread(0)
                    spread(1)
                    for n in range(steps):
                        i, m = divmod(n, M)
                        if m == 0 and i + 2 < NS:
                            spread(i + 2)
                        pe.wait_ge(s.zc_ready, n + 1)
                        pe.matmul(st.ps[:, m, 0:HALF], st.ident, z[:, n % BUFS, :],
                                  start=(i == 0), stop=(i == NS - 1)).then_inc(s.sum_done, 1)

        y_cur = sb("y_cur", [P, TURN, M, S])
        with nc.Fori(0, B // TURN) as turn, stage_sems(nc, ["cur_ready"] + NORM_SEMS) as s, nc.Block() as block:
            x_b = lambda j: st.X[:, turn * TURN + j, :]

            @block.gpsimd
            def _(pool):
                for j in range(TURN):
                    pool.tensor_copy(y_cur[:, j], gate[:].rearrange("p m (b t) -> p m b t", b=B)[:, :, turn * TURN + j, :]).then_inc(s.cur_ready, 1)
                for j in range(TURN):
                    rstd_pool(pool, st, s, j)
                for j in range(TURN):
                    store_pool(pool, st, s, x_b(j), j)

            @block.tensor
            def _(pe):
                for j in range(TURN):
                    pe.wait_ge(s.cur_ready, j + 1)
                    for k in range(M):
                        last = pe.matmul(st.ps[0:S, j, 0:D], y_cur[:, j, k, :], w_out[:, k, :], start=(k == 0), stop=(k == M - 1))
                    last.then_inc(s.y_ready, 1)
                for j in range(TURN):
                    turn_tensor(pe, st, s, TURN + j, j)

            @block.scalar
            def _(act):
                for j in range(TURN):
                    store_scalar(act, st, s, TURN + j, st.XT[:, :, turn * TURN + j, :], j)

            @block.vector
            def _(dve):
                for j in range(TURN):
                    norm_sum_vector(dve, st, s, st.ps[0:S, j, 0:D], x_b(j), None, j)
                for j in range(TURN):
                    normalise_vector(dve, st, s, j)


GATE_SEMS = ["logits_ready", "score_ready", "score_step", "top_ready", "picked_ready", "left_ready", "gate_step",
             "gate_ready", "gate_turned", "gateT_stored"]


class Gate:

    def __init__(self, nc, ctx, name, experts, top, ones_in_front, ones_behind, turns_per_gate=1):
        def sb(n, shape):
            return ctx.enter_context(nc.sbuf_tensor(f"{name}_{n}", shape, F32))

        self.experts, self.top, self.front = experts, top, ones_in_front
        self.marks = 8 - top
        self.width = ones_in_front + experts + ones_behind
        self.scores = sb("scores", [S, B, experts + self.marks])
        self.left = sb("left", [S, B, experts + self.marks])
        self.top8, self.picked = sb("top8", [S, B, 8]), sb("picked", [S, B, 8])
        self.gate = sb("gate", [S, B, self.width])
        self.total, self.rtotal = sb("total", [S, B]), sb("rtotal", [S, B])
        self.gateT = sb("gateT", [self.width, B, S])
        self.dram = nc.dram_tensor(f"{name}_gates", (self.width, turns_per_gate, TOK), F32).ap()
        self.repeats = turns_per_gate

    def wide(self, t):
        return t[:].unsqueeze(2).to_broadcast([S, B, self.experts])

    def logits(self, st):
        return st.ps[0:S, 0, 0:B * self.experts].rearrange("s (b e) -> s b e", b=B)

    def pool_marks(self, pool, s):
        pool.memset(self.scores[:], -1.0)
        pool.memset(self.picked[:], -1.0)
        pool.memset(self.gate[:], 1.0).then_inc(s.marks_set, 1)

    def tensor_logits(self, pe, st, s, x, wg):
        for b in range(B):
            for k in range(KT):
                last = pe.matmul(self.logits(st)[:, b, :], x[:, k, b, :], wg[:, k, :], start=(k == 0), stop=(k == KT - 1))
        last.then_inc(s.logits_ready, 1)

    def vector_pick(self, dve, s):
        e = self.experts
        dve.wait_ge(s.score_ready, 1)
        for b in range(B):
            dve.max(self.top8[:, b, :], self.scores[:, b, 0:e]).then_inc(s.top_ready, 1)
        dve.wait_ge(s.top_ready, B)
        dve.tensor_copy(self.picked[:, :, 0:self.top], self.top8[:, :, 0:self.top]).then_inc(s.picked_ready, 1)
        dve.wait_ge(s.picked_ready, 1)
        for b in range(B):
            dve.match_replace(self.left[:, b, :], self.picked[:, b, :], self.scores[:, b, :], 0.0).then_inc(s.left_ready, 1)
        dve.wait_ge(s.left_ready, B)
        return self.gate[:, :, self.front:self.front + e], self.scores[:, :, 0:e], self.left[:, :, 0:e]

    def tensor_turn(self, pe, st, s):
        pe.wait_ge(s.gate_ready, 1)
        for b in range(B):
            last = pe.transpose(st.ps[0:self.width, 2 + b // 4, (b % 4) * S:(b % 4 + 1) * S], self.gate[:, b, :], st.ident[0:S, 0:S])
        last.then_inc(s.gate_turned, 1)

    def scalar_store(self, act, st, s):
        act.wait_ge(s.gate_turned, 1)
        act.activation(self.gateT[:].rearrange("e (i b) t -> e i (b t)", i=2), st.ps[0:self.width, 2:4, 0:4 * S], ACT.Copy).then_inc(s.gateT_stored, 1)


def experts(nc, st, name, kind, units, unit_cols, dram_w, gate, gate_row, inputs, b2):
    HALF = TOK // 2
    geglu = kind == "geglu"
    up = 4 if geglu else 2
    n_gates = 2 if kind == "relu" else 1
    off2 = KT * up * P
    offb = off2 + 2 * D
    n_bias = unit_cols - offb
    yT = st.yT
    with ExitStack() as ctx:
        def sb(n, shape, dt=F32):
            return ctx.enter_context(nc.sbuf_tensor(f"{name}_{n}", shape, dt))

        landing = [sb(f"landing{i}", [P, unit_cols]) for i in range(2)]
        w_high = [sb(f"w_high{i}", [P, offb]) for i in range(2)]
        w_low = [sb(f"w_low{i}", [P, offb]) for i in range(2)]
        biases = [sb(f"biases{i}", [P, n_bias]) for i in range(2)] if n_bias else None
        gates = [sb(f"gates{i}", [P, n_gates, TOK]) for i in range(2)]
        x_high = [sb(f"x_high{i}", [P, KT, TOK]) for i in range(len(inputs))]
        x_low = [sb(f"x_low{i}", [P, KT, TOK]) for i in range(len(inputs))]
        act_out = sb("act_out", [P, 2, TOK]) if kind != "relu" else None
        hg = act_out if kind == "gelu" else sb("hg", [P, 2, TOK])
        hg_high, hg_low = sb("hg_high", [P, 2, TOK]), sb("hg_low", [P, 2, TOK])
        sems = ["gates_stored", "weights_loaded0", "weights_loaded1", "gates_loaded0", "gates_loaded1", "w_cut", "w_split", "x_cut", "x_split",
                "h_ready", "gelu_done", "prod_done", "hg_gated", "hg_cut", "hg_ready", "y_done", "y_copied"]
        with stage_sems(nc, sems) as s, nc.Block() as block:
            weights_loaded, gates_loaded = [s.weights_loaded0, s.weights_loaded1], [s.gates_loaded0, s.gates_loaded1]
            gate_rows = gate.dram.rearrange("e r t -> (e r) t").rearrange("(u g) t -> u g t", g=n_gates)
            CUTS = 2 if n_bias else 1

            def w1(part, sl, k, m):
                return part[sl][:, k * up * P + m * P:k * up * P + (m + 1) * P]

            def w2(part, sl, t, m):
                return part[sl][:, off2 + t * D + m * P:off2 + t * D + (m + 1) * P]

            def col(sl, i):
                return biases[sl][:, i:i + 1]

            def halves(t, i):
                return t[:, i, :].rearrange("p (j c) -> p j c", j=2)

            turns = (units + 1) // 2
            cuts = sorted({1, turns - 1} | {u // 2 for u, _ in inputs if u // 2 > 0})

            def run(eng, body):
                body(0, 0)
                for lo, hi in zip(cuts[:-1], cuts[1:]):
                    which = [n for n, (u, _) in enumerate(inputs) if u // 2 <= lo][-1]
                    with eng.Fori(lo, hi) as i:
                        body(i, which)
                body(turns - 1, len(inputs) - 1)

            def tiles_of(i):
                n = 2 if type(i) is int and 2 * i + 1 >= units else 4
                return [(c, c // 2, c % 2) for c in range(n)]

            def is_last(i, sl):
                return type(i) is int and 2 * i + sl == units - 1

            def after(eng, sem, value, least=1):
                if type(value) is not int or value >= least:
                    eng.wait_ge(sem, value)

            def three_passes(pe, out, w_hi, w_lo, x_hi, x_lo, start, stop):
                r = lambda ap: ap.bitcast(F32R)
                pe.matmul(out, r(w_lo), r(x_hi), start=start, stop=False)
                pe.matmul(out, r(w_hi), r(x_hi), start=False, stop=False)
                return pe.matmul(out, r(w_hi), r(x_lo), start=False, stop=stop)

            @block.sync
            def _(sp):
                def body(i, _):
                    for sl in sorted({sl for _, sl, _ in tiles_of(i)}):
                        u = i * 2 + sl
                        after(sp, s.w_split, 2 * u - 2)
                        sp.dma_start(landing[sl][:], dram_w[u]).then_inc(weights_loaded[sl], 16)
                        if type(i) is int and i == 0 and sl == 0:
                            for r in range(gate.repeats):
                                sp.dma_start(gate.dram[:, r, :], gate.gateT[:].rearrange("e b t -> e (b t)")).then_inc(s.gates_stored, 16)
                            sp.wait_ge(s.gates_stored, 16 * gate.repeats)
                        after(sp, s.y_done, 2 * u - 2)
                        sp.dma_start(gates[sl][:], gate_rows[gate_row(i, sl)].partition_broadcast(P)).then_inc(gates_loaded[sl], 16)
                run(sp, body)

            @block.gpsimd
            def _(pool):
                def split_weights(u, sl):
                    pool.wait_ge(s.w_cut, (u + 1) * CUTS)
                    for lo, hi in ((0, off2), (off2, offb)):
                        pool.tensor_tensor(w_low[sl][:, lo:hi].bitcast(F32R), landing[sl][:, lo:hi], w_high[sl][:, lo:hi], ALU.subtract).then_inc(s.w_split, 1)

                split_weights(0, 0)
                for n, (_, x) in enumerate(inputs[1:], 1):
                    pool.wait_ge(s.x_cut, n + 1)
                    pool.tensor_tensor(x_low[n][:].bitcast(F32R), x, x_high[n][:], ALU.subtract).then_inc(s.x_split, 1)

                def body(i, _):
                    for sl in sorted({sl for _, sl, _ in tiles_of(i)}):
                        if not is_last(i, sl):
                            split_weights(i * 2 + sl + 1, 1 - sl)
                run(pool, body)

            @block.tensor
            def _(pe):
                if b2 is not None:
                    for m in range(2):
                        for j in range(2):
                            pe.matmul(st.ps[:, 2 * m + j, 0:HALF], b2[0:gate.width, m * P:(m + 1) * P],
                                      gate.gateT[:].rearrange("e b t -> e (b t)")[:, j * HALF:(j + 1) * HALF], start=True, stop=False)

                def down(n, sl, t, first, last_tile):
                    pe.wait_ge(s.hg_ready, n + 1)
                    for m in range(2):
                        for j in range(2):
                            c = slice(j * HALF, (j + 1) * HALF)
                            last = three_passes(pe, st.ps[:, 2 * m + j, 0:HALF], w2(w_high, sl, t, m), w2(w_low, sl, t, m),
                                                hg_high[:, t, c], hg_low[:, t, c], first, last_tile)
                    last.then_inc(s.y_done, 1)

                def body(i, which):
                    tiles = tiles_of(i)
                    x_hi, x_lo = x_high[which], x_low[which]
                    pe.wait_ge(s.x_split, which + 1)
                    for c, sl, t in tiles:
                        n = i * 4 + c
                        u = i * 2 + sl
                        pe.wait_ge(s.w_split, u * 2 + 1 + t)
                        if geglu:
                            after(pe, s.gelu_done, n)
                            after(pe, s.prod_done, n)
                        elif kind == "gelu":
                            after(pe, s.gelu_done, n - 1)
                        else:
                            after(pe, s.hg_gated, n - 1)
                        for half in range(2 if geglu else 1):
                            for j in range(2):
                                bank = 4 + 2 * half + j if geglu else 4 + 2 * t + j
                                cols = slice(j * HALF, (j + 1) * HALF)
                                for k in range(KT):
                                    last = three_passes(pe, st.ps[:, bank, 0:HALF], w1(w_high, sl, k, t + 2 * half), w1(w_low, sl, k, t + 2 * half),
                                                        x_hi[:, k, cols], x_lo[:, k, cols], k == 0, k == KT - 1)
                        last.then_inc(s.h_ready, 1)
                        if not (type(i) is int and i == 0 and c == 0):
                            down(n - 1, 1 - sl if t == 0 else sl, 1 - t, b2 is None and type(i) is int and n == 1, False)
                run(pe, body)
                c, sl, t = tiles_of(turns - 1)[-1]
                down(2 * units - 1, sl, t, False, True)

            if kind != "relu":
                @block.scalar
                def _(act):
                    def body(i, _):
                        for c, sl, t in tiles_of(i):
                            n = i * 4 + c
                            act.wait_ge(s.h_ready, n + 1)
                            after(act, s.hg_ready, n - 1)
                            bank = 6 if geglu else 4 + 2 * t
                            act.activation(halves(act_out, t), st.ps[:, bank:bank + 2, 0:HALF], ACT.Gelu,
                                           bias=col(sl, 2 + t if geglu else t)).then_inc(s.gelu_done, 1)
                    run(act, body)

            @block.vector
            def _(dve):
                def cut(to, x):
                    return dve.tensor_copy(to.bitcast(F32R), x)

                def cut_weights(u, sl, loads):
                    after(dve, s.y_done, 2 * u - 2)
                    dve.wait_ge(weights_loaded[sl], loads * 16)
                    if n_bias:
                        dve.tensor_copy(biases[sl][:], landing[sl][:, offb:]).then_inc(s.w_cut, 1)
                    cut(w_high[sl][:], landing[sl][:, 0:offb]).then_inc(s.w_cut, 1)

                for n, (_, x) in enumerate(inputs):
                    cut(x_high[n][:], x).then_inc(s.x_cut, 1)
                    if n == 0:
                        dve.wait_ge(s.x_cut, 1)
                        dve.tensor_tensor(x_low[0][:].bitcast(F32R), x, x_high[0][:], ALU.subtract).then_inc(s.x_split, 1)
                        cut_weights(0, 0, 1)

                def body(i, _):
                    for c, sl, t in tiles_of(i):
                        n = i * 4 + c
                        if t == 0:
                            dve.wait_ge(gates_loaded[sl], i * 16 + 16)
                        if kind == "relu":
                            dve.wait_ge(s.h_ready, n + 1)
                            dve.scalar_tensor_tensor(halves(hg, t), st.ps[:, 4 + 2 * t:6 + 2 * t, 0:HALF], 0.0, halves(gates[sl], t),
                                                     ALU.max, ALU.mult).then_inc(s.hg_gated, 1)
                        elif geglu:
                            dve.wait_ge(s.gelu_done, n + 1)
                            dve.scalar_tensor_tensor(halves(hg, t), st.ps[:, 4:6, 0:HALF], col(sl, t), halves(act_out, t),
                                                     ALU.add, ALU.mult).then_inc(s.prod_done, 1)
                            dve.wait_ge(s.prod_done, n + 1)
                            dve.scalar_tensor_tensor(hg[:, t, :], hg[:, t, :], col(sl, 4 + t), gates[sl][:, 0, :],
                                                     ALU.mult, ALU.mult).then_inc(s.hg_gated, 1)
                        else:
                            dve.wait_ge(s.gelu_done, n + 1)
                            dve.tensor_tensor(hg[:, t, :], act_out[:, t, :], gates[sl][:, 0, :], ALU.mult).then_inc(s.hg_gated, 1)
                        dve.wait_ge(s.hg_gated, n + 1)
                        after(dve, s.y_done, n - 1)
                        cut(hg_high[:, t, :], hg[:, t, :]).then_inc(s.hg_cut, 1)
                        dve.wait_ge(s.hg_cut, n + 1)
                        dve.tensor_tensor(hg_low[:, t, :].bitcast(F32R), hg[:, t, :], hg_high[:, t, :], ALU.subtract).then_inc(s.hg_ready, 1)
                        if t == 0 and not is_last(i, sl):
                            cut_weights(i * 2 + sl + 1, 1 - sl, i + 1 + sl)
                run(dve, body)
                dve.wait_ge(s.y_done, 2 * units)
                for m in range(2):
                    dve.tensor_copy(halves(yT, m), st.ps[:, 2 * m:2 * m + 2, 0:HALF]).then_inc(s.y_copied, 1)


def experts_tail(nc, st):
    with nc.Fori(0, B // TURN) as turn, stage_sems(nc, ["cur_ready"] + NORM_SEMS) as s, nc.Block() as block:
        y = st.yT[:].rearrange("p m (b t) -> p m b t", b=B)

        @block.gpsimd
        def _(pool):
            for j in range(TURN):
                pool.tensor_copy(st.ycur[:, j], y[:, :, turn * TURN + j, :]).then_inc(s.cur_ready, 1)
            for j in range(TURN):
                rstd_pool(pool, st, s, j)
            for j in range(TURN):
                store_pool(pool, st, s, st.X[:, turn * TURN + j, :], j)

        @block.tensor
        def _(pe):
            for j in range(TURN):
                pe.wait_ge(s.cur_ready, j + 1)
                for m in range(KT):
                    last = pe.transpose(st.ps[0:S, j, m * P:(m + 1) * P], st.ycur[:, j, m, :], st.ident)
                last.then_inc(s.y_ready, 1)
            for j in range(TURN):
                turn_tensor(pe, st, s, TURN + j, j)

        @block.scalar
        def _(act):
            for j in range(TURN):
                store_scalar(act, st, s, TURN + j, st.XT[:, :, turn * TURN + j, :], j)

        @block.vector
        def _(dve):
            for j in range(TURN):
                norm_sum_vector(dve, st, s, st.ps[0:S, j, 0:D], st.X[:, turn * TURN + j, :], None, j)
            for j in range(TURN):
                normalise_vector(dve, st, s, j)


def l2_ffn(nc, st, dram):
    E, TOP, EPS = 15, 3, 1e-20
    with ExitStack() as ctx:
        sb = lambda n, shape: ctx.enter_context(nc.sbuf_tensor(f"l2f_{n}", shape, F32))
        st.yT, st.ycur = sb("yT", [P, KT, TOK]), sb("ycur", [P, TURN, KT, S])
        raw, expsum, rexpsum = sb("raw", [S, B, E]), sb("expsum", [S, B]), sb("rexpsum", [S, B])
        gate = Gate(nc, ctx, "l2f", E, TOP, 0, 2)
        with stage_sems(nc, GATE_SEMS + ["marks_set", "exp_done"]) as s, nc.Block() as block:
            @block.gpsimd
            def _(pool):
                gate.pool_marks(pool, s)

            @block.tensor
            def _(pe):
                gate.tensor_logits(pe, st, s, st.XT, st.w["f8gate"].rearrange("p (k e) -> p k e", k=KT))
                gate.tensor_turn(pe, st, s)

            @block.scalar
            def _(act):
                act.wait_ge(s.score_step, 2)
                act.activation(raw[:], raw[:], ACT.Exp).then_inc(s.exp_done, 1)
                gate.scalar_store(act, st, s)

            @block.vector
            def _(dve):
                dve.wait_ge(s.logits_ready, 1)
                dve.tensor_reduce(expsum[:], gate.logits(st), AX.X, ALU.max).then_inc(s.score_step, 1)
                dve.wait_ge(s.score_step, 1)
                dve.tensor_tensor(raw[:], gate.logits(st), gate.wide(expsum), ALU.subtract).then_inc(s.score_step, 1)
                dve.wait_ge(s.exp_done, 1)
                dve.tensor_reduce(expsum[:], raw[:], AX.X, ALU.add).then_inc(s.score_step, 1)
                dve.wait_ge(s.score_step, 3)
                dve.reciprocal(rexpsum[:], expsum[:]).then_inc(s.score_step, 1)
                dve.wait_ge(s.score_step, 4)
                dve.wait_ge(s.marks_set, 1)
                dve.tensor_tensor(gate.scores[:, :, 0:E], raw[:], gate.wide(rexpsum), ALU.mult).then_inc(s.score_ready, 1)
                out, scores, left = gate.vector_pick(dve, s)
                dve.tensor_tensor(raw[:], scores, left, ALU.subtract).then_inc(s.gate_step, 1)
                dve.tensor_reduce(gate.total[:], gate.top8[:, :, 0:TOP], AX.X, ALU.add).then_inc(s.gate_step, 1)
                dve.wait_ge(s.gate_step, 2)
                dve.tensor_scalar(gate.total[:], gate.total[:], EPS, None, ALU.add).then_inc(s.gate_step, 1)
                dve.wait_ge(s.gate_step, 3)
                dve.reciprocal(gate.rtotal[:], gate.total[:]).then_inc(s.gate_step, 1)
                dve.wait_ge(s.gate_step, 4)
                dve.tensor_tensor(out, raw[:], gate.wide(gate.rtotal), ALU.mult).then_inc(s.gate_ready, 1)

        xf = st.XT[:].rearrange("p k b t -> p k (b t)")
        experts(nc, st, "l2f", "geglu", E + 2, KT * 4 * P + 2 * D + 6, dram["l2_ffn_units"], gate,
                lambda i, sl: i * 2 + sl, [(0, xf)], st.w["f8b2"])
        experts_tail(nc, st)


def l3_ffn(nc, st, dram):
    E, TOP, EPS = 8, 2, float(np.finfo(np.float32).eps)
    with ExitStack() as ctx:
        sb = lambda n, shape: ctx.enter_context(nc.sbuf_tensor(f"l3f_{n}", shape, F32))
        st.yT, st.ycur = sb("yT", [P, KT, TOK]), sb("ycur", [P, TURN, KT, S])
        xs, xr = sb("xs", [P, KT, B, S]), sb("xr", [P, KT, B, S])
        ss, ms = sb("ss", [S, TURN]), sb("ms", [S, TURN])
        gate = Gate(nc, ctx, "l3f", E, TOP, 2, 0, turns_per_gate=2)
        with stage_sems(nc, GATE_SEMS + ["marks_set"]) as s, nc.Block() as block:
            @block.gpsimd
            def _(pool):
                gate.pool_marks(pool, s)

            @block.tensor
            def _(pe):
                gate.tensor_logits(pe, st, s, st.XT, st.w["f11gate"].rearrange("p (k e) -> p k e", k=KT))
                gate.tensor_turn(pe, st, s)

            @block.scalar
            def _(act):
                act.wait_ge(s.logits_ready, 1)
                act.wait_ge(s.marks_set, 1)
                act.activation(gate.scores[:, :, 0:E], gate.logits(st), ACT.Sigmoid).then_inc(s.score_ready, 1)
                gate.scalar_store(act, st, s)

            @block.vector
            def _(dve):
                out, scores, left = gate.vector_pick(dve, s)
                dve.tensor_reduce(gate.total[:], scores, AX.X, ALU.add).then_inc(s.gate_step, 1)
                dve.wait_ge(s.gate_step, 1)
                dve.reciprocal(gate.rtotal[:], gate.total[:]).then_inc(s.gate_step, 1)
                dve.tensor_tensor(out, scores, left, ALU.subtract).then_inc(s.gate_step, 1)
                dve.wait_ge(s.gate_step, 3)
                dve.tensor_tensor(out, out, gate.wide(gate.rtotal), ALU.mult).then_inc(s.gate_ready, 1)

        with nc.Fori(0, B // TURN) as turn, stage_sems(nc, ["sq_ready", "ms_ready", "rms_ready", "xn_ready", "xn_turned", "xs_done",
                                                            "twice_done"]) as s, nc.Block() as block:
            @block.gpsimd
            def _(pool):
                for j in range(TURN):
                    pool.wait_ge(s.sq_ready, j + 1)
                    pool.tensor_scalar(ms[:, j:j + 1], ss[:, j:j + 1], 1.0 / D, EPS, ALU.mult, ALU.add).then_inc(s.ms_ready, 1)
                    pool.wait_ge(s.ms_ready, j + 1)
                    pool.tensor_tensor(st.rstd[:, j:j + 1], ms[:, j:j + 1], st.minus_half[0:S, :], ALU.pow).then_inc(s.rms_ready, 1)

            @block.tensor
            def _(pe):
                for j in range(TURN):
                    pe.wait_ge(s.xn_ready, j + 1)
                    for k in range(KT):
                        last = pe.transpose(st.ps[:, j, k * S:(k + 1) * S], st.xnew[:, j, k * P:(k + 1) * P], st.ident[0:S, 0:S])
                    last.then_inc(s.xn_turned, 1)

            @block.scalar
            def _(act):
                for j in range(TURN):
                    act.wait_ge(s.xn_turned, j + 1)
                    for k in range(KT):
                        ps = st.ps[:, j, k * S:(k + 1) * S]
                        act.activation(xs[:, k, turn * TURN + j, :], ps, ACT.Copy, scale=st.w["f11gs"][:, k:k + 1]).then_inc(s.xs_done, 1)
                        act.activation(xr[:, k, turn * TURN + j, :], ps, ACT.Copy, scale=st.w["f11gr"][:, k:k + 1]).then_inc(s.xs_done, 1)

            @block.vector
            def _(dve):
                for j in range(TURN):
                    x_b = st.X[:, turn * TURN + j, :]
                    dve.scalar_tensor_tensor(st.resid[:, j, :], x_b, 1.0, x_b, ALU.mult, ALU.mult, accum_out=ss[:, j:j + 1]).then_inc(s.sq_ready, 1)
                for j in range(TURN):
                    x_b = st.X[:, turn * TURN + j, :]
                    dve.wait_ge(s.rms_ready, j + 1)
                    dve.tensor_scalar(st.xnew[:, j, :], x_b, st.rstd[:, j:j + 1], None, ALU.mult).then_inc(s.xn_ready, 1)
                    dve.wait_ge(s.xn_ready, j + 1)
                    dve.tensor_tensor(x_b, x_b, x_b, ALU.add).then_inc(s.twice_done, 1)

        flat = lambda t: t[:].rearrange("p k b t -> p k (b t)")
        experts(nc, st, "l3f", "gelu", 40, KT * 2 * P + 2 * D + 2, dram["l3_ffn_units"], gate,
                lambda i, sl: i, [(0, flat(xs)), (8, flat(xr))], st.w["f11b2"])
        experts_tail(nc, st)


def l1_ffn(nc, st, dram):
    E, TOP, H = 32, 4, 16
    REL = 2 * S - 1
    ROW, PITCH = 200, 3300
    scratch = nc.dram_tensor("l1f_positions", (B, S * PITCH), F32).ap()
    wq = st.w["f5q"].rearrange("p (k n) -> p k n", k=KT)
    wp = st.w["f5p"].rearrange("p (k n) -> p k n", k=KT)
    pe_table = st.w["f5pe"].rearrange("p (k n) -> p k n", k=KT)
    with ExitStack() as ctx:
        sb = lambda n, shape: ctx.enter_context(nc.sbuf_tensor(f"l1f_{n}", shape, F32))
        st.yT, st.ycur = sb("yT", [P, KT, TOK]), sb("ycur", [P, TURN, KT, S])
        x2T = sb("x2T", [P, KT, B, S])
        with ExitStack() as ctx2:
            sb2 = lambda n, shape: ctx2.enter_context(nc.sbuf_tensor(f"l1f_{n}", shape, F32))
            x1T = sb2("x1T", [P, KT, B, S])
            with ExitStack() as ctx3:
                sb3 = lambda n, shape: ctx3.enter_context(nc.sbuf_tensor(f"l1f_{n}", shape, F32))
                pT = sb3("pT", [P, KT, REL])
                q1, x1_cur = sb3("q1", [P, TURN, KT, S]), sb3("x1_cur", [P, TURN, KT, S])
                q_pad = sb3("q_between", [P, 2, H, S])
                bd = sb3("bd", [S, 2, H, REL])
                with stage_sems(nc, ["p_ready", "p_done"]) as s, nc.Block() as block:
                    @block.tensor
                    def _(pe):
                        for m in range(KT):
                            for k in range(KT):
                                last = pe.matmul(st.ps[:, m, 0:REL], wp[:, k, m * P:(m + 1) * P], pe_table[:, k, :], start=(k == 0), stop=(k == KT - 1))
                        last.then_inc(s.p_ready, 1)

                    @block.scalar
                    def _(act):
                        act.wait_ge(s.p_ready, 1)
                        act.activation(pT[:], st.ps[:, 0:KT, 0:REL], ACT.Copy).then_inc(s.p_done, 1)

                with nc.Fori(0, B // TURN) as turn, stage_sems(nc, NORM_SEMS + ["x1_stored", "q_ready", "q_copied", "q_spread", "bd_ready", "bd_copied0",
                                                                               "bd_copied1", "bd_stored0", "bd_stored1"]) as s, nc.Block() as block:
                    pairs = H // 2

                    def copy_bd(eng, n):
                        j, g = divmod(n, pairs)
                        eng.wait_ge(s.bd_ready, n + 1)
                        if j >= 2:
                            eng.wait_ge((s.bd_stored0, s.bd_stored1)[j % 2], 16 * (j // 2))
                        out, ps = bd[:, j % 2, 2 * g:2 * g + 2, :], st.ps[0:S, n % 4, 0:2 * REL].rearrange("p (h r) -> p h r", h=2)
                        if n % 2 == 0:
                            eng.tensor_copy(out, ps).then_inc(s.bd_copied0, 1)
                        else:
                            eng.activation(out, ps, ACT.Copy).then_inc(s.bd_copied1, 1)

                    @block.gpsimd
                    def _(pool):
                        for j in range(TURN):
                            pool.tensor_copy(st.resid[:, j, :], st.X[:, turn * TURN + j, :]).then_inc(s.resid_ready, 1)
                        for j in range(TURN):
                            rstd_pool(pool, st, s, j)
                        for j in range(TURN):
                            pool.wait_ge(s.q_copied, j + 1)
                            if j >= 2:
                                pool.wait_ge(s.bd_ready, (j - 1) * pairs)
                            for m in range(KT):
                                pool.tensor_tensor(q_pad[:, j % 2, 8 * m:8 * m + 8, :], q1[:, j, m, :].unsqueeze(1).to_broadcast([P, 8, S]),
                                                   st.head_mask[16].unsqueeze(2).to_broadcast([P, 8, S]), ALU.mult).then_inc(s.q_spread, 1)

                    @block.vector
                    def _(dve):
                        for j in range(TURN):
                            dve.wait_ge(s.resid_ready, j + 1)
                            norm_stats_vector(dve, st, s, j)
                        for j in range(TURN):
                            normalise_vector(dve, st, s, j, st.w["f5g1"][0:S, :], st.w["f5s1"][0:S, :])
                        for n in range(0, TURN * pairs, 2):
                            copy_bd(dve, n)

                    @block.tensor
                    def _(pe):
                        for j in range(TURN):
                            turn_tensor(pe, st, s, 4 + j, j)
                        for j in range(TURN):
                            pe.wait_ge(s.x1_stored, 2 * (j + 1))
                            for m in range(KT):
                                for k in range(KT):
                                    last = pe.matmul(st.ps[:, 4 + j, m * S:(m + 1) * S], wq[:, k, m * P:(m + 1) * P], x1_cur[:, j, k, :],
                                                     start=(k == 0), stop=(k == KT - 1))
                            last.then_inc(s.q_ready, 1)
                        for n in range(TURN * pairs):
                            j, g = divmod(n, pairs)
                            if g == 0:
                                pe.wait_ge(s.q_spread, (j + 1) * KT)
                            if n >= 4:
                                pe.wait_ge(s.bd_copied0 if n % 2 == 0 else s.bd_copied1, n // 2 - 1)
                            for i in range(2):
                                h = 2 * g + i
                                last = pe.matmul(st.ps[0:S, n % 4, i * REL:(i + 1) * REL], q_pad[:, j % 2, h, :], pT[:, h // 8, :], start=True, stop=True)
                            last.then_inc(s.bd_ready, 1)

                    @block.scalar
                    def _(act):
                        for j in range(TURN):
                            act.wait_ge(s.xnew_turned, j + 1)
                            ps = st.ps[:, 4 + j, 0:KT * S].rearrange("p (k t) -> p k t", k=KT)
                            act.activation(x1_cur[:, j], ps, ACT.Copy).then_inc(s.x1_stored, 1)
                            act.activation(x1T[:, :, turn * TURN + j, :], ps, ACT.Copy).then_inc(s.x1_stored, 1)
                        for j in range(TURN):
                            act.wait_ge(s.q_ready, j + 1)
                            act.activation(q1[:, j], st.ps[:, 4 + j, 0:KT * S].rearrange("p (m t) -> p m t", m=KT), ACT.Copy, scale=0.25).then_inc(s.q_copied, 1)
                        for n in range(1, TURN * pairs, 2):
                            copy_bd(act, n)

                    @block.sync
                    def _(sp):
                        for j in range(TURN):
                            sp.wait_ge(s.bd_copied0, (j + 1) * pairs // 2)
                            sp.wait_ge(s.bd_copied1, (j + 1) * pairs // 2)
                            rows = scratch[turn * TURN + j, :].rearrange("(i c) -> i c", c=PITCH)[:, 0:H * ROW].rearrange("i (h r) -> i h r", r=ROW)
                            sp.dma_start(rows[:, :, 0:REL], bd[:, j % 2]).then_inc((s.bd_stored0, s.bd_stored1)[j % 2], 16)
                        sp.wait_ge(s.bd_stored0, 16 * (TURN // 2))
                        sp.wait_ge(s.bd_stored1, 16 * (TURN // 2))

            def skewed(b):
                rows = scratch[b, S - 1:S - 1 + S * (PITCH - 1)].rearrange("(i c) -> i c", c=PITCH - 1)
                return rows[:, 0:H * ROW].rearrange("i (h r) -> i h r", r=ROW)[:, :, 0:S]

            w = weights(st, "f5")
            attention(nc, st, "l1f", H, 16, False, w, xT=x1T, inner=InnerNorm(st.w["f5g2"][0:S, :], st.w["f5s2"][0:S, :], x2T), bd=skewed)

        gate = Gate(nc, ctx, "l1f", E, TOP, 0, 0)
        with stage_sems(nc, GATE_SEMS + ["marks_set"]) as s, nc.Block() as block:
            @block.gpsimd
            def _(pool):
                gate.pool_marks(pool, s)

            @block.tensor
            def _(pe):
                gate.tensor_logits(pe, st, s, x2T, st.w["f5sel"].rearrange("p (k e) -> p k e", k=KT))
                gate.tensor_turn(pe, st, s)

            @block.scalar
            def _(act):
                act.wait_ge(s.logits_ready, 1)
                act.wait_ge(s.marks_set, 1)
                act.activation(gate.scores[:, :, 0:E], gate.logits(st), ACT.Sigmoid).then_inc(s.score_ready, 1)
                gate.scalar_store(act, st, s)

            @block.vector
            def _(dve):
                out, scores, left = gate.vector_pick(dve, s)
                dve.tensor_tensor(out, scores, left, ALU.subtract).then_inc(s.gate_ready, 1)

        experts(nc, st, "l1f", "relu", E // 2, KT * 2 * P + 2 * D, dram["l1_ffn_units"], gate,
                lambda i, sl: i * 2 + sl, [(0, x2T[:].rearrange("p k b t -> p k (b t)"))], None)
        experts_tail(nc, st)


def l2_attn(nc, st, dram):
    H, HD, EPS = 8, 32, 1e-6
    HPT = P // HD
    view = lambda n: st.w[n].rearrange("p (k n) -> p k n", k=KT)
    wq, wk, wrq, wrk = view("a6q"), view("a6k"), view("a6rq"), view("a6rk")
    wvg, wout = view("a6vg"), view("a6o")
    VG = D + 3 * H
    norm_w, gate_bias = st.w["a6norm"][0:S, :], st.w["a6bgates"][0:S, :]
    cos, sin, head_mask = st.w["a6cos"], st.w["a6sin"], st.w["a6heads"]
    js = range(TURN)
    with ExitStack() as ctx:
        def sb(n, shape):
            return ctx.enter_context(nc.sbuf_tensor(f"l2a_{n}", shape, F32))

        ss, ms = sb("ss", [S, TURN]), sb("ms", [S, TURN])
        hT = sb("hT", [P, TURN, KT, S])
        qk, rqk = sb("qk", [P, TURN, 2 * KT, S]), sb("rqk", [P, TURN, 2 * KT, S])
        q_pad = sb("q_pad", [P, TURN, H, S])
        vg = sb("vg", [S, TURN, VG])
        beta_pad = sb("beta_pad", [P, TURN, S])
        entries, decay = sb("entries", [S, TURN, H, S]), sb("decay", [S, TURN, H, S])
        o_sb, oT = sb("o_sb", [S, TURN, D]), sb("oT", [P, TURN, KT, S])
        with stage_sems(nc, ["first_zero"]) as s, nc.Block() as block:
            @block.gpsimd
            def _(pool):
                pool.memset(beta_pad[:], 0.0).then_inc(s.first_zero, 1)

        sems = ["sq_ready", "ms_ready", "rms_ready", "h_ready", "h_turned", "hT_ready", "vg_ready", "qk_ready", "rqk_ready",
                "vg_done", "gates_done", "qk_done", "rope_step", "rotated", "q_spread", "beta_turned", "beta_done", "f_ready",
                "entries_ready", "decay_ready", "scores_ready", "weighed_ready", "heads_done", "o_ready", "o_turned", "oT_ready"]
        with nc.Fori(0, B // TURN) as turn, stage_sems(nc, sems + NORM_SEMS) as s, nc.Block() as block:
            x_b = lambda j: st.X[:, turn * TURN + j, :]
            tiles = lambda bank, n: st.ps[:, bank, 0:n * S].rearrange("p (m t) -> p m t", m=n)
            wide = lambda t, n: t.unsqueeze(1).to_broadcast([P, n, S])

            @block.gpsimd
            def _(pool):
                for j in js:
                    pool.wait_ge(s.sq_ready, j + 1)
                    pool.tensor_scalar(ms[:, j:j + 1], ss[:, j:j + 1], 1.0 / D, EPS, ALU.mult, ALU.add).then_inc(s.ms_ready, 1)
                    pool.wait_ge(s.ms_ready, j + 1)
                    pool.tensor_tensor(st.vareps[:, j:j + 1], ms[:, j:j + 1], st.minus_half[0:S, :], ALU.pow).then_inc(s.rms_ready, 1)
                for j in js:
                    pool.wait_ge(s.gates_done, j + 1)
                    pool.tensor_tensor(entries[:, j], st.ident[0:S, 0:S].unsqueeze(1).to_broadcast([S, H, S]),
                                       vg[:, j, D:D + H].unsqueeze(2).to_broadcast([S, H, S]), ALU.mult).then_inc(s.entries_ready, 1)
                    pool.wait_ge(s.rotated, j + 1)
                    for m in range(KT):
                        pool.tensor_tensor(q_pad[:, j, m * HPT:(m + 1) * HPT, :], wide(qk[:, j, m, :], HPT),
                                           head_mask.unsqueeze(2).to_broadcast([P, HPT, S]), ALU.mult).then_inc(s.q_spread, 1)
                for j in js:
                    rstd_pool(pool, st, s, j)
                for j in js:
                    store_pool(pool, st, s, x_b(j), j)

            @block.tensor
            def _(pe):
                for j in js:
                    pe.wait_ge(s.h_ready, j + 1)
                    for k in range(KT):
                        last = pe.transpose(st.ps[:, 2 * j, k * S:(k + 1) * S], st.xnew[:, j, k * P:(k + 1) * P], st.ident[0:S, 0:S])
                    last.then_inc(s.h_turned, 1)
                for j in js:
                    pe.wait_ge(s.hT_ready, j + 1)
                    for k in range(KT):
                        last = pe.matmul(st.ps[0:S, 2 * j, 0:VG], hT[:, j, k, :], wvg[:, k, :], start=(k == 0), stop=(k == KT - 1))
                    last.then_inc(s.vg_ready, 1)
                    for i in range(2 * KT):
                        w, m = (wq, wk)[i // KT], i % KT
                        for k in range(KT):
                            last = pe.matmul(st.ps[:, 2 * j + 1, i * S:(i + 1) * S], w[:, k, m * P:(m + 1) * P], hT[:, j, k, :],
                                             start=(k == 0), stop=(k == KT - 1))
                    last.then_inc(s.qk_ready, 1)
                for j in js:
                    pe.wait_ge(s.vg_done, 2 * (j + 1))
                    for i in range(2 * KT):
                        w, m = (wrq, wrk)[i // KT], i % KT
                        for k in range(KT):
                            last = pe.matmul(st.ps[:, 2 * j, i * S:(i + 1) * S], w[:, k, m * P:(m + 1) * P], hT[:, j, k, :],
                                             start=(k == 0), stop=(k == KT - 1))
                    last.then_inc(s.rqk_ready, 1)
                for j in js:
                    pe.wait_ge(s.gates_done, j + 1)
                    pe.wait_ge(s.qk_done, j + 1)
                    pe.transpose(st.ps[0:H, 2 * j + 1, 0:S], vg[:, j, D + 2 * H:VG], st.ident[0:S, 0:S]).then_inc(s.beta_turned, 1)
                for j in js:
                    pe.wait_ge(s.beta_done, j + 1)
                    pe.wait_ge(s.rotated, j + 1)
                    for h in range(H):
                        last = pe.matmul(st.ps[0:S, 2 * j + h // 4, (h % 4) * S:(h % 4 + 1) * S],
                                         st.ident[:, h:h + 1].to_broadcast([P, S]), beta_pad[:, j, :], start=True, stop=True)
                    last.then_inc(s.f_ready, 1)
                for j in js:
                    pe.wait_ge(s.decay_ready, 2 * (j + 1))
                    pe.wait_ge(s.q_spread, KT * (j + 1))
                    for h in range(H):
                        last = pe.matmul(st.ps[0:S, 2 * j + h // 4, (h % 4) * S:(h % 4 + 1) * S], qk[:, j, KT + h // HPT, :], q_pad[:, j, h, :],
                                         start=True, stop=True)
                    last.then_inc(s.scores_ready, 1)
                for j in js:
                    pe.wait_ge(s.weighed_ready, 2 * (j + 1))
                    for h in range(H):
                        last = pe.matmul(st.ps[0:S, 2 * j, h * HD:(h + 1) * HD], decay[:, j, h, :], vg[:, j, h * HD:(h + 1) * HD], start=True, stop=True)
                    last.then_inc(s.heads_done, 1)
                for j in js:
                    pe.wait_ge(s.o_ready, j + 1)
                    for k in range(KT):
                        last = pe.transpose(st.ps[:, 2 * j + 1, k * S:(k + 1) * S], o_sb[:, j, k * P:(k + 1) * P], st.ident[0:S, 0:S])
                    last.then_inc(s.o_turned, 1)
                for j in js:
                    pe.wait_ge(s.oT_ready, j + 1)
                    for k in range(KT):
                        last = pe.matmul(st.ps[0:S, 2 * j, 0:D], oT[:, j, k, :], wout[:, k, :], start=(k == 0), stop=(k == KT - 1))
                    last.then_inc(s.y_ready, 1)
                for j in js:
                    turn_tensor(pe, st, s, 2 * j + 1, j)

            @block.scalar
            def _(act):
                for j in js:
                    act.wait_ge(s.h_turned, j + 1)
                    act.activation(hT[:, j], tiles(2 * j, KT), ACT.Copy).then_inc(s.hT_ready, 1)
                for j in js:
                    act.wait_ge(s.qk_ready, j + 1)
                    act.activation(qk[:, j], tiles(2 * j + 1, 2 * KT), ACT.Copy).then_inc(s.qk_done, 1)
                    act.wait_ge(s.vg_done, 2 * (j + 1))
                    act.activation(vg[:, j, D:VG], vg[:, j, D:VG], ACT.Sigmoid).then_inc(s.gates_done, 1)
                for j in js:
                    act.wait_ge(s.beta_turned, j + 1)
                    act.activation(beta_pad[0:H, j, 1:S], st.ps[0:H, 2 * j + 1, 1:S], ACT.Copy).then_inc(s.beta_done, 1)
                for j in js:
                    act.wait_ge(s.o_turned, j + 1)
                    act.activation(oT[:, j], tiles(2 * j + 1, KT), ACT.Copy).then_inc(s.oT_ready, 1)
                for j in js:
                    store_scalar(act, st, s, 2 * j + 1, st.XT[:, :, turn * TURN + j, :], j)

            @block.vector
            def _(dve):
                for j in js:
                    dve.scalar_tensor_tensor(st.resid[:, j, :], x_b(j), 1.0, x_b(j), ALU.mult, ALU.mult, accum_out=ss[:, j:j + 1]).then_inc(s.sq_ready, 1)
                for j in js:
                    dve.wait_ge(s.rms_ready, j + 1)
                    dve.scalar_tensor_tensor(st.xnew[:, j, :], x_b(j), st.vareps[:, j:j + 1], norm_w, ALU.mult, ALU.mult).then_inc(s.h_ready, 1)
                for j in js:
                    dve.wait_ge(s.vg_ready, j + 1)
                    dve.tensor_copy(vg[:, j, 0:D], st.ps[0:S, 2 * j, 0:D]).then_inc(s.vg_done, 1)
                    dve.tensor_tensor(vg[:, j, D:VG], st.ps[0:S, 2 * j, D:VG], gate_bias, ALU.add).then_inc(s.vg_done, 1)
                for j in js:
                    dve.wait_ge(s.rqk_ready, j + 1)
                    dve.tensor_tensor(rqk[:, j], tiles(2 * j, 2 * KT), wide(sin, 2 * KT), ALU.mult).then_inc(s.rope_step, 1)
                    dve.wait_ge(s.qk_done, j + 1)
                    dve.tensor_tensor(qk[:, j], qk[:, j], wide(cos, 2 * KT), ALU.mult).then_inc(s.rope_step, 1)
                    dve.wait_ge(s.rope_step, 2 * (j + 1))
                    dve.tensor_tensor(qk[:, j], qk[:, j], rqk[:, j], ALU.add).then_inc(s.rotated, 1)
                for j in js:
                    dve.wait_ge(s.f_ready, j + 1)
                    dve.wait_ge(s.entries_ready, j + 1)
                    for i in range(2):
                        dve.tensor_tensor_scan(decay[:, j, 4 * i:4 * i + 4, :].rearrange("s h t -> s (h t)"), st.ps[0:S, 2 * j + i, 0:4 * S],
                                               entries[:, j, 4 * i:4 * i + 4, :].rearrange("s h t -> s (h t)"), 0.0, ALU.mult, ALU.add).then_inc(s.decay_ready, 1)
                for j in js:
                    dve.wait_ge(s.decay_ready, 2 * (j + 1))
                    dve.wait_ge(s.scores_ready, j + 1)
                    for i in range(2):
                        part = decay[:, j, 4 * i:4 * i + 4, :]
                        dve.scalar_tensor_tensor(part, st.ps[0:S, 2 * j + i, 0:4 * S].rearrange("s (h t) -> s h t", h=4), float(HD) ** -0.5, part,
                                                 ALU.mult, ALU.mult).then_inc(s.weighed_ready, 1)
                for j in js:
                    dve.wait_ge(s.heads_done, j + 1)
                    dve.tensor_tensor(o_sb[:, j, :].rearrange("q (h d) -> q h d", d=HD), st.ps[0:S, 2 * j, 0:D].rearrange("q (h d) -> q h d", d=HD),
                                      vg[:, j, D + H:D + 2 * H].unsqueeze(2).to_broadcast([S, H, HD]), ALU.mult).then_inc(s.o_ready, 1)
                for j in js:
                    norm_sum_vector(dve, st, s, st.ps[0:S, 2 * j, 0:D], x_b(j), st.w["a6bo"][0:S, :], j)
                for j in js:
                    normalise_vector(dve, st, s, j)


def l2_xattn(nc, st, dram):
    H, C, TAPS, NT, EPS = 16, 512, 9, 3, 1e-5
    CT, W2 = C // P, H * TAPS
    w_hist = st.w["a7hw"].rearrange("p (k n) -> p k n", k=KT)
    w_c1 = st.w["a7cw1"].rearrange("p (k n) -> p k n", k=CT)
    w_k1 = st.w["a7kw1"].rearrange("p (k n) -> p k n", k=CT)
    w_k2 = st.w["a7kw2"].rearrange("p (k n) -> p k n", k=KT)
    rows = [min(KROWS, KEYS - t * KROWS) for t in range(NT)]
    with ExitStack() as ctx:
        sb = lambda n, shape, dt=F32: ctx.enter_context(nc.sbuf_tensor(f"l2x_{n}", shape, dt))
        kern = sb("kern", [P, B, W2])
        keep, mask_add = sb("keep", [S, S]), sb("mask_add", [S, S])
        with ExitStack() as ctx2:
            sb2 = lambda n, shape: ctx2.enter_context(nc.sbuf_tensor(f"l2x_{n}", shape, F32))
            ctx_cur, ccT = sb2("hist_cur", [P, TURN, KT, KEYS]), sb2("ccT", [P, CT, B])
            eh, ehT, g1T = sb2("eh", [KROWS, TURN, NT, C]), sb2("ehT", [P, TURN, CT, KEYS]), sb2("g1T", [P, TURN, KEYS])
            hstats, hmv = sb2("hstats", [KROWS, NT, TURN, 6]), sb2("hmv", [KROWS, NT, TURN, 2])
            hvar, hrstd = sb2("hvar", [KROWS, NT, TURN]), sb2("hrstd", [KROWS, NT, TURN])
            aw, awmax, awsum, awinv = sb2("aw", [1, TURN, KEYS]), sb2("awmax", [1, TURN]), sb2("awsum", [1, TURN]), sb2("awinv", [1, TURN])
            pcol = sb2("pcol", [KROWS, TURN, NT, TURN])
            cc = sb2("cc", [TURN, C])
            hist_rows = sb2("hist_rows", [P, 3 * C])
            hb, hg, hs = (hist_rows[:, i * C:(i + 1) * C] for i in range(3))
            with stage_sems(nc, ["buffers_set", "hist_rows_loaded"]) as s, nc.Block() as block:
                @block.sync
                def _(sp):
                    sp.dma_start(hist_rows[:], dram["hist_rows"]).then_inc(s.hist_rows_loaded, 16)
                    sp.wait_ge(s.hist_rows_loaded, 16)

                @block.gpsimd
                def _(pool):
                    pool.memset(hmv[:], 1.0).then_inc(s.buffers_set, 1)
                    pool.memset(pcol[:], 0.0).then_inc(s.buffers_set, 1)

            sems = ["cur_ready", "eh_ready", "eh_biased", "stats_done", "mv_done", "var_done", "hrstd_done", "eh_step", "eh_normed", "eh_done",
                    "turned", "ehT_done", "g1_ready", "g1_done", "aw_ready", "aw_shifted", "aw_max", "aw_exp", "aw_inverse",
                    "p_row", "p_turned", "p_col", "cc_ready", "cc_copied", "cc_turned", "cc_done"]
            js = range(TURN)
            PAIR = 2
            pairs = [range(j, j + PAIR) for j in range(0, TURN, PAIR)]
            steps = [(pair, t) for pair in pairs for t in range(NT)]
            tiles = [(j, t) for pair, t in steps for j in pair]
            turns = [(c, j) for pair in pairs for c in range(CT) for j in pair]
            with nc.Fori(0, B // TURN) as turn, stage_sems(nc, sems) as s, nc.Block() as block:
                bank = lambda j, i: 2 * j + i % 2
                part = lambda j, t: eh[0:rows[t], j, t, :]

                @block.gpsimd
                def _(pool):
                    for j in js:
                        pool.tensor_copy(ctx_cur[:, j], st.ctxT[:, turn * TURN + j, :, :]).then_inc(s.cur_ready, 1)
                    for n, (pair, t) in enumerate(steps):
                        both = slice(pair[0], pair[-1] + 1)
                        pool.wait_ge(s.mv_done, PAIR * (n + 1))
                        pool.tensor_scalar(hvar[:, t, both], hmv[:, t, both, 1], EPS, None, ALU.add).then_inc(s.var_done, 1)
                        pool.wait_ge(s.var_done, n + 1)
                        pool.tensor_tensor(hrstd[:, t, both], hvar[:, t, both], st.minus_half[0:KROWS, 0:1].to_broadcast([KROWS, PAIR]), ALU.pow).then_inc(s.hrstd_done, 1)

                @block.tensor
                def _(pe):
                    for n, (j, t) in enumerate(tiles):
                        if t == 0:
                            pe.wait_ge(s.cur_ready, j + 1)
                        if t == 2:
                            pe.wait_ge(s.eh_biased, tiles.index((j, 0)) + 1)
                        for k in range(KT):
                            last = pe.matmul(st.ps[0:rows[t], bank(j, t), 0:C], ctx_cur[:, j, k, t * KROWS:t * KROWS + rows[t]], w_hist[:, k, :],
                                             start=(k == 0), stop=(k == KT - 1))
                        last.then_inc(s.eh_ready, 1)
                    for i, pair in enumerate(pairs):
                        pe.wait_ge(s.eh_done, PAIR * NT * (i + 1))
                        for c in range(CT):
                            for j in pair:
                                if c >= 2:
                                    pe.wait_ge(s.ehT_done, turns.index((c - 2, j)) + 1)
                                for t in range(NT):
                                    last = pe.transpose(st.ps[:, bank(j, c), t * KROWS:t * KROWS + rows[t]], part(j, t)[:, c * P:(c + 1) * P],
                                                        st.ident[0:rows[t], 0:rows[t]])
                                last.then_inc(s.turned, 1)
                        for j in pair:
                            pe.wait_ge(s.ehT_done, turns.index((CT - 1, j)) + 1)
                            for c in range(CT):
                                last = pe.matmul(st.ps[:, bank(j, 0), 0:KEYS], w_c1[:, c, :], ehT[:, j, c, :], start=(c == 0), stop=(c == CT - 1))
                            last.then_inc(s.g1_ready, 1)
                        for j in pair:
                            pe.wait_ge(s.g1_done, j + 1)
                            pe.matmul(st.ps[0:1, bank(j, 1), 0:KEYS], st.w["a7cw2"], g1T[:, j, :], start=True, stop=True).then_inc(s.aw_ready, 1)
                    for j in js:
                        pe.wait_ge(s.p_row, j + 1)
                        for t in range(NT):
                            last = pe.matmul(st.ps[0:rows[t], bank(j, 0), t:t + 1], aw[0:1, j, t * KROWS:t * KROWS + rows[t]], st.ident[0:1, 0:1], start=True, stop=True)
                        last.then_inc(s.p_turned, 1)
                    for j in js:
                        pe.wait_ge(s.p_col, NT * (j + 1))
                        for t in range(NT):
                            last = pe.matmul(st.ps[0:TURN, bank(0, 1), 0:C], pcol[0:rows[t], j, t, :], part(j, t),
                                             start=(j == 0 and t == 0), stop=(j == TURN - 1 and t == NT - 1))
                    last.then_inc(s.cc_ready, 1)
                    pe.wait_ge(s.cc_copied, 1)
                    for c in range(CT):
                        last = pe.transpose(st.ps[:, bank(1, 1), c * TURN:(c + 1) * TURN], cc[:, c * P:(c + 1) * P], st.ident[0:TURN, 0:TURN])
                    last.then_inc(s.cc_turned, 1)

                @block.scalar
                def _(act):
                    for pair in pairs:
                        for n, (j, t) in enumerate(tiles):
                            if j in pair:
                                act.wait_ge(s.eh_normed, n + 1)
                                act.activation(part(j, t), part(j, t), ACT.Gelu).then_inc(s.eh_done, 1)
                        for n, (c, j) in enumerate(turns):
                            if j in pair:
                                act.wait_ge(s.turned, n + 1)
                                act.activation(ehT[:, j, c, :], st.ps[:, bank(j, c), 0:KEYS], ACT.Copy).then_inc(s.ehT_done, 1)
                        for j in pair:
                            act.wait_ge(s.g1_ready, j + 1)
                            act.activation(g1T[:, j, :], st.ps[:, bank(j, 0), 0:KEYS], ACT.Gelu, bias=st.w["a7cb1"]).then_inc(s.g1_done, 1)
                    for j in js:
                        act.wait_ge(s.aw_max, j + 1)
                        act.activation(aw[:, j, :], aw[:, j, :], ACT.Exp, bias=awmax[:, j:j + 1], accum_out=awsum[:, j:j + 1]).then_inc(s.aw_exp, 1)
                    act.wait_ge(s.cc_ready, 1)
                    act.activation(cc[:], st.ps[0:TURN, bank(0, 1), 0:C], ACT.Copy).then_inc(s.cc_copied, 1)
                    act.wait_ge(s.cc_turned, 1)
                    act.activation(ccT[:].rearrange("p c (u j) -> p c u j", j=TURN)[:, :, turn, :], st.ps[:, bank(1, 1), 0:CT * TURN].rearrange("p (c j) -> p c j", c=CT), ACT.Copy).then_inc(s.cc_done, 1)

                @block.vector
                def _(dve):
                    for i, (pair, t) in enumerate(steps):
                        for n, j in enumerate(pair, i * PAIR):
                            dve.wait_ge(s.eh_ready, n + 1)
                            dve.tensor_tensor(part(j, t), st.ps[0:rows[t], bank(j, t), 0:C], hb[0:rows[t], :], ALU.add).then_inc(s.eh_biased, 1)
                            dve.wait_ge(s.eh_biased, n + 1)
                            dve.bn_stats(hstats[0:rows[t], t, j, :], part(j, t)).then_inc(s.stats_done, 1)
                            dve.wait_ge(s.stats_done, n + 1)
                            dve.bn_aggr(hmv[0:rows[t], t, j, :], hstats[0:rows[t], t, j, :]).then_inc(s.mv_done, 1)
                        for n, j in enumerate(pair, i * PAIR):
                            dve.wait_ge(s.mv_done, n + 1)
                            dve.scalar_tensor_tensor(part(j, t), part(j, t), hmv[0:rows[t], t, j, 0:1], hg[0:rows[t], :], ALU.subtract, ALU.mult).then_inc(s.eh_step, 1)
                        dve.wait_ge(s.hrstd_done, i + 1)
                        for n, j in enumerate(pair, i * PAIR):
                            dve.wait_ge(s.eh_step, n + 1)
                            dve.scalar_tensor_tensor(part(j, t), part(j, t), hrstd[0:rows[t], t, j:j + 1], hs[0:rows[t], :], ALU.mult, ALU.add).then_inc(s.eh_normed, 1)
                    for j in js:
                        dve.wait_ge(s.aw_ready, j + 1)
                        dve.tensor_scalar(aw[:, j, :], st.ps[0:1, bank(j, 1), 0:KEYS], st.w["a7cb2"][0:1, 0:1], None, ALU.add).then_inc(s.aw_shifted, 1)
                        dve.wait_ge(s.aw_shifted, j + 1)
                        dve.tensor_reduce(awmax[:, j:j + 1], aw[:, j, :], AX.X, ALU.max, negate=True).then_inc(s.aw_max, 1)
                    for j in js:
                        dve.wait_ge(s.aw_exp, j + 1)
                        dve.reciprocal(awinv[:, j:j + 1], awsum[:, j:j + 1]).then_inc(s.aw_inverse, 1)
                        dve.wait_ge(s.aw_inverse, j + 1)
                        dve.tensor_scalar(aw[:, j, :], aw[:, j, :], awinv[:, j:j + 1], None, ALU.mult).then_inc(s.p_row, 1)
                    for j in js:
                        dve.wait_ge(s.p_turned, j + 1)
                        for t in range(NT):
                            dve.tensor_copy(pcol[0:rows[t], j, t, j:j + 1], st.ps[0:rows[t], bank(j, 0), t:t + 1]).then_inc(s.p_col, 1)

            kp, kpT, kern8 = sb2("kp", [B, D]), sb2("kpT", [P, KT, B]), sb2("kern8", [B, H, TAPS])
            kstats, kmv, kvar, krstd = sb2("kstats", [B, 6]), sb2("kmv", [B, 2]), sb2("kvar", [B, 1]), sb2("krstd", [B, 1])
            kmax, ksum = sb2("kmax", [B, H]), sb2("ksum", [B, H])
            net_rows = sb2("net_rows", [B, 3 * D + W2])
            kb1, kg, ks = (net_rows[:, i * D:(i + 1) * D] for i in range(3))
            kb2 = net_rows[:, 3 * D:3 * D + W2]
            m_u8 = ctx2.enter_context(nc.sbuf_tensor("l2x_m_u8", [S, S], U8))
            sems = ["k1_ready", "kp_step", "kvar_done", "krstd_done", "kp_normed", "kp_done", "kp_turned", "kpT_done", "k2_ready", "kern_step",
                    "kern_exp", "kern8_done", "spread_ready", "spread_act", "mask_loaded", "rows_loaded", "keep_done"]
            with stage_sems(nc, sems) as s, nc.Block() as block:
                @block.sync
                def _(sp):
                    sp.dma_start(net_rows[:], dram["kernel_net_rows"]).then_inc(s.rows_loaded, 16)
                    sp.dma_start(m_u8[:], dram["self_mask"]).then_inc(s.mask_loaded, 16)

                @block.gpsimd
                def _(pool):
                    pool.wait_ge(s.kp_step, 3)
                    pool.tensor_scalar(kvar[:], kmv[:, 1:2], EPS, None, ALU.add).then_inc(s.kvar_done, 1)
                    pool.wait_ge(s.kvar_done, 1)
                    pool.tensor_tensor(krstd[:], kvar[:], st.minus_half[0:B, :], ALU.pow).then_inc(s.krstd_done, 1)

                @block.tensor
                def _(pe):
                    for c in range(CT):
                        last = pe.matmul(st.ps[0:B, 0, 0:D], ccT[:, c, :], w_k1[:, c, :], start=(c == 0), stop=(c == CT - 1))
                    last.then_inc(s.k1_ready, 1)
                    pe.wait_ge(s.kp_done, 1)
                    for k in range(KT):
                        last = pe.transpose(st.ps[:, 1, k * B:(k + 1) * B], kp[:, k * P:(k + 1) * P], st.ident[0:B, 0:B])
                    last.then_inc(s.kp_turned, 1)
                    pe.wait_ge(s.kpT_done, 1)
                    for k in range(KT):
                        last = pe.matmul(st.ps[0:B, 2, 0:W2], kpT[:, k, :], w_k2[:, k, :], start=(k == 0), stop=(k == KT - 1))
                    last.then_inc(s.k2_ready, 1)
                    pe.wait_ge(s.kern8_done, 1)
                    for b in range(B):
                        last = pe.matmul(st.ps[:, 3 + b // 2, (b % 2) * W2:(b % 2 + 1) * W2], st.ident[0:B, b:b + 1].to_broadcast([B, P]),
                                         kern8[:].rearrange("b h t -> b (h t)"), start=True, stop=True)
                    last.then_inc(s.spread_ready, 1)

                @block.scalar
                def _(act):
                    act.wait_ge(s.kp_normed, 1)
                    act.activation(kp[:], kp[:], ACT.Gelu).then_inc(s.kp_done, 1)
                    act.wait_ge(s.kp_turned, 1)
                    act.activation(kpT[:], st.ps[:, 1, 0:KT * B].rearrange("p (k b) -> p k b", k=KT), ACT.Copy).then_inc(s.kpT_done, 1)
                    act.wait_ge(s.kern_step, 3)
                    act.activation(kern8[:], kern8[:], ACT.Exp).then_inc(s.kern_exp, 1)
                    act.wait_ge(s.spread_ready, 1)
                    act.activation(kern[:].rearrange("p (n b) w -> p n (b w)", b=2), st.ps[:, 3:7, 0:2 * W2], ACT.Copy).then_inc(s.spread_act, 1)

                @block.vector
                def _(dve):
                    dve.wait_ge(s.rows_loaded, 16)
                    dve.wait_ge(s.k1_ready, 1)
                    dve.tensor_tensor(kp[:], st.ps[0:B, 0, 0:D], kb1, ALU.add).then_inc(s.kp_step, 1)
                    dve.wait_ge(s.kp_step, 1)
                    dve.bn_stats(kstats[:], kp[:]).then_inc(s.kp_step, 1)
                    dve.wait_ge(s.kp_step, 2)
                    dve.bn_aggr(kmv[:], kstats[:]).then_inc(s.kp_step, 1)
                    dve.wait_ge(s.kp_step, 3)
                    dve.scalar_tensor_tensor(kp[:], kp[:], kmv[:, 0:1], kg, ALU.subtract, ALU.mult).then_inc(s.kp_step, 1)
                    dve.wait_ge(s.kp_step, 4)
                    dve.wait_ge(s.krstd_done, 1)
                    dve.scalar_tensor_tensor(kp[:], kp[:], krstd[:, 0:1], ks, ALU.mult, ALU.add).then_inc(s.kp_normed, 1)
                    dve.wait_ge(s.k2_ready, 1)
                    dve.tensor_tensor(kern8[:].rearrange("b h t -> b (h t)"), st.ps[0:B, 2, 0:W2], kb2, ALU.add).then_inc(s.kern_step, 1)
                    dve.wait_ge(s.kern_step, 1)
                    dve.tensor_reduce(kmax[:], kern8[:], AX.X, ALU.max).then_inc(s.kern_step, 1)
                    dve.wait_ge(s.kern_step, 2)
                    dve.tensor_tensor(kern8[:], kern8[:], kmax[:].unsqueeze(2).to_broadcast([B, H, TAPS]), ALU.subtract).then_inc(s.kern_step, 1)
                    dve.wait_ge(s.kern_exp, 1)
                    dve.tensor_reduce(ksum[:], kern8[:], AX.X, ALU.add).then_inc(s.kern_step, 1)
                    dve.wait_ge(s.kern_step, 4)
                    dve.reciprocal(kmax[:], ksum[:]).then_inc(s.kern_step, 1)
                    dve.wait_ge(s.kern_step, 5)
                    dve.tensor_tensor(kern8[:], kern8[:], kmax[:].unsqueeze(2).to_broadcast([B, H, TAPS]), ALU.mult).then_inc(s.kern8_done, 1)
                    dve.wait_ge(s.mask_loaded, 16)
                    dve.tensor_scalar(keep[:], m_u8[:], 0, None, ALU.is_equal).then_inc(s.keep_done, 1)
                    dve.wait_ge(s.keep_done, 1)
                    dve.tensor_scalar(mask_add[:], keep[:], 1.0, -MASKED, ALU.subtract, ALU.mult).then_inc(s.keep_done, 1)

        shift = [st.shift[0:S, r:r + S] for r in range(3)]
        conv = Convolution(kern=kern, shift=shift, keep=keep[:], mask=mask_add[:])
        attention(nc, st, "l2x_a", H, 16, False, weights(st, "a7"), bias={"o": st.w["a7bo"]}, conv=conv)
def k_major(w):
    n_in, n_out = w.shape
    return w.reshape(n_in // P, P, n_out).transpose(1, 0, 2).reshape(P, -1)


def per_partition(v):
    return v.reshape(-1, P).T


def on_all(v):
    return np.broadcast_to(v.reshape(1, -1), (P, v.size))


def tables():
    out = {}
    out["ident"] = np.eye(P, dtype=np.float32)
    causal = np.triu(np.ones((S, S), bool), 1)
    out["shift"] = np.eye(P, S + 2, 1, dtype=np.float32)
    for hd in (16, 64):
        out[f"head_mask{hd}"] = (np.arange(P)[:, None] // hd == np.arange(P // hd)[None, :]).astype(np.float32)
    out["causal"] = np.concatenate([np.where(causal, MASKED, 0.0), np.zeros((P - S, S))]).astype(np.float32)
    return out


def rope_of_16():
    inv = 1.0 / (10000.0 ** (np.arange(0, 16, 2, dtype=np.float32) / np.float32(16)))
    freq = np.outer(np.arange(KEYS, dtype=np.float32), inv.astype(np.float32)).astype(np.float32)
    angle = np.concatenate([freq, freq], 1)[:, np.arange(P) % 16].T
    sign = np.where(np.arange(P) % 16 < 8, -1.0, 1.0).astype(np.float32)[:, None]
    return np.cos(angle).astype(np.float32), (np.sin(angle) * sign).astype(np.float32)


def swap_halves(w, heads):
    return w.reshape(D, heads, 2, D // heads // 2)[:, :, ::-1].reshape(D, D)


def rope_of_32():
    half = np.arange(P) % 16
    inv = (np.float32(1.0) / np.power(np.float32(10000.0), np.arange(16, dtype=np.float32) / np.float32(16))).astype(np.float32)
    angle = (np.arange(S, dtype=np.float32)[None, :] * inv[half][:, None]).astype(np.float32)
    sign = np.where(np.arange(P) % 32 < 16, -1.0, 1.0).astype(np.float32)[:, None]
    return np.cos(angle), np.sin(angle) * sign


def position_table():
    pos = np.arange(-(S - 1), S, dtype=np.float32)
    inv = (1.0 / np.power(np.float32(10000.0), np.arange(0, D, 2, dtype=np.float32) / np.float32(D))).astype(np.float32)
    ang = (pos[:, None] * inv[None, :]).astype(np.float32)
    return np.stack([np.sin(ang).T, np.cos(ang).T], 1).astype(np.float32).reshape(P, -1)


def rows_on_partitions(*parts):
    rows = np.concatenate(parts)
    return np.concatenate([rows, np.zeros((P - len(rows), rows.shape[1]), rows.dtype)])


def tile_rows(w):
    return np.concatenate([w[..., :P, :], w[..., P:, :]], -1)


def expert_units(a):
    keys, values = a["L1_ffn_keys"], a["L1_ffn_values"]
    first = tile_rows(np.concatenate([keys[0::2], keys[1::2]], -1))
    second = np.concatenate([values[0::2], values[1::2]], -1)
    l1 = np.concatenate([first, second], -1)

    f = 256
    sw, sb, sm = a["L2_ffn_s_fc1_w"], a["L2_ffn_s_fc1_b"], a["L2_ffn_s_geglu_mult"]
    parts = [np.concatenate([sw[c:c + f], sw[2 * f + c:2 * f + c + f]]) for c in (0, f)]
    w1 = np.concatenate([a["L2_ffn_fc1_w"], np.stack(parts)]).transpose(0, 2, 1)
    b1 = np.concatenate([a["L2_ffn_fc1_b"], np.stack([np.concatenate([sb[c:c + f], sb[2 * f + c:2 * f + c + f]]) for c in (0, f)])])
    mult = np.concatenate([a["L2_ffn_geglu_mult"], np.stack([sm[:f], sm[f:]])])
    w2 = np.concatenate([a["L2_ffn_fc2_w"], np.stack([a["L2_ffn_s_fc2_w"][:, :f], a["L2_ffn_s_fc2_w"][:, f:]])]).transpose(0, 2, 1)
    cols = lambda v: v.reshape(len(v), -1, P).transpose(0, 2, 1)
    l2 = np.concatenate([tile_rows(w1), tile_rows(w2), cols(b1), cols(mult)], -1)

    w1 = np.concatenate([a["L3_ffn_W1_s"], a["L3_ffn_W1_r"]])
    b1 = np.concatenate([a["L3_ffn_b1_s"], a["L3_ffn_b1_r"]])
    w2 = np.concatenate([a["L3_ffn_W2_s"], a["L3_ffn_W2_r"]])
    w1 = w1.reshape(10, D, 4, 256).transpose(0, 2, 1, 3).reshape(40, D, 256)
    l3 = np.concatenate([tile_rows(w1), tile_rows(w2.reshape(40, 256, D)), cols(b1.reshape(40, 256))], -1)
    return {"l1_ffn_units": l1, "l2_ffn_units": l2, "l3_ffn_units": l3}


def pack_plan():
    T = lambda n: (lambda a: k_major(a[n].T))
    N = lambda n: (lambda a: k_major(a[n]))
    col = lambda n: (lambda a: per_partition(a[n]))
    row = lambda n: (lambda a: on_all(a[n]))
    plan = [[] for _ in range(12)]
    plan[0] = [("a0q", 512, T("L0_attn_Wq")), ("a0k", 512, T("L0_attn_Wk")),
               ("a0v", 512, T("L0_attn_Wv")), ("a0o", 512, T("L0_attn_Wo"))]
    plan[1] = [("a1q", 512, T("L0_xattn_Wq")), ("a1k", 512, T("L0_xattn_Wk")),
               ("a1v", 512, T("L0_xattn_Wv")), ("a1o", 512, T("L0_xattn_Wp")),
               ("a1bq", 2, col("L0_xattn_bq")),
               ("a1bk", 2, col("L0_xattn_bk")), ("a1bv", 256, row("L0_xattn_bv")), ("a1bo", 256, row("L0_xattn_bp"))]
    plan[2] = [("f2w", 512, N("L0_ffn_weight")), ("f2g", 256, row("L0_ffn_ln_gamma")), ("f2b", 256, row("L0_ffn_ln_beta"))]
    plan[3] = [("m_in", 2048, T("L1_attn_w_in")), ("m_conv", 16, lambda a: a["L1_attn_w_conv"].reshape(4, P, 4).transpose(1, 0, 2).reshape(P, 16)),
               ("m_xproj", 384, T("L1_attn_w_xproj")),
               ("m_dt", 512, lambda a: np.concatenate([a["L1_attn_w_dt"].T, np.zeros((64, 512), np.float32)])),
               ("m_bdt", 4, col("L1_attn_b_dt")),
               ("m_alog", 64, lambda a: a["L1_attn_A_log"].reshape(4, P, 16).transpose(1, 0, 2).reshape(P, 64)),
               ("m_d", 4, col("L1_attn_D")), ("m_out", 1024, T("L1_attn_w_out"))]
    plan[4] = [("a4q", 2048, N("L1_xattn_Wq")), ("a4k", 2048, N("L1_xattn_Wk")), ("a4v", 2048, N("L1_xattn_Wv")),
               ("a4o", 2048, N("L1_xattn_Wo")), ("a4bq", 8, col("L1_xattn_bq")), ("a4bk", 8, col("L1_xattn_bk")),
               ("a4bv", 1024, row("L1_xattn_bv")), ("a4bo", 256, row("L1_xattn_bo"))]
    plan[5] = [("f5q", 512, N("L1_ffn_wq")), ("f5k", 512, N("L1_ffn_wk")), ("f5v", 512, N("L1_ffn_wv")),
               ("f5o", 512, N("L1_ffn_wo")), ("f5p", 512, N("L1_ffn_wp")), ("f5pe", 2 * (2 * S - 1), lambda a: position_table()),
               ("f5g1", 256, row("L1_ffn_ln1_g")), ("f5s1", 256, row("L1_ffn_ln1_b")), ("f5g2", 256, row("L1_ffn_ln2_g")),
               ("f5s2", 256, row("L1_ffn_ln2_b")), ("f5sel", 64, N("L1_ffn_sel_w"))]
    plan[6] = [("a6q", 512, T("L2_attn_Wq")), ("a6k", 512, T("L2_attn_Wk")), ("a6o", 512, T("L2_attn_Wout")),
               ("a6rq", 512, lambda a: k_major(swap_halves(a["L2_attn_Wq"].T, 8))), ("a6rk", 512, lambda a: k_major(swap_halves(a["L2_attn_Wk"].T, 8))),
               ("a6vg", 560, lambda a: k_major(np.concatenate([a[f"L2_attn_W{n}"] for n in ("v", "ig", "og", "beta")]).T)),
               ("a6bgates", 24, lambda a: on_all(np.concatenate([a[f"L2_attn_b{n}"] for n in ("ig", "og", "beta")]))),
               ("a6norm", 256, row("L2_attn_norm_w")), ("a6bo", 256, row("L2_attn_bout")),
               ("a6cos", S, lambda a: rope_of_32()[0]), ("a6sin", S, lambda a: rope_of_32()[1]),
               ("a6heads", P // 32, lambda a: (np.arange(P)[:, None] // 32 == np.arange(P // 32)[None, :]).astype(np.float32))]
    plan[7] = [("a7q", 512, N("L2_xattn_Wq")), ("a7k", 512, N("L2_xattn_Wk")), ("a7v", 512, N("L2_xattn_Wv")),
               ("a7o", 512, N("L2_xattn_proj_W")), ("a7bo", 256, row("L2_xattn_proj_b")), ("a7hw", 1024, N("L2_xattn_hist_W")),
               ("a7cw1", 512, N("L2_xattn_ctx_W1")), ("a7cb1", 1, col("L2_xattn_ctx_b1")), ("a7cw2", 1, N("L2_xattn_ctx_W2")),
               ("a7cb2", 1, row("L2_xattn_ctx_b2")), ("a7kw1", 1024, N("L2_xattn_kg_W1")), ("a7kw2", 288, N("L2_xattn_kg_W2"))]
    plan[8] = [("f8gate", 30, T("L2_ffn_gate_w")),
               ("f8b2", 256, lambda a: rows_on_partitions(a["L2_ffn_fc2_b"], a["L2_ffn_s_fc2_b"][None]))]
    plan[11] = [("f11gate", 16, N("L3_ffn_centroids")), ("f11gs", 2, col("L3_ffn_g_shared")), ("f11gr", 2, col("L3_ffn_g_routed")),
                ("f11b2", 256, lambda a: rows_on_partitions(a["L3_ffn_b2_s"], a["L3_ffn_b2_r"]))]
    plan[9] = [("a9q", 512, N("L3_attn_wqk")), ("a9o", 512, N("L3_attn_wov"))]
    plan[10] = [("a10q", 512, T("L3_xattn_W_q")), ("a10k", 512, T("L3_xattn_W_k")),
                ("a10v", 512, T("L3_xattn_W_v")), ("a10o", 512, T("L3_xattn_W_o")),
                ("a10cos", KEYS, lambda a: rope_of_16()[0]), ("a10sin", KEYS, lambda a: rope_of_16()[1]), ("a10rq", 512, lambda a: k_major(swap_halves(a["L3_xattn_W_q"].T, 16))), ("a10rk", 512, lambda a: k_major(swap_halves(a["L3_xattn_W_k"].T, 16)))]
    return plan


TABLES = [("ident", P), ("causal", S), ("shift", S + 2), ("head_mask16", P // 16), ("head_mask64", P // 64)]


def lay_out(a):
    out = {
        "x_tokens": a["x"].transpose(1, 0, 2),
        "x_features": a["x"].reshape(B, S, KT, P).transpose(3, 2, 0, 1),
        "ctx_features": a["ctx_1024"].reshape(B, KEYS, KT, P).transpose(3, 0, 2, 1),
        "key_mask": a["mask_Bx1xSxS2_ik0"].reshape(B, S, KEYS),
        "self_mask": a["mask_SxS_bc0"],
    }
    out["kernel_net_rows"] = on_all(np.concatenate([a["L2_xattn_kg_b1"], a["L2_xattn_kg_ln_g"], a["L2_xattn_kg_ln_b"], a["L2_xattn_kg_b2"]]))[0:B]
    out["hist_rows"] = on_all(np.concatenate([a["L2_xattn_hist_b"], a["L2_xattn_hist_ln_g"], a["L2_xattn_hist_ln_b"]]))
    out.update(expert_units(a))
    made = tables()
    out["tables"] = np.concatenate([made[n] for n, _ in TABLES], 1)
    for i, parts in enumerate(pack_plan()):
        if parts:
            made = [np.broadcast_to(f(a), (P, n)) for _, n, f in parts]
            out[f"pack{i}"] = np.concatenate(made, 1)
    return {k: np.ascontiguousarray(v) for k, v in out.items()}


def program(nc, dram, out, stages):
    plan = pack_plan()
    st = State()
    with ExitStack() as ctx:
        def sb(n, shape, dt=F32):
            return ctx.enter_context(nc.sbuf_tensor(n, shape, dt))

        st.X = sb("X", [S, B, D])
        st.XT = sb("XT", [P, KT, B, S])
        st.ctxT = sb("ctxT", [P, B, KT, KEYS])
        st.ps = ctx.enter_context(nc.psum_tensor("ps", [P, 8, BANK], F32))
        st.resid, st.xnew = sb("resid", [S, TURN, D]), sb("xnew", [S, TURN, D])
        st.stats, st.meanvar = sb("stats", [S, TURN, 6]), sb("meanvar", [S, TURN, 2])
        st.vareps, st.rstd = sb("vareps", [S, TURN]), sb("rstd", [S, TURN])
        st.minus_half = sb("minus_half", [P, 1])
        st.tables = sb("tables_sb", [P, sum(n for _, n in TABLES)])
        ends = np.cumsum([n for _, n in TABLES])
        st.ident, st.causal, st.shift, heads16, heads64 = (st.tables[:, int(end) - n:int(end)] for (_, n), end in zip(TABLES, ends))
        st.head_mask = {16: heads16, 64: heads64}
        st.w = {}
        size = [max([sum(n for _, n, _ in plan[i]) for i in stages if i % 2 == r] + [1]) for r in range(2)]
        region = [sb(f"weights{r}", [P, size[r]]) for r in range(2)]
        packs = {}
        for i in stages:
            at = 0
            for n, c, _ in plan[i]:
                st.w[n] = region[i % 2][:, at:at + c]
                at += c
            packs[i] = region[i % 2][:, 0:at]
        start_loaded = ctx.enter_context(nc.semaphore("start_loaded"))
        half_set = ctx.enter_context(nc.semaphore("half_set"))
        pack_loaded = {i: ctx.enter_context(nc.semaphore(f"pack{i}_loaded")) for i in packs}
        x_out = ctx.enter_context(nc.semaphore("x_out"))

        with nc.Block() as block:
            @block.sync
            def _(sp):
                sp.dma_start(st.X[:], dram["x_tokens"]).then_inc(start_loaded, 16)
                sp.dma_start(st.XT[:], dram["x_features"]).then_inc(start_loaded, 16)
                sp.dma_start(st.tables[:], dram["tables"]).then_inc(start_loaded, 16)
                sp.dma_start(packs[stages[0]], dram[f"pack{stages[0]}"]).then_inc(pack_loaded[stages[0]], 16)
                sp.dma_start(st.ctxT[:], dram["ctx_features"]).then_inc(start_loaded, 16)
                sp.wait_ge(start_loaded, 64)

            @block.gpsimd
            def _(pool):
                pool.memset(st.minus_half[:], -0.5).then_inc(half_set, 1)

        for n, i in enumerate(stages):
            with nc.Block() as block:
                @block.sync
                def _(sp, n=n, i=i):
                    if n + 1 < len(stages):
                        nxt = stages[n + 1]
                        sp.dma_start(packs[nxt], dram[f"pack{nxt}"]).then_inc(pack_loaded[nxt], 16)
                    sp.wait_ge(pack_loaded[i], 16)
            STAGES[i](nc, st, dram)

        with nc.Block() as block:
            @block.sync
            def _(sp):
                sp.dma_start(out.rearrange("b t d -> t b d"), st.X[:]).then_inc(x_out, 16)
                sp.wait_ge(x_out, 16)


def weights(st, prefix):
    view = lambda n: st.w[prefix + n].rearrange("p (k n) -> p k n", k=KT) if prefix + n in st.w else None
    return Attention(q=view("q"), k=view("k"), v=view("v"), o=st.w[prefix + "o"].rearrange("p (m n) -> p m n", n=D))


def l0_attn(nc, st, dram):
    attention(nc, st, "l0a", 16, 16, False, weights(st, "a0"), mask=st.causal[0:S, :])


def l0_xattn(nc, st, dram):
    bias = scaled_query_bias(nc, st, "a1", 0.25)
    attention(nc, st, "l0x", 16, 16, True, weights(st, "a1"), bias=bias, plus_one=True)


def l1_xattn(nc, st, dram):
    bias = scaled_query_bias(nc, st, "a4", 0.125)
    attention(nc, st, "l1x", 16, 64, True, weights(st, "a4"), bias=bias)


def l3_xattn(nc, st, dram):
    view = lambda n: st.w[n].rearrange("p (k n) -> p k n", k=KT)
    rope = Rotation(cos=st.w["a10cos"], sin=st.w["a10sin"], q=view("a10rq"), k=view("a10rk"))
    attention(nc, st, "l3x", 16, 16, True, weights(st, "a10"), mask_dram=dram["key_mask"], rope=rope)


def scaled_query_bias(nc, st, prefix, scale):
    bq = st.w[prefix + "bq"]
    with stage_sems(nc, ["bias_scaled"]) as s, nc.Block() as block:
        @block.vector
        def _(dve):
            dve.tensor_scalar(bq, bq, scale, None, ALU.mult).then_inc(s.bias_scaled, 1)
    return {"q": bq, "k": st.w[prefix + "bk"], "v": st.w[prefix + "bv"], "o": st.w[prefix + "bo"]}


def l3_attn(nc, st, dram):
    attention(nc, st, "l3a", 1, 256, False, weights(st, "a9"), mask=st.causal[0:S, :])


STAGES = {0: l0_attn, 1: l0_xattn, 2: l0_ffn, 3: l1_attn, 4: l1_xattn, 5: l1_ffn, 6: l2_attn, 7: l2_xattn, 8: l2_ffn, 9: l3_attn, 10: l3_xattn, 11: l3_ffn}


def build(nc, arrays, stages=range(12)):
    dram = {n: nc.dram_tensor(n, v.shape, mybir.dt.from_np(v.dtype), kind="ExternalInput").ap() for n, v in arrays.items()}
    out = nc.dram_tensor("out_0_dram", (B, S, D), F32, kind="ExternalOutput").ap()
    program(nc, dram, out, list(stages))


def kernel(**inputs):
    import concourse.bacc as bacc
    from concourse.bass_utils import run_bass_kernel_spmd

    arrays = lay_out({k: np.asarray(v) for k, v in inputs.items()})
    nc = bacc.Bacc("TRN2", target_bir_lowering=False, num_devices=1)
    build(nc, arrays)
    return run_bass_kernel_spmd(nc, [arrays], core_ids=[0]).results[0]["out_0_dram"]
```
